# Optimizing a Trainium2 kernel written in Bass

```python
import numpy as np
import jax
import jax.numpy as jnp

def _softmax(x, axis=-1):
    return jax.nn.softmax(x, axis=axis)

def _gelu(x):
    return jax.nn.gelu(x, approximate=True)

def _silu(x):
    return jax.nn.silu(x)

def _sigmoid(x):
    return jax.nn.sigmoid(x)

def _layernorm(x, axis=-1, eps=1e-05):
    m = jnp.mean(x, axis=axis, keepdims=True)
    v = jnp.var(x, axis=axis, keepdims=True)
    return (x - m) / jnp.sqrt(v + eps)

def _scatter_add(tgt, idx, src, axis=0):
    return tgt.at[idx].add(src)

def _segment_sum(src, seg, n):
    return jax.ops.segment_sum(src, seg, n)
kernel_name = 'mk_seq_postln_d4_jaxref_r8_1915d8'

def setup_inputs(seed: int=0):
    np.random.seed(seed)
    _w = jnp.asarray

    def _L0_attn_setup():
        import jax, jax.numpy as jnp
        import numpy as np
        import math
        DIM = 128
        H = 16
        DK = DIM // H
        SEG = 64
        NN = 2
        DIL = 4
        B, L = (2, 1024)

        def _attn(q, k, v):
            scores = jnp.einsum('bshqd,bshkd->bshqk', q, k) / math.sqrt(q.shape[-1])
            a = jax.nn.softmax(scores, axis=-1)
            return jnp.einsum('bshqk,bshkd->bshqd', a, v)
        key = jax.random.key(seed)
        ks = jax.random.split(key, 9)
        scale = 1.0 / math.sqrt(DIM)

        def lin(k):
            return jax.random.normal(k, (DIM, DIM), jnp.float32) * scale
        return {'x': jax.random.normal(ks[0], (B, L, DIM), jnp.float32), 'Wq': lin(ks[1]), 'bq': jnp.zeros((DIM,), jnp.float32), 'Wk': lin(ks[2]), 'bk': jnp.zeros((DIM,), jnp.float32), 'Wv': lin(ks[3]), 'bv': jnp.zeros((DIM,), jnp.float32), 'Wo': lin(ks[4]), 'bo': jnp.zeros((DIM,), jnp.float32)}
    _L0_attn_in = _L0_attn_setup()

    def _L0_ffn_setup():
        import jax, jax.numpy as jnp
        import numpy as np
        D_MODEL = 128
        EXPANSION = 4
        D_HIDDEN = D_MODEL * EXPANSION
        NUM_STAGES = int(np.log2(D_HIDDEN))

        def butterfly(y, weights, dim):
            lead = y.shape[:-1]
            for stage in range(weights.shape[0]):
                s = 2 ** stage
                nb = dim // (2 * s)
                yr = y.reshape(*lead, nb, 2, s)
                a = yr[..., 0, :]
                b = yr[..., 1, :]
                w = weights[stage].reshape(nb, s, 2, 2)
                na = w[..., 0, 0] * a + w[..., 0, 1] * b
                nb2 = w[..., 1, 0] * a + w[..., 1, 1] * b
                y = jnp.stack([na, nb2], axis=-2).reshape(*lead, dim)
            return y
        key = jax.random.key(seed)
        ks = jax.random.split(key, 6)
        B, S = (4, 256)
        x = jax.random.normal(ks[0], (B, S, D_MODEL), jnp.float32)
        W_exp = jax.random.normal(ks[1], (D_MODEL, D_HIDDEN), jnp.float32) * 0.02
        b_exp = jnp.zeros((D_HIDDEN,), jnp.float32)
        up_weights = jax.random.normal(ks[2], (NUM_STAGES, D_HIDDEN // 2, 2, 2), jnp.float32) * 0.02
        up_bias = jnp.zeros((D_HIDDEN,), jnp.float32)
        down_weights = jax.random.normal(ks[3], (NUM_STAGES, D_HIDDEN // 2, 2, 2), jnp.float32) * 0.02
        W_con = jax.random.normal(ks[4], (D_HIDDEN, D_MODEL), jnp.float32) * 0.02
        b_con = jnp.zeros((D_MODEL,), jnp.float32)
        down_bias = jnp.zeros((D_MODEL,), jnp.float32)
        return dict(x=x, W_exp=W_exp, b_exp=b_exp, up_weights=up_weights, up_bias=up_bias, down_weights=down_weights, W_con=W_con, b_con=b_con, down_bias=down_bias)
    _L0_ffn_in = _L0_ffn_setup()

    def _L1_attn_setup():
        import jax, jax.numpy as jnp
        import numpy as np
        B, S, D_MODEL, H, D = (2, 256, 128, 16, 64)
        SCALE = 1.0 / float(np.sqrt(D))

        def _rope(t, c, s):
            d2 = t.shape[-1] // 2
            t1, t2 = (t[..., :d2], t[..., d2:])
            return jnp.concatenate([t1 * c - t2 * s, t1 * s + t2 * c], axis=-1)
        key = jax.random.key(seed)
        ks = jax.random.split(key, 5)
        x = jax.random.normal(ks[0], (B, S, D_MODEL), jnp.float32)
        qkv_w = jax.random.normal(ks[1], (3 * H * D, D_MODEL), jnp.float32) * 0.02
        out_w = jax.random.normal(ks[2], (D_MODEL, H * D), jnp.float32) * 0.02
        bias_p = jax.random.uniform(ks[3], (H, 1, 1), jnp.float32) * 2.0
        bias_a = jax.random.uniform(ks[4], (H, 1, 1), jnp.float32)
        rope_freqs = 10000.0 ** (-jnp.arange(D // 2, dtype=jnp.float32) / (D // 2))
        return {'x': x, 'qkv_w': qkv_w, 'out_w': out_w, 'bias_p': bias_p, 'bias_a': bias_a, 'rope_freqs': rope_freqs}
    _L1_attn_in = _L1_attn_setup()

    def _L1_ffn_setup():
        import jax, jax.numpy as jnp
        import numpy as np
        DIM = 128
        DEPTH = 2
        HEADS = 8
        DIM_HEAD = 64
        WINDOW = 64
        INNER = HEADS * DIM_HEAD
        HID = int(DIM * 4 * 2 / 3)
        B, N = (2, 1024)
        QK_SCALE = 8.0

        def shift_token(t):
            t1, t2 = jnp.split(t, 2, axis=-1)
            t2 = jnp.pad(t2, ((0, 0), (1, 0), (0, 0)))[:, :-1]
            return jnp.concatenate([t1, t2], axis=-1)

        def l2norm(t):
            return t / jnp.clip(jnp.linalg.norm(t, axis=-1, keepdims=True), 1e-12)

        def rotate_half(x):
            x1, x2 = jnp.split(x, 2, axis=-1)
            return jnp.concatenate([-x2, x1], axis=-1)

        def rotary_xpos(q, k):
            n = q.shape[-2]
            half_idx = jnp.arange(0, DIM_HEAD, 2, dtype=jnp.float32)
            inv_freq = 1.0 / 10000.0 ** (half_idx / DIM_HEAD)
            t = jnp.arange(n, dtype=jnp.float32)
            freqs = t[:, None] * inv_freq[None, :]
            freqs = jnp.concatenate([freqs, freqs], axis=-1)
            base = (half_idx + 0.4 * DIM_HEAD) / (1.4 * DIM_HEAD)
            power = (t - n // 2) / float(WINDOW // 2)
            scale = base[None, :] ** power[:, None]
            scale = jnp.concatenate([scale, scale], axis=-1)
            cos, sin = (jnp.cos(freqs), jnp.sin(freqs))
            q = q * cos * scale + rotate_half(q) * sin * scale
            k = k * cos / scale + rotate_half(k) * sin / scale
            return (q, k)

        def local_attention(q, k, v):
            b, h, n, d = q.shape
            w = n // WINDOW
            bq = q.reshape(b, h, w, WINDOW, d) * QK_SCALE
            bk = k.reshape(b, h, w, WINDOW, d)
            bv = v.reshape(b, h, w, WINDOW, d)

            def look_around(t):
                p = jnp.pad(t, ((0, 0), (0, 0), (1, 0), (0, 0), (0, 0)))
                return jnp.concatenate([p[:, :, :w], p[:, :, 1:]], axis=3)
            bk, bv = (look_around(bk), look_around(bv))
            bt = jnp.arange(n).reshape(w, WINDOW)
            btp = jnp.pad(bt, ((1, 0), (0, 0)), constant_values=-1)
            btk = jnp.concatenate([btp[:w], btp[1:]], axis=1)
            sim = jnp.einsum('bhwid,bhwjd->bhwij', bq, bk)
            i = bt[:, :, None]
            j = btk[:, None, :]
            mask = (i < j) | (i > j + WINDOW) | (j == -1)
            sim = jnp.where(mask, -jnp.finfo(sim.dtype).max, sim)
            attn = jax.nn.softmax(sim, axis=-1)
            out = jnp.einsum('bhwij,bhwjd->bhwid', attn, bv)
            return out.reshape(b, h, n, d)

        def _layer(x, wqkv, qs, ksc, wo, lg, lb, w1, b1, w2, b2):
            b, n, _ = x.shape
            h = shift_token(x)
            qkv = h @ wqkv
            q, k, v = jnp.split(qkv, 3, axis=-1)
            to_heads = lambda t: t.reshape(b, n, HEADS, DIM_HEAD).transpose(0, 2, 1, 3)
            q, k, v = (to_heads(q), to_heads(k), to_heads(v))
            q = l2norm(q) * qs
            k = l2norm(k) * ksc
            q, k = rotary_xpos(q, k)
            o = local_attention(q, k, v)
            o = o.transpose(0, 2, 1, 3).reshape(b, n, INNER)
            x = x + o @ wo
            h = shift_token(x)
            mu = h.mean(-1, keepdims=True)
            var = h.var(-1, keepdims=True)
            h = (h - mu) / jnp.sqrt(var + 1e-05) * lg + lb
            h = h @ w1 + b1
            a, g = jnp.split(h, 2, axis=-1)
            h = a * jax.nn.gelu(g, approximate=False)
            x = x + h @ w2 + b2
            return x
        key = jax.random.key(seed)
        ks = jax.random.split(key, 6)
        return {'x': jax.random.normal(ks[0], (B, N, DIM), jnp.float32), 'wqkv': jax.random.normal(ks[1], (DEPTH, DIM, 3 * INNER), jnp.float32) * 0.02, 'q_scale': jnp.ones((DEPTH, DIM_HEAD), jnp.float32), 'k_scale': jnp.ones((DEPTH, DIM_HEAD), jnp.float32), 'wo': jax.random.normal(ks[2], (DEPTH, INNER, DIM), jnp.float32) * 0.02, 'ln_g': jnp.ones((DEPTH, DIM), jnp.float32), 'ln_b': jnp.zeros((DEPTH, DIM), jnp.float32), 'w1': jax.random.normal(ks[3], (DEPTH, DIM, 2 * HID), jnp.float32) * 0.02, 'b1': jnp.zeros((DEPTH, 2 * HID), jnp.float32), 'w2': jax.random.normal(ks[4], (DEPTH, HID, DIM), jnp.float32) * 0.02, 'b2': jnp.zeros((DEPTH, DIM), jnp.float32)}
    _L1_ffn_in = _L1_ffn_setup()

    def _L2_attn_setup():
        import jax, jax.numpy as jnp
        import numpy as np
        import math
        DIM = 128
        HEADS = 16
        HEAD_DIM = DIM // HEADS
        key = jax.random.key(seed)
        ks = jax.random.split(key, 7)
        b, n = (2, 256)
        scale = 1.0 / math.sqrt(DIM)
        x = jax.random.normal(ks[0], (b, n, DIM), dtype=jnp.float32)
        Wq = jax.random.normal(ks[1], (DIM, DIM), dtype=jnp.float32) * scale
        Wk = jax.random.normal(ks[2], (DIM, DIM), dtype=jnp.float32) * scale
        Wv = jax.random.normal(ks[3], (DIM, DIM), dtype=jnp.float32) * scale
        Wo = jax.random.normal(ks[4], (DIM, DIM), dtype=jnp.float32) * scale
        bo = jnp.zeros((DIM,), dtype=jnp.float32)
        denom_bias = jnp.zeros((1, HEADS, 1, 1), dtype=jnp.float32)
        return {'x': x, 'Wq': Wq, 'Wk': Wk, 'Wv': Wv, 'Wo': Wo, 'bo': bo, 'denom_bias': denom_bias}
    _L2_attn_in = _L2_attn_setup()

    def _L2_ffn_setup():
        import jax, jax.numpy as jnp
        import numpy as np
        MODEL_DIM = 128
        HIDDEN = 256
        NUM_GROUPS = 2
        EXPERTS_PER_GP = 4
        NUM_EXPERTS = NUM_GROUPS * EXPERTS_PER_GP
        TOP_K = 2
        B, T = (2, 256)

        def _swiglu(x):
            a, b = jnp.split(x, 2, axis=-1)
            return jax.nn.silu(a) * b
        key = jax.random.key(seed)
        ks = jax.random.split(key, 7)
        s = 0.02
        return {'x': jax.random.normal(ks[0], (B, T, MODEL_DIM), jnp.float32), 'w_in': jax.random.normal(ks[1], (HIDDEN * 2, MODEL_DIM), jnp.float32) * s, 'w_out': jax.random.normal(ks[2], (MODEL_DIM, HIDDEN), jnp.float32) * s, 'w1': jax.random.normal(ks[3], (HIDDEN * 2, MODEL_DIM), jnp.float32) * s, 'w2': jax.random.normal(ks[4], (NUM_EXPERTS, MODEL_DIM, HIDDEN), jnp.float32) * s, 'wg': jax.random.normal(ks[5], (NUM_GROUPS, MODEL_DIM), jnp.float32) * s, 'we': jax.random.normal(ks[6], (NUM_EXPERTS, MODEL_DIM), jnp.float32) * s, 'gb': jnp.zeros((NUM_GROUPS,), jnp.float32), 'eb': jnp.zeros((NUM_EXPERTS,), jnp.float32)}
    _L2_ffn_in = _L2_ffn_setup()

    def _L3_attn_setup():
        import jax, jax.numpy as jnp
        import numpy as np
        D_MODEL = 128
        NUM_HEADS = 16
        HEAD_DIM = D_MODEL // NUM_HEADS
        EPS = 1e-08
        key = jax.random.key(seed)
        ks = jax.random.split(key, 6)
        B, T = (4, 256)
        s = 0.02
        return {'x': jax.random.normal(ks[0], (B, T, D_MODEL), dtype=jnp.float32), 'Wq': jax.random.normal(ks[1], (D_MODEL, D_MODEL), dtype=jnp.float32) * s, 'Wk': jax.random.normal(ks[2], (D_MODEL, D_MODEL), dtype=jnp.float32) * s, 'Wv': jax.random.normal(ks[3], (D_MODEL, D_MODEL), dtype=jnp.float32) * s, 'Wo': jax.random.normal(ks[4], (D_MODEL, D_MODEL), dtype=jnp.float32) * s, 'bo': jnp.zeros((D_MODEL,), dtype=jnp.float32)}
    _L3_attn_in = _L3_attn_setup()

    def _L3_ffn_setup():
        import jax, jax.numpy as jnp
        import numpy as np
        import math
        D_MODEL, D_FF, N_EXPERTS, TOP_K, N_SHARED = (128, 512, 8, 2, 1)
        B, T = (4, 128)
        SCALE = 1.0 / math.sqrt(N_SHARED + TOP_K / N_EXPERTS)
        key = jax.random.key(seed)
        ks = jax.random.split(key, 10)
        s1 = 1.0 / math.sqrt(D_MODEL)
        s2 = 1.0 / math.sqrt(D_FF)
        return {'x': jax.random.normal(ks[0], (B, T, D_MODEL), dtype=jnp.float32), 'w_router': jax.random.normal(ks[1], (N_EXPERTS, D_MODEL), dtype=jnp.float32) * s1, 'W1': jax.random.normal(ks[2], (N_EXPERTS, D_FF, D_MODEL), dtype=jnp.float32) * s1, 'b1': jax.random.normal(ks[3], (N_EXPERTS, D_FF), dtype=jnp.float32) * 0.02, 'W2': jax.random.normal(ks[4], (N_EXPERTS, D_MODEL, D_FF), dtype=jnp.float32) * s2, 'b2': jax.random.normal(ks[5], (N_EXPERTS, D_MODEL), dtype=jnp.float32) * 0.02, 'Ws1': jax.random.normal(ks[6], (D_FF, D_MODEL), dtype=jnp.float32) * s1, 'bs1': jax.random.normal(ks[7], (D_FF,), dtype=jnp.float32) * 0.02, 'Ws2': jax.random.normal(ks[8], (D_MODEL, D_FF), dtype=jnp.float32) * s2, 'bs2': jax.random.normal(ks[9], (D_MODEL,), dtype=jnp.float32) * 0.02}
    _L3_ffn_in = _L3_ffn_setup()
    _d = {'L0_attn_x': _L0_attn_in['x'], 'L0_attn_Wq': _L0_attn_in['Wq'], 'L0_attn_bq': _L0_attn_in['bq'], 'L0_attn_Wk': _L0_attn_in['Wk'], 'L0_attn_bk': _L0_attn_in['bk'], 'L0_attn_Wv': _L0_attn_in['Wv'], 'L0_attn_bv': _L0_attn_in['bv'], 'L0_attn_Wo': _L0_attn_in['Wo'], 'L0_attn_bo': _L0_attn_in['bo'], 'L0_ffn_W_exp': _L0_ffn_in['W_exp'], 'L0_ffn_b_exp': _L0_ffn_in['b_exp'], 'L0_ffn_up_weights': _L0_ffn_in['up_weights'], 'L0_ffn_up_bias': _L0_ffn_in['up_bias'], 'L0_ffn_down_weights': _L0_ffn_in['down_weights'], 'L0_ffn_W_con': _L0_ffn_in['W_con'], 'L0_ffn_b_con': _L0_ffn_in['b_con'], 'L0_ffn_down_bias': _L0_ffn_in['down_bias'], 'L1_attn_qkv_w': _L1_attn_in['qkv_w'], 'L1_attn_out_w': _L1_attn_in['out_w'], 'L1_attn_bias_p': _L1_attn_in['bias_p'], 'L1_attn_bias_a': _L1_attn_in['bias_a'], 'L1_attn_rope_freqs': _L1_attn_in['rope_freqs'], 'L1_ffn_wqkv': _L1_ffn_in['wqkv'], 'L1_ffn_q_scale': _L1_ffn_in['q_scale'], 'L1_ffn_k_scale': _L1_ffn_in['k_scale'], 'L1_ffn_wo': _L1_ffn_in['wo'], 'L1_ffn_ln_g': _L1_ffn_in['ln_g'], 'L1_ffn_ln_b': _L1_ffn_in['ln_b'], 'L1_ffn_w1': _L1_ffn_in['w1'], 'L1_ffn_b1': _L1_ffn_in['b1'], 'L1_ffn_w2': _L1_ffn_in['w2'], 'L1_ffn_b2': _L1_ffn_in['b2'], 'L2_attn_Wq': _L2_attn_in['Wq'], 'L2_attn_Wk': _L2_attn_in['Wk'], 'L2_attn_Wv': _L2_attn_in['Wv'], 'L2_attn_Wo': _L2_attn_in['Wo'], 'L2_attn_bo': _L2_attn_in['bo'], 'L2_attn_denom_bias': _L2_attn_in['denom_bias'], 'L2_ffn_w_in': _L2_ffn_in['w_in'], 'L2_ffn_w_out': _L2_ffn_in['w_out'], 'L2_ffn_w1': _L2_ffn_in['w1'], 'L2_ffn_w2': _L2_ffn_in['w2'], 'L2_ffn_wg': _L2_ffn_in['wg'], 'L2_ffn_we': _L2_ffn_in['we'], 'L2_ffn_gb': _L2_ffn_in['gb'], 'L2_ffn_eb': _L2_ffn_in['eb'], 'L3_attn_Wq': _L3_attn_in['Wq'], 'L3_attn_Wk': _L3_attn_in['Wk'], 'L3_attn_Wv': _L3_attn_in['Wv'], 'L3_attn_Wo': _L3_attn_in['Wo'], 'L3_attn_bo': _L3_attn_in['bo'], 'L3_ffn_w_router': _L3_ffn_in['w_router'], 'L3_ffn_W1': _L3_ffn_in['W1'], 'L3_ffn_b1': _L3_ffn_in['b1'], 'L3_ffn_W2': _L3_ffn_in['W2'], 'L3_ffn_b2': _L3_ffn_in['b2'], 'L3_ffn_Ws1': _L3_ffn_in['Ws1'], 'L3_ffn_bs1': _L3_ffn_in['bs1'], 'L3_ffn_Ws2': _L3_ffn_in['Ws2'], 'L3_ffn_bs2': _L3_ffn_in['bs2']}
    _x0 = _d['L0_attn_x']
    _d['L0_attn_x'] = jax.random.normal(jax.random.fold_in(jax.random.key(seed), 1), (2, 1024, 128), dtype=_x0.dtype)
    del _x0
    return _d

def reference(L0_attn_x, L0_attn_Wq, L0_attn_bq, L0_attn_Wk, L0_attn_bk, L0_attn_Wv, L0_attn_bv, L0_attn_Wo, L0_attn_bo, L0_ffn_W_exp, L0_ffn_b_exp, L0_ffn_up_weights, L0_ffn_up_bias, L0_ffn_down_weights, L0_ffn_W_con, L0_ffn_b_con, L0_ffn_down_bias, L1_attn_qkv_w, L1_attn_out_w, L1_attn_bias_p, L1_attn_bias_a, L1_attn_rope_freqs, L1_ffn_wqkv, L1_ffn_q_scale, L1_ffn_k_scale, L1_ffn_wo, L1_ffn_ln_g, L1_ffn_ln_b, L1_ffn_w1, L1_ffn_b1, L1_ffn_w2, L1_ffn_b2, L2_attn_Wq, L2_attn_Wk, L2_attn_Wv, L2_attn_Wo, L2_attn_bo, L2_attn_denom_bias, L2_ffn_w_in, L2_ffn_w_out, L2_ffn_w1, L2_ffn_w2, L2_ffn_wg, L2_ffn_we, L2_ffn_gb, L2_ffn_eb, L3_attn_Wq, L3_attn_Wk, L3_attn_Wv, L3_attn_Wo, L3_attn_bo, L3_ffn_w_router, L3_ffn_W1, L3_ffn_b1, L3_ffn_W2, L3_ffn_b2, L3_ffn_Ws1, L3_ffn_bs1, L3_ffn_Ws2, L3_ffn_bs2):

    def _L0_attn_ref(x, Wq, bq, Wk, bk, Wv, bv, Wo, bo):
        import jax, jax.numpy as jnp
        import numpy as np
        import math
        DIM = 128
        H = 16
        DK = DIM // H
        SEG = 64
        NN = 2
        DIL = 4
        B, L = (2, 1024)

        def _attn(q, k, v):
            scores = jnp.einsum('bshqd,bshkd->bshqk', q, k) / math.sqrt(q.shape[-1])
            a = jax.nn.softmax(scores, axis=-1)
            return jnp.einsum('bshqk,bshkd->bshqd', a, v)
        Bx, Lx, C = x.shape
        pad = -Lx % SEG

        def proj_chunk(W, b):
            t = x @ W + b
            t = jnp.pad(t, ((0, 0), (0, pad), (0, 0)))
            S = t.shape[1] // SEG
            t = t.reshape(Bx, S, SEG, H, DK)
            return t.transpose(0, 1, 3, 2, 4)
        q = proj_chunk(Wq, bq)
        k = proj_chunk(Wk, bk)
        v = proj_chunk(Wv, bv)
        S = q.shape[1]
        out = _attn(q, k, v)
        dil_idx = jnp.arange(0, SEG, DIL)
        kd = k[:, :, :, dil_idx, :]
        vd = v[:, :, :, dil_idx, :]
        seg_ids = jnp.arange(S)
        w = 1.0 / (2 * NN)
        for off in range(1, NN + 1):
            for sign in (-1, 1):
                n = seg_ids + sign * off
                valid = (n >= 0) & (n < S)
                nc = jnp.clip(n, 0, S - 1)
                cross = _attn(q, kd[:, nc], vd[:, nc])
                out = out + jnp.where(valid[None, :, None, None, None], cross * w, 0.0)
        out = out.transpose(0, 1, 3, 2, 4).reshape(Bx, S * SEG, C)
        out = out[:, :Lx, :]
        return out @ Wo + bo

    def _L0_ffn_ref(x, W_exp, b_exp, up_weights, up_bias, down_weights, W_con, b_con, down_bias):
        import jax, jax.numpy as jnp
        import numpy as np
        D_MODEL = 128
        EXPANSION = 4
        D_HIDDEN = D_MODEL * EXPANSION
        NUM_STAGES = int(np.log2(D_HIDDEN))

        def butterfly(y, weights, dim):
            lead = y.shape[:-1]
            for stage in range(weights.shape[0]):
                s = 2 ** stage
                nb = dim // (2 * s)
                yr = y.reshape(*lead, nb, 2, s)
                a = yr[..., 0, :]
                b = yr[..., 1, :]
                w = weights[stage].reshape(nb, s, 2, 2)
                na = w[..., 0, 0] * a + w[..., 0, 1] * b
                nb2 = w[..., 1, 0] * a + w[..., 1, 1] * b
                y = jnp.stack([na, nb2], axis=-2).reshape(*lead, dim)
            return y
        h = jnp.einsum('bsd,dh->bsh', x, W_exp) + b_exp
        h = butterfly(h, up_weights, D_HIDDEN)
        h = jax.nn.gelu(h + up_bias, approximate=False)
        h = butterfly(h, down_weights, D_HIDDEN)
        y = jnp.einsum('bsh,hd->bsd', h, W_con) + b_con
        return y + down_bias

    def _L1_attn_ref(x, qkv_w, out_w, bias_p, bias_a, rope_freqs):
        import jax, jax.numpy as jnp
        import numpy as np
        B, S, D_MODEL, H, D = (2, 256, 128, 16, 64)
        SCALE = 1.0 / float(np.sqrt(D))

        def _rope(t, c, s):
            d2 = t.shape[-1] // 2
            t1, t2 = (t[..., :d2], t[..., d2:])
            return jnp.concatenate([t1 * c - t2 * s, t1 * s + t2 * c], axis=-1)
        Bb, Ss, _ = x.shape
        qkv = (x @ qkv_w.T).reshape(Bb, Ss, 3, H, D)
        q = qkv[:, :, 0].transpose(0, 2, 1, 3)
        k = qkv[:, :, 1].transpose(0, 2, 1, 3)
        v = qkv[:, :, 2].transpose(0, 2, 1, 3)
        pos = jnp.arange(Ss, dtype=jnp.float32)
        ang = pos[:, None] * rope_freqs[None, :]
        c = jnp.cos(ang)[None, None]
        s = jnp.sin(ang)[None, None]
        q = _rope(q, c, s)
        k = _rope(k, c, s)
        scores = jnp.einsum('bhqd,bhkd->bhqk', q, k) * SCALE
        p = jnp.maximum(bias_p, 0.01)
        a = jnp.maximum(bias_a, 0.01)
        dist = jnp.abs(pos[None, :] - pos[:, None])
        kb = -p * jnp.log1p(a * dist)
        attn = jax.nn.softmax(scores + kb[None], axis=-1)
        out = jnp.einsum('bhqk,bhkd->bhqd', attn, v)
        out = out.transpose(0, 2, 1, 3).reshape(Bb, Ss, H * D)
        return out @ out_w.T

    def _L1_ffn_ref(x, wqkv, q_scale, k_scale, wo, ln_g, ln_b, w1, b1, w2, b2):
        import jax, jax.numpy as jnp
        import numpy as np
        DIM = 128
        DEPTH = 2
        HEADS = 8
        DIM_HEAD = 64
        WINDOW = 64
        INNER = HEADS * DIM_HEAD
        HID = int(DIM * 4 * 2 / 3)
        B, N = (2, 1024)
        QK_SCALE = 8.0

        def shift_token(t):
            t1, t2 = jnp.split(t, 2, axis=-1)
            t2 = jnp.pad(t2, ((0, 0), (1, 0), (0, 0)))[:, :-1]
            return jnp.concatenate([t1, t2], axis=-1)

        def l2norm(t):
            return t / jnp.clip(jnp.linalg.norm(t, axis=-1, keepdims=True), 1e-12)

        def rotate_half(x):
            x1, x2 = jnp.split(x, 2, axis=-1)
            return jnp.concatenate([-x2, x1], axis=-1)

        def rotary_xpos(q, k):
            n = q.shape[-2]
            half_idx = jnp.arange(0, DIM_HEAD, 2, dtype=jnp.float32)
            inv_freq = 1.0 / 10000.0 ** (half_idx / DIM_HEAD)
            t = jnp.arange(n, dtype=jnp.float32)
            freqs = t[:, None] * inv_freq[None, :]
            freqs = jnp.concatenate([freqs, freqs], axis=-1)
            base = (half_idx + 0.4 * DIM_HEAD) / (1.4 * DIM_HEAD)
            power = (t - n // 2) / float(WINDOW // 2)
            scale = base[None, :] ** power[:, None]
            scale = jnp.concatenate([scale, scale], axis=-1)
            cos, sin = (jnp.cos(freqs), jnp.sin(freqs))
            q = q * cos * scale + rotate_half(q) * sin * scale
            k = k * cos / scale + rotate_half(k) * sin / scale
            return (q, k)

        def local_attention(q, k, v):
            b, h, n, d = q.shape
            w = n // WINDOW
            bq = q.reshape(b, h, w, WINDOW, d) * QK_SCALE
            bk = k.reshape(b, h, w, WINDOW, d)
            bv = v.reshape(b, h, w, WINDOW, d)

            def look_around(t):
                p = jnp.pad(t, ((0, 0), (0, 0), (1, 0), (0, 0), (0, 0)))
                return jnp.concatenate([p[:, :, :w], p[:, :, 1:]], axis=3)
            bk, bv = (look_around(bk), look_around(bv))
            bt = jnp.arange(n).reshape(w, WINDOW)
            btp = jnp.pad(bt, ((1, 0), (0, 0)), constant_values=-1)
            btk = jnp.concatenate([btp[:w], btp[1:]], axis=1)
            sim = jnp.einsum('bhwid,bhwjd->bhwij', bq, bk)
            i = bt[:, :, None]
            j = btk[:, None, :]
            mask = (i < j) | (i > j + WINDOW) | (j == -1)
            sim = jnp.where(mask, -jnp.finfo(sim.dtype).max, sim)
            attn = jax.nn.softmax(sim, axis=-1)
            out = jnp.einsum('bhwij,bhwjd->bhwid', attn, bv)
            return out.reshape(b, h, n, d)

        def _layer(x, wqkv, qs, ksc, wo, lg, lb, w1, b1, w2, b2):
            b, n, _ = x.shape
            h = shift_token(x)
            qkv = h @ wqkv
            q, k, v = jnp.split(qkv, 3, axis=-1)
            to_heads = lambda t: t.reshape(b, n, HEADS, DIM_HEAD).transpose(0, 2, 1, 3)
            q, k, v = (to_heads(q), to_heads(k), to_heads(v))
            q = l2norm(q) * qs
            k = l2norm(k) * ksc
            q, k = rotary_xpos(q, k)
            o = local_attention(q, k, v)
            o = o.transpose(0, 2, 1, 3).reshape(b, n, INNER)
            x = x + o @ wo
            h = shift_token(x)
            mu = h.mean(-1, keepdims=True)
            var = h.var(-1, keepdims=True)
            h = (h - mu) / jnp.sqrt(var + 1e-05) * lg + lb
            h = h @ w1 + b1
            a, g = jnp.split(h, 2, axis=-1)
            h = a * jax.nn.gelu(g, approximate=False)
            x = x + h @ w2 + b2
            return x
        for l in range(DEPTH):
            x = _layer(x, wqkv[l], q_scale[l], k_scale[l], wo[l], ln_g[l], ln_b[l], w1[l], b1[l], w2[l], b2[l])
        return x

    def _L2_attn_ref(x, Wq, Wk, Wv, Wo, bo, denom_bias):
        import jax, jax.numpy as jnp
        import numpy as np
        import math
        DIM = 128
        HEADS = 16
        HEAD_DIM = DIM // HEADS
        b, n, d = x.shape
        h, hd = (HEADS, HEAD_DIM)

        def split_heads(t):
            return t.reshape(b, n, h, hd).transpose(0, 2, 1, 3)
        q = split_heads(x @ Wq.T)
        k = split_heads(x @ Wk.T)
        v = split_heads(x @ Wv.T)
        sim = jnp.einsum('bhid,bhjd->bhij', q, k) / math.sqrt(hd)
        causal_mask = jnp.triu(jnp.ones((n, n), dtype=bool), k=1)
        neg = -jnp.finfo(sim.dtype).max
        sim = jnp.where(causal_mask, neg, sim)
        sim_max = jnp.max(sim, axis=-1, keepdims=True)
        exp_sim = jnp.exp(sim - sim_max)
        denom = jnp.sum(exp_sim, axis=-1, keepdims=True) + jnp.exp(denom_bias)
        attn = exp_sim / denom
        out = jnp.einsum('bhij,bhjd->bhid', attn, v)
        out = out.transpose(0, 2, 1, 3).reshape(b, n, d)
        return out @ Wo.T + bo

    def _L2_ffn_ref(x, w_in, w_out, w1, w2, wg, we, gb, eb):
        import jax, jax.numpy as jnp
        import numpy as np
        MODEL_DIM = 128
        HIDDEN = 256
        NUM_GROUPS = 2
        EXPERTS_PER_GP = 4
        NUM_EXPERTS = NUM_GROUPS * EXPERTS_PER_GP
        TOP_K = 2
        B, T = (2, 256)

        def _swiglu(x):
            a, b = jnp.split(x, 2, axis=-1)
            return jax.nn.silu(a) * b
        Bs, Ts, C = x.shape
        S = Bs * Ts
        flat = x.reshape(S, C)
        shared = _swiglu(flat @ w_in.T) @ w_out.T
        g_probs = jax.nn.softmax(flat @ wg.T + gb, axis=-1)
        g_idx = jnp.argmax(g_probs, axis=-1)
        e_logits = flat @ we.T + eb
        egid = jnp.arange(NUM_EXPERTS) // EXPERTS_PER_GP
        masked = jnp.where(g_idx[:, None] == egid[None, :], e_logits, -jnp.inf)
        e_probs = jax.nn.softmax(masked, axis=-1)
        g_prob = jnp.take_along_axis(g_probs, g_idx[:, None], axis=1)
        p_expert = e_probs * g_prob
        topv, topi = jax.lax.top_k(p_expert, TOP_K)
        w_se = jnp.zeros((S, NUM_EXPERTS), x.dtype).at[jnp.arange(S)[:, None], topi].add(topv)
        h = _swiglu(flat @ w1.T)
        routed = jnp.zeros_like(shared)
        for e in range(NUM_EXPERTS):
            routed = routed + h * w_se[:, e:e + 1] @ w2[e].T
        return (shared + routed).reshape(Bs, Ts, C)

    def _L3_attn_ref(x, Wq, Wk, Wv, Wo, bo):
        import jax, jax.numpy as jnp
        import numpy as np
        D_MODEL = 128
        NUM_HEADS = 16
        HEAD_DIM = D_MODEL // NUM_HEADS
        EPS = 1e-08
        B, T, _ = x.shape
        H, D = (NUM_HEADS, HEAD_DIM)
        scale = jnp.sqrt(jnp.asarray(D, dtype=x.dtype))
        q = (x @ Wq.T).reshape(B, T, H, D).transpose(0, 2, 1, 3)
        k = (x @ Wk.T).reshape(B, T, H, D).transpose(0, 2, 1, 3)
        v = (x @ Wv.T).reshape(B, T, H, D).transpose(0, 2, 1, 3)
        s = jnp.einsum('bhtd,bhsd->bhts', q, k) / scale
        m = jnp.max(s, axis=-1, keepdims=True)
        e = jnp.exp(s - m)
        num = jnp.einsum('bhts,bhsd->bhtd', e, v)
        den = jnp.sum(e, axis=-1, keepdims=True) + EPS
        out = (num / den).transpose(0, 2, 1, 3).reshape(B, T, H * D)
        return out @ Wo.T + bo

    def _L3_ffn_ref(x, w_router, W1, b1, W2, b2, Ws1, bs1, Ws2, bs2):
        import jax, jax.numpy as jnp
        import numpy as np
        import math
        D_MODEL, D_FF, N_EXPERTS, TOP_K, N_SHARED = (128, 512, 8, 2, 1)
        B, T = (4, 128)
        SCALE = 1.0 / math.sqrt(N_SHARED + TOP_K / N_EXPERTS)
        logits = jnp.einsum('btd,ed->bte', x, w_router)
        probs = jax.nn.softmax(logits, axis=-1)
        vals, idx = jax.lax.top_k(probs, TOP_K)
        gates = jnp.sum(jax.nn.one_hot(idx, N_EXPERTS, dtype=x.dtype) * vals[..., None], axis=-2)
        hs = jax.nn.gelu(jnp.einsum('btd,fd->btf', x, Ws1) + bs1)
        acc = jnp.einsum('btf,df->btd', hs, Ws2) + bs2
        h = jax.nn.gelu(jnp.einsum('btd,efd->btef', x, W1) + b1)
        y = jnp.einsum('btef,edf->bted', h, W2) + b2
        acc = acc + jnp.einsum('bted,bte->btd', y, gates)
        return SCALE * acc
    x = L0_attn_x
    x = _layernorm(x + _L0_attn_ref(x, L0_attn_Wq, L0_attn_bq, L0_attn_Wk, L0_attn_bk, L0_attn_Wv, L0_attn_bv, L0_attn_Wo, L0_attn_bo), axis=-1)
    x = _layernorm(x + _L0_ffn_ref(x, L0_ffn_W_exp, L0_ffn_b_exp, L0_ffn_up_weights, L0_ffn_up_bias, L0_ffn_down_weights, L0_ffn_W_con, L0_ffn_b_con, L0_ffn_down_bias), axis=-1)
    x = _layernorm(x + _L1_attn_ref(x, L1_attn_qkv_w, L1_attn_out_w, L1_attn_bias_p, L1_attn_bias_a, L1_attn_rope_freqs), axis=-1)
    x = _layernorm(x + _L1_ffn_ref(x, L1_ffn_wqkv, L1_ffn_q_scale, L1_ffn_k_scale, L1_ffn_wo, L1_ffn_ln_g, L1_ffn_ln_b, L1_ffn_w1, L1_ffn_b1, L1_ffn_w2, L1_ffn_b2), axis=-1)
    x = _layernorm(x + _L2_attn_ref(x, L2_attn_Wq, L2_attn_Wk, L2_attn_Wv, L2_attn_Wo, L2_attn_bo, L2_attn_denom_bias), axis=-1)
    x = _layernorm(x + _L2_ffn_ref(x, L2_ffn_w_in, L2_ffn_w_out, L2_ffn_w1, L2_ffn_w2, L2_ffn_wg, L2_ffn_we, L2_ffn_gb, L2_ffn_eb), axis=-1)
    x = _layernorm(x + _L3_attn_ref(x, L3_attn_Wq, L3_attn_Wk, L3_attn_Wv, L3_attn_Wo, L3_attn_bo), axis=-1)
    x = _layernorm(x + _L3_ffn_ref(x, L3_ffn_w_router, L3_ffn_W1, L3_ffn_b1, L3_ffn_W2, L3_ffn_b2, L3_ffn_Ws1, L3_ffn_bs1, L3_ffn_Ws2, L3_ffn_bs2), axis=-1)
    return x

_drawn_inputs = setup_inputs


def setup_inputs(seed=0):
    import zlib

    import numpy as np

    out = dict(_drawn_inputs(seed))
    spreads = {'L0_attn_bq': (0.0, 0.1),
     'L0_attn_bk': (0.0, 2.0),
     'L0_attn_bv': (0.0, 0.1),
     'L0_attn_bo': (0.0, 0.1),
     'L0_ffn_b_exp': (0.0, 0.1),
     'L0_ffn_up_bias': (0.0, 0.1),
     'L0_ffn_b_con': (0.0, 0.1),
     'L0_ffn_down_bias': (0.0, 0.1),
     'L1_ffn_q_scale': (1.0, 0.6),
     'L1_ffn_k_scale': (1.0, 0.6),
     'L1_ffn_ln_g': (1.0, 0.6),
     'L1_ffn_ln_b': (0.0, 0.8),
     'L1_ffn_b1': (0.0, 0.637),
     'L1_ffn_b2': (0.0, 0.1),
     'L2_attn_bo': (0.0, 0.1),
     'L2_attn_denom_bias': (0.0, 0.8),
     'L2_ffn_gb': (0.0, 0.8),
     'L2_ffn_eb': (0.0, 0.8),
     'L3_attn_bo': (0.0, 0.1)}
    factors = {'L1_attn_bias_a': 3.0,
     'L1_attn_rope_freqs': 95.382,
     'L1_ffn_w1': 4.012,
     'L1_ffn_w2': 3.868,
     'L2_ffn_w_in': 4.145,
     'L2_ffn_w_out': 4.028,
     'L2_ffn_w1': 8.0,
     'L2_ffn_w2': 8.0,
     'L2_ffn_wg': 8.0,
     'L2_ffn_we': 8.0,
     'L3_attn_Wq': 8.0,
     'L3_attn_Wk': 8.0,
     'L3_ffn_b1': 8.0,
     'L3_ffn_b2': 8.0,
     'L3_ffn_bs1': 5.698,
     'L3_ffn_bs2': 3.385}
    for name, (base, spread) in spreads.items():
        noise = np.random.default_rng([zlib.crc32(name.encode()), seed]).standard_normal(out[name].shape)
        drawn = base * np.exp(spread * noise) if base else spread * noise
        out[name] = jnp.asarray(drawn.astype(out[name].dtype))
    for name, factor in factors.items():
        out[name] = (out[name] * factor).astype(out[name].dtype)
    return out
```

```python
from contextlib import ExitStack

import numpy as np

import concourse.bass as bass
from concourse import mybir

F32 = mybir.dt.float32
BF16 = mybir.dt.bfloat16
ALU = mybir.AluOpType
ACT = mybir.ActivationFunctionType
AX = mybir.AxisListType
ds = bass.ds

P = 128
B, L, C = 2, 1024, 128
TPB = L // P
TILES = B * TPB
GROUP = 4
NG = TILES // GROUP
PAD = 192
XB = L + 2 * PAD
EPS = 1e-5
HUGE = 3.0e38


class Signal:

    def __init__(self, sem, per, step=1):
        self.sem, self.per, self.step = sem, per, step

    def start(self, eng):
        if self.per:
            eng.sem_inc(self.sem, self.per * self.step)

    def at(self, it, k):
        assert k < self.per and k >= -self.per, (k, self.per)
        return (it * self.per + (self.per + k + 1)) * self.step if self.step != 1 else it * self.per + (self.per + k + 1)


class Chain:

    def __init__(self, eng, events, it=0):
        self.eng, self.events, self.it, self.n = eng, events, it, 0

    def done(self, ins):
        ins.then_inc(self.events.sem, 1)
        self.n += 1
        return ins

    def wait(self):
        self.eng.wait_ge(self.events.sem, self.events.at(self.it, self.n - 1))

    def step(self, ins):
        self.done(ins)
        self.wait()

    def wait_apart(self, passed):
        self.wait()
        self.eng.sem_inc(passed, 1)

    def close(self):
        assert self.n == self.events.per, f"{self.events.sem}: {self.n} events, {self.events.per} declared"


class Count:

    def wait_apart(self, passed):
        self.wait()

    def __init__(self, eng, sem):
        self.eng, self.sem, self.n = eng, sem, 0

    def done(self, ins):
        ins.then_inc(self.sem, 1)
        self.n += 1
        return ins

    def wait(self):
        self.eng.wait_ge(self.sem, self.n)

    def step(self, ins):
        self.done(ins)
        self.wait()


def order(slots, lead, units, lag=2):
    out = []
    for n in range(slots + lag + 1):
        if n < slots:
            out.append(("S", n))
        if 0 <= n - lead - lag < units:
            out.append(("T", n - lead - lag))
        if 0 <= n - lead - lag - 1 < units:
            out.append(("V", n - lead - lag - 1))
    return out


class Kernel:

    def __init__(self, nc, ctx, dram):
        self.nc, self.ctx, self.dram = nc, ctx, dram
        self.numbers = {}
        self.ident = self.sb("ident", [P, P])
        self.ones = self.sb("ones", [P, 512])
        self.x_tok = self.sb("x_tok", [P, TILES * C])
        self.xT = self.sb("xT", [P, B * XB])
        self.xn = self.sb("x_new", [P, 2, 512])
        self.res = self.sb("residual", [P, 2, 512])
        self.stats = self.sb("ln_stats", [P, 2, GROUP, 6])
        self.mv = self.sb("ln_mean_var", [P, 2, GROUP, 2])
        self.rstd = self.sb("ln_rstd", [P, 2, 3, GROUP])
        self.ps = [ctx.enter_context(nc.psum_tensor(f"bank{i}", [P, 1024 if i < 2 else 512], F32))
                   for i in range(6)]
        self.ps_scores = [self.ps[0], self.ps[1]]
        self.ps_turned = [self.ps[2], self.ps[3]]
        self.ps_out = [self.ps[4], self.ps[5]]

    def sb(self, name, shape, dt=F32, ctx=None):
        return (ctx or self.ctx).enter_context(self.nc.sbuf_tensor(name, shape, dt))

    def sem(self, name, ctx):
        if ctx not in self.numbers:
            self.numbers[ctx] = []
            ctx.callback(self.clear, ctx)
        s = ctx.enter_context(self.nc.semaphore(name))
        self.numbers[ctx].append(s.num)
        return s

    def clear(self, ctx):
        numbers = sorted(self.numbers.pop(ctx))
        while numbers:
            n = 1
            while n < len(numbers) and numbers[n] == numbers[0] + n:
                n += 1
            self.nc.gpsimd.sem_clear(range(numbers[0], numbers[0] + n))
            numbers = numbers[n:]


def xcol(g):
    return (g // 2) * XB + PAD + (g % 2) * 512



class Norm:

    DVE_STEPS = 13

    def __init__(self, k, ctx, name, per):
        self.k = k
        self.y_full = Signal(k.sem(name + "_y_full", ctx), per)
        self.y_free = Signal(k.sem(name + "_y_free", ctx), per)
        self.var_ready = Signal(k.sem(name + "_var_ready", ctx), per)
        self.root_ready = Signal(k.sem(name + "_root_ready", ctx), per)
        self.xn_ready = Signal(k.sem(name + "_xn_ready", ctx), per)
        self.turned = Signal(k.sem(name + "_turned", ctx), per)
        self.xT_ready = Signal(k.sem(name + "_xT_ready", ctx), per)
        self.passed = k.sem(name + "_passed", ctx)

    def start(self, pe, dve, act):
        if pe is not None:
            self.y_full.start(pe), self.turned.start(pe)
        if dve is not None:
            self.y_free.start(dve), self.var_ready.start(dve), self.xn_ready.start(dve)
        if act is not None:
            self.root_ready.start(act), self.xT_ready.start(act)

    def vector(self, dve, chain, it, e, slot, tile0, y, scale=None, normed=True, also=None, more=None,
               y_full=None, y_free=None):
        k, nc = self.k, self.k.nc
        x = k.x_tok[:, ds(tile0 * C, 512)]
        res = k.res[:, slot, :]
        full, e_full = y_full or (self.y_full, e)
        free, e_free = y_free or (self.y_free, e)
        dve.wait_ge(full.sem, full.at(it, e_full))
        if scale is None:
            nc.vector.tensor_tensor(res, x, y, ALU.add).then_inc(free.sem, 1)
        else:
            nc.vector.scalar_tensor_tensor(res, y, scale, x, ALU.mult, ALU.add).then_inc(free.sem, 1)
        dve.wait_ge(free.sem, free.at(it, e_free))
        if also is not None:
            chain.step(nc.vector.tensor_tensor(res, res, also, ALU.add))
        if more is not None:
            more(res)
        if not normed:
            chain.step(nc.vector.tensor_scalar(x, res, 1.0, None, ALU.mult))
            dve.wait_ge(self.turned.sem, self.turned.at(it, e - 2))
            nc.vector.tensor_scalar(k.xn[:, slot, :], res, 1.0, None, ALU.mult).then_inc(self.xn_ready.sem, 1)
            return
        for i in range(GROUP):
            chain.done(nc.vector.bn_stats(k.stats[:, slot, i, :], res[:, i * C:(i + 1) * C]))
        chain.wait_apart(self.passed)
        for i in range(GROUP):
            chain.done(nc.vector.bn_aggr(k.mv[:, slot, i, :], k.stats[:, slot, i, :]))
        chain.wait()
        nc.vector.tensor_scalar(k.rstd[:, slot, 0, :], k.mv[:, slot, :, 1], EPS, None, ALU.add
                                ).then_inc(self.var_ready.sem, 1)
        dve.wait_ge(self.root_ready.sem, self.root_ready.at(it, e))
        chain.step(nc.vector.reciprocal(k.rstd[:, slot, 2, :], k.rstd[:, slot, 1, :]))
        dve.wait_ge(self.turned.sem, self.turned.at(it, e - 2))
        for i in range(GROUP):
            chain.done(nc.vector.tensor_scalar(k.xn[:, slot, i * C:(i + 1) * C], res[:, i * C:(i + 1) * C],
                                               k.mv[:, slot, i, 0:1], k.rstd[:, slot, 2, i:i + 1],
                                               ALU.subtract, ALU.mult))
        chain.wait()
        nc.vector.tensor_scalar(x, k.xn[:, slot, :], 1.0, None, ALU.mult).then_inc(self.xn_ready.sem, 1)
        dve.wait_ge(self.xn_ready.sem, self.xn_ready.at(it, e))

    def scalar_root(self, act, it, e, slot):
        k = self.k
        act.wait_ge(self.var_ready.sem, self.var_ready.at(it, e))
        k.nc.scalar.activation(k.rstd[:, slot, 1, :], k.rstd[:, slot, 0, :], ACT.Sqrt
                               ).then_inc(self.root_ready.sem, 1)

    def tensor(self, pe, it, e, slot, bank):
        k = self.k
        pe.wait_ge(self.xn_ready.sem, self.xn_ready.at(it, e))
        pe.wait_ge(self.xT_ready.sem, self.xT_ready.at(it, e - 1))
        for i in range(GROUP):
            mm = pe.transpose(bank[:, i * P:(i + 1) * P], k.xn[:, slot, i * C:(i + 1) * C], k.ident[:, :])
        mm.then_inc(self.turned.sem, 1)

    def scalar_store(self, act, it, e, bank, col):
        k = self.k
        act.wait_ge(self.turned.sem, self.turned.at(it, e))
        k.nc.scalar.copy(k.xT[:, ds(col, 512)], bank[:, 0:512]).then_inc(self.xT_ready.sem, 1)


def load_x(k):
    nc = k.nc
    with ExitStack() as ctx:
        sem = lambda n: k.sem("in_" + n, ctx)
        loaded, made, zeroed = sem("x_loaded"), sem("ident_made"), sem("xT_zeroed")
        turned, taken = sem("x_turned"), sem("x_taken")
        block = ctx.enter_context(nc.Block())

        @block.sync
        def _(sp):
            sp.dma_start(k.x_tok[:, :].rearrange("p (t c) -> p t c", c=C),
                         k.dram["L0_attn_x"].rearrange("b (t p) c -> p (b t) c", p=P)).then_inc(loaded, 16)

        @block.gpsimd
        def _(pool):
            nc.gpsimd.memset(k.ident[:, :], 0.0).then_inc(made, 1)
            nc.gpsimd.memset(k.ones[:, :], 1.0).then_inc(made, 1)
            pool.wait_ge(made, 2)
            nc.gpsimd.affine_select(out=k.ident[:, :], in_=k.ident[:, :], compare_op=ALU.not_equal, fill=1.0,
                                    base=0, pattern=[[-1, P]], channel_multiplier=1).then_inc(made, 1)
            for b in range(B):
                nc.gpsimd.memset(k.xT[:, b * XB:b * XB + PAD], 0.0)
                nc.gpsimd.memset(k.xT[:, b * XB + PAD + L:(b + 1) * XB], 0.0).then_inc(zeroed, 1)
            pool.wait_ge(zeroed, 2)

        @block.tensor
        def _(pe):
            pe.wait_ge(made, 3)
            pe.wait_ge(loaded, 16)
            for g in range(NG):
                if g >= 2:
                    pe.wait_ge(taken, g - 1)
                for i in range(GROUP):
                    mm = pe.transpose(k.ps_turned[g % 2][:, i * P:(i + 1) * P],
                                      k.x_tok[:, (GROUP * g + i) * C:(GROUP * g + i + 1) * C], k.ident[:, :])
                mm.then_inc(turned, 1)

        @block.scalar
        def _(act):
            for g in range(NG):
                act.wait_ge(turned, g + 1)
                nc.scalar.copy(k.xT[:, xcol(g):xcol(g) + 512], k.ps_turned[g % 2][:, :]).then_inc(taken, 1)
            act.wait_ge(taken, NG)


def project_out(k, name, o_tok, chunks, wo, w_dram, bias, bias_dram, normed=True):
    nc = k.nc
    with ExitStack() as ctx:
        sem = lambda n: k.sem(name + n, ctx)
        oT = k.sb(name + "_oT", [P, 2, 512], ctx=ctx)
        w_loaded = sem("_w_loaded")
        o_turned = Signal(sem("_o_turned"), NG * chunks)
        o_taken = Signal(sem("_o_taken"), NG * chunks)
        own = sem("_own_dve")
        norm = Norm(k, ctx, name, NG)
        block = ctx.enter_context(nc.Block())

        @block.sync
        def _(sp):
            sp.dma_start(wo, w_dram).then_inc(w_loaded, 16)
            if bias is not None:
                sp.dma_start(bias, bias_dram).then_inc(w_loaded, 16)

        @block.tensor
        def _(pe):
            norm.start(pe, None, None)
            o_turned.start(pe)
            pe.wait_ge(w_loaded, 32 if bias is not None else 16)
            for g in range(NG + 1):
                if g < NG:
                    y = k.ps_out[g % 2]
                    for c in range(chunks):
                        n = g * chunks + c
                        bank = k.ps_turned[n % 2]
                        pe.wait_ge(o_taken.sem, o_taken.at(0, n - 2))
                        for i in range(GROUP):
                            mm = pe.transpose(bank[:, i * P:(i + 1) * P],
                                              o_tok[:, GROUP * g + i, c * P:(c + 1) * P], k.ident[:, :])
                        mm.then_inc(o_turned.sem, 1)
                        if c == 0:
                            pe.wait_ge(norm.y_free.sem, norm.y_free.at(0, g - 2))
                        pe.wait_ge(o_taken.sem, o_taken.at(0, n))
                        for i in range(GROUP):
                            last = c == chunks - 1 and bias is None
                            mm = pe.matmul(y[:, i * C:(i + 1) * C], oT[:, n % 2, i * P:(i + 1) * P],
                                           wo[:, c * C:(c + 1) * C], start=(c == 0 and i == 0),
                                           stop=last and i == GROUP - 1, skip_group_check=True)
                    if bias is not None:
                        for i in range(GROUP):
                            mm = pe.matmul(y[:, i * C:(i + 1) * C], k.ones[0:1, 0:P], bias,
                                           start=False, stop=i == GROUP - 1, skip_group_check=True)
                    mm.then_inc(norm.y_full.sem, 1)
                if g >= 1:
                    norm.tensor(pe, 0, g - 1, (g - 1) % 2, k.ps_scores[0])

        @block.scalar
        def _(act):
            norm.start(None, None, act)
            o_taken.start(act)
            for g in range(NG + 1):
                if g < NG:
                    for c in range(chunks):
                        n = g * chunks + c
                        act.wait_ge(o_turned.sem, o_turned.at(0, n))
                        nc.scalar.copy(oT[:, n % 2, :], k.ps_turned[n % 2][:, :]).then_inc(o_taken.sem, 1)
                if g >= 1:
                    norm.scalar_store(act, 0, g - 1, k.ps_scores[0], xcol(g - 1))
                if g < NG and normed:
                    norm.scalar_root(act, 0, g, g % 2)
            act.wait_ge(norm.xT_ready.sem, norm.xT_ready.at(0, NG - 1))

        @block.vector
        def _(dve):
            norm.start(None, dve, None)
            chain = Count(dve, own)
            for g in range(NG):
                norm.vector(dve, chain, 0, g, g % 2, GROUP * g, k.ps_out[g % 2][:, :], normed=normed)


def project_turned(k, name, groups, chunks, oT, w, w_dram, bias, bias_dram):
    nc = k.nc
    n_g = len(groups)
    with ExitStack() as ctx:
        sem = lambda n: k.sem(name + n, ctx)
        w_loaded = sem("_w_loaded")
        own = sem("_own_dve")
        norm = Norm(k, ctx, name, n_g)
        block = ctx.enter_context(nc.Block())

        @block.sync
        def _(sp):
            sp.dma_start(w, w_dram).then_inc(w_loaded, 16)
            if bias is not None:
                sp.dma_start(bias, bias_dram).then_inc(w_loaded, 16)

        @block.tensor
        def _(pe):
            norm.start(pe, None, None)
            pe.wait_ge(w_loaded, 32 if bias is not None else 16)
            for e in range(n_g + 1):
                if e < n_g:
                    y = k.ps_out[e % 2]
                    pe.wait_ge(norm.y_free.sem, norm.y_free.at(0, e - 2) if e >= 2 else 1)
                    for i in range(GROUP):
                        for c in range(chunks):
                            mm = pe.matmul(y[:, i * C:(i + 1) * C], oT(c, GROUP * groups[e] + i), w[:, c, :],
                                           start=c == 0, stop=c == chunks - 1 and bias is None)
                        if bias is not None:
                            mm = pe.matmul(y[:, i * C:(i + 1) * C], k.ones[0:1, 0:P], bias, start=False, stop=True)
                    mm.then_inc(norm.y_full.sem, 1)
                if e >= 1:
                    norm.tensor(pe, 0, e - 1, (e - 1) % 2, k.ps_scores[0])

        @block.scalar
        def _(act):
            norm.start(None, None, act)
            for e in range(n_g + 1):
                if e < n_g:
                    norm.scalar_root(act, 0, e, e % 2)
                if e >= 1:
                    norm.scalar_store(act, 0, e - 1, k.ps_scores[0], xcol(groups[e - 1]))
            act.wait_ge(norm.xT_ready.sem, norm.xT_ready.at(0, n_g - 1))

        @block.vector
        def _(dve):
            norm.start(None, dve, None)
            chain = Count(dve, own)
            for e in range(n_g):
                norm.vector(dve, chain, 0, e, e % 2, GROUP * groups[e], k.ps_out[e % 2][:, :])



L0_HEADS, L0_D, SEG, DIL = 16, 8, 64, 4
L0_GROUPS = 10


def l0_attention(k):
    nc, d = k.nc, k.dram
    U = 4
    with ExitStack() as ctx:
        sem = lambda n: k.sem("l0_" + n, ctx)
        sb = lambda n, s: k.sb("l0_" + n, s, ctx=ctx)
        wq, wk, wv, wo = (sb(n, [P, C]) for n in ("wq", "wk", "wv", "wo"))
        bqk = sb("bqk", [P, 2])
        bv, bo = sb("bv", [1, C]), sb("bo", [1, C])
        hmask = sb("hmask", [P, L0_HEADS])
        gweight = sb("gweight", [P, TPB, L0_GROUPS])
        qT = sb("qT", [P, B * L])
        kT = sb("kT", [P, B * XB])
        v_own = sb("v_own", [P, TILES, C])
        v_dil = sb("v_dil", [P, TILES, C])
        qm = sb("q_masked", [P, B * L])
        o_tok = sb("o_tok", [P, TILES, C])
        probs = sb("probs", [P, 2, 1024])
        probsT = sb("probsT", [P, 2, 1024])
        gmax = sb("gmax", [P, 2, 4, L0_GROUPS])
        gsum = sb("gsum", [P, 2, 4, L0_GROUPS])
        ginv = sb("ginv", [P, 2, 4, L0_GROUPS])
        hcol = sb("hcol", [P, 1])

        with ExitStack() as c2:
            loaded, proj_full, proj_taken = (k.sem("l0p_" + n, c2) for n in ("loaded", "full", "taken"))
            block = c2.enter_context(nc.Block())
            xb = lambda t: (t // TPB) * XB + (t % TPB) * P
            jobs = ([("q", i) for i in range(4)] + [("k", i) for i in range(6)]
                    + [("v", i) for i in range(4)] + [("vd", i) for i in range(4)])

            @block.sync
            def _(sp):
                for out, src in ((wq, d["L0_attn_Wq"]), (wk, d["L0_attn_Wk"]), (wv, d["L0_attn_Wv"]),
                                 (bqk, d["L0_bqk"]), (bv, d["L0_attn_bv"]),
                                 (hmask, d["head_mask8"])):
                    sp.dma_start(out[:, :], src).then_inc(loaded, 16)
                sp.dma_start(gweight[:, :, :], d["L0_group_weights"]).then_inc(loaded, 16)

            @block.tensor
            def _(pe):
                pe.wait_ge(loaded, 16 * 7)
                for n, (kind, i) in enumerate(jobs):
                    bank = k.ps_out[n % 2]
                    if n >= 2:
                        pe.wait_ge(proj_taken, n - 1)
                    if kind == "q":
                        mm = pe.matmul(bank[:, :], wq[:, :], k.xT[:, xcol(i):xcol(i) + 512], start=True, stop=True)
                    elif kind == "k":
                        w = min(512, B * XB - i * 512)
                        mm = pe.matmul(bank[:, 0:w], wk[:, :], k.xT[:, i * 512:i * 512 + w], start=True, stop=True)
                    else:
                        for s in range(GROUP):
                            c0 = xb(GROUP * i + s)
                            x = (k.xT[:, c0 + PAD:c0 + PAD + P] if kind == "v" else
                                 k.xT[:, c0:c0 + (P - 1) * DIL + 1:DIL])
                            pe.matmul(bank[:, s * C:(s + 1) * C], x, wv[:, :], start=(s == 0), stop=False,
                                      skip_group_check=True)
                            mm = pe.matmul(bank[:, s * C:(s + 1) * C], k.ones[0:1, 0:P], bv[:, :], start=False,
                                           stop=s == GROUP - 1, skip_group_check=True)
                    mm.then_inc(proj_full, 1)

            @block.scalar
            def _(act):
                for n, (kind, i) in enumerate(jobs):
                    bank = k.ps_out[n % 2]
                    act.wait_ge(proj_full, n + 1)
                    if kind == "q":
                        ins = nc.scalar.activation(qT[:, i * 512:(i + 1) * 512], bank[:, :], ACT.Identity,
                                                   bias=bqk[:, 0:1])
                    elif kind == "k":
                        w = min(512, B * XB - i * 512)
                        ins = nc.scalar.activation(kT[:, i * 512:i * 512 + w], bank[:, 0:w], ACT.Identity,
                                                   bias=bqk[:, 1:2])
                    else:
                        v = v_own if kind == "v" else v_dil
                        ins = nc.scalar.copy(v[:, GROUP * i:GROUP * (i + 1), :],
                                             bank[:, :].rearrange("p (t c) -> p t c", c=C))
                    ins.then_inc(proj_taken, 1)
                act.wait_ge(proj_taken, len(jobs))

        with ExitStack() as c2:
            sm = lambda n: k.sem("l0a_" + n, c2)
            s_full = [Signal(sm(f"scores_full{i}"), U // 2) for i in range(2)]
            s_free = [Signal(sm(f"scores_free{i}"), U // 2) for i in range(2)]
            q_ready = Signal(sm("q_ready"), B)
            shifted = Signal(sm("shifted"), U)
            e_raw = Signal(sm("exp_done"), U)
            e_full = Signal(sm("probs_ready"), U)
            inv_ready = Signal(sm("inv_ready"), U)
            t_full = [Signal(sm(f"turned_full{i}"), U) for i in range(2)]
            t_done = [Signal(sm(f"turned_taken{i}"), U) for i in range(2)]
            o_full = Signal(sm("out_full"), 1)
            o_free = Signal(sm("out_taken"), 1)
            hc = Signal(sm("mask_column"), 1)
            own_dve = Signal(sm("own_dve"), U * 6)
            block = c2.enter_context(nc.Block())
            plan = order(U, 0, U)
            o_bank = k.ps_out[0][:, 0:TILES * L0_D].rearrange("p (t c) -> p t c", c=L0_D)

            def groups(t, s):
                v = t[:, s, :] if len(t.shape) == 3 else t[:, :]
                v = v.rearrange("p (t q) -> p t q", t=4)
                return (v[:, :, 0:P].rearrange("p t (g q) -> p t g q", g=2),
                        v[:, :, P:2 * P].rearrange("p t (g q) -> p t g q", g=8))

            def wide(v, s, shape, a, b):
                return v[:, s, :, a:b].unsqueeze(3).broadcast_to(shape)

            @block.gpsimd
            def _(pool):
                q_ready.start(pool)
                e_full.start(pool)
                hc.start(pool)
                with pool.Fori(0, L0_HEADS) as h:
                    def mask(b):
                        pool.wait_ge(s_full[1].sem, s_full[1].at(h, b - 2))
                        nc.gpsimd.tensor_tensor(qm[:, b * L:(b + 1) * L], qT[:, b * L:(b + 1) * L],
                                                hcol[:, 0:1].broadcast_to([P, L]), ALU.mult).then_inc(q_ready.sem, 1)
                    pool.wait_ge(q_ready.sem, q_ready.at(h, -1))
                    nc.gpsimd.tensor_copy(hcol[:, :], hmask[:, ds(h, 1)]).then_inc(hc.sem, 1)
                    pool.wait_ge(hc.sem, hc.at(h, 0))
                    mask(0)
                    mask(1)
                    for u in range(U):
                        pool.wait_ge(e_raw.sem, e_raw.at(h, u))
                        pool.wait_ge(inv_ready.sem, inv_ready.at(h, u))
                        eo, ed = groups(probs, u % 2)
                        nc.gpsimd.tensor_tensor(eo, eo, wide(ginv, u % 2, [P, 4, 2, SEG], 0, 2), ALU.mult)
                        nc.gpsimd.tensor_tensor(ed, ed, wide(ginv, u % 2, [P, 4, 8, 16], 2, 10), ALU.mult
                                                ).then_inc(e_full.sem, 1)

            @block.tensor
            def _(pe):
                for s in (*s_full, *t_full, o_full):
                    s.start(pe)
                with pe.Fori(0, L0_HEADS) as h:
                    for what, u in plan:
                        if what == "S":
                            slot, b = u % 2, u // 2
                            pe.wait_ge(s_free[slot].sem, s_free[slot].at(h, u // 2 - 1))
                            if u % 2 == 0:
                                pe.wait_ge(q_ready.sem, q_ready.at(h, b))
                            for i in range(4):
                                j = (4 * u + i) % TPB
                                qs = qm[:, b * L + j * P:b * L + (j + 1) * P]
                                c0 = b * XB + j * P
                                pe.matmul(k.ps_scores[slot][:, i * 256:i * 256 + P], qs,
                                          kT[:, c0 + PAD:c0 + PAD + P], start=True, stop=True)
                                mm = pe.matmul(k.ps_scores[slot][:, i * 256 + P:(i + 1) * 256], qs,
                                               kT[:, c0:c0 + (P - 1) * DIL + 1:DIL], start=True, stop=True)
                            mm.then_inc(s_full[slot].sem, 1)
                        elif what == "T":
                            pe.wait_ge(e_full.sem, e_full.at(h, u))
                            turn(pe, k, probs[:, u % 2, :], t_full, t_done, h, u)
                        else:
                            for half in range(2):
                                pe.wait_ge(t_done[half].sem, t_done[half].at(h, u))
                            if u == 0:
                                pe.wait_ge(o_free.sem, o_free.at(h, -1))
                            for i in range(4):
                                t = 4 * u + i
                                for part, v in enumerate((v_own, v_dil)):
                                    c0 = (2 * i + part) * P
                                    mm = pe.matmul(o_bank[:, t, :], probsT[:, u % 2, c0:c0 + P],
                                                   v[:, t, ds(h * L0_D, L0_D)], start=part == 0, stop=part == 1)
                            if u == U - 1:
                                mm.then_inc(o_full.sem, 1)

            @block.vector
            def _(dve):
                for s in (*s_free, shifted, inv_ready, own_dve):
                    s.start(dve)
                with dve.Fori(0, L0_HEADS) as h:
                    chain = Chain(dve, own_dve, h)
                    for u in range(U):
                        s = u % 2
                        scores, sd = groups(k.ps_scores[s], s)
                        eo, ed = groups(probs, s)
                        dve.wait_ge(s_full[s].sem, s_full[s].at(h, u // 2))
                        dve.wait_ge(inv_ready.sem, inv_ready.at(h, u - 1))
                        chain.done(nc.vector.tensor_reduce(gmax[:, s, :, 0:2], scores, AX.X, ALU.max))
                        chain.step(nc.vector.tensor_reduce(gmax[:, s, :, 2:10], sd, AX.X, ALU.max))
                        dve.wait_ge(t_full[1].sem, t_full[1].at(h, u - 2))
                        nc.vector.tensor_tensor(eo, scores, wide(gmax, s, [P, 4, 2, SEG], 0, 2), ALU.subtract
                                                ).then_inc(own_dve.sem, 1)
                        chain.n += 1
                        nc.vector.tensor_tensor(ed, sd, wide(gmax, s, [P, 4, 8, 16], 2, 10), ALU.subtract
                                                ).then_inc(shifted.sem, 1)
                        dve.wait_ge(shifted.sem, shifted.at(h, u))
                        dve.sem_inc(s_free[s].sem, 1)
                        dve.wait_ge(e_raw.sem, e_raw.at(h, u))
                        chain.done(nc.vector.tensor_reduce(gsum[:, s, :, 0:2], eo, AX.X, ALU.add))
                        chain.step(nc.vector.tensor_reduce(gsum[:, s, :, 2:10], ed, AX.X, ALU.add))
                        chain.step(nc.vector.reciprocal(ginv[:, s, :, :], gsum[:, s, :, :]))
                        j0 = (4 * u) % TPB
                        nc.vector.tensor_tensor(ginv[:, s, :, :], ginv[:, s, :, :],
                                                gweight[:, j0:j0 + 4, :], ALU.mult).then_inc(inv_ready.sem, 1)
                    chain.close()

            @block.scalar
            def _(act):
                for s in (e_raw, *t_done, o_free):
                    s.start(act)
                with act.Fori(0, L0_HEADS) as h:
                    for what, u in plan:
                        if what == "S":
                            act.wait_ge(shifted.sem, shifted.at(h, u))
                            nc.scalar.activation(probs[:, u % 2, :], probs[:, u % 2, :], ACT.Exp
                                                 ).then_inc(e_raw.sem, 1)
                        elif what == "T":
                            for half in range(2):
                                take_turned(nc.scalar, k, probsT[:, u % 2, :], t_full, t_done, h, u, half)
                    act.wait_ge(o_full.sem, o_full.at(h, 0))
                    nc.scalar.copy(o_tok[:, :, ds(h * L0_D, L0_D)], o_bank).then_inc(o_free.sem, 1)

        project_out(k, "l0o", o_tok, 1, wo[:, :], d["L0_attn_Wo"], bo[:, :], d["L0_attn_bo"])


def every(half, u):
    return u


def turn(pe, k, probs, t_full, t_done, it, u, blocks=8, event=every):
    for half in range((blocks + 3) // 4):
        e = event(half, u)
        pe.wait_ge(t_done[half].sem, t_done[half].at(it, e - 1))
        for c in range(4 * half, min(blocks, 4 * half + 4)):
            mm = pe.transpose(k.ps_turned[half][:, (c % 4) * P:(c % 4 + 1) * P], probs[:, c * P:(c + 1) * P],
                              k.ident[:, :])
        mm.then_inc(t_full[half].sem, 1)


def take_turned(eng, k, probsT, t_full, t_done, it, u, half, blocks=8, event=every):
    n = min(4, blocks - 4 * half)
    eng.wait_ge(t_full[half].sem, t_full[half].at(it, event(half, u)))
    out, src = probsT[:, half * 512:half * 512 + n * P], k.ps_turned[half][:, 0:n * P]
    ins = eng.copy(out, src) if eng is k.nc.scalar else eng.tensor_copy(out, src)
    ins.then_inc(t_done[half].sem, 1)



L0_HID, L0_STAGES = 512, 9


def butterfly(eng, own, rows, buf, tmp, coef, down):
    for n in range(L0_STAGES):
        stage = L0_STAGES - 1 - n if down else n
        s = 2 ** stage
        nb = L0_HID // (2 * s)
        src = buf[0:rows, n % 2, :].rearrange("p (n i s) -> p n i s", i=2, s=s)
        dst = buf[0:rows, (n + 1) % 2, :].rearrange("p (n o s) -> p n o s", o=2, s=s)
        w = coef[0:rows, stage * 1024:(stage + 1) * 1024].rearrange("p (n s o i) -> p n o i s", s=s, o=2, i=2)
        for o in range(2):
            for i in range(2):
                block = w[:, :, i, o, :] if down else w[:, :, o, i, :]
                t = tmp[0:rows, i, o * 256:(o + 1) * 256].rearrange("p (n s) -> p n s", s=s)
                own.done(eng.tensor_tensor(t, src[:, :, i, :], block, ALU.mult))
        own.wait()
        t = tmp[0:rows, :, :].rearrange("p i (o n s) -> p i n o s", o=2, s=s)
        for o in range(2):
            own.done(eng.tensor_tensor(dst[:, :, o, :], t[:, 0, :, o, :], t[:, 1, :, o, :], ALU.add))
        own.wait()


def l0_ffn(k):
    nc, d = k.nc, k.dram
    CH = L0_HID // P
    with ExitStack() as ctx:
        sb = lambda n, s: k.sb("f0_" + n, s, ctx=ctx)
        up = sb("up", [P, 2, L0_HID])
        upb = sb("up_bias_row", [1, 2, L0_HID])
        down = sb("down", [P, 2, L0_HID])
        w_down = sb("w_down", [P, CH * C])
        bias_h = sb("bias_h", [P, CH])
        up_bias = sb("up_bias", [P, CH])
        bias_y = sb("bias_y", [2, C])
        hid = sb("hid", [P, 2, CH, 512])
        with ExitStack() as c2:
            loaded = [k.sem(f"f0_loaded{i}", c2) for i in range(3)]
            own_pool, own_dve, own_bias, turned, taken = (k.sem("f0_" + n, c2) for n in (
                "own_pool", "own_dve", "own_bias", "down_turned", "taken"))
            up_coef = k.sb("f0_up_coef", [P, L0_STAGES * 1024], ctx=c2)
            down_coef = k.sb("f0_down_coef", [P, L0_STAGES * 1024], ctx=c2)
            tmp = [k.sb(f"f0_tmp{i}", [P, 2, L0_HID], ctx=c2) for i in range(2)]
            block = c2.enter_context(nc.Block())
            DONE = L0_STAGES * 6

            @block.sync
            def _(sp):
                sp.dma_start(up_coef[:, :], d["L0_up_weights"].partition_broadcast(P)).then_inc(loaded[0], 16)
                sp.dma_start(up[:, 0, :], d["L0_ffn_W_exp"]).then_inc(loaded[0], 16)
                sp.dma_start(down_coef[:, :], d["L0_down_weights"].partition_broadcast(P)).then_inc(loaded[1], 16)
                sp.dma_start(down[:, 0, :], d["L0_W_con_T"]).then_inc(loaded[1], 16)
                sp.dma_start(upb[:, 0, :], d["L0_ffn_b_exp"]).then_inc(loaded[2], 16)
                sp.dma_start(up_bias[:, :], d["L0_up_bias"]).then_inc(loaded[2], 16)
                sp.dma_start(bias_y[:, :], d["L0_y_bias"]).then_inc(loaded[2], 16)

            @block.gpsimd
            def _(pool):
                pool.wait_ge(loaded[0], 32)
                butterfly(nc.gpsimd, Count(pool, own_pool), P, up, tmp[0], up_coef, False)

            @block.vector
            def _(dve):
                dve.wait_ge(loaded[1], 32)
                butterfly(nc.vector, Count(dve, own_dve), P, down, tmp[1], down_coef, True)
                dve.wait_ge(loaded[0], 32)
                dve.wait_ge(loaded[2], 48)
                butterfly(nc.vector, Count(dve, own_bias), 1, upb, tmp[1], up_coef, False)
                dve.wait_ge(turned, 1)
                nc.vector.tensor_copy(w_down[:, :], k.ps_turned[0][:, :]).then_inc(taken, 1)
                dve.wait_ge(turned, 2)
                nc.vector.tensor_tensor(bias_h[:, :], k.ps_turned[1][:, 0:CH], up_bias[:, :], ALU.add
                                        ).then_inc(taken, 1)
                dve.wait_ge(taken, 2)

            @block.tensor
            def _(pe):
                pe.wait_ge(own_dve, DONE)
                for c in range(CH):
                    mm = pe.transpose(k.ps_turned[0][:, c * P:(c + 1) * P], down[:, 1, c * P:(c + 1) * P],
                                      k.ident[:, :])
                mm.then_inc(turned, 1)
                pe.wait_ge(own_bias, DONE)
                for c in range(CH):
                    mm = pe.matmul(k.ps_turned[1][:, c:c + 1], upb[:, 1, c * P:(c + 1) * P], k.ones[0:1, 0:1],
                                   start=True, stop=True)
                mm.then_inc(turned, 1)

        feed_forward(k, "f0", hid, CH, [P] * CH, lambda c: up[:, 1, c * P:(c + 1) * P],
                     lambda c: w_down[:, c * C:(c + 1) * C], bias_y[:, :],
                     lambda c: (ACT.Gelu, bias_h[:, c:c + 1]))


def feed_forward(k, name, hid, chunks, rows, w_up, w_down, bias_y, act_of):
    nc = k.nc
    HALVES = NG // B
    with ExitStack() as ctx:
        sem = lambda n: k.sem(name + n, ctx)
        per = HALVES * chunks // 2
        h_full = [Signal(sem(f"_h_full{i}"), per) for i in range(2)]
        h_ready = [Signal(sem(f"_h_ready{i}"), per) for i in range(2)]
        own = Signal(sem("_own_dve"), HALVES * Norm.DVE_STEPS)
        norm = Norm(k, ctx, name, HALVES)
        block = ctx.enter_context(nc.Block())

        @block.tensor
        def _(pe):
            norm.start(pe, None, None)
            for s in h_full:
                s.start(pe)
            with pe.Fori(0, B) as b:
                for g in range(HALVES):
                    for c in range(chunks):
                        n = g * chunks + c
                        pe.wait_ge(h_ready[n % 2].sem, h_ready[n % 2].at(b, n // 2 - 1))
                        pe.matmul(k.ps_scores[n % 2][0:rows[c], 0:512], w_up(c),
                                  k.xT[:, ds(b * XB + PAD + g * 512, 512)], start=True, stop=True
                                  ).then_inc(h_full[n % 2].sem, 1)
                for g in range(HALVES):
                    y = k.ps_out[g]
                    pe.wait_ge(norm.y_free.sem, norm.y_free.at(b, g - 2))
                    for c in range(chunks):
                        n = g * chunks + c
                        pe.wait_ge(h_ready[n % 2].sem, h_ready[n % 2].at(b, n // 2))
                        for i in range(GROUP):
                            pe.matmul(y[:, i * C:(i + 1) * C], hid[0:rows[c], g, c, i * P:(i + 1) * P], w_down(c),
                                      start=(c == 0 and i == 0), stop=False, skip_group_check=True)
                    kb = bias_y.shape[0]
                    for i in range(GROUP):
                        mm = pe.matmul(y[:, i * C:(i + 1) * C], k.ones[0:kb, 0:P], bias_y, start=False,
                                       stop=i == GROUP - 1, skip_group_check=True)
                    mm.then_inc(norm.y_full.sem, 1)
                for g in range(HALVES):
                    norm.tensor(pe, b, g, g, k.ps_turned[0])

        @block.scalar
        def _(act):
            norm.start(None, None, act)
            for s in h_ready:
                s.start(act)
            with act.Fori(0, B) as b:
                for g in range(HALVES):
                    for c in range(chunks):
                        n = g * chunks + c
                        func, bias = act_of(c)
                        act.wait_ge(h_full[n % 2].sem, h_full[n % 2].at(b, n // 2))
                        nc.scalar.activation(hid[0:rows[c], g, c, :], k.ps_scores[n % 2][0:rows[c], 0:512], func,
                                             bias=bias).then_inc(h_ready[n % 2].sem, 1)
                for g in range(HALVES):
                    norm.scalar_root(act, b, g, g)
                for g in range(HALVES):
                    norm.scalar_store(act, b, g, k.ps_turned[0], b * XB + PAD + g * 512)

        @block.vector
        def _(dve):
            norm.start(None, dve, None)
            own.start(dve)
            with dve.Fori(0, B) as b:
                chain = Chain(dve, own, b)
                for g in range(HALVES):
                    norm.vector(dve, chain, b, g, g, b * TPB + g * GROUP, k.ps_out[g][:, :])
                chain.close()



L1_HEADS, L1_D = 16, 64
PAIRS = L1_HEADS // 2
TABLE = 2 * L - P
TWO_PI = 2 * np.pi
PI_A = 6.28125
PI_B = float(np.floor((TWO_PI - PI_A) * 2 ** 19) / 2 ** 19)
PI_C = float(TWO_PI - PI_A - PI_B)
ROUND = 1.5 * 2 ** 23


def l1_attention(k):
    nc, d = k.nc, k.dram
    LEAD, U = 6, 16
    N = LEAD + U
    with ExitStack() as ctx:
        sb = lambda n, s: k.sb("l1_" + n, s, ctx=ctx)
        o_tok = sb("o_tok", [P, TILES, L1_HEADS * L1_D])
        with ExitStack() as c2:
            sb = lambda n, s, dt=F32: k.sb("l1_" + n, s, dt, ctx=c2)
            rope = sb("rope", [P, 4, L])
            dist = sb("dist", [P, TABLE])
            nbias = sb("neg_bias", [P, 2, TABLE])
            ap = sb("bias_ap", [P, 2 * L1_HEADS])
            cols = sb("bias_cols", [P, 4])
            w = sb("w", [P, 5 * P])
            xb = sb("x_batch", [P, L])
            qk = sb("qk", [P, 2, L])
            v = sb("v", [P, TPB, P])
            rot = sb("rot", [P, 2, 2, 512])
            probs = sb("probs", [P, 2, 1024])
            probsT = sb("probsT", [P, 2, 1024])
            nmax = sb("neg_max", [P, U])
            rsum = sb("row_sum", [P, U])
            rinv = sb("row_inv", [P, 2, TPB])
            with ExitStack() as c3:
                sem = lambda n: k.sem("l1t_" + n, c3)
                loaded, made, own, roots = sem("loaded"), sem("iotas"), sem("own_dve"), sem("acts")
                ints = k.sb("l1_ints", [P, TABLE], mybir.dt.int32, ctx=c3)
                posi = k.sb("l1_posi", [P, L], mybir.dt.int32, ctx=c3)
                freq = k.sb("l1_freq", [P, 3], ctx=c3)
                ang, turns = (k.sb("l1_" + n, [P, L], ctx=c3) for n in ("ang", "turns"))
                block = c3.enter_context(nc.Block())

                @block.sync
                def _(sp):
                    sp.dma_start(freq[:, :], d["L1_freq"]).then_inc(loaded, 16)
                    sp.dma_start(ap[:, :], d["L1_bias_ap"].partition_broadcast(P)).then_inc(loaded, 16)

                @block.gpsimd
                def _(pool):
                    nc.gpsimd.iota(posi[:, :], [[1, L]], base=0, channel_multiplier=0).then_inc(made, 1)
                    nc.gpsimd.iota(ints[:, :], [[1, TABLE]], base=P - L, channel_multiplier=-1).then_inc(made, 1)

                @block.vector
                def _(dve):
                    c = Count(dve, own)
                    v_ = nc.vector
                    dve.wait_ge(loaded, 32)
                    dve.wait_ge(made, 2)
                    c.done(v_.tensor_scalar(ap[:, :], ap[:, :], 0.01, None, ALU.max))
                    c.done(v_.tensor_copy(dist[:, :], ints[:, :]))
                    c.step(v_.tensor_copy(turns[:, :], posi[:, :]))
                    c.step(v_.tensor_scalar(ang[:, :], turns[:, :], freq[:, 0:1], None, ALU.mult))
                    c.step(v_.tensor_scalar(turns[:, :], ang[:, :], 1 / TWO_PI, ROUND, ALU.mult, ALU.add))
                    c.step(v_.tensor_scalar(turns[:, :], turns[:, :], ROUND, None, ALU.subtract))
                    for part in (PI_A, PI_B, PI_C):
                        c.step(v_.scalar_tensor_tensor(ang[:, :], turns[:, :], -part, ang[:, :], ALU.mult, ALU.add))
                    c.step(v_.tensor_scalar(ang[:, :], ang[:, :], 3.1415925, -3.1415925, ALU.min, ALU.max))
                    dve.wait_ge(roots, 4)
                    c.done(v_.tensor_scalar(rope[:, 3, :], rope[:, 1, :], freq[:, 1:2], None, ALU.mult))
                    c.done(v_.tensor_scalar(rope[:, 2, :], rope[:, 0, :], 1.0, None, ALU.mult))
                    c.step(v_.tensor_scalar(rope[:, 0, :], rope[:, 0, :], -0.125, None, ALU.mult))
                    c.step(v_.tensor_scalar(rope[:, 1, :], rope[:, 1, :], freq[:, 1:2], -0.125, ALU.mult, ALU.mult))

                @block.scalar
                def _(act):
                    act.wait_ge(own, 2)
                    nc.scalar.activation(dist[:, :], dist[:, :], ACT.Abs).then_inc(roots, 1)
                    act.wait_ge(own, 10)
                    nc.scalar.activation(rope[:, 1, :], ang[:, :], ACT.Sin).then_inc(roots, 1)
                    nc.scalar.activation(turns[:, :], ang[:, :], ACT.Abs).then_inc(roots, 1)
                    act.wait_ge(roots, 3)
                    nc.scalar.activation(rope[:, 0, :], turns[:, :], ACT.Sin, bias=freq[:, 2:3], scale=-1.0
                                         ).then_inc(roots, 1)

            with ExitStack() as c3:
                sm = lambda n: k.sem("l1a_" + n, c3)
                s_full = [Signal(sm(f"slot_full{i}"), N // 2) for i in range(2)]
                s_free = [Signal(sm(f"slot_free{i}"), N // 2) for i in range(2)]
                w_loaded = sm("w_loaded")
                cols_ready = Signal(sm("cols"), 4)
                logs = Signal(sm("logs"), 2)
                bias_ready = Signal(sm("bias_ready"), 2)
                xb_ready = Signal(sm("xb_ready"), 1)
                rotated = Signal(sm("rotated"), 4)
                prod = Signal(sm("rot_first"), 4)
                qk_ready = Signal(sm("qk_ready"), 4)
                v_ready = Signal(sm("v_ready"), 2)
                e_full = Signal(sm("probs_ready"), U)
                t_full = [Signal(sm(f"turned_full{i}"), U) for i in range(2)]
                t_done = [Signal(sm(f"turned_taken{i}"), U) for i in range(2)]
                o_full = Signal(sm("out_full"), 2)
                o_free = Signal(sm("out_taken"), 2)
                inv = Signal(sm("inv"), 2)
                passed = sm("passed")
                block = c3.enter_context(nc.Block())
                plan = order(N, LEAD, U)
                o_bank = [k.ps_out[j][:, :].rearrange("p (t c) -> p t c", c=L1_D) for j in range(2)]

                def slot_full(n):
                    return s_full[n % 2], n // 2

                @block.sync
                def _(sp):
                    sp.dma_start(w[:, :], d["L1_qkv"][0, :, :]).then_inc(w_loaded, 16)
                    with sp.Fori(0, PAIRS - 1) as hp:
                        sp.wait_ge(s_full[1].sem, s_full[1].at(hp * 2 + 1, LEAD // 2 - 1))
                        sp.dma_start(w[:, :], d["L1_qkv"][ds(hp + 1, 1), :, :].rearrange("o p c -> p (o c)")
                                     ).then_inc(w_loaded, 16)

                @block.gpsimd
                def _(pool):
                    for s in (cols_ready, bias_ready, xb_ready, qk_ready):
                        s.start(pool)
                    with pool.Fori(0, PAIRS) as hp:
                        pool.wait_ge(bias_ready.sem, bias_ready.at(hp, -1))
                        pool.sem_inc(passed, 1)
                        for i in range(4):
                            nc.gpsimd.tensor_copy(cols[:, i:i + 1], ap[:, ds(hp * 2 + (i // 2) * L1_HEADS + i % 2, 1)]
                                                  ).then_inc(cols_ready.sem, 1)
                        for b in range(B):
                            it = hp * 2 + b
                            pool.wait_ge(s_full[1].sem, s_full[1].at(it, LEAD // 2 - 1 - N // 2))
                            pool.sem_inc(passed, 1)
                            nc.gpsimd.tensor_copy(xb[:, :], k.xT[:, ds(b * XB + PAD, L)]).then_inc(xb_ready.sem, 1)
                            for n in range(4):
                                pool.wait_ge(rotated.sem, rotated.at(it, n))
                                nc.gpsimd.tensor_tensor(qk[:, n // 2, (n % 2) * 512:(n % 2 + 1) * 512],
                                                        rot[:, n % 2, 0, :], rot[:, n % 2, 1, :], ALU.add
                                                        ).then_inc(qk_ready.sem, 1)
                            if b == 0:
                                for j in range(2):
                                    pool.wait_ge(logs.sem, logs.at(hp, j))
                                    nc.gpsimd.tensor_tensor(nbias[:, j, :], nbias[:, j, :],
                                                            cols[:, 2 + j:3 + j].broadcast_to([P, TABLE]), ALU.mult
                                                            ).then_inc(bias_ready.sem, 1)

                @block.tensor
                def _(pe):
                    for s in (*s_full, *t_full, o_full):
                        s.start(pe)
                    with pe.Fori(0, PAIRS) as hp:
                        with pe.Fori(0, B) as b:
                            it = hp * 2 + b
                            for what, n in plan:
                                if what == "S":
                                    slot = k.ps_scores[n % 2]
                                    pe.wait_ge(s_free[n % 2].sem, s_free[n % 2].at(it, n // 2 - 1))
                                    if n == 0:
                                        pe.wait_ge(w_loaded, hp * 16 + 16)
                                    if n < 4:
                                        for i in range(2):
                                            c0 = (n // 2) * 2 * P + i * P
                                            mm = pe.matmul(slot[:, i * 512:(i + 1) * 512], w[:, c0:c0 + P],
                                                           k.xT[:, ds(b * XB + PAD + (n % 2) * 512, 512)],
                                                           start=True, stop=True)
                                    elif n < LEAD:
                                        if n == 4:
                                            pe.wait_ge(xb_ready.sem, xb_ready.at(it, 0))
                                        for i in range(4):
                                            c0 = ((n - 4) * 4 + i) * P
                                            mm = pe.matmul(slot[:, i * P:(i + 1) * P], xb[:, c0:c0 + P],
                                                           w[:, 4 * P:5 * P], start=True, stop=True)
                                    else:
                                        u = n - LEAD
                                        j, qt = u // TPB, u % TPB
                                        if u == 0:
                                            pe.wait_ge(qk_ready.sem, qk_ready.at(it, 3))
                                        rows = slice(j * L1_D, (j + 1) * L1_D)
                                        for i in range(2):
                                            mm = pe.matmul(slot[:, i * 512:(i + 1) * 512],
                                                           qk[rows, 0, qt * P:(qt + 1) * P],
                                                           qk[rows, 1, i * 512:(i + 1) * 512], start=True, stop=True)
                                    mm.then_inc(s_full[n % 2].sem, 1)
                                elif what == "T":
                                    pe.wait_ge(e_full.sem, e_full.at(it, n))
                                    turn(pe, k, probs[:, n % 2, :], t_full, t_done, it, n)
                                else:
                                    j, qt = n // TPB, n % TPB
                                    for half in range(2):
                                        pe.wait_ge(t_done[half].sem, t_done[half].at(it, n))
                                    if n == 0:
                                        pe.wait_ge(v_ready.sem, v_ready.at(it, 1))
                                    if qt == 0:
                                        pe.wait_ge(o_free.sem, o_free.at(it, j - 2))
                                    for t in range(TPB):
                                        mm = pe.matmul(o_bank[j][:, qt, :], probsT[:, n % 2, t * P:(t + 1) * P],
                                                       v[:, t, j * L1_D:(j + 1) * L1_D], start=t == 0,
                                                       stop=t == TPB - 1)
                                    if qt == TPB - 1:
                                        mm.then_inc(o_full.sem, 1)

                @block.vector
                def _(dve):
                    for s in (*s_free, rotated, prod, t_done[1], o_free, inv):
                        s.start(dve)
                    with dve.Fori(0, PAIRS) as hp:
                        with dve.Fori(0, B) as b:
                            it = hp * 2 + b
                            for what, n in plan:
                                slot = k.ps_scores[n % 2]
                                if what == "S" and n < 4:
                                    f, at = slot_full(n)
                                    dve.wait_ge(f.sem, f.at(it, at))
                                    dve.wait_ge(qk_ready.sem, qk_ready.at(it, n - 2))
                                    cols_ = slice((n % 2) * 512, (n % 2 + 1) * 512)
                                    nc.vector.tensor_tensor(rot[:, n % 2, 0, :], slot[:, 0:512],
                                                            rope[:, (n // 2) * 2, cols_], ALU.mult
                                                            ).then_inc(prod.sem, 1)
                                    nc.vector.tensor_tensor(rot[:, n % 2, 1, :], slot[:, 512:1024],
                                                            rope[:, (n // 2) * 2 + 1, cols_], ALU.mult
                                                            ).then_inc(rotated.sem, 1)
                                    dve.wait_ge(rotated.sem, rotated.at(it, n))
                                    dve.sem_inc(s_free[n % 2].sem, 1)
                                elif what == "S" and n >= LEAD:
                                    u = n - LEAD
                                    j, qt = u // TPB, u % TPB
                                    f, at = slot_full(n)
                                    dve.wait_ge(f.sem, f.at(it, at))
                                    dve.wait_ge(t_full[1].sem, t_full[1].at(it, u - 2))
                                    if qt == 0:
                                        dve.wait_ge(bias_ready.sem, bias_ready.at(hp, j))
                                    dve.sem_inc(passed, 1)
                                    c0 = L - P - qt * P
                                    nc.vector.tensor_tensor_reduce(
                                        probs[:, u % 2, :], slot[:, :], nbias[:, j, c0:c0 + L], 1.0, HUGE,
                                        ALU.add, ALU.min, nmax[:, u:u + 1]).then_inc(s_free[n % 2].sem, 1)
                                elif what == "T":
                                    take_turned(nc.vector, k, probsT[:, n % 2, :], t_full, t_done, it, n, 1)
                                elif what == "V" and n % TPB == TPB - 1:
                                    j = n // TPB
                                    dve.wait_ge(o_full.sem, o_full.at(it, j))
                                    nc.vector.reciprocal(rinv[:, j, :], rsum[:, j * TPB:(j + 1) * TPB]
                                                         ).then_inc(inv.sem, 1)
                                    dve.wait_ge(inv.sem, inv.at(it, j))
                                    nc.vector.tensor_tensor(
                                        o_tok[:, ds(b * TPB, TPB), ds((hp * 2 + j) * L1_D, L1_D)], o_bank[j],
                                        rinv[:, j, :].unsqueeze(2).broadcast_to([P, TPB, L1_D]), ALU.mult
                                        ).then_inc(o_free.sem, 1)

                @block.scalar
                def _(act):
                    for s in (logs, v_ready, e_full, t_done[0]):
                        s.start(act)
                    with act.Fori(0, PAIRS) as hp:
                        act.wait_ge(cols_ready.sem, cols_ready.at(hp, 3))
                        act.wait_ge(s_free[1].sem, s_free[1].at(hp * 2, -1))
                        for j in range(2):
                            nc.scalar.activation(nbias[:, j, :], dist[:, :], ACT.Ln, bias=1.0,
                                                 scale=cols[:, j:j + 1]).then_inc(logs.sem, 1)
                        with act.Fori(0, B) as b:
                            it = hp * 2 + b
                            for what, n in plan:
                                if what == "S" and 4 <= n < LEAD:
                                    f, at = slot_full(n)
                                    act.wait_ge(f.sem, f.at(it, at))
                                    nc.scalar.copy(v[:, (n - 4) * 4:(n - 3) * 4, :],
                                                   k.ps_scores[n % 2][:, 0:512].rearrange("p (t c) -> p t c", c=P)
                                                   ).then_inc(v_ready.sem, 1)
                                    act.wait_ge(v_ready.sem, v_ready.at(it, n - 4))
                                    act.sem_inc(s_free[n % 2].sem, 1)
                                elif what == "S" and n >= LEAD:
                                    u = n - LEAD
                                    act.wait_ge(s_free[n % 2].sem, s_free[n % 2].at(it, n // 2))
                                    nc.scalar.activation(probs[:, u % 2, :], probs[:, u % 2, :], ACT.Exp,
                                                         bias=nmax[:, u:u + 1], scale=-1.0,
                                                         accum_out=rsum[:, u:u + 1]).then_inc(e_full.sem, 1)
                                elif what == "T":
                                    take_turned(nc.scalar, k, probsT[:, n % 2, :], t_full, t_done, it, n, 0)

        wo = k.sb("l1_wo", [P, 8 * C], ctx=ctx)
        project_out(k, "l1o", o_tok, 8, wo[:, :], d["L1_out_w"], None, None)



F1_DEPTH, F1_HEADS, F1_D, WINDOW = 2, 8, 64, 64
F1_INNER = F1_HEADS * F1_D
F1_HID = 341
HEAD_AT = (0, 2, 1, 3)
F1_ROWS = [P, P, F1_HID - 2 * P]


def l1_ffn(k):
    nc, d = k.nc, k.dram
    with ExitStack() as ctx:
        x_in = k.sb("f1_x_in", [P, TILES * C], ctx=ctx)
        tabs = k.sb("f1_xpos", [P, 2, TPB, 2, F1_D], ctx=ctx)
        mask = k.sb("f1_mask", [P, 5, 2 * P], ctx=ctx)
        with ExitStack() as c2:
            loaded, made, kept = (k.sem("f1_" + n, c2) for n in ("loaded", "made", "kept"))
            block = c2.enter_context(nc.Block())

            @block.sync
            def _(sp):
                sp.dma_start(tabs[:, :, :, :, :], d["F1_xpos"]).then_inc(loaded, 16)
                sp.wait_ge(loaded, 16)

            @block.vector
            def _(dve):
                nc.vector.tensor_copy(x_in[:, :], k.x_tok[:, :]).then_inc(kept, 1)
                dve.wait_ge(kept, 1)

            @block.gpsimd
            def _(pool):
                own = Count(pool, made)
                g = nc.gpsimd
                own.step(g.memset(mask[:, :, :], 0.0))
                own.step(g.affine_select(out=mask[:, :, :], in_=mask[:, :, :], compare_op=ALU.is_ge, fill=-HUGE,
                                         base=P, pattern=[[0, 5], [-1, 2 * P]], channel_multiplier=1))
                own.step(g.affine_select(out=mask[:, :, :], in_=mask[:, :, :], compare_op=ALU.is_ge, fill=-HUGE,
                                         base=WINDOW - P, pattern=[[0, 5], [1, 2 * P]], channel_multiplier=-1))
                own.step(g.memset(mask[:, 0, 0:P], -HUGE))

        for layer in range(F1_DEPTH):
            l1_local_attention(k, layer, tabs, mask)
            l1_geglu(k, layer, x_in)


def shifted(g, own, dst, xT, col, width):
    own.step(g.tensor_copy(dst[:, 0:width], xT[:, ds(col - 1, width)]))
    return g.tensor_copy(dst[0:64, 0:width], xT[0:64, ds(col, width)])


def l1_local_attention(k, layer, tabs, mask):
    nc, d = k.nc, k.dram
    name = f"f1a{layer}"
    LEAD, U = 6, 4
    N = LEAD + U
    IT = TPB // 2
    with ExitStack() as ctx:
        o_tok = k.sb(name + "_o_tok", [P, TILES, F1_INNER], ctx=ctx)
        with ExitStack() as c2:
            sb = lambda n, s: k.sb(name + n, s, ctx=c2)
            w = sb("_w", [P, 3 * F1_INNER])
            scales = sb("_scales", [P, 2, 2, F1_D])
            tab = sb("_tab", [P, 2, TPB, 2, F1_D])
            hs = sb("_h", [P, 2, P])
            sq = sb("_sq", [P, 2, 1024])
            ss = sb("_ss", [P, 2, 16])
            root = sb("_root", [P, 2, 16])
            rn = sb("_rn", [P, 2, 2, 16])
            qkn = sb("_qkn", [P, 2, 1024])
            t1 = sb("_t1", [P, 2, 1024])
            qkT = sb("_qkT", [P, 2, 8, P])
            k_prev = sb("_k_prev", [P, 4, P])
            v = sb("_v", [P, 2, F1_INNER])
            v_prev = sb("_v_prev", [P, F1_INNER])
            probs = sb("_probs", [P, 2, 1024])
            probsT = sb("_probsT", [P, 2, 1024])
            nmax = sb("_nmax", [P, 2, 4])
            rsum = sb("_rsum", [P, U * 4])
            rinv = sb("_rinv", [P, 2, 8])
            sm = lambda n: k.sem(name + "_" + n, c2)
            w_loaded = sm("w_loaded")
            s_full = [Signal(sm(f"slot_full{i}"), N // 2) for i in range(2)]
            s_free = [Signal(sm(f"slot_free{i}"), N // 2) for i in range(2)]
            tab_ready = sm("tab_ready")
            cleared = sm("cleared")
            h_ready = Signal(sm("h_ready"), 2)
            squared = Signal(sm("squared"), 2)
            summed = Signal(sm("summed"), 2)
            rooted = Signal(sm("rooted"), 2)
            inverse = Signal(sm("inverse"), 4)
            normed = Signal(sm("normed"), 2)
            first = Signal(sm("first"), 2)
            second = Signal(sm("second"), 2)
            roped = Signal(sm("roped"), 2)
            own_pool = Signal(sm("own_pool"), 2)
            passed = sm("passed")
            kept = Signal(sm("kept"), 1)
            qkT_ready = Signal(sm("qkT_ready"), 2)
            v_ready = Signal(sm("v_ready"), 2)
            max_ready = Signal(sm("max_ready"), U)
            e_full = Signal(sm("probs_ready"), U)
            t_full = [Signal(sm(f"turned_full{i}"), U) for i in range(2)]
            t_done = [Signal(sm(f"turned_taken{i}"), U) for i in range(2)]
            o_full = Signal(sm("out_full"), 2)
            o_free = Signal(sm("out_taken"), 2)
            inv = Signal(sm("inv"), 2)
            block = c2.enter_context(nc.Block())
            plan = order(N, LEAD, U)

            def heads(t):
                return t.rearrange("p (a h e) -> p a h e", a=2, e=F1_D)

            def swapped(out, src, table):
                hf = F1_D // 2
                for lo, hi in ((0, hf), (hf, 0)):
                    yield (heads(out)[:, :, :, lo:lo + hf], heads(src)[:, :, :, hi:hi + hf],
                           table[:, :, lo:lo + hf].unsqueeze(2).broadcast_to([P, 2, F1_HEADS, hf]))

            @block.sync
            def _(sp):
                sp.dma_start(scales[:, :, :, :], d[f"F1_scales{layer}"].partition_broadcast(P)).then_inc(w_loaded, 16)
                sp.dma_start(w[:, :], d["L1_ffn_wqkv"][layer, :, :]).then_inc(w_loaded, 16)

            @block.gpsimd
            def _(pool):
                for s in (h_ready, first, roped, kept, own_pool):
                    s.start(pool)
                nc.gpsimd.memset(qkT[:, 1, :, :], 0.0)
                nc.gpsimd.memset(v[:, 1, :], 0.0).then_inc(cleared, 1)
                pool.wait_ge(cleared, 1)
                pool.wait_ge(tab_ready, 4)
                with pool.Fori(0, B) as b:
                    with pool.Fori(0, IT) as i:
                        it = b * IT + i
                        chain = Chain(pool, own_pool, it)
                        for s in range(2):
                            pool.wait_ge(s_full[1].sem, s_full[1].at(it, s - N // 2))
                            shifted(nc.gpsimd, chain, hs[:, s, :], k.xT, b * XB + PAD + (i * 2 + s) * P, P
                                    ).then_inc(h_ready.sem, 1)
                        pool.wait_ge(o_full.sem, o_full.at(it, -1))
                        pool.sem_inc(passed, 1)
                        nc.gpsimd.tensor_copy(k_prev[:, :, :], qkT[:, 1, 4:8, :])
                        nc.gpsimd.tensor_copy(v_prev[:, :], v[:, 1, :]).then_inc(kept.sem, 1)
                        for s in range(2):
                            pool.wait_ge(normed.sem, normed.at(it, s))
                            pool.wait_ge(s_full[s].sem, s_full[s].at(it, 2 - N // 2))
                            t = tab[:, 0, ds(i * 2 + s, 1), :, :].rearrange("p o a e -> p (o a) e")
                            for a in range(2):
                                ins = nc.gpsimd.tensor_tensor(
                                    heads(t1[:, s, :])[:, a, :, :], heads(qkn[:, s, :])[:, a, :, :],
                                    t[:, a, :].unsqueeze(1).broadcast_to([P, F1_HEADS, F1_D]), ALU.mult)
                            ins.then_inc(first.sem, 1)
                            pool.wait_ge(first.sem, first.at(it, s))
                            pool.wait_ge(second.sem, second.at(it, s))
                            nc.gpsimd.tensor_tensor(t1[:, s, :], t1[:, s, :], sq[:, s, :], ALU.add
                                                    ).then_inc(roped.sem, 1)

            @block.tensor
            def _(pe):
                for s in (*s_full, *t_full, o_full):
                    s.start(pe)
                pe.wait_ge(w_loaded, 32)
                pe.wait_ge(cleared, 1)
                with pe.Fori(0, B) as b:
                    with pe.Fori(0, IT) as i:
                        it = b * IT + i
                        for what, n in plan:
                            if what == "S":
                                slot = k.ps_scores[n % 2]
                                pe.wait_ge(s_free[n % 2].sem, s_free[n % 2].at(it, n // 2 - 1))
                                if n < 4:
                                    s = n // 2
                                    if n % 2 == 0:
                                        pe.wait_ge(h_ready.sem, h_ready.at(it, s))
                                    for c in ((0, 1) if n % 2 == 0 else (2,)):
                                        mm = pe.matmul(slot[:, (c % 2) * 512:(c % 2 + 1) * 512], hs[:, s, :],
                                                       w[:, c * 512:(c + 1) * 512], start=True, stop=True)
                                elif n < LEAD:
                                    s = n - 4
                                    pe.wait_ge(roped.sem, roped.at(it, s))
                                    for c in range(8):
                                        mm = pe.transpose(slot[:, c * P:(c + 1) * P], t1[:, s, c * P:(c + 1) * P],
                                                          k.ident[:, :])
                                else:
                                    s, u = (n - LEAD) // 2, n - LEAD
                                    pe.wait_ge(qkT_ready.sem, qkT_ready.at(it, s))
                                    if u == 0:
                                        pe.wait_ge(kept.sem, kept.at(it, 0))
                                    for hi in range(4):
                                        h = 4 * (u % 2) + HEAD_AT[hi]
                                        rows = slice((h % 2) * F1_D, (h % 2 + 1) * F1_D)
                                        for part in range(2):
                                            kb = (k_prev[rows, h // 2, :] if s == 0 and part == 0 else
                                                  qkT[rows, s - 1 + part, 4 + h // 2, :])
                                            c0 = hi * 256 + part * P
                                            mm = pe.matmul(slot[:, c0:c0 + P], qkT[rows, s, h // 2, :], kb,
                                                           start=True, stop=True)
                                mm.then_inc(s_full[n % 2].sem, 1)
                            elif what == "T":
                                pe.wait_ge(e_full.sem, e_full.at(it, n))
                                turn(pe, k, probs[:, n % 2, :], t_full, t_done, it, n)
                            else:
                                s = n // 2
                                for half in range(2):
                                    pe.wait_ge(t_done[half].sem, t_done[half].at(it, n))
                                if n % 2 == 0:
                                    pe.wait_ge(v_ready.sem, v_ready.at(it, s))
                                    pe.wait_ge(o_free.sem, o_free.at(it, s - 2))
                                for hi in range(4):
                                    h = 4 * (n % 2) + HEAD_AT[hi]
                                    for part in range(2):
                                        vb = v_prev if s == 0 and part == 0 else v[:, s - 1 + part, :]
                                        c0 = (hi * 2 + part) * P
                                        mm = pe.matmul(k.ps_out[s][:, h * F1_D:(h + 1) * F1_D],
                                                       probsT[:, n % 2, c0:c0 + P], vb[:, h * F1_D:(h + 1) * F1_D],
                                                       start=part == 0, stop=part == 1)
                                if n % 2 == 1:
                                    mm.then_inc(o_full.sem, 1)

            @block.vector
            def _(dve):
                for s in (*s_free, summed, inverse, normed, second, max_ready, t_done[1], o_free, inv):
                    s.start(dve)
                dve.wait_ge(w_loaded, 32)
                for a in range(2):
                    for qk in range(2):
                        nc.vector.tensor_tensor(tab[:, a, :, qk, :], tabs[:, a, :, qk, :],
                                                scales[:, a, qk, :].unsqueeze(1).broadcast_to([P, TPB, F1_D]),
                                                ALU.mult).then_inc(tab_ready, 1)
                dve.wait_ge(tab_ready, 4)
                with dve.Fori(0, B) as b:
                    with dve.Fori(0, IT) as i:
                        it = b * IT + i
                        own = Chain(dve, inverse, it)
                        for what, n in plan:
                            slot = k.ps_scores[n % 2]
                            if what == "S" and n in (1, 3):
                                s = n // 2
                                dve.wait_ge(squared.sem, squared.at(it, s))
                                nc.vector.tensor_reduce(ss[:, s, :], sq[:, s, :].rearrange(
                                    "p (h e) -> p h e", e=F1_D), AX.X, ALU.add).then_inc(summed.sem, 1)
                                dve.wait_ge(rooted.sem, rooted.at(it, s))
                                own.step(nc.vector.tensor_scalar(rn[:, s, 0, :], root[:, s, :], 1e-12, None, ALU.max))
                                own.step(nc.vector.reciprocal(rn[:, s, 1, :], rn[:, s, 0, :]))
                                nc.vector.tensor_tensor(
                                    qkn[:, s, :].rearrange("p (h e) -> p h e", e=F1_D),
                                    k.ps_scores[0][:, :].rearrange("p (h e) -> p h e", e=F1_D),
                                    rn[:, s, 1, :].unsqueeze(2).broadcast_to([P, 16, F1_D]), ALU.mult
                                    ).then_inc(s_free[0].sem, 1)
                                dve.wait_ge(s_free[0].sem, s_free[0].at(it, s))
                                dve.sem_inc(normed.sem, 1)
                                t = tab[:, 1, ds(i * 2 + s, 1), :, :].rearrange("p o a e -> p (o a) e")
                                for out, src, table in swapped(sq[:, s, :], qkn[:, s, :], t):
                                    for a in range(2):
                                        ins = nc.vector.tensor_tensor(out[:, a], src[:, a], table[:, a], ALU.mult)
                                ins.then_inc(second.sem, 1)
                            elif what == "S" and n >= LEAD:
                                u = n - LEAD
                                s = u // 2
                                dve.wait_ge(s_full[n % 2].sem, s_full[n % 2].at(it, n // 2))
                                dve.wait_ge(t_full[1].sem, t_full[1].at(it, u - 2))
                                m = mask[:, ds(i, 1), :] if s == 0 else mask[:, 4:5, :]
                                p3 = probs[:, u % 2, :].rearrange("p (h q) -> p h q", h=4)
                                nc.vector.tensor_tensor(p3, slot[:, :].rearrange("p (h q) -> p h q", h=4),
                                                        m.broadcast_to([P, 4, 2 * P]), ALU.add
                                                        ).then_inc(s_free[n % 2].sem, 1)
                                dve.wait_ge(s_free[n % 2].sem, s_free[n % 2].at(it, n // 2))
                                nc.vector.tensor_reduce(nmax[:, u % 2, :], p3, AX.X, ALU.max, negate=True
                                                        ).then_inc(max_ready.sem, 1)
                            elif what == "T":
                                take_turned(nc.vector, k, probsT[:, n % 2, :], t_full, t_done, it, n, 1)
                            elif what == "V" and n % 2 == 1:
                                s = n // 2
                                dve.wait_ge(o_full.sem, o_full.at(it, s))
                                nc.vector.reciprocal(rinv[:, s, :], rsum[:, s * 8:(s + 1) * 8]).then_inc(inv.sem, 1)
                                dve.wait_ge(inv.sem, inv.at(it, s))
                                nc.vector.tensor_tensor(
                                    o_tok[:, ds(it * 2 + s, 1), :].rearrange("p o (h e) -> p (o h) e", e=F1_D),
                                    k.ps_out[s][:, :].rearrange("p (h e) -> p h e", e=F1_D),
                                    rinv[:, s, :].unsqueeze(2).broadcast_to([P, F1_HEADS, F1_D]), ALU.mult
                                    ).then_inc(o_free.sem, 1)

            @block.scalar
            def _(act):
                for s in (squared, rooted, qkT_ready, v_ready, e_full, t_done[0]):
                    s.start(act)
                with act.Fori(0, B) as b:
                    with act.Fori(0, IT) as i:
                        it = b * IT + i
                        for what, n in plan:
                            slot = k.ps_scores[n % 2]
                            if what == "S" and n < LEAD:
                                act.wait_ge(s_full[n % 2].sem, s_full[n % 2].at(it, n // 2))
                                if n in (0, 2):
                                    act.wait_ge(roped.sem, roped.at(it, n // 2 - 2))
                                    nc.scalar.activation(sq[:, n // 2, :], slot[:, :], ACT.Square
                                                         ).then_inc(squared.sem, 1)
                                elif n in (1, 3):
                                    s = n // 2
                                    if n == 1:
                                        act.wait_ge(kept.sem, kept.at(it, 0))
                                    nc.scalar.copy(v[:, s, :], slot[:, 0:512]).then_inc(v_ready.sem, 1)
                                    act.wait_ge(v_ready.sem, v_ready.at(it, s))
                                    act.sem_inc(s_free[1].sem, 1)
                                    act.wait_ge(summed.sem, summed.at(it, s))
                                    nc.scalar.activation(root[:, s, :], ss[:, s, :], ACT.Sqrt
                                                         ).then_inc(rooted.sem, 1)
                                else:
                                    s = n - 4
                                    nc.scalar.copy(qkT[:, s, :, :], slot[:, :].rearrange("p (c q) -> p c q", q=P)
                                                   ).then_inc(qkT_ready.sem, 1)
                                    act.wait_ge(qkT_ready.sem, qkT_ready.at(it, s))
                                    act.sem_inc(s_free[n % 2].sem, 1)
                            elif what == "S":
                                u = n - LEAD
                                act.wait_ge(max_ready.sem, max_ready.at(it, u))
                                for hi in range(4):
                                    p1 = probs[:, u % 2, hi * 256:(hi + 1) * 256]
                                    at = u * 4 + HEAD_AT[hi]
                                    ins = nc.scalar.activation(p1, p1, ACT.Exp, bias=nmax[:, u % 2, hi:hi + 1],
                                                               accum_out=rsum[:, at:at + 1])
                                ins.then_inc(e_full.sem, 1)
                            elif what == "T":
                                take_turned(nc.scalar, k, probsT[:, n % 2, :], t_full, t_done, it, n, 0)

        wo = k.sb(name + "_wo", [P, 4 * C], ctx=ctx)
        project_out(k, name + "o", o_tok, 4, wo[:, :], d["F1_wo"][layer, :, :], None, None, normed=False)


def l1_geglu(k, layer, x_in):
    nc, d = k.nc, k.dram
    name = f"f1g{layer}"
    last = layer == F1_DEPTH - 1
    CH, HALVES = 3, NG // B
    with ExitStack() as ctx:
        sb = lambda n, s: k.sb(name + n, s, ctx=ctx)
        sem = lambda n: k.sem(name + n, ctx)
        w1 = sb("_w1", [P, 2 * F1_HID])
        w2 = sb("_w2", [P, CH, C])
        cols = sb("_cols", [P, 8])
        b2 = sb("_b2", [1, C])
        hs = sb("_h", [P, 2, 512])
        hn = sb("_hn", [P, 2, 512])
        hT = sb("_hT", [P, 2, 512])
        stats = sb("_stats", [P, 2, GROUP, 6])
        mv = sb("_mv", [P, 2, GROUP, 2])
        rs = sb("_rs", [P, 2, 3, GROUP])
        gate = sb("_gate", [P, 2, 512])
        hid = sb("_hid", [P, 2, CH, 512])
        w_loaded = sem("_w_loaded")
        own_pool = Signal(sem("_own_pool"), HALVES)
        h_ready = Signal(sem("_h_ready"), HALVES)
        ht_full = Signal(sem("_ht_full"), HALVES)
        var = Signal(sem("_var"), HALVES)
        root = Signal(sem("_root"), HALVES)
        hn_ready = Signal(sem("_hn_ready"), HALVES)
        hb_full = Signal(sem("_hb_full"), HALVES)
        hT_ready = Signal(sem("_hT_ready"), HALVES)
        per = HALVES * CH // 2
        u_full = [Signal(sem(f"_u_full{i}"), per) for i in range(2)]
        gate_ready = Signal(sem("_gate_ready"), HALVES * CH)
        hid_ready = [Signal(sem(f"_hid_ready{i}"), per) for i in range(2)]
        passed = sem("_passed")
        own = Signal(sem("_own_dve"), HALVES * ((Norm.DVE_STEPS + 1 if last else 1) + 12))
        norm = Norm(k, ctx, name + "n", HALVES)
        block = ctx.enter_context(nc.Block())

        @block.sync
        def _(sp):
            for out, src in ((w1, d["L1_ffn_w1"][layer, :, :]), (cols, d["F1_cols"][layer, :, :]),
                             (b2, d["L1_ffn_b2"][layer:layer + 1, :])):
                sp.dma_start(out[:, :], src).then_inc(w_loaded, 16)
            sp.dma_start(w2[:, :, :], d["F1_w2"][layer, :, :, :]).then_inc(w_loaded, 16)

        @block.gpsimd
        def _(pool):
            h_ready.start(pool)
            own_pool.start(pool)
            with pool.Fori(0, B) as b:
                chain = Chain(pool, own_pool, b)
                for g in range(HALVES):
                    pool.wait_ge(ht_full.sem, ht_full.at(b, g - HALVES))
                    shifted(nc.gpsimd, chain, hs[:, g, :], k.xT, b * XB + PAD + g * 512, 512).then_inc(h_ready.sem, 1)

        @block.tensor
        def _(pe):
            norm.start(pe, None, None)
            for s in (ht_full, hb_full, *u_full):
                s.start(pe)
            pe.wait_ge(w_loaded, 64)
            with pe.Fori(0, B) as b:
                for g in range(HALVES):
                    pe.wait_ge(h_ready.sem, h_ready.at(b, g))
                    pe.wait_ge(norm.xT_ready.sem, norm.xT_ready.at(b, -1))
                    for i in range(GROUP):
                        mm = pe.transpose(k.ps_turned[g][:, i * P:(i + 1) * P], hs[:, g, i * P:(i + 1) * P],
                                          k.ident[:, :])
                    mm.then_inc(ht_full.sem, 1)
                for g in range(HALVES):
                    pe.wait_ge(hn_ready.sem, hn_ready.at(b, g))
                    for i in range(GROUP):
                        mm = pe.transpose(k.ps_turned[g][:, i * P:(i + 1) * P], hn[:, g, i * P:(i + 1) * P],
                                          k.ident[:, :])
                    mm.then_inc(hb_full.sem, 1)
                for g in range(HALVES):
                    pe.wait_ge(hT_ready.sem, hT_ready.at(b, g))
                    for c in range(CH):
                        n = g * CH + c
                        pe.wait_ge(hid_ready[n % 2].sem, hid_ready[n % 2].at(b, n // 2 - 1))
                        for part in range(2):
                            c0 = part * F1_HID + c * P
                            mm = pe.matmul(k.ps_scores[n % 2][0:F1_ROWS[c], part * 512:(part + 1) * 512],
                                           w1[:, c0:c0 + F1_ROWS[c]], hT[:, g, :], start=True, stop=True)
                        mm.then_inc(u_full[n % 2].sem, 1)
                for g in range(HALVES):
                    y = k.ps_out[g]
                    pe.wait_ge(norm.y_free.sem, norm.y_free.at(b, g - 2))
                    for c in range(CH):
                        n = g * CH + c
                        pe.wait_ge(hid_ready[n % 2].sem, hid_ready[n % 2].at(b, n // 2))
                        for i in range(GROUP):
                            pe.matmul(y[:, i * C:(i + 1) * C], hid[0:F1_ROWS[c], g, c, i * P:(i + 1) * P],
                                      w2[0:F1_ROWS[c], c, :], start=(c == 0 and i == 0), stop=False,
                                      skip_group_check=True)
                    for i in range(GROUP):
                        mm = pe.matmul(y[:, i * C:(i + 1) * C], k.ones[0:1, 0:P], b2[:, :], start=False,
                                       stop=i == GROUP - 1, skip_group_check=True)
                    mm.then_inc(norm.y_full.sem, 1)
                for g in range(HALVES):
                    norm.tensor(pe, b, g, g, k.ps_turned[0])

        @block.scalar
        def _(act):
            norm.start(None, None, act)
            for s in (root, hT_ready, gate_ready):
                s.start(act)
            with act.Fori(0, B) as b:
                for g in range(HALVES):
                    act.wait_ge(var.sem, var.at(b, g))
                    nc.scalar.activation(rs[:, g, 1, :], rs[:, g, 0, :], ACT.Sqrt).then_inc(root.sem, 1)
                for g in range(HALVES):
                    act.wait_ge(hb_full.sem, hb_full.at(b, g))
                    nc.scalar.activation(hT[:, g, :], k.ps_turned[g][:, :], ACT.Identity, bias=cols[:, 1:2],
                                         scale=cols[:, 0:1]).then_inc(hT_ready.sem, 1)
                for g in range(HALVES):
                    for c in range(CH):
                        n = g * CH + c
                        act.wait_ge(u_full[n % 2].sem, u_full[n % 2].at(b, n // 2))
                        act.wait_ge(hid_ready[n % 2].sem, hid_ready[n % 2].at(b, n // 2 - 1))
                        nc.scalar.activation(gate[0:F1_ROWS[c], n % 2, :],
                                             k.ps_scores[n % 2][0:F1_ROWS[c], 512:1024], ACT.Gelu,
                                             bias=cols[0:F1_ROWS[c], 5 + c:6 + c]).then_inc(gate_ready.sem, 1)
                if last:
                    for g in range(HALVES):
                        norm.scalar_root(act, b, g, g)
                for g in range(HALVES):
                    norm.scalar_store(act, b, g, k.ps_turned[0], b * XB + PAD + g * 512)

        @block.vector
        def _(dve):
            norm.start(None, dve, None)
            for s in (var, hn_ready, *hid_ready, own):
                s.start(dve)
            with dve.Fori(0, B) as b:
                chain = Chain(dve, own, b)
                for g in range(HALVES):
                    dve.wait_ge(ht_full.sem, ht_full.at(b, g))
                    dve.sem_inc(passed, 1)
                    for i in range(GROUP):
                        chain.done(nc.vector.bn_stats(stats[:, g, i, :], k.ps_turned[g][:, i * P:(i + 1) * P]))
                    chain.wait_apart(passed)
                    for i in range(GROUP):
                        chain.done(nc.vector.bn_aggr(mv[:, g, i, :], stats[:, g, i, :]))
                    chain.wait()
                    nc.vector.tensor_scalar(rs[:, g, 0, :], mv[:, g, :, 1], EPS, None, ALU.add).then_inc(var.sem, 1)
                for g in range(HALVES):
                    dve.wait_ge(root.sem, root.at(b, g))
                    chain.step(nc.vector.reciprocal(rs[:, g, 2, :], rs[:, g, 1, :]))
                    for i in range(GROUP):
                        ins = nc.vector.tensor_scalar(hn[:, g, i * C:(i + 1) * C],
                                                      k.ps_turned[g][:, i * P:(i + 1) * P], mv[:, g, i, 0:1],
                                                      rs[:, g, 2, i:i + 1], ALU.subtract, ALU.mult)
                        if i < GROUP - 1:
                            chain.done(ins)
                    ins.then_inc(hn_ready.sem, 1)
                for g in range(HALVES):
                    for c in range(CH):
                        n = g * CH + c
                        r = F1_ROWS[c]
                        dve.wait_ge(gate_ready.sem, gate_ready.at(b, n))
                        nc.vector.scalar_tensor_tensor(hid[0:r, g, c, :], k.ps_scores[n % 2][0:r, 0:512],
                                                       cols[0:r, 2 + c:3 + c], gate[0:r, n % 2, :], ALU.add,
                                                       ALU.mult).then_inc(hid_ready[n % 2].sem, 1)
                for g in range(HALVES):
                    tile0 = b * TPB + g * GROUP
                    norm.vector(dve, chain, b, g, g, tile0, k.ps_out[g][:, :], normed=last,
                                also=x_in[:, ds(tile0 * C, 512)] if last else None)
                chain.close()



def small_head_attention(k, name, inputs, causal, denom, wo_dram, bo_dram):
    nc, d = k.nc, k.dram
    H, D = 16, 8
    SET = 4
    SETS = H // SET
    U = SET * TPB
    RING = 4
    LAG = 3
    ROWS = 9 * D
    scratch = [nc.dram_tensor(f"{name}_parts_{i}", (3, P, B * L), BF16, kind="Internal").ap() for i in "qk"]
    with ExitStack() as ctx:
        sb = lambda n, s, dt=F32: k.sb(name + n, s, dt, ctx=ctx)
        w = sb("_w", [P, 3 * C])
        wo, bo = sb("_wo", [P, SETS, C]), sb("_bo", [1, C])
        extra = sb("_extra", [P, H])
        tri = sb("_tri", [P, 7 * P])
        v = sb("_v", [P, TILES, C])
        oT = sb("_oT", [P, B * SETS * L])
        with ExitStack() as c2:
            loaded, full, taken, own, split, moved = (k.sem(name + "p_" + n, c2) for n in (
                "loaded", "full", "taken", "own", "split", "moved"))
            raw = k.sb(name + "_raw", [P, 2, 512], ctx=c2)
            rest = k.sb(name + "_rest", [P, 2, 2, 512], ctx=c2)
            parts = k.sb(name + "_parts", [P, 2, 3, B * L], BF16, ctx=c2)
            block = c2.enter_context(nc.Block())
            jobs = [(kind, i) for i in range(NG) for kind in range(2)] + [(2, i) for i in range(NG)]

            @block.sync
            def _(sp):
                sp.dma_start(w[:, :], d[inputs]).then_inc(loaded, 16)
                if denom is not None:
                    sp.dma_start(extra[:, :], d[denom].partition_broadcast(P)).then_inc(loaded, 16)
                for i in range(2):
                    sp.wait_ge(split, 4 * (2 * (NG - 1) + i + 1))
                    sp.dma_start(scratch[i].rearrange("s p t -> p s t"), parts[:, i, :, :]).then_inc(moved, 16)
                sp.wait_ge(moved, 32)

            @block.gpsimd
            def _(pool):
                if denom is None:
                    nc.gpsimd.memset(extra[:, :], 1e-8).then_inc(own, 1)
                if causal:
                    nc.gpsimd.memset(tri[:, :], 0.0).then_inc(own, 1)
                    pool.wait_ge(own, 1)
                    nc.gpsimd.affine_select(out=tri[:, :], in_=tri[:, :], compare_op=ALU.is_ge, fill=-HUGE,
                                            base=3 * P, pattern=[[-1, 7 * P]], channel_multiplier=1).then_inc(own, 1)
                    pool.wait_ge(own, 2)
                pool.wait_ge(own, 1)

            @block.tensor
            def _(pe):
                pe.wait_ge(loaded, 16 if denom is None else 32)
                for n, (kind, i) in enumerate(jobs):
                    bank = k.ps_out[n % 2]
                    if n >= 2:
                        pe.wait_ge(taken, n - 1)
                    if kind < 2:
                        mm = pe.matmul(bank[:, :], w[:, kind * C:(kind + 1) * C], k.xT[:, xcol(i):xcol(i) + 512],
                                       start=True, stop=True)
                    else:
                        for s in range(GROUP):
                            c0 = xcol(i) + s * P
                            mm = pe.matmul(bank[:, s * C:(s + 1) * C], k.xT[:, c0:c0 + P], w[:, 2 * C:3 * C],
                                           start=True, stop=True)
                    mm.then_inc(full, 1)

            @block.scalar
            def _(act):
                for n, (kind, i) in enumerate(jobs):
                    act.wait_ge(full, n + 1)
                    if kind < 2:
                        if n >= 2:
                            act.wait_ge(split, 4 * (n - 1))
                        nc.scalar.activation(raw[:, n % 2, :], k.ps_out[n % 2][:, :], ACT.Copy,
                                             scale=float(D ** -0.5) if kind == 0 else 1.0).then_inc(taken, 1)
                    else:
                        nc.scalar.copy(v[:, GROUP * i:GROUP * (i + 1), :], k.ps_out[n % 2][:, :].rearrange("p (t c) -> p t c", c=C)
                                       ).then_inc(taken, 1)
                if denom is not None:
                    act.wait_ge(loaded, 32)
                    nc.scalar.activation(extra[:, :], extra[:, :], ACT.Exp).then_inc(taken, 1)
                act.wait_ge(taken, len(jobs) + (denom is not None))

            @block.vector
            def _(dve):
                own_ = Count(dve, split)
                for n, (kind, i) in enumerate(jobs[:2 * NG]):
                    dve.wait_ge(taken, n + 1)
                    c = slice(i * 512, (i + 1) * 512)
                    x, r = raw[:, n % 2, :], rest[:, n % 2, :, :]
                    own_.step(nc.vector.tensor_copy(parts[:, kind, 0, c], x))
                    own_.step(nc.vector.tensor_tensor(r[:, 0, :], x, parts[:, kind, 0, c], ALU.subtract))
                    own_.step(nc.vector.tensor_copy(parts[:, kind, 1, c], r[:, 0, :]))
                    own_.step(nc.vector.tensor_tensor(parts[:, kind, 2, c], r[:, 0, :], parts[:, kind, 1, c],
                                                      ALU.subtract))

        with ExitStack() as c2:
            sb = lambda n, s, dt=F32: k.sb(name + n, s, dt, ctx=c2)
            qs = sb("_q_rows", [P, SET, L], BF16)
            ks = sb("_k_rows", [P, SET, L], BF16)
            vz = sb("_v_set", [P, SET, TPB, 4 * D])
            ex = sb("_extra_set", [P, SET])
            probs = sb("_probs", [P, RING, 1024])
            probsT = sb("_probsT", [P, 2, 1024])
            nmax = sb("_nmax", [P, U])
            rsum = sb("_rsum", [P, U])
            den = sb("_den", [P, 2, U])
            sm = lambda n: k.sem(name + "a_" + n, c2)
            blocks = (lambda u: max(4, u % TPB + 1)) if causal else (lambda u: TPB)
            second = [blocks(u) > 4 for u in range(U)]

            def event(half, u):
                if half == 0:
                    return u
                u, less = (u, 0) if u >= 0 else (u + U, sum(second))
                return sum(second[:u + 1]) - 1 - less

            cleared = sm("cleared")
            s_full = [Signal(sm(f"scores_full{i}"), U // 2) for i in range(2)]
            rows_ready = [Signal(sm(f"rows_ready{j}"), 6, 16) for j in range(SET)]
            v_ready = Signal(sm("v_ready"), 1)
            masked = Signal(sm("masked"), U)
            max_ready = Signal(sm("max_ready"), U)
            e_full = Signal(sm("exp_done"), U)
            inv_ready = Signal(sm("inv_ready"), 2 * U)
            p_full = Signal(sm("probs_ready"), U)
            t_full = [Signal(sm("turned_full0"), U), Signal(sm("turned_full1"), sum(second))]
            t_done = [Signal(sm("turned_taken0"), U), Signal(sm("turned_taken1"), sum(second))]
            o_full = Signal(sm("out_full"), 1)
            o_free = [Signal(sm(f"out_taken{i}"), 1) for i in range(2)]
            passed = sm("passed")
            block = c2.enter_context(nc.Block())
            plan = order(U, 0, U, LAG)

            @block.sync
            def _(sp):
                for s in rows_ready:
                    s.start(sp)
                sp.wait_ge(cleared, 1)
                with sp.Fori(0, B) as b:
                    with sp.Fori(0, SETS) as st:
                        it = b * SETS + st
                        for j in range(SET):
                            sp.wait_ge(s_full[1].sem, s_full[1].at(it, 4 * (j + 1) - 1 - U // 2))
                            r0 = st * (SET * D) + j * D
                            for i in range(3):
                                block_rows = slice(3 * i * D, 3 * (i + 1) * D)
                                q_rows = scratch[0][i, ds(r0, D), ds(b * L, L)].unsqueeze(0).broadcast_to([3, D, L])
                                sp.dma_start(qs[block_rows, j, :], q_rows).then_inc(rows_ready[j].sem, 16)
                                k_rows = scratch[1][:, ds(r0, D), ds(b * L, L)]
                                sp.dma_start(ks[block_rows, j, :], k_rows).then_inc(rows_ready[j].sem, 16)

            @block.gpsimd
            def _(pool):
                for s in (v_ready, p_full):
                    s.start(pool)
                nc.gpsimd.memset(qs[:, :, :], 0.0)
                nc.gpsimd.memset(vz[:, :, :, :], 0.0)
                nc.gpsimd.memset(ks[:, :, :], 0.0).then_inc(cleared, 1)
                pool.wait_ge(cleared, 1)
                with pool.Fori(0, B) as b:
                    with pool.Fori(0, SETS) as st:
                        it = b * SETS + st
                        pool.wait_ge(o_full.sem, o_full.at(it, -1))
                        pool.sem_inc(passed, 1)
                        nc.gpsimd.tensor_copy(ex[:, :], extra[:, ds(st * SET, SET)])
                        for j in range(SET):
                            ins = nc.gpsimd.tensor_copy(vz[:, j, :, j * D:(j + 1) * D],
                                                        v[:, ds(b * TPB, TPB), ds(st * (SET * D) + j * D, D)])
                        ins.then_inc(v_ready.sem, 1)
                        for u in range(U):
                            pool.wait_ge(inv_ready.sem, inv_ready.at(it, 2 * u + 1))
                            nk = blocks(u) * P
                            p = probs[:, u % RING, 0:nk]
                            nc.gpsimd.tensor_tensor(p, p, den[:, 1, u:u + 1].broadcast_to([P, nk]), ALU.mult
                                                    ).then_inc(p_full.sem, 1)

            @block.tensor
            def _(pe):
                for s in (*s_full, *t_full, o_full):
                    s.start(pe)
                with pe.Fori(0, B) as b:
                    with pe.Fori(0, SETS) as st:
                        it = b * SETS + st
                        for what, u in plan:
                            j, qt = u // TPB, u % TPB
                            if what == "S":
                                pe.wait_ge(e_full.sem, e_full.at(it, u - 2))
                                if qt == 0:
                                    pe.wait_ge(rows_ready[j].sem, rows_ready[j].at(it, 5))
                                nk = blocks(u) * P
                                for c in range(0, nk, 512):
                                    n = min(512, nk - c)
                                    mm = pe.matmul(k.ps_scores[u % 2][:, c:c + n], qs[:, j, qt * P:(qt + 1) * P],
                                                   ks[:, j, c:c + n], start=True, stop=True)
                                mm.then_inc(s_full[u % 2].sem, 1)
                            elif what == "T":
                                pe.wait_ge(p_full.sem, p_full.at(it, u))
                                turn(pe, k, probs[:, u % RING, :], t_full, t_done, it, u, blocks(u), event)
                            else:
                                for half in range(1 + second[u]):
                                    pe.wait_ge(t_done[half].sem, t_done[half].at(it, event(half, u)))
                                if u == 0:
                                    pe.wait_ge(v_ready.sem, v_ready.at(it, 0))
                                if u in (0, 4):
                                    pe.wait_ge(o_free[u // 4].sem, o_free[u // 4].at(it, -1))
                                bank, c0 = k.ps_out[qt // 4], (qt % 4) * P
                                for t in range(blocks(u)):
                                    g = t % 4
                                    mm = pe.matmul(bank[32 * g:32 * g + 32, c0:c0 + P], vz[:, j, t, :],
                                                   probsT[:, u % 2, t * P:(t + 1) * P],
                                                   start=j == 0 and qt % 4 == 0 and t < 4,
                                                   stop=j == SET - 1 and qt % 4 == 3 and t >= blocks(u) - 4,
                                                   skip_group_check=True)
                                if u == U - 1:
                                    mm.then_inc(o_full.sem, 1)

            @block.vector
            def _(dve):
                for s in (masked, max_ready, inv_ready, t_done[1], o_free[1]):
                    s.start(dve)
                with dve.Fori(0, B) as b:
                    with dve.Fori(0, SETS) as st:
                        it = b * SETS + st

                        def inverse(u):
                            j = u // TPB
                            dve.wait_ge(e_full.sem, e_full.at(it, u))
                            if u == 0:
                                dve.wait_ge(v_ready.sem, v_ready.at(it, 0))
                            nc.vector.tensor_tensor(den[:, 0, u:u + 1], rsum[:, u:u + 1], ex[:, j:j + 1], ALU.add
                                                    ).then_inc(inv_ready.sem, 1)
                            dve.wait_ge(inv_ready.sem, inv_ready.at(it, 2 * u))
                            nc.vector.reciprocal(den[:, 1, u:u + 1], den[:, 0, u:u + 1]
                                                 ).then_inc(inv_ready.sem, 1)

                        for what, u in plan:
                            j, qt = u // TPB, u % TPB
                            slot = k.ps_scores[u % 2]
                            if what == "S":
                                dve.wait_ge(s_full[u % 2].sem, s_full[u % 2].at(it, u // 2))
                                if causal:
                                    if qt < 4:
                                        part, m = slot[:, 0:512], tri[:, (3 - qt) * P:(3 - qt) * P + 512]
                                    else:
                                        part, m = slot[:, qt * P:(qt + 1) * P], tri[:, 3 * P:4 * P]
                                    nc.vector.tensor_tensor(part, part, m, ALU.add).then_inc(masked.sem, 1)
                                    dve.wait_ge(masked.sem, masked.at(it, u))
                                nc.vector.tensor_reduce(nmax[:, u:u + 1], slot[:, 0:blocks(u) * P], AX.X, ALU.max,
                                                        negate=True).then_inc(max_ready.sem, 1)
                                if u >= 1:
                                    inverse(u - 1)
                                if u == U - 1:
                                    inverse(u)
                            elif what == "T" and second[u]:
                                take_turned(nc.vector, k, probsT[:, u % 2, :], t_full, t_done, it, u, 1, blocks(u),
                                            event)
                        dve.wait_ge(o_full.sem, o_full.at(it, 0))
                        nc.vector.tensor_scalar(oT[:, ds(it * L + 512, 512)], k.ps_out[1][:, :], 1.0, None, ALU.mult
                                                ).then_inc(o_free[1].sem, 1)

            @block.scalar
            def _(act):
                for s in (e_full, t_done[0], o_free[0]):
                    s.start(act)
                with act.Fori(0, B) as b:
                    with act.Fori(0, SETS) as st:
                        it = b * SETS + st
                        for what, u in plan:
                            if what == "S":
                                act.wait_ge(max_ready.sem, max_ready.at(it, u))
                                half = int(second[(u - RING) % U])
                                act.wait_ge(t_full[half].sem, t_full[half].at(it, event(half, u - RING)))
                                nk = blocks(u) * P
                                nc.scalar.activation(probs[:, u % RING, 0:nk], k.ps_scores[u % 2][:, 0:nk], ACT.Exp,
                                                     bias=nmax[:, u:u + 1], accum_out=rsum[:, u:u + 1]
                                                     ).then_inc(e_full.sem, 1)
                            elif what == "T":
                                take_turned(nc.scalar, k, probsT[:, u % 2, :], t_full, t_done, it, u, 0, blocks(u),
                                            event)
                        act.wait_ge(o_full.sem, o_full.at(it, 0))
                        nc.scalar.copy(oT[:, ds(it * L, 512)], k.ps_out[0][:, :]).then_inc(o_free[0].sem, 1)

        def tile_of(c, t):
            c0 = ((t // TPB) * SETS + c) * L + (t % TPB) * P
            return oT[:, c0:c0 + P]

        project_turned(k, name + "o", range(NG), SETS, tile_of, wo[:, :, :], d[wo_dram], bo[:, :], d[bo_dram])


def l2_attention(k):
    small_head_attention(k, "l2", "L2_qkv", True, "L2_denom_bias", "L2_wo", "L2_attn_bo")


def l3_attention(k):
    small_head_attention(k, "l3", "L3_qkv", False, None, "L3_wo", "L3_attn_bo")



EXPERTS = 8


def softmax_rows(dve, own, probs, scores, tmp, passes, acts, n):
    v = dve
    T, E = probs.shape[1], probs.shape[2]
    own.step(v.tensor_reduce(tmp, scores, AX.X, ALU.max))
    v.tensor_tensor(probs, scores, tmp.unsqueeze(2).broadcast_to([P, T, E]), ALU.subtract).then_inc(passes, 1)
    own.eng.wait_ge(acts, n)
    own.step(v.tensor_reduce(tmp, probs, AX.X, ALU.add))
    own.step(v.reciprocal(tmp, tmp))
    own.step(v.tensor_tensor(probs, probs, tmp.unsqueeze(2).broadcast_to([P, T, E]), ALU.mult))


def top_two(dve, own, gates, probs, rank, tmp, hit, scale):
    v = dve
    T, E = probs.shape[1], probs.shape[2]
    wide = tmp.unsqueeze(2).broadcast_to([P, T, E])
    for n in range(2):
        own.step(v.tensor_reduce(tmp, probs, AX.X, ALU.max))
        own.step(v.tensor_tensor(hit, probs, wide, ALU.is_equal))
        own.step(v.tensor_tensor(hit, hit, rank, ALU.mult))
        own.step(v.tensor_reduce(tmp, hit, AX.X, ALU.max))
        own.step(v.tensor_tensor(hit, rank, wide, ALU.is_equal))
        if n == 0:
            own.step(v.scalar_tensor_tensor(gates, probs, scale, hit, ALU.mult, ALU.mult))
            own.step(v.scalar_tensor_tensor(probs, hit, -4.0, probs, ALU.mult, ALU.add))
        else:
            own.step(v.scalar_tensor_tensor(probs, probs, scale, hit, ALU.mult, ALU.mult))
            own.step(v.tensor_tensor(gates, gates, probs, ALU.add))


def route(k, name, w_dram, b_dram, rank, gates, scale, groups):
    nc, d = k.nc, k.dram
    n_in = EXPERTS + groups
    with ExitStack() as ctx:
        sb = lambda n, s: k.sb(name + n, s, ctx=ctx)
        loaded, logits, own_s, passes, acts = (k.sem(name + n, ctx) for n in (
            "_loaded", "_logits", "_own", "_passes", "_acts"))
        w, bias = sb("_w", [P, n_in]), sb("_b", [1, n_in])
        lg = sb("_lg", [P, TILES, n_in])
        probs = sb("_probs", [P, TILES, EXPERTS])
        hit = sb("_hit", [P, TILES, EXPERTS])
        tmp = sb("_tmp", [P, TILES])
        gp = sb("_gp", [P, TILES, 2])
        sel = sb("_sel", [P, TILES, 2])
        best = sb("_best", [P, TILES])
        block = ctx.enter_context(nc.Block())
        bank = k.ps_out[0][:, 0:TILES * n_in].rearrange("p (t e) -> p t e", e=n_in)

        @block.sync
        def _(sp):
            sp.dma_start(w[:, :], d[w_dram]).then_inc(loaded, 16)
            sp.dma_start(rank[:, :, :], d["rank"]).then_inc(loaded, 16)
            if b_dram:
                sp.dma_start(bias[:, :], d[b_dram]).then_inc(loaded, 16)

        @block.tensor
        def _(pe):
            pe.wait_ge(loaded, 48 if b_dram else 32)
            for t in range(TILES):
                c0 = xcol(t // GROUP) + (t % GROUP) * P
                mm = pe.matmul(bank[:, t, :], k.xT[:, c0:c0 + P], w[:, :], start=True, stop=not b_dram)
                if b_dram:
                    mm = pe.matmul(bank[:, t, :], k.ones[0:1, 0:P], bias[:, :], start=False, stop=True)
            mm.then_inc(logits, 1)

        @block.scalar
        def _(act):
            if groups:
                act.wait_ge(passes, 1)
                nc.scalar.activation(gp[:, :, :], gp[:, :, :], ACT.Exp).then_inc(acts, 1)
            n = 2 if groups else 1
            act.wait_ge(passes, n)
            nc.scalar.activation(probs[:, :, :], probs[:, :, :], ACT.Exp).then_inc(acts, 1)
            act.wait_ge(acts, n)

        @block.vector
        def _(dve):
            own = Count(dve, own_s)
            v = nc.vector
            dve.wait_ge(logits, 1)
            dve.wait_ge(loaded, 48 if b_dram else 32)
            own.step(v.tensor_copy(lg[:, :, :], bank))
            if groups:
                softmax_rows(v, own, gp[:, :, :], lg[:, :, 0:groups], tmp[:, :], passes, acts, 1)
                own.done(v.tensor_tensor(best[:, :], gp[:, :, 0], gp[:, :, 1], ALU.max))
                own.done(v.tensor_tensor(sel[:, :, 0], gp[:, :, 0], gp[:, :, 1], ALU.is_ge))
                own.step(v.tensor_tensor(sel[:, :, 1], gp[:, :, 1], gp[:, :, 0], ALU.is_gt))
                own.step(v.tensor_scalar(sel[:, :, :], sel[:, :, :], HUGE, -HUGE, ALU.mult, ALU.add))
                per = EXPERTS // groups
                for g in range(groups):
                    e = lg[:, :, groups + g * per:groups + (g + 1) * per]
                    own.done(v.tensor_tensor(e, e, sel[:, :, g].unsqueeze(2).broadcast_to([P, TILES, per]), ALU.add))
                own.wait()
            softmax_rows(v, own, probs[:, :, :], lg[:, :, groups:n_in], tmp[:, :], passes, acts, 2 if groups else 1)
            if groups:
                own.step(v.tensor_tensor(probs[:, :, :], probs[:, :, :],
                                         best[:, :].unsqueeze(2).broadcast_to([P, TILES, EXPERTS]), ALU.mult))
            top_two(v, own, gates[:, :, :], probs[:, :, :], rank[:, :, :], tmp[:, :], hit[:, :, :], scale)



F2_HID = 256


def l2_ffn(k):
    nc, d = k.nc, k.dram
    CH, HALVES = F2_HID // P, NG // B
    NP = 2 * CH
    with ExitStack() as ctx:
        sb = lambda n, s: k.sb("f2" + n, s, ctx=ctx)
        rank = sb("_rank", [P, TILES, EXPERTS])
        gates = sb("_gates", [P, TILES, EXPERTS])
        w_up = sb("_w_up", [P, NP, 2, P])
        w_out = sb("_w_out", [P, CH, C])
        w2 = sb("_w2", [P, CH, EXPERTS * C])
        silu = sb("_silu", [P, 2, 512])
        hid = sb("_hid", [P, 2, NP, 512])
        prod = sb("_prod", [P, 2, EXPERTS, C])
        part = sb("_part", [P, 2, C])
        route(k, "f2r", "L2_router_w", "L2_router_b", rank, gates, 1.0, 2)
        sem = lambda n: k.sem("f2" + n, ctx)
        w_loaded = sem("_w_loaded")
        per = HALVES * NP // 2
        u_full = [Signal(sem(f"_u_full{i}"), per) for i in range(2)]
        silu_ready = Signal(sem("_silu_ready"), HALVES * NP)
        hid_ready = [Signal(sem(f"_hid_ready{i}"), per) for i in range(2)]
        r_full = [Signal(sem(f"_r_full{i}"), HALVES * GROUP // 2) for i in range(2)]
        r_free = [Signal(sem(f"_r_free{i}"), HALVES * GROUP // 2) for i in range(2)]
        own = Signal(sem("_own_dve"), HALVES * (Norm.DVE_STEPS + 2 * GROUP))
        norm = Norm(k, ctx, "f2n", HALVES)
        block = ctx.enter_context(nc.Block())

        @block.sync
        def _(sp):
            sp.dma_start(w_up[:, :, :, :], d["L2_w_up"]).then_inc(w_loaded, 16)
            sp.dma_start(w_out[:, :, :], d["L2_w_out"]).then_inc(w_loaded, 16)
            sp.dma_start(w2[:, :, :], d["L2_w2"]).then_inc(w_loaded, 16)

        @block.tensor
        def _(pe):
            norm.start(pe, None, None)
            for s in (*u_full, *r_full):
                s.start(pe)
            pe.wait_ge(w_loaded, 48)
            with pe.Fori(0, B) as b:
                for g in range(HALVES):
                    for c in range(NP):
                        n = g * NP + c
                        pe.wait_ge(hid_ready[n % 2].sem, hid_ready[n % 2].at(b, n // 2 - 1))
                        pe.wait_ge(r_free[n % 2].sem, r_free[n % 2].at(b, -1))
                        for i in range(2):
                            mm = pe.matmul(k.ps_scores[n % 2][:, i * 512:(i + 1) * 512], w_up[:, c, i, :],
                                           k.xT[:, ds(b * XB + PAD + g * 512, 512)], start=True, stop=True)
                        mm.then_inc(u_full[n % 2].sem, 1)
                for g in range(HALVES):
                    y = k.ps_out[g]
                    pe.wait_ge(norm.y_free.sem, norm.y_free.at(b, g - 2))
                    for c in range(CH):
                        n = g * NP + c
                        pe.wait_ge(hid_ready[n % 2].sem, hid_ready[n % 2].at(b, n // 2))
                        for i in range(GROUP):
                            mm = pe.matmul(y[:, i * C:(i + 1) * C], hid[:, g, c, i * P:(i + 1) * P], w_out[:, c, :],
                                           start=(c == 0 and i == 0), stop=c == CH - 1 and i == GROUP - 1,
                                           skip_group_check=True)
                    mm.then_inc(norm.y_full.sem, 1)
                for s in range(2):
                    pe.wait_ge(hid_ready[s].sem, hid_ready[s].at(b, per - 1))
                for g in range(HALVES):
                    for i in range(GROUP):
                        n = g * GROUP + i
                        slot = k.ps_scores[n % 2]
                        pe.wait_ge(r_free[n % 2].sem, r_free[n % 2].at(b, n // 2 - 1))
                        for h in range(2):
                            for c in range(CH):
                                mm = pe.matmul(slot[:, h * 512:(h + 1) * 512], hid[:, g, CH + c, i * P:(i + 1) * P],
                                               w2[:, c, h * 512:(h + 1) * 512], start=c == 0, stop=c == CH - 1)
                        mm.then_inc(r_full[n % 2].sem, 1)
                for g in range(HALVES):
                    norm.tensor(pe, b, g, g, k.ps_turned[0])

        @block.scalar
        def _(act):
            norm.start(None, None, act)
            silu_ready.start(act)
            with act.Fori(0, B) as b:
                for g in range(HALVES):
                    for c in range(NP):
                        n = g * NP + c
                        act.wait_ge(u_full[n % 2].sem, u_full[n % 2].at(b, n // 2))
                        act.wait_ge(hid_ready[n % 2].sem, hid_ready[n % 2].at(b, n // 2 - 1))
                        nc.scalar.activation(silu[:, n % 2, :], k.ps_scores[n % 2][:, 0:512], ACT.Silu
                                             ).then_inc(silu_ready.sem, 1)
                for g in range(HALVES):
                    norm.scalar_root(act, b, g, g)
                for g in range(HALVES):
                    norm.scalar_store(act, b, g, k.ps_turned[0], b * XB + PAD + g * 512)

        @block.vector
        def _(dve):
            norm.start(None, dve, None)
            for s in (*hid_ready, *r_free, own):
                s.start(dve)
            with dve.Fori(0, B) as b:
                chain = Chain(dve, own, b)
                for g in range(HALVES):
                    for c in range(NP):
                        n = g * NP + c
                        dve.wait_ge(silu_ready.sem, silu_ready.at(b, n))
                        nc.vector.tensor_tensor(hid[:, g, c, :], k.ps_scores[n % 2][:, 512:1024], silu[:, n % 2, :],
                                                ALU.mult).then_inc(hid_ready[n % 2].sem, 1)
                for g in range(HALVES):
                    tile0 = b * TPB + g * GROUP

                    def routed(res):
                        for i in range(GROUP):
                            n = g * GROUP + i
                            s = n % 2
                            dve.wait_ge(r_full[s].sem, r_full[s].at(b, n // 2))
                            gate = gates[:, ds(tile0 + i, 1), :].rearrange("p o e -> p (o e)")
                            nc.vector.tensor_tensor(
                                prod[:, s, :, :], k.ps_scores[s][:, :].rearrange("p (e c) -> p e c", c=C),
                                gate.unsqueeze(2).broadcast_to([P, EXPERTS, C]), ALU.mult).then_inc(r_free[s].sem, 1)
                            dve.wait_ge(r_free[s].sem, r_free[s].at(b, n // 2))
                            chain.step(nc.vector.tensor_reduce(
                                part[:, s, :], prod[:, s, :, :].rearrange("p e c -> p c e"), AX.X, ALU.add))
                            r = res[:, i * C:(i + 1) * C]
                            chain.step(nc.vector.tensor_tensor(r, r, part[:, s, :], ALU.add))

                    norm.vector(dve, chain, b, g, g, tile0, k.ps_out[g][:, :], more=routed)
                chain.close()



F3_HID = 512
F3_SCALE = float(1.0 / np.sqrt(1.25))


def l3_ffn(k):
    nc, d = k.nc, k.dram
    CH, HALVES, E = F3_HID // P, NG // B, EXPERTS + 1
    with ExitStack() as ctx:
        sb = lambda n, s: k.sb("f3" + n, s, ctx=ctx)
        rank = sb("_rank", [P, TILES, EXPERTS])
        gates = sb("_gates", [P, TILES, EXPERTS])
        w1 = sb("_w1", [P, E, F3_HID])
        w2 = sb("_w2", [P, E, CH, C])
        b1 = sb("_b1", [P, E * CH])
        b2 = sb("_b2", [1, E * C])
        hid = sb("_hid", [P, 2, CH, 512])
        scaled = sb("_scaled", [P, 2, 512])
        route(k, "f3r", "L3_router_w", None, rank, gates, F3_SCALE, 0)
        sem = lambda n: k.sem("f3" + n, ctx)
        w_loaded = sem("_w_loaded")
        per = HALVES * E * CH // 4
        h_full = [Signal(sem(f"_h_full{i}"), per) for i in range(4)]
        h_ready = [Signal(sem(f"_h_ready{i}"), per) for i in range(4)]
        e_full = [Signal(sem(f"_e_full{i}"), HALVES * E // 2) for i in range(2)]
        e_free = [Signal(sem(f"_e_free{i}"), HALVES * E // 2) for i in range(2)]
        own = Signal(sem("_own_dve"), HALVES * (Norm.DVE_STEPS + EXPERTS))
        norm = Norm(k, ctx, "f3n", HALVES)
        block = ctx.enter_context(nc.Block())

        def bank(n):
            return k.ps_scores[(n % 4) // 2][:, (n % 2) * 512:(n % 2 + 1) * 512]

        @block.sync
        def _(sp):
            sp.dma_start(w1[:, :, :], d["L3_w1"]).then_inc(w_loaded, 16)
            sp.dma_start(w2[:, :, :, :], d["L3_w2"]).then_inc(w_loaded, 16)
            sp.dma_start(b1[:, :], d["L3_b1"]).then_inc(w_loaded, 16)
            sp.dma_start(b2[:, :], d["L3_b2"]).then_inc(w_loaded, 16)

        @block.tensor
        def _(pe):
            norm.start(pe, None, None)
            for s in (*h_full, *e_full):
                s.start(pe)
            pe.wait_ge(w_loaded, 64)

            def up(b, m):
                g, e = m // E, m % E
                for c in range(CH):
                    n = m * CH + c
                    pe.wait_ge(h_ready[n % 4].sem, h_ready[n % 4].at(b, n // 4 - 1))
                    if c == 0:
                        pe.wait_ge(e_full[m % 2].sem, e_full[m % 2].at(b, m // 2 - 1))
                    pe.matmul(bank(n), w1[:, e, c * P:(c + 1) * P], k.xT[:, ds(b * XB + PAD + g * 512, 512)],
                              start=True, stop=True).then_inc(h_full[n % 4].sem, 1)

            def down(b, m):
                g, e = m // E, m % E
                y = k.ps_out[m % 2]
                pe.wait_ge(e_free[m % 2].sem, e_free[m % 2].at(b, m // 2 - 1))
                for c in range(CH):
                    n = m * CH + c
                    pe.wait_ge(h_ready[n % 4].sem, h_ready[n % 4].at(b, n // 4))
                    for i in range(GROUP):
                        pe.matmul(y[:, i * C:(i + 1) * C], hid[:, m % 2, c, i * P:(i + 1) * P], w2[:, e, c, :],
                                  start=(c == 0 and i == 0), stop=False, skip_group_check=True)
                for i in range(GROUP):
                    mm = pe.matmul(y[:, i * C:(i + 1) * C], k.ones[0:1, 0:P], b2[:, e * C:(e + 1) * C], start=False,
                                   stop=i == GROUP - 1, skip_group_check=True)
                mm.then_inc(e_full[m % 2].sem, 1)

            with pe.Fori(0, B) as b:
                for m in range(HALVES * E):
                    up(b, m)
                    if m >= 1:
                        down(b, m - 1)
                down(b, HALVES * E - 1)
                for g in range(HALVES):
                    norm.tensor(pe, b, g, g, k.ps_turned[0])

        @block.scalar
        def _(act):
            norm.start(None, None, act)
            for s in h_ready:
                s.start(act)
            with act.Fori(0, B) as b:
                for n in range(HALVES * E * CH):
                    m, c = n // CH, n % CH
                    act.wait_ge(h_full[n % 4].sem, h_full[n % 4].at(b, n // 4))
                    if c == 0:
                        act.wait_ge(e_full[m % 2].sem, e_full[m % 2].at(b, m // 2 - 1))
                    at = (m % E) * CH + c
                    nc.scalar.activation(hid[:, m % 2, c, :], bank(n), ACT.Gelu_apprx_tanh, bias=b1[:, at:at + 1]
                                         ).then_inc(h_ready[n % 4].sem, 1)
                    if n == (E + 1) * CH - 1:
                        norm.scalar_root(act, b, 0, 0)
                norm.scalar_root(act, b, 1, 1)
                for g in range(HALVES):
                    norm.scalar_store(act, b, g, k.ps_turned[0], b * XB + PAD + g * 512)

        @block.vector
        def _(dve):
            norm.start(None, dve, None)
            for s in (*e_free, own):
                s.start(dve)
            with dve.Fori(0, B) as b:
                chain = Chain(dve, own, b)
                for g in range(HALVES):
                    tile0 = b * TPB + g * GROUP

                    def experts(res):
                        for e in range(1, E):
                            m = g * E + e
                            s = m % 2
                            dve.wait_ge(e_full[s].sem, e_full[s].at(b, m // 2))
                            gate = gates[:, ds(tile0, GROUP), e - 1:e].broadcast_to([P, GROUP, C])
                            nc.vector.tensor_tensor(
                                scaled[:, s, :].rearrange("p (t c) -> p t c", c=C),
                                k.ps_out[s][:, :].rearrange("p (t c) -> p t c", c=C), gate, ALU.mult
                                ).then_inc(e_free[s].sem, 1)
                            dve.wait_ge(e_free[s].sem, e_free[s].at(b, m // 2))
                            chain.step(nc.vector.tensor_tensor(res, res, scaled[:, s, :], ALU.add))

                    m0 = g * E
                    norm.vector(dve, chain, b, g, g, tile0, k.ps_out[m0 % 2][:, :], scale=F3_SCALE, more=experts,
                                y_full=(e_full[m0 % 2], m0 // 2), y_free=(e_free[m0 % 2], m0 // 2))
                chain.close()



def layouts(inputs):
    a = {n: np.asarray(v) for n, v in inputs.items()}
    out = {n: a[n] for n in ("L0_attn_x", "L0_attn_Wq", "L0_attn_Wk", "L0_attn_Wv", "L0_attn_Wo")}
    out["L0_bqk"] = np.stack([a["L0_attn_bq"], a["L0_attn_bk"]], 1)
    for n in ("L0_attn_bv", "L0_attn_bo"):
        out[n] = a[n][None, :]
    f32 = np.float32
    p = np.arange(P)
    out["head_mask8"] = ((p[:, None] // 8 == np.arange(16)[None, :]) / np.sqrt(8.0)).astype(f32)
    w = np.zeros((P, TPB, L0_GROUPS), f32)
    for j in range(TPB):
        for half in range(2):
            rows = slice(64 * half, 64 * half + 64)
            w[rows, j, half] = 1.0
            for off in (-2, -1, 1, 2):
                if 0 <= 2 * j + half + off < L // SEG:
                    w[rows, j, 2 + half + off + 3] = 0.25
    out["L0_group_weights"] = w
    out["L0_ffn_W_exp"] = a["L0_ffn_W_exp"]
    out["L0_W_con_T"] = a["L0_ffn_W_con"].T
    out["L0_ffn_b_exp"] = a["L0_ffn_b_exp"][None, :]
    out["L0_up_bias"] = a["L0_ffn_up_bias"].reshape(4, P).T
    out["L0_y_bias"] = np.stack([a["L0_ffn_b_con"], a["L0_ffn_down_bias"]])
    out["L0_up_weights"] = a["L0_ffn_up_weights"].reshape(-1)
    out["L0_down_weights"] = a["L0_ffn_down_weights"].reshape(-1)
    w = a["L1_attn_qkv_w"].reshape(3, PAIRS, 2, L1_D, C)
    swap = np.roll(w, L1_D // 2, axis=3)
    w = np.stack([w[0], swap[0], w[1], swap[1], w[2]], 1)
    out["L1_qkv"] = w.transpose(0, 4, 1, 2, 3).reshape(PAIRS, C, 5 * P)
    out["L1_out_w"] = a["L1_attn_out_w"].T.reshape(8, P, C).transpose(1, 0, 2).reshape(P, 8 * C)
    sign = np.where(p % L1_D < L1_D // 2, -1.0, 1.0).astype(f32)
    out["L1_freq"] = np.stack([np.tile(a["L1_attn_rope_freqs"], 4), sign, np.full(P, np.pi / 2, f32)], 1)
    out["L1_bias_ap"] = np.concatenate([a["L1_attn_bias_a"].reshape(-1), a["L1_attn_bias_p"].reshape(-1)])
    half = np.arange(0, F1_D, 2, dtype=f32)
    t = np.arange(L, dtype=f32)
    fr = t[:, None] * (f32(1.0) / f32(10000.0) ** (half / f32(F1_D)))[None, :]
    base = (half + f32(0.4 * F1_D)) / f32(1.4 * F1_D)
    scale = base[None, :] ** ((t - L // 2) / f32(WINDOW // 2))[:, None]
    cos, sin = np.cos(fr.astype(np.float64)).astype(f32), np.sin(fr.astype(np.float64)).astype(f32)
    two = lambda x, y: np.concatenate([x, y], 1)
    cq, sq = two(cos * scale, cos * scale) * f32(8), two(-sin * scale, sin * scale) * f32(8)
    ck, sk = two(cos / scale, cos / scale), two(-sin / scale, sin / scale)
    xpos = np.stack([np.stack([cq, ck]), np.stack([sq, sk])]).astype(f32)
    out["F1_xpos"] = xpos.reshape(2, 2, TPB, P, F1_D).transpose(3, 0, 2, 1, 4)
    for layer in range(F1_DEPTH):
        both = np.stack([a["L1_ffn_q_scale"][layer], a["L1_ffn_k_scale"][layer]])
        out[f"F1_scales{layer}"] = np.stack([both, np.roll(both, F1_D // 2, axis=1)])
    for n in ("L1_ffn_wqkv", "L1_ffn_w1", "L1_ffn_b2"):
        out[n] = a[n]
    out["F1_wo"] = a["L1_ffn_wo"].reshape(F1_DEPTH, 4, P, C).transpose(0, 2, 1, 3).reshape(F1_DEPTH, P, 4 * C)
    cols = np.zeros((F1_DEPTH, P, 8), f32)
    w2 = np.zeros((F1_DEPTH, P, 3, C), f32)
    cols[:, :, 0], cols[:, :, 1] = a["L1_ffn_ln_g"], a["L1_ffn_ln_b"]
    for c, r in enumerate(F1_ROWS):
        cols[:, 0:r, 2 + c] = a["L1_ffn_b1"][:, c * P:c * P + r]
        cols[:, 0:r, 5 + c] = a["L1_ffn_b1"][:, F1_HID + c * P:F1_HID + c * P + r]
        w2[:, 0:r, c, :] = a["L1_ffn_w2"][:, c * P:c * P + r, :]
    out["F1_cols"], out["F1_w2"] = cols, w2
    for n in ("L2", "L3"):
        out[n + "_qkv"] = np.concatenate([a[f"{n}_attn_W{m}"].T for m in "qkv"], 1)
        wo = a[n + "_attn_Wo"].T.reshape(4, 32, C)
        out[n + "_wo"] = np.tile(wo, (1, 4, 1)).transpose(1, 0, 2)
        out[n + "_attn_bo"] = a[n + "_attn_bo"][None, :]
    out["L2_denom_bias"] = a["L2_attn_denom_bias"].reshape(-1)
    out["rank"] = np.broadcast_to(np.arange(EXPERTS, 0, -1, dtype=f32), (P, TILES, EXPERTS))
    out["L2_router_w"] = np.concatenate([a["L2_ffn_wg"], a["L2_ffn_we"]], 0).T
    out["L2_router_b"] = np.concatenate([a["L2_ffn_gb"], a["L2_ffn_eb"]])[None, :]
    pairs = lambda w: w.reshape(2, F2_HID // P, P, C).transpose(3, 1, 0, 2)
    out["L2_w_up"] = np.concatenate([pairs(a["L2_ffn_w_in"]), pairs(a["L2_ffn_w1"])], 1)
    out["L2_w_out"] = a["L2_ffn_w_out"].T.reshape(F2_HID // P, P, C).transpose(1, 0, 2)
    out["L2_w2"] = a["L2_ffn_w2"].reshape(EXPERTS, C, F2_HID // P, P).transpose(3, 2, 0, 1).reshape(
        P, F2_HID // P, EXPERTS * C)
    out["L3_router_w"] = a["L3_ffn_w_router"].T
    all_of = lambda s, e: np.concatenate([a["L3_ffn_" + s][None], a["L3_ffn_" + e]], 0)
    out["L3_w1"] = all_of("Ws1", "W1").transpose(2, 0, 1)
    out["L3_w2"] = all_of("Ws2", "W2").reshape(9, C, 4, P).transpose(3, 0, 2, 1)
    out["L3_b1"] = all_of("bs1", "b1").reshape(9 * 4, P).T
    out["L3_b2"] = all_of("bs2", "b2").reshape(1, -1)
    return {n: np.ascontiguousarray(v) for n, v in out.items()}


STAGES = [l0_attention, l0_ffn, l1_attention, l1_ffn, l2_attention, l2_ffn, l3_attention, l3_ffn]


def build(nc, dram, out, stages=99):
    with ExitStack() as ctx:
        k = Kernel(nc, ctx, dram)
        load_x(k)
        for stage in STAGES[:stages]:
            stage(k)
        with ExitStack() as c2:
            stored = k.sem("stored", c2)
            block = c2.enter_context(nc.Block())

            @block.sync
            def _(sp):
                sp.dma_start(out.rearrange("b (t p) c -> p (b t) c", p=P),
                             k.x_tok[:, :].rearrange("p (t c) -> p t c", c=C)).then_inc(stored, 16)
                sp.wait_ge(stored, 16)


def kernel(**inputs):
    import concourse.bacc as bacc
    from concourse.bass_utils import run_bass_kernel_spmd

    nc = bacc.Bacc("TRN2", target_bir_lowering=False, num_devices=1)
    arrays = layouts(inputs)
    dram = {n: nc.dram_tensor("in_" + n, v.shape, mybir.dt.from_np(v.dtype), kind="ExternalInput").ap()
            for n, v in arrays.items()}
    out = nc.dram_tensor("out_x", (B, L, C), F32, kind="ExternalOutput").ap()
    build(nc, dram, out)
    r = run_bass_kernel_spmd(nc, [{"in_" + n: v for n, v in arrays.items()}], core_ids=[0])
    return r.results[0]["out_x"]
```

```python
from contextlib import ExitStack

import numpy as np

import concourse.bass as bass
from concourse import mybir

F32 = mybir.dt.float32
BF16 = mybir.dt.bfloat16
ALU = mybir.AluOpType
ACT = mybir.ActivationFunctionType
AX = mybir.AxisListType
ds = bass.ds

P = 128
B, L, C = 2, 1024, 128
TPB = L // P
TILES = B * TPB
GROUP = 4
NG = TILES // GROUP
PAD = 192
XB = L + 2 * PAD
EPS = 1e-5
HUGE = 3.0e38


class Signal:

    def __init__(self, sem, per, step=1):
        self.sem, self.per, self.step = sem, per, step

    def start(self, eng):
        if self.per:
            eng.sem_inc(self.sem, self.per * self.step)

    def at(self, it, k):
        assert k < self.per and k >= -self.per, (k, self.per)
        return (it * self.per + (self.per + k + 1)) * self.step if self.step != 1 else it * self.per + (self.per + k + 1)


class Chain:

    def __init__(self, eng, events, it=0):
        self.eng, self.events, self.it, self.n = eng, events, it, 0

    def done(self, ins):
        ins.then_inc(self.events.sem, 1)
        self.n += 1
        return ins

    def wait(self):
        self.eng.wait_ge(self.events.sem, self.events.at(self.it, self.n - 1))

    def step(self, ins):
        self.done(ins)
        self.wait()

    def wait_apart(self, passed):
        self.wait()
        self.eng.sem_inc(passed, 1)

    def close(self):
        assert self.n == self.events.per, f"{self.events.sem}: {self.n} events, {self.events.per} declared"


class Count:

    def wait_apart(self, passed):
        self.wait()

    def __init__(self, eng, sem):
        self.eng, self.sem, self.n = eng, sem, 0

    def done(self, ins):
        ins.then_inc(self.sem, 1)
        self.n += 1
        return ins

    def wait(self):
        self.eng.wait_ge(self.sem, self.n)

    def step(self, ins):
        self.done(ins)
        self.wait()


def order(slots, lead, units, lag=2):
    out = []
    for n in range(slots + lag + 1):
        if n < slots:
            out.append(("S", n))
        if 0 <= n - lead - lag < units:
            out.append(("T", n - lead - lag))
        if 0 <= n - lead - lag - 1 < units:
            out.append(("V", n - lead - lag - 1))
    return out


def order_pairs(slots, lead, units, lag):
    out = []
    for n in range(slots + lag + 1):
        u = n - lead - lag
        if n < slots:
            out.append(("S", n))
        if 0 < u <= units and u % 2 == 0:
            out.append(("V", u // 2 - 1))
        if 0 <= u < units:
            out.append(("T", u))
    return out


class Kernel:

    def __init__(self, nc, ctx, dram):
        self.nc, self.ctx, self.dram = nc, ctx, dram
        self.numbers = {}
        self.ident = self.sb("ident", [P, P])
        self.ones = self.sb("ones", [P, 512])
        self.x_tok = self.sb("x_tok", [P, TILES * C])
        self.xT = self.sb("xT", [P, B * XB])
        self.xn = self.sb("x_new", [P, 2, 512])
        self.res = self.sb("residual", [P, 2, 512])
        self.stats = self.sb("ln_stats", [P, 2, GROUP, 6])
        self.mv = self.sb("ln_mean_var", [P, 2, GROUP, 2])
        self.rstd = self.sb("ln_rstd", [P, 2, 3, GROUP])
        self.ps = [ctx.enter_context(nc.psum_tensor(f"bank{i}", [P, 1024 if i < 2 else 512], F32))
                   for i in range(6)]
        self.ps_scores = [self.ps[0], self.ps[1]]
        self.ps_turned = [self.ps[2], self.ps[3]]
        self.ps_out = [self.ps[4], self.ps[5]]

    def sb(self, name, shape, dt=F32, ctx=None):
        return (ctx or self.ctx).enter_context(self.nc.sbuf_tensor(name, shape, dt))

    def sem(self, name, ctx):
        if ctx not in self.numbers:
            self.numbers[ctx] = []
            ctx.callback(self.clear, ctx)
        s = ctx.enter_context(self.nc.semaphore(name))
        self.numbers[ctx].append(s.num)
        return s

    def clear(self, ctx):
        numbers = sorted(self.numbers.pop(ctx))
        while numbers:
            n = 1
            while n < len(numbers) and numbers[n] == numbers[0] + n:
                n += 1
            self.nc.gpsimd.sem_clear(range(numbers[0], numbers[0] + n))
            numbers = numbers[n:]


def xcol(g):
    return (g // 2) * XB + PAD + (g % 2) * 512



class Norm:

    DVE_STEPS = 13

    def __init__(self, k, ctx, name, per):
        self.k = k
        self.y_full = Signal(k.sem(name + "_y_full", ctx), per)
        self.y_free = Signal(k.sem(name + "_y_free", ctx), per)
        self.var_ready = Signal(k.sem(name + "_var_ready", ctx), per)
        self.root_ready = Signal(k.sem(name + "_root_ready", ctx), per)
        self.xn_ready = Signal(k.sem(name + "_xn_ready", ctx), per)
        self.turned = Signal(k.sem(name + "_turned", ctx), per)
        self.xT_ready = Signal(k.sem(name + "_xT_ready", ctx), per)
        self.passed = k.sem(name + "_passed", ctx)

    def start(self, pe, dve, act):
        if pe is not None:
            self.y_full.start(pe), self.turned.start(pe)
        if dve is not None:
            self.y_free.start(dve), self.var_ready.start(dve), self.xn_ready.start(dve)
        if act is not None:
            self.root_ready.start(act), self.xT_ready.start(act)

    def vector(self, dve, chain, it, e, slot, tile0, y, scale=None, normed=True, also=None, more=None,
               y_full=None, y_free=None):
        k, nc = self.k, self.k.nc
        x = k.x_tok[:, ds(tile0 * C, 512)]
        res = k.res[:, slot, :]
        full, e_full = y_full or (self.y_full, e)
        free, e_free = y_free or (self.y_free, e)
        dve.wait_ge(full.sem, full.at(it, e_full))
        if scale is None:
            nc.vector.tensor_tensor(res, x, y, ALU.add).then_inc(free.sem, 1)
        else:
            nc.vector.scalar_tensor_tensor(res, y, scale, x, ALU.mult, ALU.add).then_inc(free.sem, 1)
        dve.wait_ge(free.sem, free.at(it, e_free))
        if also is not None:
            chain.step(nc.vector.tensor_tensor(res, res, also, ALU.add))
        if more is not None:
            more(res)
        if not normed:
            chain.step(nc.vector.tensor_scalar(x, res, 1.0, None, ALU.mult))
            dve.wait_ge(self.turned.sem, self.turned.at(it, e - 2))
            nc.vector.tensor_scalar(k.xn[:, slot, :], res, 1.0, None, ALU.mult).then_inc(self.xn_ready.sem, 1)
            return
        for i in range(GROUP):
            chain.done(nc.vector.bn_stats(k.stats[:, slot, i, :], res[:, i * C:(i + 1) * C]))
        chain.wait_apart(self.passed)
        for i in range(GROUP):
            chain.done(nc.vector.bn_aggr(k.mv[:, slot, i, :], k.stats[:, slot, i, :]))
        chain.wait()
        nc.vector.tensor_scalar(k.rstd[:, slot, 0, :], k.mv[:, slot, :, 1], EPS, None, ALU.add
                                ).then_inc(self.var_ready.sem, 1)
        dve.wait_ge(self.root_ready.sem, self.root_ready.at(it, e))
        chain.step(nc.vector.reciprocal(k.rstd[:, slot, 2, :], k.rstd[:, slot, 1, :]))
        dve.wait_ge(self.turned.sem, self.turned.at(it, e - 2))
        for i in range(GROUP):
            chain.done(nc.vector.tensor_scalar(k.xn[:, slot, i * C:(i + 1) * C], res[:, i * C:(i + 1) * C],
                                               k.mv[:, slot, i, 0:1], k.rstd[:, slot, 2, i:i + 1],
                                               ALU.subtract, ALU.mult))
        chain.wait()
        nc.vector.tensor_scalar(x, k.xn[:, slot, :], 1.0, None, ALU.mult).then_inc(self.xn_ready.sem, 1)
        dve.wait_ge(self.xn_ready.sem, self.xn_ready.at(it, e))

    def scalar_root(self, act, it, e, slot):
        k = self.k
        act.wait_ge(self.var_ready.sem, self.var_ready.at(it, e))
        k.nc.scalar.activation(k.rstd[:, slot, 1, :], k.rstd[:, slot, 0, :], ACT.Sqrt
                               ).then_inc(self.root_ready.sem, 1)

    def tensor(self, pe, it, e, slot, bank):
        k = self.k
        pe.wait_ge(self.xn_ready.sem, self.xn_ready.at(it, e))
        pe.wait_ge(self.xT_ready.sem, self.xT_ready.at(it, e - 1))
        for i in range(GROUP):
            mm = pe.transpose(bank[:, i * P:(i + 1) * P], k.xn[:, slot, i * C:(i + 1) * C], k.ident[:, :])
        mm.then_inc(self.turned.sem, 1)

    def scalar_store(self, act, it, e, bank, col):
        k = self.k
        act.wait_ge(self.turned.sem, self.turned.at(it, e))
        k.nc.scalar.copy(k.xT[:, ds(col, 512)], bank[:, 0:512]).then_inc(self.xT_ready.sem, 1)


def load_x(k):
    nc = k.nc
    with ExitStack() as ctx:
        sem = lambda n: k.sem("in_" + n, ctx)
        loaded, made, zeroed = sem("x_loaded"), sem("ident_made"), sem("xT_zeroed")
        turned, taken = sem("x_turned"), sem("x_taken")
        block = ctx.enter_context(nc.Block())

        @block.sync
        def _(sp):
            sp.dma_start(k.x_tok[:, :].rearrange("p (t c) -> p t c", c=C),
                         k.dram["L0_attn_x"].rearrange("b (t p) c -> p (b t) c", p=P)).then_inc(loaded, 16)

        @block.gpsimd
        def _(pool):
            nc.gpsimd.memset(k.ident[:, :], 0.0).then_inc(made, 1)
            nc.gpsimd.memset(k.ones[:, :], 1.0).then_inc(made, 1)
            pool.wait_ge(made, 2)
            nc.gpsimd.affine_select(out=k.ident[:, :], in_=k.ident[:, :], compare_op=ALU.not_equal, fill=1.0,
                                    base=0, pattern=[[-1, P]], channel_multiplier=1).then_inc(made, 1)
            for b in range(B):
                nc.gpsimd.memset(k.xT[:, b * XB:b * XB + PAD], 0.0)
                nc.gpsimd.memset(k.xT[:, b * XB + PAD + L:(b + 1) * XB], 0.0).then_inc(zeroed, 1)
            pool.wait_ge(zeroed, 2)

        @block.tensor
        def _(pe):
            pe.wait_ge(made, 3)
            pe.wait_ge(loaded, 16)
            for g in range(NG):
                if g >= 2:
                    pe.wait_ge(taken, g - 1)
                for i in range(GROUP):
                    mm = pe.transpose(k.ps_turned[g % 2][:, i * P:(i + 1) * P],
                                      k.x_tok[:, (GROUP * g + i) * C:(GROUP * g + i + 1) * C], k.ident[:, :])
                mm.then_inc(turned, 1)

        @block.scalar
        def _(act):
            for g in range(NG):
                act.wait_ge(turned, g + 1)
                nc.scalar.copy(k.xT[:, xcol(g):xcol(g) + 512], k.ps_turned[g % 2][:, :]).then_inc(taken, 1)
            act.wait_ge(taken, NG)


def project_out(k, name, o_tok, chunks, wo, w_dram, bias, bias_dram, normed=True):
    nc = k.nc
    with ExitStack() as ctx:
        sem = lambda n: k.sem(name + n, ctx)
        oT = k.sb(name + "_oT", [P, 2, 512], ctx=ctx)
        w_loaded = sem("_w_loaded")
        o_turned = Signal(sem("_o_turned"), NG * chunks)
        o_taken = Signal(sem("_o_taken"), NG * chunks)
        own = sem("_own_dve")
        norm = Norm(k, ctx, name, NG)
        block = ctx.enter_context(nc.Block())

        @block.sync
        def _(sp):
            sp.dma_start(wo, w_dram).then_inc(w_loaded, 16)
            if bias is not None:
                sp.dma_start(bias, bias_dram).then_inc(w_loaded, 16)

        @block.tensor
        def _(pe):
            norm.start(pe, None, None)
            o_turned.start(pe)
            pe.wait_ge(w_loaded, 32 if bias is not None else 16)
            for g in range(NG + 1):
                if g < NG:
                    y = k.ps_out[g % 2]
                    for c in range(chunks):
                        n = g * chunks + c
                        bank = k.ps_turned[n % 2]
                        pe.wait_ge(o_taken.sem, o_taken.at(0, n - 2))
                        for i in range(GROUP):
                            mm = pe.transpose(bank[:, i * P:(i + 1) * P],
                                              o_tok[:, GROUP * g + i, c * P:(c + 1) * P], k.ident[:, :])
                        mm.then_inc(o_turned.sem, 1)
                        if c == 0:
                            pe.wait_ge(norm.y_free.sem, norm.y_free.at(0, g - 2))
                        pe.wait_ge(o_taken.sem, o_taken.at(0, n))
                        for i in range(GROUP):
                            last = c == chunks - 1 and bias is None
                            mm = pe.matmul(y[:, i * C:(i + 1) * C], oT[:, n % 2, i * P:(i + 1) * P],
                                           wo[:, c * C:(c + 1) * C], start=(c == 0 and i == 0),
                                           stop=last and i == GROUP - 1, skip_group_check=True)
                    if bias is not None:
                        for i in range(GROUP):
                            mm = pe.matmul(y[:, i * C:(i + 1) * C], k.ones[0:1, 0:P], bias,
                                           start=False, stop=i == GROUP - 1, skip_group_check=True)
                    mm.then_inc(norm.y_full.sem, 1)
                if g >= 1:
                    norm.tensor(pe, 0, g - 1, (g - 1) % 2, k.ps_scores[0])

        @block.scalar
        def _(act):
            norm.start(None, None, act)
            o_taken.start(act)
            for g in range(NG + 1):
                if g < NG:
                    for c in range(chunks):
                        n = g * chunks + c
                        act.wait_ge(o_turned.sem, o_turned.at(0, n))
                        nc.scalar.copy(oT[:, n % 2, :], k.ps_turned[n % 2][:, :]).then_inc(o_taken.sem, 1)
                if g >= 1:
                    norm.scalar_store(act, 0, g - 1, k.ps_scores[0], xcol(g - 1))
                if g < NG and normed:
                    norm.scalar_root(act, 0, g, g % 2)
            act.wait_ge(norm.xT_ready.sem, norm.xT_ready.at(0, NG - 1))

        @block.vector
        def _(dve):
            norm.start(None, dve, None)
            chain = Count(dve, own)
            for g in range(NG):
                norm.vector(dve, chain, 0, g, g % 2, GROUP * g, k.ps_out[g % 2][:, :], normed=normed)


def project_turned(k, name, groups, chunks, oT, w, w_dram, bias, bias_dram, normed=True):
    nc = k.nc
    n_g = len(groups)
    with ExitStack() as ctx:
        sem = lambda n: k.sem(name + n, ctx)
        w_loaded = sem("_w_loaded")
        own = sem("_own_dve")
        norm = Norm(k, ctx, name, n_g)
        block = ctx.enter_context(nc.Block())

        @block.sync
        def _(sp):
            sp.dma_start(w, w_dram).then_inc(w_loaded, 16)
            if bias is not None:
                sp.dma_start(bias, bias_dram).then_inc(w_loaded, 16)

        @block.tensor
        def _(pe):
            norm.start(pe, None, None)
            pe.wait_ge(w_loaded, 32 if bias is not None else 16)
            for e in range(n_g + 1):
                if e < n_g:
                    y = k.ps_out[e % 2]
                    pe.wait_ge(norm.y_free.sem, norm.y_free.at(0, e - 2) if e >= 2 else 1)
                    for i in range(GROUP):
                        for c in range(chunks):
                            mm = pe.matmul(y[:, i * C:(i + 1) * C], oT(c, GROUP * groups[e] + i), w[:, c, :],
                                           start=c == 0, stop=c == chunks - 1 and bias is None)
                        if bias is not None:
                            mm = pe.matmul(y[:, i * C:(i + 1) * C], k.ones[0:1, 0:P], bias, start=False, stop=True)
                    mm.then_inc(norm.y_full.sem, 1)
                if e >= 1:
                    norm.tensor(pe, 0, e - 1, (e - 1) % 2, k.ps_scores[0])

        @block.scalar
        def _(act):
            norm.start(None, None, act)
            for e in range(n_g + 1):
                if e < n_g and normed:
                    norm.scalar_root(act, 0, e, e % 2)
                if e >= 1:
                    norm.scalar_store(act, 0, e - 1, k.ps_scores[0], xcol(groups[e - 1]))
            act.wait_ge(norm.xT_ready.sem, norm.xT_ready.at(0, n_g - 1))

        @block.vector
        def _(dve):
            norm.start(None, dve, None)
            chain = Count(dve, own)
            for e in range(n_g):
                norm.vector(dve, chain, 0, e, e % 2, GROUP * groups[e], k.ps_out[e % 2][:, :], normed=normed)



L0_HEADS, L0_D, SEG, DIL = 16, 8, 64, 4
L0_GROUPS = 10


def l0_attention(k):
    nc, d = k.nc, k.dram
    U = 4
    with ExitStack() as ctx:
        sem = lambda n: k.sem("l0_" + n, ctx)
        sb = lambda n, s: k.sb("l0_" + n, s, ctx=ctx)
        wq, wk, wv, wo = (sb(n, [P, C]) for n in ("wq", "wk", "wv", "wo"))
        bqk = sb("bqk", [P, 2])
        bv, bo = sb("bv", [1, C]), sb("bo", [1, C])
        hmask = sb("hmask", [P, L0_HEADS])
        gweight = sb("gweight", [P, TPB, L0_GROUPS])
        qT = sb("qT", [P, B * L])
        kT = sb("kT", [P, B * XB])
        v_own = sb("v_own", [P, TILES, C])
        v_dil = sb("v_dil", [P, TILES, C])
        qm = sb("q_masked", [P, B * L])
        o_tok = sb("o_tok", [P, TILES, C])
        probs = sb("probs", [P, 2, 1024])
        probsT = sb("probsT", [P, 2, 1024])
        gmax = sb("gmax", [P, 2, 4, L0_GROUPS])
        gsum = sb("gsum", [P, 2, 4, L0_GROUPS])
        ginv = sb("ginv", [P, 2, 4, L0_GROUPS])
        hcol = sb("hcol", [P, 1])

        with ExitStack() as c2:
            loaded, proj_full, proj_taken = (k.sem("l0p_" + n, c2) for n in ("loaded", "full", "taken"))
            block = c2.enter_context(nc.Block())
            xb = lambda t: (t // TPB) * XB + (t % TPB) * P
            jobs = ([("q", i) for i in range(4)] + [("k", i) for i in range(6)]
                    + [("v", i) for i in range(4)] + [("vd", i) for i in range(4)])

            @block.sync
            def _(sp):
                for out, src in ((wq, d["L0_attn_Wq"]), (wk, d["L0_attn_Wk"]), (wv, d["L0_attn_Wv"]),
                                 (bqk, d["L0_bqk"]), (bv, d["L0_attn_bv"]),
                                 (hmask, d["head_mask8"])):
                    sp.dma_start(out[:, :], src).then_inc(loaded, 16)
                sp.dma_start(gweight[:, :, :], d["L0_group_weights"]).then_inc(loaded, 16)

            @block.tensor
            def _(pe):
                pe.wait_ge(loaded, 16 * 7)
                for n, (kind, i) in enumerate(jobs):
                    bank = k.ps_out[n % 2]
                    if n >= 2:
                        pe.wait_ge(proj_taken, n - 1)
                    if kind == "q":
                        mm = pe.matmul(bank[:, :], wq[:, :], k.xT[:, xcol(i):xcol(i) + 512], start=True, stop=True)
                    elif kind == "k":
                        w = min(512, B * XB - i * 512)
                        mm = pe.matmul(bank[:, 0:w], wk[:, :], k.xT[:, i * 512:i * 512 + w], start=True, stop=True)
                    else:
                        for s in range(GROUP):
                            c0 = xb(GROUP * i + s)
                            x = (k.xT[:, c0 + PAD:c0 + PAD + P] if kind == "v" else
                                 k.xT[:, c0:c0 + (P - 1) * DIL + 1:DIL])
                            pe.matmul(bank[:, s * C:(s + 1) * C], x, wv[:, :], start=(s == 0), stop=False,
                                      skip_group_check=True)
                            mm = pe.matmul(bank[:, s * C:(s + 1) * C], k.ones[0:1, 0:P], bv[:, :], start=False,
                                           stop=s == GROUP - 1, skip_group_check=True)
                    mm.then_inc(proj_full, 1)

            @block.scalar
            def _(act):
                for n, (kind, i) in enumerate(jobs):
                    bank = k.ps_out[n % 2]
                    act.wait_ge(proj_full, n + 1)
                    if kind == "q":
                        ins = nc.scalar.activation(qT[:, i * 512:(i + 1) * 512], bank[:, :], ACT.Identity,
                                                   bias=bqk[:, 0:1])
                    elif kind == "k":
                        w = min(512, B * XB - i * 512)
                        ins = nc.scalar.activation(kT[:, i * 512:i * 512 + w], bank[:, 0:w], ACT.Identity,
                                                   bias=bqk[:, 1:2])
                    else:
                        v = v_own if kind == "v" else v_dil
                        ins = nc.scalar.copy(v[:, GROUP * i:GROUP * (i + 1), :],
                                             bank[:, :].rearrange("p (t c) -> p t c", c=C))
                    ins.then_inc(proj_taken, 1)
                act.wait_ge(proj_taken, len(jobs))

        with ExitStack() as c2:
            sm = lambda n: k.sem("l0a_" + n, c2)
            s_full = [Signal(sm(f"scores_full{i}"), U // 2) for i in range(2)]
            s_free = [Signal(sm(f"scores_free{i}"), U // 2) for i in range(2)]
            q_ready = Signal(sm("q_ready"), B)
            shifted = Signal(sm("shifted"), U)
            e_raw = Signal(sm("exp_done"), U)
            e_full = Signal(sm("probs_ready"), U)
            inv_ready = Signal(sm("inv_ready"), U)
            t_full = [Signal(sm(f"turned_full{i}"), U) for i in range(2)]
            t_done = [Signal(sm(f"turned_taken{i}"), U) for i in range(2)]
            o_full = Signal(sm("out_full"), 1)
            o_free = Signal(sm("out_taken"), 1)
            hc = Signal(sm("mask_column"), 1)
            own_dve = Signal(sm("own_dve"), U * 6)
            block = c2.enter_context(nc.Block())
            plan = order(U, 0, U)
            o_bank = k.ps_out[0][:, 0:TILES * L0_D].rearrange("p (t c) -> p t c", c=L0_D)

            def groups(t, s):
                v = t[:, s, :] if len(t.shape) == 3 else t[:, :]
                v = v.rearrange("p (t q) -> p t q", t=4)
                return (v[:, :, 0:P].rearrange("p t (g q) -> p t g q", g=2),
                        v[:, :, P:2 * P].rearrange("p t (g q) -> p t g q", g=8))

            def wide(v, s, shape, a, b):
                return v[:, s, :, a:b].unsqueeze(3).broadcast_to(shape)

            @block.gpsimd
            def _(pool):
                q_ready.start(pool)
                e_full.start(pool)
                hc.start(pool)
                with pool.Fori(0, L0_HEADS) as h:
                    def mask(b):
                        pool.wait_ge(s_full[1].sem, s_full[1].at(h, b - 2))
                        nc.gpsimd.tensor_tensor(qm[:, b * L:(b + 1) * L], qT[:, b * L:(b + 1) * L],
                                                hcol[:, 0:1].broadcast_to([P, L]), ALU.mult).then_inc(q_ready.sem, 1)
                    pool.wait_ge(q_ready.sem, q_ready.at(h, -1))
                    nc.gpsimd.tensor_copy(hcol[:, :], hmask[:, ds(h, 1)]).then_inc(hc.sem, 1)
                    pool.wait_ge(hc.sem, hc.at(h, 0))
                    mask(0)
                    mask(1)
                    for u in range(U):
                        pool.wait_ge(e_raw.sem, e_raw.at(h, u))
                        pool.wait_ge(inv_ready.sem, inv_ready.at(h, u))
                        eo, ed = groups(probs, u % 2)
                        nc.gpsimd.tensor_tensor(eo, eo, wide(ginv, u % 2, [P, 4, 2, SEG], 0, 2), ALU.mult)
                        nc.gpsimd.tensor_tensor(ed, ed, wide(ginv, u % 2, [P, 4, 8, 16], 2, 10), ALU.mult
                                                ).then_inc(e_full.sem, 1)

            @block.tensor
            def _(pe):
                for s in (*s_full, *t_full, o_full):
                    s.start(pe)
                with pe.Fori(0, L0_HEADS) as h:
                    for what, u in plan:
                        if what == "S":
                            slot, b = u % 2, u // 2
                            pe.wait_ge(s_free[slot].sem, s_free[slot].at(h, u // 2 - 1))
                            if u % 2 == 0:
                                pe.wait_ge(q_ready.sem, q_ready.at(h, b))
                            for i in range(4):
                                j = (4 * u + i) % TPB
                                qs = qm[:, b * L + j * P:b * L + (j + 1) * P]
                                c0 = b * XB + j * P
                                pe.matmul(k.ps_scores[slot][:, i * 256:i * 256 + P], qs,
                                          kT[:, c0 + PAD:c0 + PAD + P], start=True, stop=True)
                                mm = pe.matmul(k.ps_scores[slot][:, i * 256 + P:(i + 1) * 256], qs,
                                               kT[:, c0:c0 + (P - 1) * DIL + 1:DIL], start=True, stop=True)
                            mm.then_inc(s_full[slot].sem, 1)
                        elif what == "T":
                            pe.wait_ge(e_full.sem, e_full.at(h, u))
                            turn(pe, k, probs[:, u % 2, :], t_full, t_done, h, u)
                        else:
                            for half in range(2):
                                pe.wait_ge(t_done[half].sem, t_done[half].at(h, u))
                            if u == 0:
                                pe.wait_ge(o_free.sem, o_free.at(h, -1))
                            for i in range(4):
                                t = 4 * u + i
                                for part, v in enumerate((v_own, v_dil)):
                                    c0 = (2 * i + part) * P
                                    mm = pe.matmul(o_bank[:, t, :], probsT[:, u % 2, c0:c0 + P],
                                                   v[:, t, ds(h * L0_D, L0_D)], start=part == 0, stop=part == 1)
                            if u == U - 1:
                                mm.then_inc(o_full.sem, 1)

            @block.vector
            def _(dve):
                for s in (*s_free, shifted, inv_ready, own_dve):
                    s.start(dve)
                with dve.Fori(0, L0_HEADS) as h:
                    chain = Chain(dve, own_dve, h)
                    for u in range(U):
                        s = u % 2
                        scores, sd = groups(k.ps_scores[s], s)
                        eo, ed = groups(probs, s)
                        dve.wait_ge(s_full[s].sem, s_full[s].at(h, u // 2))
                        dve.wait_ge(inv_ready.sem, inv_ready.at(h, u - 1))
                        chain.done(nc.vector.tensor_reduce(gmax[:, s, :, 0:2], scores, AX.X, ALU.max))
                        chain.step(nc.vector.tensor_reduce(gmax[:, s, :, 2:10], sd, AX.X, ALU.max))
                        dve.wait_ge(t_full[1].sem, t_full[1].at(h, u - 2))
                        nc.vector.tensor_tensor(eo, scores, wide(gmax, s, [P, 4, 2, SEG], 0, 2), ALU.subtract
                                                ).then_inc(own_dve.sem, 1)
                        chain.n += 1
                        nc.vector.tensor_tensor(ed, sd, wide(gmax, s, [P, 4, 8, 16], 2, 10), ALU.subtract
                                                ).then_inc(shifted.sem, 1)
                        dve.wait_ge(shifted.sem, shifted.at(h, u))
                        dve.sem_inc(s_free[s].sem, 1)
                        dve.wait_ge(e_raw.sem, e_raw.at(h, u))
                        chain.done(nc.vector.tensor_reduce(gsum[:, s, :, 0:2], eo, AX.X, ALU.add))
                        chain.step(nc.vector.tensor_reduce(gsum[:, s, :, 2:10], ed, AX.X, ALU.add))
                        chain.step(nc.vector.reciprocal(ginv[:, s, :, :], gsum[:, s, :, :]))
                        j0 = (4 * u) % TPB
                        nc.vector.tensor_tensor(ginv[:, s, :, :], ginv[:, s, :, :],
                                                gweight[:, j0:j0 + 4, :], ALU.mult).then_inc(inv_ready.sem, 1)
                    chain.close()

            @block.scalar
            def _(act):
                for s in (e_raw, *t_done, o_free):
                    s.start(act)
                with act.Fori(0, L0_HEADS) as h:
                    for what, u in plan:
                        if what == "S":
                            act.wait_ge(shifted.sem, shifted.at(h, u))
                            nc.scalar.activation(probs[:, u % 2, :], probs[:, u % 2, :], ACT.Exp
                                                 ).then_inc(e_raw.sem, 1)
                        elif what == "T":
                            for half in range(2):
                                take_turned(nc.scalar, k, probsT[:, u % 2, :], t_full, t_done, h, u, half)
                    act.wait_ge(o_full.sem, o_full.at(h, 0))
                    nc.scalar.copy(o_tok[:, :, ds(h * L0_D, L0_D)], o_bank).then_inc(o_free.sem, 1)

        project_out(k, "l0o", o_tok, 1, wo[:, :], d["L0_attn_Wo"], bo[:, :], d["L0_attn_bo"])


def every(half, u):
    return u


def turn(pe, k, probs, t_full, t_done, it, u, blocks=8, event=every):
    for half in range((blocks + 3) // 4):
        e = event(half, u)
        pe.wait_ge(t_done[half].sem, t_done[half].at(it, e - 1))
        for c in range(4 * half, min(blocks, 4 * half + 4)):
            mm = pe.transpose(k.ps_turned[half][:, (c % 4) * P:(c % 4 + 1) * P], probs[:, c * P:(c + 1) * P],
                              k.ident[:, :])
        mm.then_inc(t_full[half].sem, 1)


def take_turned(eng, k, probsT, t_full, t_done, it, u, half, blocks=8, event=every):
    n = min(4, blocks - 4 * half)
    eng.wait_ge(t_full[half].sem, t_full[half].at(it, event(half, u)))
    out, src = probsT[:, half * 512:half * 512 + n * P], k.ps_turned[half][:, 0:n * P]
    ins = eng.copy(out, src) if eng is k.nc.scalar else eng.tensor_copy(out, src)
    ins.then_inc(t_done[half].sem, 1)



L0_HID, L0_STAGES = 512, 9


def butterfly(eng, own, rows, buf, tmp, coef, down):
    for n in range(L0_STAGES):
        stage = L0_STAGES - 1 - n if down else n
        s = 2 ** stage
        nb = L0_HID // (2 * s)
        src = buf[0:rows, n % 2, :].rearrange("p (n i s) -> p n i s", i=2, s=s)
        dst = buf[0:rows, (n + 1) % 2, :].rearrange("p (n o s) -> p n o s", o=2, s=s)
        w = coef[0:rows, stage * 1024:(stage + 1) * 1024].rearrange("p (n s o i) -> p n o i s", s=s, o=2, i=2)
        for o in range(2):
            for i in range(2):
                block = w[:, :, i, o, :] if down else w[:, :, o, i, :]
                t = tmp[0:rows, i, o * 256:(o + 1) * 256].rearrange("p (n s) -> p n s", s=s)
                own.done(eng.tensor_tensor(t, src[:, :, i, :], block, ALU.mult))
        own.wait()
        t = tmp[0:rows, :, :].rearrange("p i (o n s) -> p i n o s", o=2, s=s)
        for o in range(2):
            own.done(eng.tensor_tensor(dst[:, :, o, :], t[:, 0, :, o, :], t[:, 1, :, o, :], ALU.add))
        own.wait()


def l0_ffn(k):
    nc, d = k.nc, k.dram
    CH = L0_HID // P
    with ExitStack() as ctx:
        sb = lambda n, s: k.sb("f0_" + n, s, ctx=ctx)
        up = sb("up", [P, 2, L0_HID])
        upb = sb("up_bias_row", [1, 2, L0_HID])
        down = sb("down", [P, 2, L0_HID])
        w_down = sb("w_down", [P, CH * C])
        bias_h = sb("bias_h", [P, CH])
        up_bias = sb("up_bias", [P, CH])
        bias_y = sb("bias_y", [2, C])
        hid = sb("hid", [P, 2, CH, 512])
        with ExitStack() as c2:
            loaded = [k.sem(f"f0_loaded{i}", c2) for i in range(3)]
            own_pool, own_dve, own_bias, turned, taken = (k.sem("f0_" + n, c2) for n in (
                "own_pool", "own_dve", "own_bias", "down_turned", "taken"))
            up_coef = k.sb("f0_up_coef", [P, L0_STAGES * 1024], ctx=c2)
            down_coef = k.sb("f0_down_coef", [P, L0_STAGES * 1024], ctx=c2)
            tmp = [k.sb(f"f0_tmp{i}", [P, 2, L0_HID], ctx=c2) for i in range(2)]
            block = c2.enter_context(nc.Block())
            DONE = L0_STAGES * 6

            @block.sync
            def _(sp):
                sp.dma_start(up_coef[:, :], d["L0_up_weights"].partition_broadcast(P)).then_inc(loaded[0], 16)
                sp.dma_start(up[:, 0, :], d["L0_ffn_W_exp"]).then_inc(loaded[0], 16)
                sp.dma_start(down_coef[:, :], d["L0_down_weights"].partition_broadcast(P)).then_inc(loaded[1], 16)
                sp.dma_start(down[:, 0, :], d["L0_W_con_T"]).then_inc(loaded[1], 16)
                sp.dma_start(upb[:, 0, :], d["L0_ffn_b_exp"]).then_inc(loaded[2], 16)
                sp.dma_start(up_bias[:, :], d["L0_up_bias"]).then_inc(loaded[2], 16)
                sp.dma_start(bias_y[:, :], d["L0_y_bias"]).then_inc(loaded[2], 16)

            @block.gpsimd
            def _(pool):
                pool.wait_ge(loaded[0], 32)
                butterfly(nc.gpsimd, Count(pool, own_pool), P, up, tmp[0], up_coef, False)

            @block.vector
            def _(dve):
                dve.wait_ge(loaded[1], 32)
                butterfly(nc.vector, Count(dve, own_dve), P, down, tmp[1], down_coef, True)
                dve.wait_ge(loaded[0], 32)
                dve.wait_ge(loaded[2], 48)
                butterfly(nc.vector, Count(dve, own_bias), 1, upb, tmp[1], up_coef, False)
                dve.wait_ge(turned, 1)
                nc.vector.tensor_copy(w_down[:, :], k.ps_turned[0][:, :]).then_inc(taken, 1)
                dve.wait_ge(turned, 2)
                nc.vector.tensor_tensor(bias_h[:, :], k.ps_turned[1][:, 0:CH], up_bias[:, :], ALU.add
                                        ).then_inc(taken, 1)
                dve.wait_ge(taken, 2)

            @block.tensor
            def _(pe):
                pe.wait_ge(own_dve, DONE)
                for c in range(CH):
                    mm = pe.transpose(k.ps_turned[0][:, c * P:(c + 1) * P], down[:, 1, c * P:(c + 1) * P],
                                      k.ident[:, :])
                mm.then_inc(turned, 1)
                pe.wait_ge(own_bias, DONE)
                for c in range(CH):
                    mm = pe.matmul(k.ps_turned[1][:, c:c + 1], upb[:, 1, c * P:(c + 1) * P], k.ones[0:1, 0:1],
                                   start=True, stop=True)
                mm.then_inc(turned, 1)

        feed_forward(k, "f0", hid, CH, [P] * CH, lambda c: up[:, 1, c * P:(c + 1) * P],
                     lambda c: w_down[:, c * C:(c + 1) * C], bias_y[:, :],
                     lambda c: (ACT.Gelu, bias_h[:, c:c + 1]))


def feed_forward(k, name, hid, chunks, rows, w_up, w_down, bias_y, act_of):
    nc = k.nc
    HALVES = NG // B
    with ExitStack() as ctx:
        sem = lambda n: k.sem(name + n, ctx)
        per = HALVES * chunks // 2
        h_full = [Signal(sem(f"_h_full{i}"), per) for i in range(2)]
        h_ready = [Signal(sem(f"_h_ready{i}"), per) for i in range(2)]
        own = Signal(sem("_own_dve"), HALVES * Norm.DVE_STEPS)
        norm = Norm(k, ctx, name, HALVES)
        block = ctx.enter_context(nc.Block())

        @block.tensor
        def _(pe):
            norm.start(pe, None, None)
            for s in h_full:
                s.start(pe)
            with pe.Fori(0, B) as b:
                for g in range(HALVES):
                    for c in range(chunks):
                        n = g * chunks + c
                        pe.wait_ge(h_ready[n % 2].sem, h_ready[n % 2].at(b, n // 2 - 1))
                        pe.matmul(k.ps_scores[n % 2][0:rows[c], 0:512], w_up(c),
                                  k.xT[:, ds(b * XB + PAD + g * 512, 512)], start=True, stop=True
                                  ).then_inc(h_full[n % 2].sem, 1)
                for g in range(HALVES):
                    y = k.ps_out[g]
                    pe.wait_ge(norm.y_free.sem, norm.y_free.at(b, g - 2))
                    for c in range(chunks):
                        n = g * chunks + c
                        pe.wait_ge(h_ready[n % 2].sem, h_ready[n % 2].at(b, n // 2))
                        for i in range(GROUP):
                            pe.matmul(y[:, i * C:(i + 1) * C], hid[0:rows[c], g, c, i * P:(i + 1) * P], w_down(c),
                                      start=(c == 0 and i == 0), stop=False, skip_group_check=True)
                    kb = bias_y.shape[0]
                    for i in range(GROUP):
                        mm = pe.matmul(y[:, i * C:(i + 1) * C], k.ones[0:kb, 0:P], bias_y, start=False,
                                       stop=i == GROUP - 1, skip_group_check=True)
                    mm.then_inc(norm.y_full.sem, 1)
                for g in range(HALVES):
                    norm.tensor(pe, b, g, g, k.ps_turned[0])

        @block.scalar
        def _(act):
            norm.start(None, None, act)
            for s in h_ready:
                s.start(act)
            with act.Fori(0, B) as b:
                for g in range(HALVES):
                    for c in range(chunks):
                        n = g * chunks + c
                        func, bias = act_of(c)
                        act.wait_ge(h_full[n % 2].sem, h_full[n % 2].at(b, n // 2))
                        nc.scalar.activation(hid[0:rows[c], g, c, :], k.ps_scores[n % 2][0:rows[c], 0:512], func,
                                             bias=bias).then_inc(h_ready[n % 2].sem, 1)
                for g in range(HALVES):
                    norm.scalar_root(act, b, g, g)
                for g in range(HALVES):
                    norm.scalar_store(act, b, g, k.ps_turned[0], b * XB + PAD + g * 512)

        @block.vector
        def _(dve):
            norm.start(None, dve, None)
            own.start(dve)
            with dve.Fori(0, B) as b:
                chain = Chain(dve, own, b)
                for g in range(HALVES):
                    norm.vector(dve, chain, b, g, g, b * TPB + g * GROUP, k.ps_out[g][:, :])
                chain.close()



L1_HEADS, L1_D = 16, 64
PAIRS = L1_HEADS // 2
TABLE = 2 * L - P
TWO_PI = 2 * np.pi
PI_A = 6.28125
PI_B = float(np.floor((TWO_PI - PI_A) * 2 ** 19) / 2 ** 19)
PI_C = float(TWO_PI - PI_A - PI_B)
ROUND = 1.5 * 2 ** 23


def l1_attention(k):
    nc, d = k.nc, k.dram
    LEAD, U = 6, 16
    N = LEAD + U
    RING, LAG = 4, 3
    with ExitStack() as ctx:
        sb = lambda n, s: k.sb("l1_" + n, s, ctx=ctx)
        oT = sb("oT", [P, PAIRS, B * L])
        with ExitStack() as c2:
            sb = lambda n, s, dt=F32: k.sb("l1_" + n, s, dt, ctx=c2)
            rope = sb("rope", [P, 4, L])
            dist = sb("dist", [P, TABLE])
            nbias = sb("neg_bias", [P, 2, TABLE])
            ap = sb("bias_ap", [P, 2 * L1_HEADS])
            cols = sb("bias_cols", [P, 4])
            w = sb("w", [P, 5 * P])
            xb = sb("x_batch", [P, L])
            head = sb("head_rows", [P, 2])
            q = sb("q", [P, 2, L])
            kr = sb("k", [P, L])
            v = sb("v", [P, TPB, P])
            rot = sb("rot", [P, 2, 2, 512])
            probs = sb("probs", [P, RING, 1024])
            probsT = sb("probsT", [P, 2, 1024])
            nmax = sb("neg_max", [P, U])
            rsum = sb("row_sum", [P, U])
            rinv = sb("row_inv", [P, U])
            with ExitStack() as c3:
                sem = lambda n: k.sem("l1t_" + n, c3)
                loaded, made, own, roots = sem("loaded"), sem("iotas"), sem("own_dve"), sem("acts")
                ints = k.sb("l1_ints", [P, TABLE], mybir.dt.int32, ctx=c3)
                posi = k.sb("l1_posi", [P, L], mybir.dt.int32, ctx=c3)
                freq = k.sb("l1_freq", [P, 3], ctx=c3)
                ang, turns = (k.sb("l1_" + n, [P, L], ctx=c3) for n in ("ang", "turns"))
                block = c3.enter_context(nc.Block())

                @block.sync
                def _(sp):
                    sp.dma_start(freq[:, :], d["L1_freq"]).then_inc(loaded, 16)
                    sp.dma_start(ap[:, :], d["L1_bias_ap"].partition_broadcast(P)).then_inc(loaded, 16)

                @block.gpsimd
                def _(pool):
                    nc.gpsimd.iota(posi[:, :], [[1, L]], base=0, channel_multiplier=0).then_inc(made, 1)
                    nc.gpsimd.iota(ints[:, :], [[1, TABLE]], base=P - L, channel_multiplier=-1).then_inc(made, 1)
                    nc.gpsimd.memset(head[:, :], 1.0).then_inc(made, 1)
                    pool.wait_ge(made, 3)
                    nc.gpsimd.affine_select(out=head[:, 0:1], in_=head[:, 0:1], compare_op=ALU.is_ge, fill=0.0,
                                            base=L1_D - 1, pattern=[[0, 1]], channel_multiplier=-1)
                    nc.gpsimd.affine_select(out=head[:, 1:2], in_=head[:, 1:2], compare_op=ALU.is_ge, fill=0.0,
                                            base=-L1_D, pattern=[[0, 1]], channel_multiplier=1).then_inc(made, 1)
                    pool.wait_ge(made, 4)

                @block.vector
                def _(dve):
                    c = Count(dve, own)
                    v_ = nc.vector
                    dve.wait_ge(loaded, 32)
                    dve.wait_ge(made, 2)
                    c.done(v_.tensor_scalar(ap[:, :], ap[:, :], 0.01, None, ALU.max))
                    c.done(v_.tensor_copy(dist[:, :], ints[:, :]))
                    c.step(v_.tensor_copy(turns[:, :], posi[:, :]))
                    c.step(v_.tensor_scalar(ang[:, :], turns[:, :], freq[:, 0:1], None, ALU.mult))
                    c.step(v_.tensor_scalar(turns[:, :], ang[:, :], 1 / TWO_PI, ROUND, ALU.mult, ALU.add))
                    c.step(v_.tensor_scalar(turns[:, :], turns[:, :], ROUND, None, ALU.subtract))
                    for part in (PI_A, PI_B, PI_C):
                        c.step(v_.scalar_tensor_tensor(ang[:, :], turns[:, :], -part, ang[:, :], ALU.mult, ALU.add))
                    c.step(v_.tensor_scalar(ang[:, :], ang[:, :], 3.1415925, -3.1415925, ALU.min, ALU.max))
                    dve.wait_ge(roots, 4)
                    c.done(v_.tensor_scalar(rope[:, 3, :], rope[:, 1, :], freq[:, 1:2], None, ALU.mult))
                    c.done(v_.tensor_scalar(rope[:, 2, :], rope[:, 0, :], 1.0, None, ALU.mult))
                    c.step(v_.tensor_scalar(rope[:, 0, :], rope[:, 0, :], -0.125, None, ALU.mult))
                    c.step(v_.tensor_scalar(rope[:, 1, :], rope[:, 1, :], freq[:, 1:2], -0.125, ALU.mult, ALU.mult))

                @block.scalar
                def _(act):
                    act.wait_ge(own, 2)
                    nc.scalar.activation(dist[:, :], dist[:, :], ACT.Abs).then_inc(roots, 1)
                    act.wait_ge(own, 10)
                    nc.scalar.activation(rope[:, 1, :], ang[:, :], ACT.Sin).then_inc(roots, 1)
                    nc.scalar.activation(turns[:, :], ang[:, :], ACT.Abs).then_inc(roots, 1)
                    act.wait_ge(roots, 3)
                    nc.scalar.activation(rope[:, 0, :], turns[:, :], ACT.Sin, bias=freq[:, 2:3], scale=-1.0
                                         ).then_inc(roots, 1)

            with ExitStack() as c3:
                sm = lambda n: k.sem("l1a_" + n, c3)
                s_full = [Signal(sm(f"slot_full{i}"), N // 2) for i in range(2)]
                s_free = [Signal(sm(f"slot_free{i}"), N // 2) for i in range(2)]
                w_loaded = sm("w_loaded")
                cols_ready = Signal(sm("cols"), 4)
                logs = Signal(sm("logs"), 2)
                bias_ready = Signal(sm("bias_ready"), 2)
                xb_ready = Signal(sm("xb_ready"), 1)
                rotated = Signal(sm("rotated"), 4)
                prod = Signal(sm("rot_first"), 4)
                summed = Signal(sm("q_summed"), 2)
                qk_ready = Signal(sm("qk_ready"), 4)
                v_ready = Signal(sm("v_ready"), 2)
                e_full = Signal(sm("exp_done"), U)
                inv_ready = Signal(sm("inv_ready"), U)
                p_full = Signal(sm("probs_ready"), U)
                t_full = [Signal(sm(f"turned_full{i}"), U) for i in range(2)]
                t_done = [Signal(sm(f"turned_taken{i}"), U) for i in range(2)]
                o_full = [Signal(sm(f"out_full{i}"), 1) for i in range(2)]
                o_free = [Signal(sm(f"out_taken{i}"), 1) for i in range(2)]
                passed = sm("passed")
                block = c3.enter_context(nc.Block())
                plan = order_pairs(N, LEAD, U, LAG)

                def slot_full(n):
                    return s_full[n % 2], n // 2

                @block.sync
                def _(sp):
                    sp.dma_start(w[:, :], d["L1_qkv"][0, :, :]).then_inc(w_loaded, 16)
                    with sp.Fori(0, PAIRS - 1) as hp:
                        sp.wait_ge(s_full[1].sem, s_full[1].at(hp * 2 + 1, LEAD // 2 - 1))
                        sp.dma_start(w[:, :], d["L1_qkv"][ds(hp + 1, 1), :, :].rearrange("o p c -> p (o c)")
                                     ).then_inc(w_loaded, 16)

                @block.gpsimd
                def _(pool):
                    for s in (cols_ready, bias_ready, summed, qk_ready, p_full):
                        s.start(pool)
                    with pool.Fori(0, PAIRS) as hp:
                        pool.wait_ge(bias_ready.sem, bias_ready.at(hp, -1))
                        pool.sem_inc(passed, 1)
                        for i in range(4):
                            nc.gpsimd.tensor_copy(cols[:, i:i + 1], ap[:, ds(hp * 2 + (i // 2) * L1_HEADS + i % 2, 1)]
                                                  ).then_inc(cols_ready.sem, 1)
                        for b in range(B):
                            it = hp * 2 + b
                            for n in range(4):
                                pool.wait_ge(rotated.sem, rotated.at(it, n))
                                half = slice((n % 2) * 512, (n % 2 + 1) * 512)
                                r = rot[:, n % 2, :, :]
                                if n < 2:
                                    nc.gpsimd.tensor_tensor(r[:, 0, :], r[:, 0, :], r[:, 1, :], ALU.add
                                                            ).then_inc(summed.sem, 1)
                                    pool.wait_ge(summed.sem, summed.at(it, n))
                                    for j in range(2):
                                        ins = nc.gpsimd.tensor_tensor(
                                            q[:, j, half], r[:, 0, :], head[:, j:j + 1].broadcast_to([P, 512]),
                                            ALU.mult)
                                else:
                                    ins = nc.gpsimd.tensor_tensor(kr[:, half], r[:, 0, :], r[:, 1, :], ALU.add)
                                ins.then_inc(qk_ready.sem, 1)
                            if b == 0:
                                for j in range(2):
                                    pool.wait_ge(logs.sem, logs.at(hp, j))
                                    nc.gpsimd.tensor_tensor(nbias[:, j, :], nbias[:, j, :],
                                                            cols[:, 2 + j:3 + j].broadcast_to([P, TABLE]), ALU.mult
                                                            ).then_inc(bias_ready.sem, 1)
                            for u in range(U):
                                pool.wait_ge(inv_ready.sem, inv_ready.at(it, u))
                                p = probs[:, u % RING, :]
                                nc.gpsimd.tensor_tensor(p, p, rinv[:, u:u + 1].broadcast_to([P, L]), ALU.mult
                                                        ).then_inc(p_full.sem, 1)

                @block.tensor
                def _(pe):
                    for s in (*s_full, *t_full, *o_full):
                        s.start(pe)
                    with pe.Fori(0, PAIRS) as hp:
                        with pe.Fori(0, B) as b:
                            it = hp * 2 + b
                            for what, n in plan:
                                if what == "S":
                                    slot = k.ps_scores[n % 2]
                                    pe.wait_ge(s_free[n % 2].sem, s_free[n % 2].at(it, n // 2 - 1))
                                    if n == 0:
                                        pe.wait_ge(w_loaded, hp * 16 + 16)
                                    if n < 4:
                                        for i in range(2):
                                            c0 = (n // 2) * 2 * P + i * P
                                            mm = pe.matmul(slot[:, i * 512:(i + 1) * 512], w[:, c0:c0 + P],
                                                           k.xT[:, ds(b * XB + PAD + (n % 2) * 512, 512)],
                                                           start=True, stop=True)
                                    elif n < LEAD:
                                        if n == 4:
                                            pe.wait_ge(xb_ready.sem, xb_ready.at(it, 0))
                                        for i in range(4):
                                            c0 = ((n - 4) * 4 + i) * P
                                            mm = pe.matmul(slot[:, i * P:(i + 1) * P], xb[:, c0:c0 + P],
                                                           w[:, 4 * P:5 * P], start=True, stop=True)
                                    else:
                                        u = n - LEAD
                                        j, qt = u % 2, u // 2
                                        if u == 0:
                                            pe.wait_ge(qk_ready.sem, qk_ready.at(it, 3))
                                        for i in range(2):
                                            mm = pe.matmul(slot[:, i * 512:(i + 1) * 512],
                                                           q[:, j, qt * P:(qt + 1) * P],
                                                           kr[:, i * 512:(i + 1) * 512], start=True, stop=True)
                                    mm.then_inc(s_full[n % 2].sem, 1)
                                elif what == "T":
                                    pe.wait_ge(p_full.sem, p_full.at(it, n))
                                    turn(pe, k, probs[:, n % RING, :], t_full, t_done, it, n)
                                else:
                                    qt = n
                                    for half in range(2):
                                        pe.wait_ge(t_done[half].sem, t_done[half].at(it, 2 * qt + 1))
                                    if qt == 0:
                                        pe.wait_ge(v_ready.sem, v_ready.at(it, 1))
                                    bank, c0 = qt // 4, (qt % 4) * P
                                    if qt % 4 == 0:
                                        pe.wait_ge(o_free[bank].sem, o_free[bank].at(it, -1))
                                    for t in range(TPB):
                                        for j in range(2):
                                            mm = pe.matmul(k.ps_out[bank][j * L1_D:(j + 1) * L1_D, c0:c0 + P],
                                                           v[:, t, j * L1_D:(j + 1) * L1_D],
                                                           probsT[:, j, t * P:(t + 1) * P],
                                                           start=qt % 4 == 0 and t == 0,
                                                           stop=qt % 4 == 3 and t == TPB - 1,
                                                           skip_group_check=True)
                                    if qt % 4 == 3:
                                        mm.then_inc(o_full[bank].sem, 1)

                @block.vector
                def _(dve):
                    for s in (*s_free, rotated, prod, t_done[1], o_free[1], inv_ready):
                        s.start(dve)
                    with dve.Fori(0, PAIRS) as hp:
                        with dve.Fori(0, B) as b:
                            it = hp * 2 + b

                            def inverse(u):
                                dve.wait_ge(e_full.sem, e_full.at(it, u))
                                nc.vector.reciprocal(rinv[:, u:u + 1], rsum[:, u:u + 1]).then_inc(inv_ready.sem, 1)

                            for what, n in plan:
                                slot = k.ps_scores[n % 2]
                                if what == "S" and n < 4:
                                    f, at = slot_full(n)
                                    dve.wait_ge(f.sem, f.at(it, at))
                                    dve.wait_ge(qk_ready.sem, qk_ready.at(it, n - 2))
                                    cols_ = slice((n % 2) * 512, (n % 2 + 1) * 512)
                                    nc.vector.tensor_tensor(rot[:, n % 2, 0, :], slot[:, 0:512],
                                                            rope[:, (n // 2) * 2, cols_], ALU.mult
                                                            ).then_inc(prod.sem, 1)
                                    nc.vector.tensor_tensor(rot[:, n % 2, 1, :], slot[:, 512:1024],
                                                            rope[:, (n // 2) * 2 + 1, cols_], ALU.mult
                                                            ).then_inc(rotated.sem, 1)
                                    dve.wait_ge(rotated.sem, rotated.at(it, n))
                                    dve.sem_inc(s_free[n % 2].sem, 1)
                                elif what == "S" and n >= LEAD:
                                    u = n - LEAD
                                    j, qt = u % 2, u // 2
                                    f, at = slot_full(n)
                                    dve.wait_ge(f.sem, f.at(it, at))
                                    dve.wait_ge(t_full[1].sem, t_full[1].at(it, u - RING))
                                    if qt == 0:
                                        dve.wait_ge(bias_ready.sem, bias_ready.at(hp, j))
                                    dve.sem_inc(passed, 1)
                                    c0 = L - P - qt * P
                                    nc.vector.tensor_tensor_reduce(
                                        probs[:, u % RING, :], slot[:, :], nbias[:, j, c0:c0 + L], 1.0, HUGE,
                                        ALU.add, ALU.min, nmax[:, u:u + 1]).then_inc(s_free[n % 2].sem, 1)
                                    if u >= 1:
                                        inverse(u - 1)
                                    if u == U - 1:
                                        inverse(u)
                                elif what == "T":
                                    take_turned(nc.vector, k, probsT[:, n % 2, :], t_full, t_done, it, n, 1)
                            dve.wait_ge(o_full[1].sem, o_full[1].at(it, 0))
                            nc.vector.tensor_scalar(oT[:, ds(hp, 1), ds(b * L + 512, 512)],
                                                    k.ps_out[1][:, :].rearrange("p (o c) -> p o c", o=1), 1.0, None,
                                                    ALU.mult).then_inc(o_free[1].sem, 1)

                @block.scalar
                def _(act):
                    for s in (logs, v_ready, xb_ready, e_full, t_done[0], o_free[0]):
                        s.start(act)
                    with act.Fori(0, PAIRS) as hp:
                        act.wait_ge(cols_ready.sem, cols_ready.at(hp, 3))
                        act.wait_ge(s_free[1].sem, s_free[1].at(hp * 2, -1))
                        for j in range(2):
                            nc.scalar.activation(nbias[:, j, :], dist[:, :], ACT.Ln, bias=1.0,
                                                 scale=cols[:, j:j + 1]).then_inc(logs.sem, 1)
                        with act.Fori(0, B) as b:
                            it = hp * 2 + b
                            act.wait_ge(s_full[1].sem, s_full[1].at(it, LEAD // 2 - 1 - N // 2))
                            act.sem_inc(passed, 1)
                            nc.scalar.activation(xb[:, :], k.xT[:, ds(b * XB + PAD, L)], ACT.Copy
                                                 ).then_inc(xb_ready.sem, 1)
                            for what, n in plan:
                                if what == "S" and 4 <= n < LEAD:
                                    f, at = slot_full(n)
                                    act.wait_ge(f.sem, f.at(it, at))
                                    nc.scalar.copy(v[:, (n - 4) * 4:(n - 3) * 4, :],
                                                   k.ps_scores[n % 2][:, 0:512].rearrange("p (t c) -> p t c", c=P)
                                                   ).then_inc(v_ready.sem, 1)
                                    act.wait_ge(v_ready.sem, v_ready.at(it, n - 4))
                                    act.sem_inc(s_free[n % 2].sem, 1)
                                elif what == "S" and n >= LEAD:
                                    u = n - LEAD
                                    act.wait_ge(s_free[n % 2].sem, s_free[n % 2].at(it, n // 2))
                                    nc.scalar.activation(probs[:, u % RING, :], probs[:, u % RING, :], ACT.Exp,
                                                         bias=nmax[:, u:u + 1], scale=-1.0,
                                                         accum_out=rsum[:, u:u + 1]).then_inc(e_full.sem, 1)
                                elif what == "T":
                                    take_turned(nc.scalar, k, probsT[:, n % 2, :], t_full, t_done, it, n, 0)
                                elif what == "V" and n == 5:
                                    act.wait_ge(o_full[0].sem, o_full[0].at(it, 0))
                                    nc.scalar.copy(oT[:, ds(hp, 1), ds(b * L, 512)],
                                                   k.ps_out[0][:, :].rearrange("p (o c) -> p o c", o=1)
                                                   ).then_inc(o_free[0].sem, 1)

        wo = k.sb("l1_wo", [P, PAIRS, C], ctx=ctx)
        project_turned(k, "l1o", range(NG), PAIRS, lambda c, t: oT[:, c, t * P:(t + 1) * P], wo[:, :, :],
                       d["L1_out_w"], None, None)



F1_DEPTH, F1_HEADS, F1_D, WINDOW = 2, 8, 64, 64
F1_INNER = F1_HEADS * F1_D
F1_HID = 341
HEAD_AT = (0, 2, 1, 3)
F1_ROWS = [P, P, F1_HID - 2 * P]


def l1_ffn(k):
    nc, d = k.nc, k.dram
    x_in = nc.dram_tensor("f1_x_in", (P, TILES * C), F32, kind="Internal").ap()
    with ExitStack() as ctx:
        kept = k.sem("f1_kept", ctx)
        block = ctx.enter_context(nc.Block())

        @block.sync
        def _(sp):
            sp.dma_start(x_in, k.x_tok[:, :]).then_inc(kept, 16)
            sp.wait_ge(kept, 16)

    for layer in range(F1_DEPTH):
        l1_local_attention(k, layer)
        l1_geglu(k, layer, x_in)


def shifted(g, own, dst, xT, col, width):
    own.step(g.tensor_copy(dst[:, 0:width], xT[:, ds(col - 1, width)]))
    return g.tensor_copy(dst[0:64, 0:width], xT[0:64, ds(col, width)])


def l1_local_attention(k, layer):
    nc, d = k.nc, k.dram
    name = f"f1a{layer}"
    PAIRS_, T = F1_HEADS // 2, TPB
    R_LAG, LAG, RING = 2, 3, 4
    with ExitStack() as ctx:
        oT = k.sb(name + "_oT", [P, PAIRS_, B * L], ctx=ctx)
        with ExitStack() as c2:
            sb = lambda n, s: k.sb(name + n, s, ctx=c2)
            w = sb("_w", [P, 3 * F1_INNER])
            scales = sb("_scales", [P, 2, 2, F1_D])
            tab = sb("_tab", [P, 2, T, 2, F1_D])
            mask = sb("_mask", [P, 2, P])
            hs = sb("_h", [P, WINDOW + L])
            buf = sb("_buf", [P, 6, 1024])
            sq, qkn, t1 = buf[:, 0:2, :], buf[:, 2:4, :], buf[:, 4:6, :]
            probs, probsT = buf[:, 0:RING, :], buf[:, 4:6, :]
            ss = sb("_ss", [P, T, 16])
            root = sb("_root", [P, T, 16])
            rn = sb("_rn", [P, 2, 2, 16])
            qT = sb("_qT", [P, 2, PAIRS_, L])
            kT = sb("_kT", [P, PAIRS_, WINDOW + L])
            v = sb("_v", [P, 2, T, F1_INNER])
            nmax = sb("_nmax", [P, 2, F1_HEADS])
            rsum = sb("_rsum", [P, T, F1_HEADS])
            rinv = sb("_rinv", [P, T, F1_HEADS])
            sm = lambda n: k.sem(name + "_" + n, c2)
            w_loaded = sm("w_loaded")
            tab_ready = sm("tab_ready")
            cleared = sm("cleared")
            h_ready = Signal(sm("h_ready"), 2)
            qk_full = Signal(sm("qk_full"), T)
            qk_free = Signal(sm("qk_free"), T)
            v_full = Signal(sm("v_full"), 2 * T)
            v_ready = Signal(sm("v_ready"), 2 * T)
            squared = Signal(sm("squared"), T)
            summed = Signal(sm("summed"), T)
            rooted = Signal(sm("rooted"), T)
            inverse = Signal(sm("inverse"), 2 * T)
            first = Signal(sm("first"), T)
            second = Signal(sm("second"), T)
            roped = Signal(sm("roped"), T)
            r_full = Signal(sm("rope_turned"), 2 * T)
            r_done = Signal(sm("qkT_ready"), 2 * T)
            s_full = Signal(sm("scores_full"), T)
            s_free = Signal(sm("scores_taken"), T)
            max_ready = Signal(sm("max_ready"), T)
            e_full = Signal(sm("exp_done"), T)
            inv_ready = Signal(sm("inv_ready"), T)
            p_full = Signal(sm("probs_ready"), T)
            t_full = [Signal(sm(f"turned_full{i}"), T) for i in range(2)]
            t_done = [Signal(sm(f"turned_taken{i}"), T) for i in range(2)]
            o_full = Signal(sm("out_full"), T)
            o_free = Signal(sm("out_taken"), T)
            passed = sm("passed")
            block = c2.enter_context(nc.Block())
            plan = order(T, 0, T, LAG)

            def heads(t):
                return t.rearrange("p (a h e) -> p a h e", a=2, e=F1_D)

            def swapped(out, src, table):
                hf = F1_D // 2
                for lo, hi in ((0, hf), (hf, 0)):
                    yield (heads(out)[:, :, :, lo:lo + hf], heads(src)[:, :, :, hi:hi + hf],
                           table[:, :, lo:lo + hf].unsqueeze(2).broadcast_to([P, 2, F1_HEADS, hf]))

            @block.sync
            def _(sp):
                for out, src in ((tab[:, :, :, :, :], d["F1_xpos"]), (mask[:, :, :], d["F1_mask"]),
                                 (scales[:, :, :, :], d[f"F1_scales{layer}"].partition_broadcast(P)),
                                 (w[:, :], d["L1_ffn_wqkv"][layer, :, :])):
                    sp.dma_start(out, src).then_inc(w_loaded, 16)

            @block.gpsimd
            def _(pool):
                for s in (first, roped, p_full):
                    s.start(pool)
                nc.gpsimd.memset(kT[:, :, 0:WINDOW], 0.0)
                nc.gpsimd.memset(qT[:, :, :, :], 0.0).then_inc(cleared, 1)
                pool.wait_ge(cleared, 1)
                pool.wait_ge(tab_ready, 4)
                with pool.Fori(0, B) as b:
                    for t in range(T):
                        s = t % 2
                        pool.wait_ge(qk_free.sem, qk_free.at(b, t))
                        if t >= 2:
                            pool.wait_ge(r_full.sem, r_full.at(b, 2 * (t - 2) + 1))
                        for a in range(2):
                            ins = nc.gpsimd.tensor_tensor(
                                heads(t1[:, s, :])[:, a, :, :], heads(qkn[:, s, :])[:, a, :, :],
                                tab[:, 0, t, a, :].unsqueeze(1).broadcast_to([P, F1_HEADS, F1_D]), ALU.mult)
                        ins.then_inc(first.sem, 1)
                        pool.wait_ge(first.sem, first.at(b, t))
                        pool.wait_ge(second.sem, second.at(b, t))
                        nc.gpsimd.tensor_tensor(t1[:, s, :], t1[:, s, :], sq[:, s, :], ALU.add
                                                ).then_inc(roped.sem, 1)
                    for t in range(T):
                        pool.wait_ge(inv_ready.sem, inv_ready.at(b, t))
                        p3 = probs[:, t % RING, :].rearrange("p (h q) -> p h q", q=P)
                        nc.gpsimd.tensor_tensor(p3, p3, rinv[:, t, :].unsqueeze(2).broadcast_to([P, F1_HEADS, P]),
                                                ALU.mult).then_inc(p_full.sem, 1)

            @block.tensor
            def _(pe):
                for s in (qk_full, v_full, r_full, s_full, *t_full, o_full):
                    s.start(pe)
                pe.wait_ge(w_loaded, 64)
                pe.wait_ge(cleared, 1)
                with pe.Fori(0, B) as b:
                    for t in range(T + R_LAG):
                        if t < T:
                            if t % (T // 2) == 0:
                                pe.wait_ge(h_ready.sem, h_ready.at(b, t // (T // 2)))
                            f = qk_free if t >= 2 else s_free
                            pe.wait_ge(f.sem, f.at(b, t - 2))
                            own, before = (hs[:, c0:c0 + P] for c0 in (WINDOW + t * P, t * P))
                            for c in range(2):
                                mm = pe.matmul(k.ps_scores[t % 2][:, c * 512:(c + 1) * 512], own,
                                               w[:, c * 512:(c + 1) * 512], start=True, stop=True)
                            mm.then_inc(qk_full.sem, 1)
                            for i, h in enumerate((before, own)):
                                f, e = (v_ready, 2 * t - 2 + i) if t else (o_free, i - 2)
                                pe.wait_ge(f.sem, f.at(b, e))
                                pe.matmul(k.ps_out[i][:, :], h, w[:, 2 * F1_INNER:3 * F1_INNER],
                                          start=True, stop=True).then_inc(v_full.sem, 1)
                        if t >= R_LAG:
                            r = t - R_LAG
                            pe.wait_ge(roped.sem, roped.at(b, r))
                            for i in range(2):
                                if r:
                                    pe.wait_ge(r_done.sem, r_done.at(b, 2 * r - 2 + i))
                                else:
                                    pe.wait_ge(t_done[i].sem, t_done[i].at(b, -1))
                                for c in range(4):
                                    c0 = (4 * i + c) * P
                                    mm = pe.transpose(k.ps_turned[i][:, c * P:(c + 1) * P], t1[:, r % 2, c0:c0 + P],
                                                      k.ident[:, :])
                                mm.then_inc(r_full.sem, 1)
                    for what, t in plan:
                        if what == "S":
                            f, e = (s_free, t - 2) if t >= 2 else (qk_free, T - 2 + t)
                            pe.wait_ge(f.sem, f.at(b, e))
                            pe.wait_ge(r_done.sem, r_done.at(b, 2 * t + 1))
                            for h in range(F1_HEADS):
                                for win in range(2):
                                    q0 = t * P + win * WINDOW
                                    mm = pe.matmul(
                                        k.ps_scores[t % 2][win * WINDOW:(win + 1) * WINDOW, h * P:(h + 1) * P],
                                        qT[:, h % 2, h // 2, q0:q0 + WINDOW], kT[:, h // 2, q0:q0 + P],
                                        start=True, stop=True)
                            mm.then_inc(s_full.sem, 1)
                        elif what == "T":
                            pe.wait_ge(p_full.sem, p_full.at(b, t))
                            if t == 0:
                                for i in range(2):
                                    pe.wait_ge(r_done.sem, r_done.at(b, 2 * T - 2 + i))
                            turn(pe, k, probs[:, t % RING, :], t_full, t_done, b, t)
                        else:
                            for half in range(2):
                                pe.wait_ge(t_done[half].sem, t_done[half].at(b, t))
                            if t < 2:
                                pe.wait_ge(v_ready.sem, v_ready.at(b, 2 * T - 1))
                            else:
                                pe.wait_ge(o_free.sem, o_free.at(b, t - 2))
                            for pair in range(PAIRS_):
                                for win in range(2):
                                    for j in range(2):
                                        h = 2 * pair + j
                                        c0 = win * WINDOW
                                        mm = pe.matmul(
                                            k.ps_out[t % 2][j * F1_D:(j + 1) * F1_D,
                                                            pair * P + c0:pair * P + c0 + WINDOW],
                                            v[:, win, t, h * F1_D:(h + 1) * F1_D],
                                            probsT[:, t % 2, h * P + c0:h * P + c0 + WINDOW], start=True, stop=True)
                            mm.then_inc(o_full.sem, 1)

            @block.vector
            def _(dve):
                for s in (summed, inverse, qk_free, second, s_free, max_ready, inv_ready, t_done[1], o_free):
                    s.start(dve)
                dve.wait_ge(w_loaded, 64)
                for a in range(2):
                    for qk in range(2):
                        nc.vector.tensor_tensor(tab[:, a, :, qk, :], tab[:, a, :, qk, :],
                                                scales[:, a, qk, :].unsqueeze(1).broadcast_to([P, T, F1_D]),
                                                ALU.mult).then_inc(tab_ready, 1)
                dve.wait_ge(tab_ready, 4)
                with dve.Fori(0, B) as b:
                    own = Chain(dve, inverse, b)
                    for t in range(T + 1):
                        s = t % 2
                        if t < T:
                            dve.wait_ge(squared.sem, squared.at(b, t))
                            nc.vector.tensor_reduce(ss[:, t, :], sq[:, s, :].rearrange(
                                "p (h e) -> p h e", e=F1_D), AX.X, ALU.add).then_inc(summed.sem, 1)
                        if t:
                            u = t - 1
                            dve.wait_ge(summed.sem, summed.at(b, u))
                            for out, src, table in swapped(sq[:, u % 2, :], qkn[:, u % 2, :], tab[:, 1, u, :, :]):
                                for a in range(2):
                                    ins = nc.vector.tensor_tensor(out[:, a], src[:, a], table[:, a], ALU.mult)
                            ins.then_inc(second.sem, 1)
                        if t < T:
                            dve.wait_ge(rooted.sem, rooted.at(b, t))
                            own.step(nc.vector.tensor_scalar(rn[:, s, 0, :], root[:, t, :], 1e-12, None, ALU.max))
                            own.step(nc.vector.reciprocal(rn[:, s, 1, :], rn[:, s, 0, :]))
                            if t >= 2:
                                dve.wait_ge(first.sem, first.at(b, t - 2))
                            nc.vector.tensor_tensor(
                                qkn[:, s, :].rearrange("p (h e) -> p h e", e=F1_D),
                                k.ps_scores[s][:, :].rearrange("p (h e) -> p h e", e=F1_D),
                                rn[:, s, 1, :].unsqueeze(2).broadcast_to([P, 16, F1_D]), ALU.mult
                                ).then_inc(qk_free.sem, 1)
                            dve.wait_ge(qk_free.sem, qk_free.at(b, t))
                    dve.wait_ge(roped.sem, roped.at(b, T - 1))
                    for what, t in plan:
                        if what == "S":
                            dve.wait_ge(s_full.sem, s_full.at(b, t))
                            if t >= RING:
                                dve.wait_ge(t_full[1].sem, t_full[1].at(b, t - RING))
                            p3 = probs[:, t % RING, :].rearrange("p (h q) -> p h q", q=P)
                            nc.vector.tensor_tensor(
                                p3, k.ps_scores[t % 2][:, :].rearrange("p (h q) -> p h q", q=P),
                                mask[:, min(t, 1):min(t, 1) + 1, :].broadcast_to([P, F1_HEADS, P]), ALU.add
                                ).then_inc(s_free.sem, 1)
                            dve.wait_ge(s_free.sem, s_free.at(b, t))
                            nc.vector.tensor_reduce(nmax[:, t % 2, :], p3, AX.X, ALU.max, negate=True
                                                    ).then_inc(max_ready.sem, 1)
                        if what == "S" and t >= 1 or what == "T" and t == T - LAG:
                            u = t - 1 if what == "S" else T - 1
                            dve.wait_ge(e_full.sem, e_full.at(b, u))
                            nc.vector.reciprocal(rinv[:, u, :], rsum[:, u, :]).then_inc(inv_ready.sem, 1)
                        if what == "T":
                            take_turned(nc.vector, k, probsT[:, t % 2, :], t_full, t_done, b, t, 1)
                        elif what == "V":
                            dve.wait_ge(o_full.sem, o_full.at(b, t))
                            nc.vector.tensor_scalar(oT[:, :, ds(b * L + t * P, P)],
                                                    k.ps_out[t % 2][:, :].rearrange("p (c q) -> p c q", q=P), 1.0,
                                                    None, ALU.mult).then_inc(o_free.sem, 1)

            @block.scalar
            def _(act):
                for s in (h_ready, squared, rooted, r_done, v_ready, e_full, t_done[0]):
                    s.start(act)
                with act.Fori(0, B) as b:
                    act.wait_ge(v_full.sem, v_full.at(b, -1))
                    act.sem_inc(passed, 1)
                    edges = (0, WINDOW + L // 2, WINDOW + L)
                    for half in range(2):
                        c0, c1 = edges[half:half + 2]
                        for lo in (0, 64):
                            at = b * XB + (PAD - WINDOW - lo // 64 + c0)
                            ins = nc.scalar.activation(hs[lo:lo + 64, c0:c1], k.xT[lo:lo + 64, ds(at, c1 - c0)],
                                                       ACT.Copy)
                        ins.then_inc(h_ready.sem, 1)
                    for t in range(T + R_LAG):
                        if t < T:
                            act.wait_ge(qk_full.sem, qk_full.at(b, t))
                            if t >= 2:
                                act.wait_ge(roped.sem, roped.at(b, t - 2))
                            nc.scalar.activation(sq[:, t % 2, :], k.ps_scores[t % 2][:, :], ACT.Square
                                                 ).then_inc(squared.sem, 1)
                            for i in range(2):
                                act.wait_ge(v_full.sem, v_full.at(b, 2 * t + i))
                                nc.scalar.copy(v[:, i, t, :], k.ps_out[i][:, :]).then_inc(v_ready.sem, 1)
                                if i == 0:
                                    act.wait_ge(summed.sem, summed.at(b, t))
                                    nc.scalar.activation(root[:, t, :], ss[:, t, :], ACT.Sqrt
                                                         ).then_inc(rooted.sem, 1)
                        if t >= R_LAG:
                            r = t - R_LAG
                            act.wait_ge(r_full.sem, r_full.at(b, 2 * r))
                            for j in range(2):
                                rows = slice(j * F1_D, (j + 1) * F1_D)
                                ins = nc.scalar.copy(qT[rows, j, :, r * P:(r + 1) * P],
                                                     k.ps_turned[0][rows, :].rearrange("p (c q) -> p c q", q=P))
                            ins.then_inc(r_done.sem, 1)
                            act.wait_ge(r_full.sem, r_full.at(b, 2 * r + 1))
                            nc.scalar.copy(kT[:, :, WINDOW + r * P:WINDOW + (r + 1) * P],
                                           k.ps_turned[1][:, :].rearrange("p (c q) -> p c q", q=P)
                                           ).then_inc(r_done.sem, 1)
                    for what, t in plan:
                        if what == "S":
                            act.wait_ge(max_ready.sem, max_ready.at(b, t))
                            for h in range(F1_HEADS):
                                p1 = probs[:, t % RING, h * P:(h + 1) * P]
                                ins = nc.scalar.activation(p1, p1, ACT.Exp, bias=nmax[:, t % 2, h:h + 1],
                                                           accum_out=rsum[:, t, h:h + 1])
                            ins.then_inc(e_full.sem, 1)
                        elif what == "T":
                            take_turned(nc.scalar, k, probsT[:, t % 2, :], t_full, t_done, b, t, 0)

        wo = k.sb(name + "_wo", [P, 4, C], ctx=ctx)
        project_turned(k, name + "o", range(NG), 4, lambda c, t: oT[:, c, t * P:(t + 1) * P], wo[:, :, :],
                       d["F1_wo"][layer, :, :, :], None, None, normed=False)


def l1_geglu(k, layer, x_in):
    nc, d = k.nc, k.dram
    name = f"f1g{layer}"
    last = layer == F1_DEPTH - 1
    CH, HALVES = 3, NG // B
    with ExitStack() as ctx:
        sb = lambda n, s: k.sb(name + n, s, ctx=ctx)
        sem = lambda n: k.sem(name + n, ctx)
        w1 = sb("_w1", [P, 2 * F1_HID])
        w2 = sb("_w2", [P, CH, C])
        cols = sb("_cols", [P, 8])
        b2 = sb("_b2", [1, C])
        hs = sb("_h", [P, 2, 512])
        hn = sb("_hn", [P, 2, 512])
        hT = sb("_hT", [P, 2, 512])
        stats = sb("_stats", [P, 2, GROUP, 6])
        mv = sb("_mv", [P, 2, GROUP, 2])
        rs = sb("_rs", [P, 2, 3, GROUP])
        gate = sb("_gate", [P, 2, 512])
        hid = sb("_hid", [P, 2, CH, 512])
        x0 = sb("_x_in", [P, TILES * C]) if last else None
        w_loaded, x_loaded = sem("_w_loaded"), sem("_x_loaded")
        own_pool = Signal(sem("_own_pool"), HALVES)
        h_ready = Signal(sem("_h_ready"), HALVES)
        ht_full = Signal(sem("_ht_full"), HALVES)
        var = Signal(sem("_var"), HALVES)
        root = Signal(sem("_root"), HALVES)
        hn_ready = Signal(sem("_hn_ready"), HALVES)
        hb_full = Signal(sem("_hb_full"), HALVES)
        hT_ready = Signal(sem("_hT_ready"), HALVES)
        per = HALVES * CH // 2
        u_full = [Signal(sem(f"_u_full{i}"), per) for i in range(2)]
        gate_ready = Signal(sem("_gate_ready"), HALVES * CH)
        hid_ready = [Signal(sem(f"_hid_ready{i}"), per) for i in range(2)]
        passed = sem("_passed")
        own = Signal(sem("_own_dve"), HALVES * ((Norm.DVE_STEPS + 1 if last else 1) + 12))
        norm = Norm(k, ctx, name + "n", HALVES)
        block = ctx.enter_context(nc.Block())

        @block.sync
        def _(sp):
            for out, src in ((w1, d["L1_ffn_w1"][layer, :, :]), (cols, d["F1_cols"][layer, :, :]),
                             (b2, d["L1_ffn_b2"][layer:layer + 1, :])):
                sp.dma_start(out[:, :], src).then_inc(w_loaded, 16)
            sp.dma_start(w2[:, :, :], d["F1_w2"][layer, :, :, :]).then_inc(w_loaded, 16)
            if last:
                sp.dma_start(x0[:, :], x_in).then_inc(x_loaded, 16)

        @block.gpsimd
        def _(pool):
            h_ready.start(pool)
            own_pool.start(pool)
            with pool.Fori(0, B) as b:
                chain = Chain(pool, own_pool, b)
                for g in range(HALVES):
                    pool.wait_ge(ht_full.sem, ht_full.at(b, g - HALVES))
                    shifted(nc.gpsimd, chain, hs[:, g, :], k.xT, b * XB + PAD + g * 512, 512).then_inc(h_ready.sem, 1)

        @block.tensor
        def _(pe):
            norm.start(pe, None, None)
            for s in (ht_full, hb_full, *u_full):
                s.start(pe)
            pe.wait_ge(w_loaded, 64)
            with pe.Fori(0, B) as b:
                for g in range(HALVES):
                    pe.wait_ge(h_ready.sem, h_ready.at(b, g))
                    pe.wait_ge(norm.xT_ready.sem, norm.xT_ready.at(b, -1))
                    for i in range(GROUP):
                        mm = pe.transpose(k.ps_turned[g][:, i * P:(i + 1) * P], hs[:, g, i * P:(i + 1) * P],
                                          k.ident[:, :])
                    mm.then_inc(ht_full.sem, 1)
                for g in range(HALVES):
                    pe.wait_ge(hn_ready.sem, hn_ready.at(b, g))
                    for i in range(GROUP):
                        mm = pe.transpose(k.ps_turned[g][:, i * P:(i + 1) * P], hn[:, g, i * P:(i + 1) * P],
                                          k.ident[:, :])
                    mm.then_inc(hb_full.sem, 1)
                for g in range(HALVES):
                    pe.wait_ge(hT_ready.sem, hT_ready.at(b, g))
                    for c in range(CH):
                        n = g * CH + c
                        pe.wait_ge(hid_ready[n % 2].sem, hid_ready[n % 2].at(b, n // 2 - 1))
                        for part in range(2):
                            c0 = part * F1_HID + c * P
                            mm = pe.matmul(k.ps_scores[n % 2][0:F1_ROWS[c], part * 512:(part + 1) * 512],
                                           w1[:, c0:c0 + F1_ROWS[c]], hT[:, g, :], start=True, stop=True)
                        mm.then_inc(u_full[n % 2].sem, 1)
                for g in range(HALVES):
                    y = k.ps_out[g]
                    pe.wait_ge(norm.y_free.sem, norm.y_free.at(b, g - 2))
                    for c in range(CH):
                        n = g * CH + c
                        pe.wait_ge(hid_ready[n % 2].sem, hid_ready[n % 2].at(b, n // 2))
                        for i in range(GROUP):
                            pe.matmul(y[:, i * C:(i + 1) * C], hid[0:F1_ROWS[c], g, c, i * P:(i + 1) * P],
                                      w2[0:F1_ROWS[c], c, :], start=(c == 0 and i == 0), stop=False,
                                      skip_group_check=True)
                    for i in range(GROUP):
                        mm = pe.matmul(y[:, i * C:(i + 1) * C], k.ones[0:1, 0:P], b2[:, :], start=False,
                                       stop=i == GROUP - 1, skip_group_check=True)
                    mm.then_inc(norm.y_full.sem, 1)
                for g in range(HALVES):
                    norm.tensor(pe, b, g, g, k.ps_turned[0])

        @block.scalar
        def _(act):
            norm.start(None, None, act)
            for s in (root, hT_ready, gate_ready):
                s.start(act)
            with act.Fori(0, B) as b:
                for g in range(HALVES):
                    act.wait_ge(var.sem, var.at(b, g))
                    nc.scalar.activation(rs[:, g, 1, :], rs[:, g, 0, :], ACT.Sqrt).then_inc(root.sem, 1)
                for g in range(HALVES):
                    act.wait_ge(hb_full.sem, hb_full.at(b, g))
                    nc.scalar.activation(hT[:, g, :], k.ps_turned[g][:, :], ACT.Identity, bias=cols[:, 1:2],
                                         scale=cols[:, 0:1]).then_inc(hT_ready.sem, 1)
                for g in range(HALVES):
                    for c in range(CH):
                        n = g * CH + c
                        act.wait_ge(u_full[n % 2].sem, u_full[n % 2].at(b, n // 2))
                        act.wait_ge(hid_ready[n % 2].sem, hid_ready[n % 2].at(b, n // 2 - 1))
                        nc.scalar.activation(gate[0:F1_ROWS[c], n % 2, :],
                                             k.ps_scores[n % 2][0:F1_ROWS[c], 512:1024], ACT.Gelu,
                                             bias=cols[0:F1_ROWS[c], 5 + c:6 + c]).then_inc(gate_ready.sem, 1)
                if last:
                    for g in range(HALVES):
                        norm.scalar_root(act, b, g, g)
                for g in range(HALVES):
                    norm.scalar_store(act, b, g, k.ps_turned[0], b * XB + PAD + g * 512)

        @block.vector
        def _(dve):
            norm.start(None, dve, None)
            for s in (var, hn_ready, *hid_ready, own):
                s.start(dve)
            if last:
                dve.wait_ge(x_loaded, 16)
            with dve.Fori(0, B) as b:
                chain = Chain(dve, own, b)
                for g in range(HALVES):
                    dve.wait_ge(ht_full.sem, ht_full.at(b, g))
                    dve.sem_inc(passed, 1)
                    for i in range(GROUP):
                        chain.done(nc.vector.bn_stats(stats[:, g, i, :], k.ps_turned[g][:, i * P:(i + 1) * P]))
                    chain.wait_apart(passed)
                    for i in range(GROUP):
                        chain.done(nc.vector.bn_aggr(mv[:, g, i, :], stats[:, g, i, :]))
                    chain.wait()
                    nc.vector.tensor_scalar(rs[:, g, 0, :], mv[:, g, :, 1], EPS, None, ALU.add).then_inc(var.sem, 1)
                for g in range(HALVES):
                    dve.wait_ge(root.sem, root.at(b, g))
                    chain.step(nc.vector.reciprocal(rs[:, g, 2, :], rs[:, g, 1, :]))
                    for i in range(GROUP):
                        ins = nc.vector.tensor_scalar(hn[:, g, i * C:(i + 1) * C],
                                                      k.ps_turned[g][:, i * P:(i + 1) * P], mv[:, g, i, 0:1],
                                                      rs[:, g, 2, i:i + 1], ALU.subtract, ALU.mult)
                        if i < GROUP - 1:
                            chain.done(ins)
                    ins.then_inc(hn_ready.sem, 1)
                for g in range(HALVES):
                    for c in range(CH):
                        n = g * CH + c
                        r = F1_ROWS[c]
                        dve.wait_ge(gate_ready.sem, gate_ready.at(b, n))
                        nc.vector.scalar_tensor_tensor(hid[0:r, g, c, :], k.ps_scores[n % 2][0:r, 0:512],
                                                       cols[0:r, 2 + c:3 + c], gate[0:r, n % 2, :], ALU.add,
                                                       ALU.mult).then_inc(hid_ready[n % 2].sem, 1)
                for g in range(HALVES):
                    tile0 = b * TPB + g * GROUP
                    norm.vector(dve, chain, b, g, g, tile0, k.ps_out[g][:, :], normed=last,
                                also=x0[:, ds(tile0 * C, 512)] if last else None)
                chain.close()



def small_head_attention(k, name, inputs, causal, denom, wo_dram, bo_dram):
    nc, d = k.nc, k.dram
    H, D = 16, 8
    SET_PAIRS = 2
    PAIRS_ALL = B * H // 2
    SETS = PAIRS_ALL // SET_PAIRS
    STEPS = 2 * TPB
    LEADS = TPB // 2
    steps = [(0, n) for n in range(LEADS)]
    for n in range(TPB - LEADS):
        steps += [(1, n), (0, LEADS + n)]
    steps += [(1, n) for n in range(TPB - LEADS, TPB)]
    step_of = {s: m for m, s in enumerate(steps)}
    v_slot = lambda kb: step_of[1, 0] + 2 + 2 * kb
    MAX_ROW, PARTS = 96, 3
    scratch = [nc.dram_tensor(f"{name}_parts_{i}", (PARTS, B * P, L), BF16, kind="Internal").ap() for i in "qk"]
    with ExitStack() as ctx:
        sb = lambda n, s, dt=F32: k.sb(name + n, s, dt, ctx=ctx)
        w = sb("_w", [P, 3 * C])
        wo, bo = sb("_wo", [P, 1, C]), sb("_bo", [1, C])
        extra = sb("_extra", [P, 1])
        tri = sb("_tri", [P, 512])
        tile_rows = sb("_tile_rows", [P, TPB])
        gather = sb("_gather", [P, 4, P + 96])
        v = sb("_v", [P, B * C, TPB])
        acc = sb("_acc", [P, SETS, 512])
        oT = sb("_oT", [P, B * L])
        with ExitStack() as c2:
            loaded, full, taken, own, split, moved = (k.sem(name + "p_" + n, c2) for n in (
                "loaded", "full", "taken", "own", "split", "moved"))
            raw = k.sb(name + "_raw", [P, 2, 512], ctx=c2)
            rest = k.sb(name + "_rest", [P, 2, 2, 512], ctx=c2)
            parts = k.sb(name + "_parts", [P, 2, PARTS, B * L], BF16, ctx=c2)
            block = c2.enter_context(nc.Block())
            jobs = [(kind, i) for i in range(NG) for kind in range(2)] + [(2, i) for i in range(NG)]

            @block.sync
            def _(sp):
                sp.dma_start(w[:, :], d[inputs]).then_inc(loaded, 16)
                if denom is not None:
                    sp.dma_start(extra[:, :], d[denom]).then_inc(loaded, 16)
                sp.dma_start(tile_rows[:, :], d["tile_rows"]).then_inc(moved, 16)
                sp.dma_start(gather[:, :, :], d["gather"]).then_inc(moved, 16)
                for b in range(B):
                    for i in range(2):
                        sp.wait_ge(split, 4 * (2 * (2 * b + 1) + i + 1))
                        sp.dma_start(scratch[i][:, b * P:(b + 1) * P, :].rearrange("s p t -> p s t"),
                                     parts[:, i, :, b * L:(b + 1) * L]).then_inc(moved, 16)
                sp.wait_ge(moved, 96)

            @block.gpsimd
            def _(pool):
                if denom is None:
                    nc.gpsimd.memset(extra[:, :], 1e-8).then_inc(own, 1)
                if causal:
                    nc.gpsimd.memset(tri[:, :], 0.0).then_inc(own, 1)
                    pool.wait_ge(own, 1)
                    nc.gpsimd.affine_select(out=tri[:, :], in_=tri[:, :], compare_op=ALU.is_ge, fill=HUGE,
                                            base=3 * P, pattern=[[-1, 512]], channel_multiplier=1).then_inc(own, 1)
                    pool.wait_ge(own, 2)
                pool.wait_ge(own, 1)

            @block.tensor
            def _(pe):
                pe.wait_ge(loaded, 16 if denom is None else 32)
                for n, (kind, i) in enumerate(jobs):
                    bank = k.ps_out[n % 2]
                    if n >= 2:
                        pe.wait_ge(taken, n - 1)
                    if kind < 2:
                        mm = pe.matmul(bank[:, :], w[:, kind * C:(kind + 1) * C], k.xT[:, xcol(i):xcol(i) + 512],
                                       start=True, stop=True)
                    else:
                        for t in range(GROUP):
                            c0 = xcol(i) + t * P
                            mm = pe.matmul(bank[:, t * C:(t + 1) * C], k.xT[:, c0:c0 + P], w[:, 2 * C:3 * C],
                                           start=True, stop=True)
                    mm.then_inc(full, 1)

            @block.scalar
            def _(act):
                for n, (kind, i) in enumerate(jobs):
                    act.wait_ge(full, n + 1)
                    bank = k.ps_out[n % 2][:, :]
                    if kind < 2:
                        if n >= 2:
                            act.wait_ge(split, 4 * (n - 1))
                        nc.scalar.activation(raw[:, n % 2, :], bank, ACT.Copy,
                                             scale=-float(D ** -0.5) if kind == 0 else 1.0).then_inc(taken, 1)
                    else:
                        b, t0 = i // 2, (i % 2) * GROUP
                        nc.scalar.copy(v[:, b * C:(b + 1) * C, t0:t0 + GROUP],
                                       bank.rearrange("p (t c) -> p c t", c=C)).then_inc(taken, 1)
                if denom is not None:
                    act.wait_ge(loaded, 32)
                    nc.scalar.activation(extra[:, :], extra[:, :], ACT.Exp).then_inc(taken, 1)
                act.wait_ge(taken, len(jobs) + (denom is not None))

            @block.vector
            def _(dve):
                own_ = Count(dve, split)
                for n, (kind, i) in enumerate(jobs[:2 * NG]):
                    dve.wait_ge(taken, n + 1)
                    c = slice(i * 512, (i + 1) * 512)
                    x, r = raw[:, n % 2, :], rest[:, n % 2, :, :]
                    own_.step(nc.vector.tensor_copy(parts[:, kind, 0, c], x))
                    own_.step(nc.vector.tensor_tensor(r[:, 0, :], x, parts[:, kind, 0, c], ALU.subtract))
                    own_.step(nc.vector.tensor_copy(parts[:, kind, 1, c], r[:, 0, :]))
                    own_.step(nc.vector.tensor_tensor(parts[:, kind, 2, c], r[:, 0, :], parts[:, kind, 1, c],
                                                      ALU.subtract))

        with ExitStack() as c2:
            sb = lambda n, s, dt=F32: k.sb(name + n, s, dt, ctx=c2)
            qs = sb("_q_rows", [P, 2, 2, L], BF16)
            ks = sb("_k_rows", [P, 2, 2, L], BF16)
            zeros = sb("_zeros", [P, L], BF16)
            vz = sb("_v_pair", [P, 2, 2, TPB, 32])
            pT = sb("_probs_T", [P, STEPS, L])
            junk = sb("_junk", [P, 512])
            mins = sb("_mins", [P, 2, 2, TPB])
            low = sb("_lowest", [P, 2, 2, TPB])
            low_b = sb("_low_bf16", [P, 2, 2, TPB], BF16)
            low_p = sb("_low_parts", [P, 2, PARTS * TPB])
            sm = lambda n: k.sem(name + "a_" + n, c2)

            pieces = []
            for qt in range(TPB):
                seen = (qt + 1) * P if causal else L
                pieces += [(qt, c, min(512, seen - c)) for c in range(0, seen, 512)]
            per_head = len(pieces)
            last_piece = {qt: max(i for i, p in enumerate(pieces) if p[0] == qt) for qt in range(TPB)}
            first_query = (lambda kb: kb * P) if causal else (lambda kb: 0)

            cleared = sm("cleared")
            rows_ready = [[Signal(sm(f"rows_ready{par}{j}"), 7, 16) for j in range(2)] for par in range(2)]
            s_full = [Signal(sm(f"s_full{i}"), per_head) for i in range(2)]
            min_ready = Signal(sm("min_ready"), 2 * per_head)
            lowest = Signal(sm("lowest"), 2)
            low_ready = Signal(sm("low_ready"), 12)
            turned = Signal(sm("low_turned"), 2)
            max_rows = Signal(sm("max_rows"), 2)
            r_full = [Signal(sm(f"r_full{i}"), TPB) for i in range(2)]
            e_full = Signal(sm("exp_done"), STEPS)
            cut = Signal(sm("cut"), STEPS)
            v_ready = Signal(sm("v_ready"), 1)
            v_done = Signal(sm("v_done"), TPB)
            acc_free = Signal(sm("acc_taken"), 1)
            passed, passed_dve = sm("passed"), sm("passed_dve")
            block = c2.enter_context(nc.Block())
            s_bank, r_slot, acc_bank, low_bank = k.ps_turned, k.ps_scores, k.ps_out[0], k.ps_out[1]

            def turn_plan(scores, values, before):
                out = []
                for n in range(STEPS):
                    if scores:
                        out += [("S", n // TPB, (n % TPB, 0))]
                        out += {TPB: [("split", 0, 0)], TPB + 1: [("turn", 0, 0)], TPB + 2: [("rows", 0, 0)]}.get(n, [])
                    if values:
                        out += {0: [("split", 1, 1)], 1: [("turn", 1, 1)], 2: [("rows", 1, 1)]}.get(n, [])
                        out += [("R", 1, n)]
                    if scores:
                        out += [("S", n // TPB, (n % TPB, 1))]
                    for kb in range(TPB):
                        if values and v_slot(kb) == n:
                            out += [("V", 1, kb)]
                        if before and v_slot(kb) == n + STEPS:
                            out += [("V", 2, kb)]
                return out

            def turns(eng, body):
                body(0, 0, turn_plan(True, False, False))
                body(0, 1, turn_plan(True, True, False))
                with eng.Fori(1, SETS) as s:
                    body(s, 0, turn_plan(True, True, True))
                    body(s, 1, turn_plan(True, True, True))
                body(SETS, 0, turn_plan(False, True, True))
                body(SETS, 1, turn_plan(False, False, True))

            def pair(s, par, back=0):
                return s * 2 + (par - back)

            @block.sync
            def _(sp):
                for par in range(2):
                    for j in range(2):
                        rows_ready[par][j].start(sp)
                sp.wait_ge(cleared, 3)

                def load(s, par):
                    for j in range(2):
                        if not isinstance(s, int):
                            m = step_of[j, TPB - 1]
                            f = r_full[m % 2]
                            sp.wait_ge(f.sem, f.at(pair(s, par, 2), m // 2))
                        r0 = s * (4 * D) + (2 * par + j) * D
                        done = rows_ready[par][j].sem
                        sp.dma_start(qs[MAX_ROW:P, par, j, :], zeros[MAX_ROW:P, :]).then_inc(done, 16)
                        for i in range(PARTS):
                            block_rows = slice(PARTS * i * D, PARTS * (i + 1) * D)
                            q_rows = scratch[0][i, ds(r0, D), :].unsqueeze(0).broadcast_to([PARTS, D, L])
                            sp.dma_start(qs[block_rows, par, j, :], q_rows).then_inc(done, 16)
                            sp.dma_start(ks[block_rows, par, j, :], scratch[1][:, ds(r0, D), :]).then_inc(done, 16)

                load(0, 0)
                load(0, 1)
                with sp.Fori(1, SETS) as s:
                    load(s, 0)
                    load(s, 1)

            @block.gpsimd
            def _(pool):
                for s in (low_ready, cut, v_ready):
                    s.start(pool)
                nc.gpsimd.memset(mins[:, :, :, :], HUGE)
                nc.gpsimd.memset(qs[:, :, :, :], 0.0)
                nc.gpsimd.memset(zeros[:, :], 0.0)
                for par in range(2):
                    nc.gpsimd.memset(vz[:, par, :, :, :], 0.0)
                nc.gpsimd.memset(ks[:, :, :, :], 0.0).then_inc(cleared, 1)
                pool.wait_ge(cleared, 1)
                for par in range(2):
                    ins = nc.gpsimd.memset(vz[:, par, :, :, 16 * par + D:16 * par + 2 * D], 1.0)
                ins.then_inc(cleared, 1)
                pool.wait_ge(cleared, 2)
                nc.gpsimd.memset(ks[MAX_ROW:P, :, :, :], -1.0).then_inc(cleared, 1)
                pool.wait_ge(cleared, 3)

                def body(s, par, plan):
                    if ("R", 1, 0) in plan:
                        c = (par - 1) % 2
                        p = pair(s, par, 1)
                        if not isinstance(s, int) or p >= 2:
                            pool.wait_ge(v_done.sem, v_done.at(pair(s, par, 3), TPB - 1))
                            pool.sem_inc(passed, 1)
                        for j in range(2):
                            at = p * (2 * D) + j * D
                            ins = nc.gpsimd.tensor_copy(
                                vz[:, c, j, :, 16 * c:16 * c + D].rearrange("p t d -> p d t"), v[:, ds(at, D), :])
                        ins.then_inc(v_ready.sem, 1)
                    for what, x, n in plan:
                        if what == "split":
                            p = pair(s, par, n)
                            j = x
                            pool.wait_ge(lowest.sem, lowest.at(p, j))
                            chain = Chain(pool, low_ready, p)
                            chain.n = 6 * j
                            lo, lb, lp = low[:, j, :, :], low_b[:, j, :, :], low_p[:, j, :]
                            g, one = nc.gpsimd, k.ones[:, 0:TPB]
                            chain.step(g.tensor_tensor(lb[:, 0, :], lo[:, 0, :], one, ALU.mult))
                            chain.step(g.tensor_tensor(lp[:, 0:TPB], lb[:, 0, :], one, ALU.mult))
                            chain.step(g.tensor_tensor(lo[:, 1, :], lo[:, 0, :], lp[:, 0:TPB], ALU.subtract))
                            chain.step(g.tensor_tensor(lb[:, 1, :], lo[:, 1, :], one, ALU.mult))
                            chain.step(g.tensor_tensor(lp[:, TPB:2 * TPB], lb[:, 1, :], one, ALU.mult))
                            chain.done(g.tensor_tensor(lp[:, 2 * TPB:], lo[:, 1, :], lp[:, TPB:2 * TPB],
                                                       ALU.subtract))
                        elif what == "R" and causal:
                            kb = steps[n][1]
                            pool.wait_ge(e_full.sem, e_full.at(pair(s, par, 1), n))
                            pool.sem_inc(passed, 1)
                            diag = pT[:, n, kb * P:(kb + 1) * P]
                            nc.gpsimd.affine_select(out=diag, in_=diag, compare_op=ALU.is_ge, fill=0.0, base=0,
                                                    pattern=[[1, P]], channel_multiplier=-1).then_inc(cut.sem, 1)

                turns(pool, body)

            @block.tensor
            def _(pe):
                for s in (*s_full, turned, *r_full, v_done):
                    s.start(pe)
                pe.wait_ge(cleared, 3)

                def body(s, par, plan):
                    for what, x, n in plan:
                        if what == "S":
                            j, (qt, half) = x, n
                            p = pair(s, par)
                            if qt == 0 and half == 0:
                                r = rows_ready[par][j]
                                pe.wait_ge(r.sem, r.at(s, 6))
                            for i, (t, c, width) in enumerate(pieces):
                                if (t, c // 512) != (qt, half):
                                    continue
                                e = j * per_head + i
                                pe.wait_ge(min_ready.sem, min_ready.at(p, e - 2))
                                pe.matmul(s_bank[e % 2][:, 0:width], qs[0:P, par, j, qt * P:(qt + 1) * P],
                                          ks[0:P, par, j, c:c + width], start=True, stop=True
                                          ).then_inc(s_full[e % 2].sem, 1)
                        elif what == "turn":
                            p, j = pair(s, par, n), x
                            pe.wait_ge(low_ready.sem, low_ready.at(p, 6 * j + 5))
                            pe.transpose(low_bank[0:PARTS * TPB, j * P:(j + 1) * P], low_p[:, j, :],
                                         k.ident[:, :]).then_inc(turned.sem, 1)
                        elif what == "R":
                            p, c = pair(s, par, 1), (par - 1) % 2
                            j, kb = steps[n]
                            if kb == 0:
                                pe.wait_ge(max_rows.sem, max_rows.at(p, j))
                            pe.wait_ge(e_full.sem, e_full.at(p, n - 2))
                            for half in range(2):
                                c0 = max(first_query(kb), half * 512)
                                if c0 < (half + 1) * 512:
                                    mm = pe.matmul(r_slot[n % 2][:, c0:(half + 1) * 512],
                                                   ks[:, c, j, kb * P:(kb + 1) * P], qs[:, c, j, c0:(half + 1) * 512],
                                                   start=True, stop=True)
                            mm.then_inc(r_full[n % 2].sem, 1)
                        elif what == "V":
                            p, c, kb = pair(s, par, x), (par - x) % 2, n
                            if kb == 0:
                                pe.wait_ge(v_ready.sem, v_ready.at(p, 0))
                                if c == 0:
                                    set_ = s if par == 1 else s - 1
                                    pe.wait_ge(acc_free.sem, acc_free.at(set_, -1))
                            ready = cut if causal else e_full
                            pe.wait_ge(ready.sem, ready.at(p, step_of[1, kb]))
                            for j in range(2):
                                for half in range(2):
                                    c0 = max(first_query(kb), half * 512)
                                    if c0 < (half + 1) * 512:
                                        g = 2 * j + half
                                        mm = pe.matmul(acc_bank[32 * g:32 * g + 32, c0 - half * 512:512],
                                                       vz[:, c, j, kb, :],
                                                       pT[:, step_of[j, kb], c0:(half + 1) * 512],
                                                       start=c == 0 and kb == 0, stop=c == 1 and kb == TPB - 1,
                                                       skip_group_check=True)
                            mm.then_inc(v_done.sem, 1)

                turns(pe, body)

            @block.vector
            def _(dve):
                for s in (min_ready, lowest, max_rows):
                    s.start(dve)
                dve.wait_ge(cleared, 3)

                def body(s, par, plan):
                    for what, x, n in plan:
                        if what == "S":
                            j, (qt, half) = x, n
                            p = pair(s, par)
                            for i, (t, c, width) in enumerate(pieces):
                                if (t, c // 512) != (qt, half):
                                    continue
                                e = j * per_head + i
                                f = s_full[e % 2]
                                dve.wait_ge(f.sem, f.at(p, e // 2))
                                bank = s_bank[e % 2][:, 0:width]
                                low_ = mins[:, j, c // 512, qt:qt + 1]
                                if causal and i == last_piece[qt]:
                                    dve.wait_ge(min_ready.sem, min_ready.at(p, e - 1))
                                    dve.sem_inc(passed_dve, 1)
                                    ins = nc.vector.tensor_tensor_reduce(
                                        junk[:, 0:width], bank, tri[:, 512 - width:512], 1.0, HUGE, ALU.add,
                                        ALU.min, low_)
                                else:
                                    ins = nc.vector.tensor_reduce(low_, bank, AX.X, ALU.min)
                                ins.then_inc(min_ready.sem, 1)
                        elif what == "split":
                            p, j = pair(s, par, n), x
                            dve.wait_ge(min_ready.sem, min_ready.at(p, (j + 1) * per_head - 1))
                            nc.vector.tensor_tensor(low[:, j, 0, :], mins[:, j, 0, :], mins[:, j, 1, :], ALU.min
                                                    ).then_inc(lowest.sem, 1)
                        elif what == "rows":
                            p, c, j = pair(s, par, n), (par - n) % 2, x
                            dve.wait_ge(turned.sem, turned.at(p, j))
                            rows = PARTS * TPB
                            nc.vector.tensor_tensor(
                                qs[MAX_ROW:MAX_ROW + rows, c, j, :].rearrange("p (t q) -> p t q", q=P),
                                low_bank[0:rows, j * P:(j + 1) * P].unsqueeze(1).broadcast_to([rows, TPB, P]),
                                tile_rows[0:rows, :].unsqueeze(2).broadcast_to([rows, TPB, P]), ALU.mult
                                ).then_inc(max_rows.sem, 1)

                turns(dve, body)

            @block.scalar
            def _(act):
                for s in (e_full, acc_free):
                    s.start(act)

                def body(s, par, plan):
                    for what, x, n in plan:
                        if what == "R":
                            p, kb = pair(s, par, 1), steps[n][1]
                            f = r_full[n % 2]
                            act.wait_ge(f.sem, f.at(p, n // 2))
                            c0 = first_query(kb)
                            nc.scalar.activation(pT[:, n, c0:L], r_slot[n % 2][:, c0:L], ACT.Exp, scale=-1.0
                                                 ).then_inc(e_full.sem, 1)
                        elif what == "V" and (par - x) % 2 == 1 and n == TPB - 1:
                            act.wait_ge(v_done.sem, v_done.at(pair(s, par, x), n))
                            nc.scalar.copy(acc[:, ds(s - 1, 1), :],
                                           acc_bank[:, :].rearrange("p (o c) -> p o c", o=1)
                                           ).then_inc(acc_free.sem, 1)

                turns(act, body)

        with ExitStack() as c2:
            full, used, ready = (k.sem(name + "g_" + n, c2) for n in ("gathered", "used", "inverse"))
            den = k.sb(name + "_den", [P, 2, 512], ctx=c2)
            block = c2.enter_context(nc.Block())
            PER = SETS // B

            @block.tensor
            def _(pe):
                for n in range(NG):
                    if n >= 2:
                        pe.wait_ge(used, n - 1)
                    for kind in (1, 0):
                        bank = k.ps_scores[n % 2][:, kind * 512:(kind + 1) * 512]
                        for s in range(PER):
                            w0 = 96 - 32 * s
                            mm = pe.matmul(bank, gather[:, 2 * (n % 2) + kind, w0:w0 + P],
                                           acc[:, (n // 2) * PER + s, :], start=s == 0, stop=s == PER - 1)
                        mm.then_inc(full, 1)

            @block.vector
            def _(dve):
                own_ = Count(dve, ready)
                for n in range(NG):
                    slot = k.ps_scores[n % 2]
                    dve.wait_ge(full, 2 * n + 1)
                    own_.step(nc.vector.tensor_scalar(den[:, 0, :], slot[:, 512:1024], extra[:, 0:1], None, ALU.add))
                    own_.step(nc.vector.reciprocal(den[:, 1, :], den[:, 0, :]))
                    dve.wait_ge(full, 2 * n + 2)
                    nc.vector.tensor_tensor(oT[:, n * 512:(n + 1) * 512], slot[:, 0:512], den[:, 1, :], ALU.mult
                                            ).then_inc(used, 1)
                    dve.wait_ge(used, n + 1)

        project_turned(k, name + "o", range(NG), 1, lambda c, t: oT[:, t * P:(t + 1) * P], wo[:, :, :],
                       d[wo_dram], bo[:, :], d[bo_dram])


def l2_attention(k):
    small_head_attention(k, "l2", "L2_qkv", True, "L2_denom_bias", "L2_wo", "L2_attn_bo")


def l3_attention(k):
    small_head_attention(k, "l3", "L3_qkv", False, None, "L3_wo", "L3_attn_bo")



EXPERTS = 8


def softmax_rows(dve, own, probs, scores, tmp, passes, acts, n):
    v = dve
    T, E = probs.shape[1], probs.shape[2]
    own.step(v.tensor_reduce(tmp, scores, AX.X, ALU.max))
    v.tensor_tensor(probs, scores, tmp.unsqueeze(2).broadcast_to([P, T, E]), ALU.subtract).then_inc(passes, 1)
    own.eng.wait_ge(acts, n)
    own.step(v.tensor_reduce(tmp, probs, AX.X, ALU.add))
    own.step(v.reciprocal(tmp, tmp))
    own.step(v.tensor_tensor(probs, probs, tmp.unsqueeze(2).broadcast_to([P, T, E]), ALU.mult))


def top_two(dve, own, gates, probs, rank, tmp, hit, scale):
    v = dve
    T, E = probs.shape[1], probs.shape[2]
    wide = tmp.unsqueeze(2).broadcast_to([P, T, E])
    for n in range(2):
        own.step(v.tensor_reduce(tmp, probs, AX.X, ALU.max))
        own.step(v.tensor_tensor(hit, probs, wide, ALU.is_equal))
        own.step(v.tensor_tensor(hit, hit, rank, ALU.mult))
        own.step(v.tensor_reduce(tmp, hit, AX.X, ALU.max))
        own.step(v.tensor_tensor(hit, rank, wide, ALU.is_equal))
        if n == 0:
            own.step(v.scalar_tensor_tensor(gates, probs, scale, hit, ALU.mult, ALU.mult))
            own.step(v.scalar_tensor_tensor(probs, hit, -4.0, probs, ALU.mult, ALU.add))
        else:
            own.step(v.scalar_tensor_tensor(probs, probs, scale, hit, ALU.mult, ALU.mult))
            own.step(v.tensor_tensor(gates, gates, probs, ALU.add))


def route(k, name, w_dram, b_dram, rank, gates, scale, groups):
    nc, d = k.nc, k.dram
    n_in = EXPERTS + groups
    with ExitStack() as ctx:
        sb = lambda n, s: k.sb(name + n, s, ctx=ctx)
        loaded, logits, own_s, passes, acts = (k.sem(name + n, ctx) for n in (
            "_loaded", "_logits", "_own", "_passes", "_acts"))
        w, bias = sb("_w", [P, n_in]), sb("_b", [1, n_in])
        lg = sb("_lg", [P, TILES, n_in])
        probs = sb("_probs", [P, TILES, EXPERTS])
        hit = sb("_hit", [P, TILES, EXPERTS])
        tmp = sb("_tmp", [P, TILES])
        gp = sb("_gp", [P, TILES, 2])
        sel = sb("_sel", [P, TILES, 2])
        best = sb("_best", [P, TILES])
        block = ctx.enter_context(nc.Block())
        bank = k.ps_out[0][:, 0:TILES * n_in].rearrange("p (t e) -> p t e", e=n_in)

        @block.sync
        def _(sp):
            sp.dma_start(w[:, :], d[w_dram]).then_inc(loaded, 16)
            sp.dma_start(rank[:, :, :], d["rank"]).then_inc(loaded, 16)
            if b_dram:
                sp.dma_start(bias[:, :], d[b_dram]).then_inc(loaded, 16)

        @block.tensor
        def _(pe):
            pe.wait_ge(loaded, 48 if b_dram else 32)
            for t in range(TILES):
                c0 = xcol(t // GROUP) + (t % GROUP) * P
                mm = pe.matmul(bank[:, t, :], k.xT[:, c0:c0 + P], w[:, :], start=True, stop=not b_dram)
                if b_dram:
                    mm = pe.matmul(bank[:, t, :], k.ones[0:1, 0:P], bias[:, :], start=False, stop=True)
            mm.then_inc(logits, 1)

        @block.scalar
        def _(act):
            if groups:
                act.wait_ge(passes, 1)
                nc.scalar.activation(gp[:, :, :], gp[:, :, :], ACT.Exp).then_inc(acts, 1)
            n = 2 if groups else 1
            act.wait_ge(passes, n)
            nc.scalar.activation(probs[:, :, :], probs[:, :, :], ACT.Exp).then_inc(acts, 1)
            act.wait_ge(acts, n)

        @block.vector
        def _(dve):
            own = Count(dve, own_s)
            v = nc.vector
            dve.wait_ge(logits, 1)
            dve.wait_ge(loaded, 48 if b_dram else 32)
            own.step(v.tensor_copy(lg[:, :, :], bank))
            if groups:
                softmax_rows(v, own, gp[:, :, :], lg[:, :, 0:groups], tmp[:, :], passes, acts, 1)
                own.done(v.tensor_tensor(best[:, :], gp[:, :, 0], gp[:, :, 1], ALU.max))
                own.done(v.tensor_tensor(sel[:, :, 0], gp[:, :, 0], gp[:, :, 1], ALU.is_ge))
                own.step(v.tensor_tensor(sel[:, :, 1], gp[:, :, 1], gp[:, :, 0], ALU.is_gt))
                own.step(v.tensor_scalar(sel[:, :, :], sel[:, :, :], HUGE, -HUGE, ALU.mult, ALU.add))
                per = EXPERTS // groups
                for g in range(groups):
                    e = lg[:, :, groups + g * per:groups + (g + 1) * per]
                    own.done(v.tensor_tensor(e, e, sel[:, :, g].unsqueeze(2).broadcast_to([P, TILES, per]), ALU.add))
                own.wait()
            softmax_rows(v, own, probs[:, :, :], lg[:, :, groups:n_in], tmp[:, :], passes, acts, 2 if groups else 1)
            if groups:
                own.step(v.tensor_tensor(probs[:, :, :], probs[:, :, :],
                                         best[:, :].unsqueeze(2).broadcast_to([P, TILES, EXPERTS]), ALU.mult))
            top_two(v, own, gates[:, :, :], probs[:, :, :], rank[:, :, :], tmp[:, :], hit[:, :, :], scale)



F2_HID = 256


def l2_ffn(k):
    nc, d = k.nc, k.dram
    CH, HALVES = F2_HID // P, NG // B
    NP = 2 * CH
    with ExitStack() as ctx:
        sb = lambda n, s: k.sb("f2" + n, s, ctx=ctx)
        rank = sb("_rank", [P, TILES, EXPERTS])
        gates = sb("_gates", [P, TILES, EXPERTS])
        w_up = sb("_w_up", [P, NP, 2, P])
        w_out = sb("_w_out", [P, CH, C])
        w2 = sb("_w2", [P, CH, EXPERTS * C])
        silu = sb("_silu", [P, 2, 512])
        hid = sb("_hid", [P, 2, NP, 512])
        prod = sb("_prod", [P, 2, EXPERTS, C])
        part = sb("_part", [P, 2, C])
        route(k, "f2r", "L2_router_w", "L2_router_b", rank, gates, 1.0, 2)
        sem = lambda n: k.sem("f2" + n, ctx)
        w_loaded = sem("_w_loaded")
        per = HALVES * NP // 2
        u_full = [Signal(sem(f"_u_full{i}"), per) for i in range(2)]
        silu_ready = Signal(sem("_silu_ready"), HALVES * NP)
        hid_ready = [Signal(sem(f"_hid_ready{i}"), per) for i in range(2)]
        r_full = [Signal(sem(f"_r_full{i}"), HALVES * GROUP // 2) for i in range(2)]
        r_free = [Signal(sem(f"_r_free{i}"), HALVES * GROUP // 2) for i in range(2)]
        own = Signal(sem("_own_dve"), HALVES * (Norm.DVE_STEPS + 2 * GROUP))
        norm = Norm(k, ctx, "f2n", HALVES)
        block = ctx.enter_context(nc.Block())

        @block.sync
        def _(sp):
            sp.dma_start(w_up[:, :, :, :], d["L2_w_up"]).then_inc(w_loaded, 16)
            sp.dma_start(w_out[:, :, :], d["L2_w_out"]).then_inc(w_loaded, 16)
            sp.dma_start(w2[:, :, :], d["L2_w2"]).then_inc(w_loaded, 16)

        @block.tensor
        def _(pe):
            norm.start(pe, None, None)
            for s in (*u_full, *r_full):
                s.start(pe)
            pe.wait_ge(w_loaded, 48)
            with pe.Fori(0, B) as b:
                for g in range(HALVES):
                    for c in range(NP):
                        n = g * NP + c
                        pe.wait_ge(hid_ready[n % 2].sem, hid_ready[n % 2].at(b, n // 2 - 1))
                        pe.wait_ge(r_free[n % 2].sem, r_free[n % 2].at(b, -1))
                        for i in range(2):
                            mm = pe.matmul(k.ps_scores[n % 2][:, i * 512:(i + 1) * 512], w_up[:, c, i, :],
                                           k.xT[:, ds(b * XB + PAD + g * 512, 512)], start=True, stop=True)
                        mm.then_inc(u_full[n % 2].sem, 1)
                for g in range(HALVES):
                    y = k.ps_out[g]
                    pe.wait_ge(norm.y_free.sem, norm.y_free.at(b, g - 2))
                    for c in range(CH):
                        n = g * NP + c
                        pe.wait_ge(hid_ready[n % 2].sem, hid_ready[n % 2].at(b, n // 2))
                        for i in range(GROUP):
                            mm = pe.matmul(y[:, i * C:(i + 1) * C], hid[:, g, c, i * P:(i + 1) * P], w_out[:, c, :],
                                           start=(c == 0 and i == 0), stop=c == CH - 1 and i == GROUP - 1,
                                           skip_group_check=True)
                    mm.then_inc(norm.y_full.sem, 1)
                for s in range(2):
                    pe.wait_ge(hid_ready[s].sem, hid_ready[s].at(b, per - 1))
                for g in range(HALVES):
                    for i in range(GROUP):
                        n = g * GROUP + i
                        slot = k.ps_scores[n % 2]
                        pe.wait_ge(r_free[n % 2].sem, r_free[n % 2].at(b, n // 2 - 1))
                        for h in range(2):
                            for c in range(CH):
                                mm = pe.matmul(slot[:, h * 512:(h + 1) * 512], hid[:, g, CH + c, i * P:(i + 1) * P],
                                               w2[:, c, h * 512:(h + 1) * 512], start=c == 0, stop=c == CH - 1)
                        mm.then_inc(r_full[n % 2].sem, 1)
                for g in range(HALVES):
                    norm.tensor(pe, b, g, g, k.ps_turned[0])

        @block.scalar
        def _(act):
            norm.start(None, None, act)
            silu_ready.start(act)
            with act.Fori(0, B) as b:
                for g in range(HALVES):
                    for c in range(NP):
                        n = g * NP + c
                        act.wait_ge(u_full[n % 2].sem, u_full[n % 2].at(b, n // 2))
                        act.wait_ge(hid_ready[n % 2].sem, hid_ready[n % 2].at(b, n // 2 - 1))
                        nc.scalar.activation(silu[:, n % 2, :], k.ps_scores[n % 2][:, 0:512], ACT.Silu
                                             ).then_inc(silu_ready.sem, 1)
                for g in range(HALVES):
                    norm.scalar_root(act, b, g, g)
                for g in range(HALVES):
                    norm.scalar_store(act, b, g, k.ps_turned[0], b * XB + PAD + g * 512)

        @block.vector
        def _(dve):
            norm.start(None, dve, None)
            for s in (*hid_ready, *r_free, own):
                s.start(dve)
            with dve.Fori(0, B) as b:
                chain = Chain(dve, own, b)
                for g in range(HALVES):
                    for c in range(NP):
                        n = g * NP + c
                        dve.wait_ge(silu_ready.sem, silu_ready.at(b, n))
                        nc.vector.tensor_tensor(hid[:, g, c, :], k.ps_scores[n % 2][:, 512:1024], silu[:, n % 2, :],
                                                ALU.mult).then_inc(hid_ready[n % 2].sem, 1)
                for g in range(HALVES):
                    tile0 = b * TPB + g * GROUP

                    def routed(res):
                        for i in range(GROUP):
                            n = g * GROUP + i
                            s = n % 2
                            dve.wait_ge(r_full[s].sem, r_full[s].at(b, n // 2))
                            gate = gates[:, ds(tile0 + i, 1), :].rearrange("p o e -> p (o e)")
                            nc.vector.tensor_tensor(
                                prod[:, s, :, :], k.ps_scores[s][:, :].rearrange("p (e c) -> p e c", c=C),
                                gate.unsqueeze(2).broadcast_to([P, EXPERTS, C]), ALU.mult).then_inc(r_free[s].sem, 1)
                            dve.wait_ge(r_free[s].sem, r_free[s].at(b, n // 2))
                            chain.step(nc.vector.tensor_reduce(
                                part[:, s, :], prod[:, s, :, :].rearrange("p e c -> p c e"), AX.X, ALU.add))
                            r = res[:, i * C:(i + 1) * C]
                            chain.step(nc.vector.tensor_tensor(r, r, part[:, s, :], ALU.add))

                    norm.vector(dve, chain, b, g, g, tile0, k.ps_out[g][:, :], more=routed)
                chain.close()



F3_HID = 512
F3_SCALE = float(1.0 / np.sqrt(1.25))


def l3_ffn(k):
    nc, d = k.nc, k.dram
    CH, HALVES, E = F3_HID // P, NG // B, EXPERTS + 1
    with ExitStack() as ctx:
        sb = lambda n, s: k.sb("f3" + n, s, ctx=ctx)
        rank = sb("_rank", [P, TILES, EXPERTS])
        gates = sb("_gates", [P, TILES, EXPERTS])
        w1 = sb("_w1", [P, E, F3_HID])
        w2 = sb("_w2", [P, E, CH, C])
        b1 = sb("_b1", [P, E * CH])
        b2 = sb("_b2", [1, E * C])
        hid = sb("_hid", [P, 2, CH, 512])
        scaled = sb("_scaled", [P, 2, 512])
        route(k, "f3r", "L3_router_w", None, rank, gates, F3_SCALE, 0)
        sem = lambda n: k.sem("f3" + n, ctx)
        w_loaded = sem("_w_loaded")
        per = HALVES * E * CH // 4
        h_full = [Signal(sem(f"_h_full{i}"), per) for i in range(4)]
        h_ready = [Signal(sem(f"_h_ready{i}"), per) for i in range(4)]
        e_full = [Signal(sem(f"_e_full{i}"), HALVES * E // 2) for i in range(2)]
        e_free = [Signal(sem(f"_e_free{i}"), HALVES * E // 2) for i in range(2)]
        own = Signal(sem("_own_dve"), HALVES * (Norm.DVE_STEPS + EXPERTS))
        norm = Norm(k, ctx, "f3n", HALVES)
        block = ctx.enter_context(nc.Block())

        def bank(n):
            return k.ps_scores[(n % 4) // 2][:, (n % 2) * 512:(n % 2 + 1) * 512]

        @block.sync
        def _(sp):
            sp.dma_start(w1[:, :, :], d["L3_w1"]).then_inc(w_loaded, 16)
            sp.dma_start(w2[:, :, :, :], d["L3_w2"]).then_inc(w_loaded, 16)
            sp.dma_start(b1[:, :], d["L3_b1"]).then_inc(w_loaded, 16)
            sp.dma_start(b2[:, :], d["L3_b2"]).then_inc(w_loaded, 16)

        @block.tensor
        def _(pe):
            norm.start(pe, None, None)
            for s in (*h_full, *e_full):
                s.start(pe)
            pe.wait_ge(w_loaded, 64)

            def up(b, m):
                g, e = m // E, m % E
                for c in range(CH):
                    n = m * CH + c
                    pe.wait_ge(h_ready[n % 4].sem, h_ready[n % 4].at(b, n // 4 - 1))
                    if c == 0:
                        pe.wait_ge(e_full[m % 2].sem, e_full[m % 2].at(b, m // 2 - 1))
                    pe.matmul(bank(n), w1[:, e, c * P:(c + 1) * P], k.xT[:, ds(b * XB + PAD + g * 512, 512)],
                              start=True, stop=True).then_inc(h_full[n % 4].sem, 1)

            def down(b, m):
                g, e = m // E, m % E
                y = k.ps_out[m % 2]
                pe.wait_ge(e_free[m % 2].sem, e_free[m % 2].at(b, m // 2 - 1))
                for c in range(CH):
                    n = m * CH + c
                    pe.wait_ge(h_ready[n % 4].sem, h_ready[n % 4].at(b, n // 4))
                    for i in range(GROUP):
                        pe.matmul(y[:, i * C:(i + 1) * C], hid[:, m % 2, c, i * P:(i + 1) * P], w2[:, e, c, :],
                                  start=(c == 0 and i == 0), stop=False, skip_group_check=True)
                for i in range(GROUP):
                    mm = pe.matmul(y[:, i * C:(i + 1) * C], k.ones[0:1, 0:P], b2[:, e * C:(e + 1) * C], start=False,
                                   stop=i == GROUP - 1, skip_group_check=True)
                mm.then_inc(e_full[m % 2].sem, 1)

            with pe.Fori(0, B) as b:
                for m in range(HALVES * E):
                    up(b, m)
                    if m >= 1:
                        down(b, m - 1)
                down(b, HALVES * E - 1)
                for g in range(HALVES):
                    norm.tensor(pe, b, g, g, k.ps_turned[0])

        @block.scalar
        def _(act):
            norm.start(None, None, act)
            for s in h_ready:
                s.start(act)
            with act.Fori(0, B) as b:
                for n in range(HALVES * E * CH):
                    m, c = n // CH, n % CH
                    act.wait_ge(h_full[n % 4].sem, h_full[n % 4].at(b, n // 4))
                    if c == 0:
                        act.wait_ge(e_full[m % 2].sem, e_full[m % 2].at(b, m // 2 - 1))
                    at = (m % E) * CH + c
                    nc.scalar.activation(hid[:, m % 2, c, :], bank(n), ACT.Gelu_apprx_tanh, bias=b1[:, at:at + 1]
                                         ).then_inc(h_ready[n % 4].sem, 1)
                    if n == (E + 1) * CH - 1:
                        norm.scalar_root(act, b, 0, 0)
                norm.scalar_root(act, b, 1, 1)
                for g in range(HALVES):
                    norm.scalar_store(act, b, g, k.ps_turned[0], b * XB + PAD + g * 512)

        @block.vector
        def _(dve):
            norm.start(None, dve, None)
            for s in (*e_free, own):
                s.start(dve)
            with dve.Fori(0, B) as b:
                chain = Chain(dve, own, b)
                for g in range(HALVES):
                    tile0 = b * TPB + g * GROUP

                    def experts(res):
                        for e in range(1, E):
                            m = g * E + e
                            s = m % 2
                            dve.wait_ge(e_full[s].sem, e_full[s].at(b, m // 2))
                            gate = gates[:, ds(tile0, GROUP), e - 1:e].broadcast_to([P, GROUP, C])
                            nc.vector.tensor_tensor(
                                scaled[:, s, :].rearrange("p (t c) -> p t c", c=C),
                                k.ps_out[s][:, :].rearrange("p (t c) -> p t c", c=C), gate, ALU.mult
                                ).then_inc(e_free[s].sem, 1)
                            dve.wait_ge(e_free[s].sem, e_free[s].at(b, m // 2))
                            chain.step(nc.vector.tensor_tensor(res, res, scaled[:, s, :], ALU.add))

                    m0 = g * E
                    norm.vector(dve, chain, b, g, g, tile0, k.ps_out[m0 % 2][:, :], scale=F3_SCALE, more=experts,
                                y_full=(e_full[m0 % 2], m0 // 2), y_free=(e_free[m0 % 2], m0 // 2))
                chain.close()



def layouts(inputs):
    a = {n: np.asarray(v) for n, v in inputs.items()}
    out = {n: a[n] for n in ("L0_attn_x", "L0_attn_Wq", "L0_attn_Wk", "L0_attn_Wv", "L0_attn_Wo")}
    out["L0_bqk"] = np.stack([a["L0_attn_bq"], a["L0_attn_bk"]], 1)
    for n in ("L0_attn_bv", "L0_attn_bo"):
        out[n] = a[n][None, :]
    f32 = np.float32
    p = np.arange(P)
    out["head_mask8"] = ((p[:, None] // 8 == np.arange(16)[None, :]) / np.sqrt(8.0)).astype(f32)
    w = np.zeros((P, TPB, L0_GROUPS), f32)
    for j in range(TPB):
        for half in range(2):
            rows = slice(64 * half, 64 * half + 64)
            w[rows, j, half] = 1.0
            for off in (-2, -1, 1, 2):
                if 0 <= 2 * j + half + off < L // SEG:
                    w[rows, j, 2 + half + off + 3] = 0.25
    out["L0_group_weights"] = w
    out["L0_ffn_W_exp"] = a["L0_ffn_W_exp"]
    out["L0_W_con_T"] = a["L0_ffn_W_con"].T
    out["L0_ffn_b_exp"] = a["L0_ffn_b_exp"][None, :]
    out["L0_up_bias"] = a["L0_ffn_up_bias"].reshape(4, P).T
    out["L0_y_bias"] = np.stack([a["L0_ffn_b_con"], a["L0_ffn_down_bias"]])
    out["L0_up_weights"] = a["L0_ffn_up_weights"].reshape(-1)
    out["L0_down_weights"] = a["L0_ffn_down_weights"].reshape(-1)
    w = a["L1_attn_qkv_w"].reshape(3, PAIRS, 2, L1_D, C)
    swap = np.roll(w, L1_D // 2, axis=3)
    w = np.stack([w[0], swap[0], w[1], swap[1], w[2]], 1)
    out["L1_qkv"] = w.transpose(0, 4, 1, 2, 3).reshape(PAIRS, C, 5 * P)
    out["L1_out_w"] = a["L1_attn_out_w"].T.reshape(8, P, C).transpose(1, 0, 2)
    sign = np.where(p % L1_D < L1_D // 2, -1.0, 1.0).astype(f32)
    out["L1_freq"] = np.stack([np.tile(a["L1_attn_rope_freqs"], 4), sign, np.full(P, np.pi / 2, f32)], 1)
    out["L1_bias_ap"] = np.concatenate([a["L1_attn_bias_a"].reshape(-1), a["L1_attn_bias_p"].reshape(-1)])
    half = np.arange(0, F1_D, 2, dtype=f32)
    t = np.arange(L, dtype=f32)
    fr = t[:, None] * (f32(1.0) / f32(10000.0) ** (half / f32(F1_D)))[None, :]
    base = (half + f32(0.4 * F1_D)) / f32(1.4 * F1_D)
    scale = base[None, :] ** ((t - L // 2) / f32(WINDOW // 2))[:, None]
    cos, sin = np.cos(fr.astype(np.float64)).astype(f32), np.sin(fr.astype(np.float64)).astype(f32)
    two = lambda x, y: np.concatenate([x, y], 1)
    cq, sq = two(cos * scale, cos * scale) * f32(8), two(-sin * scale, sin * scale) * f32(8)
    ck, sk = two(cos / scale, cos / scale), two(-sin / scale, sin / scale)
    xpos = np.stack([np.stack([cq, ck]), np.stack([sq, sk])]).astype(f32)
    out["F1_xpos"] = xpos.reshape(2, 2, TPB, P, F1_D).transpose(3, 0, 2, 1, 4)
    for layer in range(F1_DEPTH):
        both = np.stack([a["L1_ffn_q_scale"][layer], a["L1_ffn_k_scale"][layer]])
        out[f"F1_scales{layer}"] = np.stack([both, np.roll(both, F1_D // 2, axis=1)])
    for n in ("L1_ffn_wqkv", "L1_ffn_w1", "L1_ffn_b2"):
        out[n] = a[n]
    out["F1_wo"] = a["L1_ffn_wo"].reshape(F1_DEPTH, 4, P, C).transpose(0, 2, 1, 3)
    cols = np.zeros((F1_DEPTH, P, 8), f32)
    w2 = np.zeros((F1_DEPTH, P, 3, C), f32)
    cols[:, :, 0], cols[:, :, 1] = a["L1_ffn_ln_g"], a["L1_ffn_ln_b"]
    for c, r in enumerate(F1_ROWS):
        cols[:, 0:r, 2 + c] = a["L1_ffn_b1"][:, c * P:c * P + r]
        cols[:, 0:r, 5 + c] = a["L1_ffn_b1"][:, F1_HID + c * P:F1_HID + c * P + r]
        w2[:, 0:r, c, :] = a["L1_ffn_w2"][:, c * P:c * P + r, :]
    out["F1_cols"], out["F1_w2"] = cols, w2
    for n in ("L2", "L3"):
        out[n + "_qkv"] = np.concatenate([a[f"{n}_attn_W{m}"].T for m in "qkv"], 1)
        out[n + "_wo"] = a[n + "_attn_Wo"].T[:, None, :]
        out[n + "_attn_bo"] = a[n + "_attn_bo"][None, :]
    out["L2_denom_bias"] = np.repeat(a["L2_attn_denom_bias"].reshape(-1), 8)[:, None]
    gather = np.zeros((2, 2, 2, 2, 8, 2, 2, P + 96), f32)
    for j, half, pair, kind, e in np.ndindex(2, 2, 2, 2, 8):
        gather[j, half, pair, kind, e, half, kind, 96 + 16 * pair + 8 * j + e] = 1.0
    out["gather"] = gather.reshape(P, 4, P + 96)
    i, j = (p % WINDOW)[:, None], np.arange(P)[None, :]
    seen = (j >= i) & (j <= i + WINDOW)
    seen = np.stack([seen & ((p[:, None] >= WINDOW) | (j >= WINDOW)), seen], 1)
    out["F1_mask"] = np.where(seen, 0.0, -HUGE).astype(f32)
    out["tile_rows"] = (p[:, None] % TPB == np.arange(TPB)[None, :]).astype(f32)
    out["rank"] = np.broadcast_to(np.arange(EXPERTS, 0, -1, dtype=f32), (P, TILES, EXPERTS))
    out["L2_router_w"] = np.concatenate([a["L2_ffn_wg"], a["L2_ffn_we"]], 0).T
    out["L2_router_b"] = np.concatenate([a["L2_ffn_gb"], a["L2_ffn_eb"]])[None, :]
    pairs = lambda w: w.reshape(2, F2_HID // P, P, C).transpose(3, 1, 0, 2)
    out["L2_w_up"] = np.concatenate([pairs(a["L2_ffn_w_in"]), pairs(a["L2_ffn_w1"])], 1)
    out["L2_w_out"] = a["L2_ffn_w_out"].T.reshape(F2_HID // P, P, C).transpose(1, 0, 2)
    out["L2_w2"] = a["L2_ffn_w2"].reshape(EXPERTS, C, F2_HID // P, P).transpose(3, 2, 0, 1).reshape(
        P, F2_HID // P, EXPERTS * C)
    out["L3_router_w"] = a["L3_ffn_w_router"].T
    all_of = lambda s, e: np.concatenate([a["L3_ffn_" + s][None], a["L3_ffn_" + e]], 0)
    out["L3_w1"] = all_of("Ws1", "W1").transpose(2, 0, 1)
    out["L3_w2"] = all_of("Ws2", "W2").reshape(9, C, 4, P).transpose(3, 0, 2, 1)
    out["L3_b1"] = all_of("bs1", "b1").reshape(9 * 4, P).T
    out["L3_b2"] = all_of("bs2", "b2").reshape(1, -1)
    return {n: np.ascontiguousarray(v) for n, v in out.items()}


STAGES = [l0_attention, l0_ffn, l1_attention, l1_ffn, l2_attention, l2_ffn, l3_attention, l3_ffn]


def build(nc, dram, out, stages=99):
    with ExitStack() as ctx:
        k = Kernel(nc, ctx, dram)
        load_x(k)
        for stage in STAGES[:stages]:
            stage(k)
        with ExitStack() as c2:
            stored = k.sem("stored", c2)
            block = c2.enter_context(nc.Block())

            @block.sync
            def _(sp):
                sp.dma_start(out.rearrange("b (t p) c -> p (b t) c", p=P),
                             k.x_tok[:, :].rearrange("p (t c) -> p t c", c=C)).then_inc(stored, 16)
                sp.wait_ge(stored, 16)


def kernel(**inputs):
    import concourse.bacc as bacc
    from concourse.bass_utils import run_bass_kernel_spmd

    nc = bacc.Bacc("TRN2", target_bir_lowering=False, num_devices=1)
    arrays = layouts(inputs)
    dram = {n: nc.dram_tensor("in_" + n, v.shape, mybir.dt.from_np(v.dtype), kind="ExternalInput").ap()
            for n, v in arrays.items()}
    out = nc.dram_tensor("out_x", (B, L, C), F32, kind="ExternalOutput").ap()
    build(nc, dram, out)
    r = run_bass_kernel_spmd(nc, [{"in_" + n: v for n, v in arrays.items()}], core_ids=[0])
    return r.results[0]["out_x"]
```

```python
from contextlib import ExitStack

import numpy as np

import concourse.bass as bass
from concourse import mybir

F32 = mybir.dt.float32
BF16 = mybir.dt.bfloat16
ALU = mybir.AluOpType
ACT = mybir.ActivationFunctionType
AX = mybir.AxisListType
ds = bass.ds

P = 128
B, L, C = 2, 1024, 128
TPB = L // P
TILES = B * TPB
GROUP = 4
NG = TILES // GROUP
PAD = 192
XB = L + 2 * PAD
EPS = 1e-5
HUGE = 3.0e38


class Signal:

    def __init__(self, sem, per, step=1):
        self.sem, self.per, self.step = sem, per, step

    def start(self, eng):
        if self.per:
            eng.sem_inc(self.sem, self.per * self.step)

    def at(self, it, k):
        assert k < self.per and k >= -self.per, (k, self.per)
        return (it * self.per + (self.per + k + 1)) * self.step if self.step != 1 else it * self.per + (self.per + k + 1)


class Chain:

    def __init__(self, eng, events, it=0):
        self.eng, self.events, self.it, self.n = eng, events, it, 0

    def done(self, ins):
        ins.then_inc(self.events.sem, 1)
        self.n += 1
        return ins

    def wait(self):
        self.eng.wait_ge(self.events.sem, self.events.at(self.it, self.n - 1))

    def step(self, ins):
        self.done(ins)
        self.wait()

    def wait_apart(self, passed):
        self.wait()
        self.eng.sem_inc(passed, 1)

    def close(self):
        assert self.n == self.events.per, f"{self.events.sem}: {self.n} events, {self.events.per} declared"


class Count:

    def wait_apart(self, passed):
        self.wait()

    def __init__(self, eng, sem):
        self.eng, self.sem, self.n = eng, sem, 0

    def done(self, ins):
        ins.then_inc(self.sem, 1)
        self.n += 1
        return ins

    def wait(self):
        self.eng.wait_ge(self.sem, self.n)

    def step(self, ins):
        self.done(ins)
        self.wait()


def order(slots, lead, units, lag=2):
    out = []
    for n in range(slots + lag + 1):
        if n < slots:
            out.append(("S", n))
        if 0 <= n - lead - lag < units:
            out.append(("T", n - lead - lag))
        if 0 <= n - lead - lag - 1 < units:
            out.append(("V", n - lead - lag - 1))
    return out


class Kernel:

    def __init__(self, nc, ctx, dram):
        self.nc, self.ctx, self.dram = nc, ctx, dram
        self.numbers = {}
        self.ident = self.sb("ident", [P, P])
        self.ones = self.sb("ones", [P, 512])
        self.x_tok = self.sb("x_tok", [P, TILES * C])
        self.xT = self.sb("xT", [P, B * XB])
        self.xn = self.sb("x_new", [P, 2, 512])
        self.res = self.sb("residual", [P, 2, 512])
        self.stats = self.sb("ln_stats", [P, 2, GROUP, 6])
        self.mv = self.sb("ln_mean_var", [P, 2, GROUP, 2])
        self.rstd = self.sb("ln_rstd", [P, 2, 3, GROUP])
        self.ps = [ctx.enter_context(nc.psum_tensor(f"bank{i}", [P, 1024 if i < 2 else 512], F32))
                   for i in range(6)]
        self.ps_scores = [self.ps[0], self.ps[1]]
        self.ps_turned = [self.ps[2], self.ps[3]]
        self.ps_out = [self.ps[4], self.ps[5]]

    def sb(self, name, shape, dt=F32, ctx=None):
        return (ctx or self.ctx).enter_context(self.nc.sbuf_tensor(name, shape, dt))

    def sem(self, name, ctx):
        if ctx not in self.numbers:
            self.numbers[ctx] = []
            ctx.callback(self.clear, ctx)
        s = ctx.enter_context(self.nc.semaphore(name))
        self.numbers[ctx].append(s.num)
        return s

    def clear(self, ctx):
        numbers = sorted(self.numbers.pop(ctx))
        while numbers:
            n = 1
            while n < len(numbers) and numbers[n] == numbers[0] + n:
                n += 1
            self.nc.gpsimd.sem_clear(range(numbers[0], numbers[0] + n))
            numbers = numbers[n:]


def xcol(g):
    return (g // 2) * XB + PAD + (g % 2) * 512



class Norm:

    DVE_STEPS = 13

    def __init__(self, k, ctx, name, per):
        self.k = k
        self.y_full = Signal(k.sem(name + "_y_full", ctx), per)
        self.y_free = Signal(k.sem(name + "_y_free", ctx), per)
        self.var_ready = Signal(k.sem(name + "_var_ready", ctx), per)
        self.root_ready = Signal(k.sem(name + "_root_ready", ctx), per)
        self.xn_ready = Signal(k.sem(name + "_xn_ready", ctx), per)
        self.turned = Signal(k.sem(name + "_turned", ctx), per)
        self.xT_ready = Signal(k.sem(name + "_xT_ready", ctx), per)
        self.passed = k.sem(name + "_passed", ctx)

    def start(self, pe, dve, act):
        if pe is not None:
            self.y_full.start(pe), self.turned.start(pe)
        if dve is not None:
            self.y_free.start(dve), self.var_ready.start(dve), self.xn_ready.start(dve)
        if act is not None:
            self.root_ready.start(act), self.xT_ready.start(act)

    def vector(self, dve, chain, it, e, slot, tile0, y, scale=None, normed=True, also=None, more=None,
               y_full=None, y_free=None, wait_y=True):
        self.vector_stats(dve, chain, it, e, slot, tile0, y, scale, normed, also, more, y_full, y_free, wait_y)
        self.vector_scale(dve, chain, it, e, slot, tile0, normed)

    def vector_pipelined(self, dve, chain, it, groups):
        for n in range(len(groups) + 1):
            if n < len(groups):
                args, more = groups[n]
                self.vector_stats(dve, chain, it, *args, **more)
            if n >= 1:
                args, more = groups[n - 1]
                self.vector_scale(dve, chain, it, *args[:3], normed=more.get("normed", True))

    def vector_stats(self, dve, chain, it, e, slot, tile0, y, scale=None, normed=True, also=None, more=None,
                     y_full=None, y_free=None, wait_y=True):
        k, nc = self.k, self.k.nc
        x = k.x_tok[:, ds(tile0 * C, 512)]
        res = k.res[:, slot, :]
        full, e_full = y_full or (self.y_full, e)
        free, e_free = y_free or (self.y_free, e)
        if wait_y:
            dve.wait_ge(full.sem, full.at(it, e_full))
        if scale is None:
            nc.vector.tensor_tensor(res, x, y, ALU.add).then_inc(free.sem, 1)
        else:
            nc.vector.scalar_tensor_tensor(res, y, scale, x, ALU.mult, ALU.add).then_inc(free.sem, 1)
        dve.wait_ge(free.sem, free.at(it, e_free))
        if also is not None:
            chain.step(nc.vector.tensor_tensor(res, res, also, ALU.add))
        if more is not None:
            more(res)
        if not normed:
            chain.step(nc.vector.tensor_scalar(x, res, 1.0, None, ALU.mult))
            return
        for i in range(GROUP):
            chain.done(nc.vector.bn_stats(k.stats[:, slot, i, :], res[:, i * C:(i + 1) * C]))
        chain.wait_apart(self.passed)
        for i in range(GROUP):
            chain.done(nc.vector.bn_aggr(k.mv[:, slot, i, :], k.stats[:, slot, i, :]))
        chain.wait()
        nc.vector.tensor_scalar(k.rstd[:, slot, 0, :], k.mv[:, slot, :, 1], EPS, None, ALU.add
                                ).then_inc(self.var_ready.sem, 1)

    def vector_scale(self, dve, chain, it, e, slot, tile0, normed=True):
        k, nc = self.k, self.k.nc
        x, res = k.x_tok[:, ds(tile0 * C, 512)], k.res[:, slot, :]
        if not normed:
            dve.wait_ge(self.turned.sem, self.turned.at(it, e - 2))
            nc.vector.tensor_scalar(k.xn[:, slot, :], res, 1.0, None, ALU.mult).then_inc(self.xn_ready.sem, 1)
            dve.wait_ge(self.xn_ready.sem, self.xn_ready.at(it, e))
            return
        dve.wait_ge(self.root_ready.sem, self.root_ready.at(it, e))
        chain.step(nc.vector.reciprocal(k.rstd[:, slot, 2, :], k.rstd[:, slot, 1, :]))
        dve.wait_ge(self.turned.sem, self.turned.at(it, e - 2))
        for i in range(GROUP):
            ins = nc.vector.tensor_scalar(k.xn[:, slot, i * C:(i + 1) * C], res[:, i * C:(i + 1) * C],
                                          k.mv[:, slot, i, 0:1], k.rstd[:, slot, 2, i:i + 1],
                                          ALU.subtract, ALU.mult)
            if i < GROUP - 1:
                chain.done(ins)
        ins.then_inc(self.xn_ready.sem, 1)
        dve.wait_ge(self.xn_ready.sem, self.xn_ready.at(it, e))
        chain.step(nc.vector.tensor_scalar(x, k.xn[:, slot, :], 1.0, None, ALU.mult))

    def scalar_root(self, act, it, e, slot):
        k = self.k
        act.wait_ge(self.var_ready.sem, self.var_ready.at(it, e))
        k.nc.scalar.activation(k.rstd[:, slot, 1, :], k.rstd[:, slot, 0, :], ACT.Sqrt
                               ).then_inc(self.root_ready.sem, 1)

    def tensor(self, pe, it, e, slot, bank):
        k = self.k
        pe.wait_ge(self.xn_ready.sem, self.xn_ready.at(it, e))
        pe.wait_ge(self.xT_ready.sem, self.xT_ready.at(it, e - 1))
        for i in range(GROUP):
            mm = pe.transpose(bank[:, i * P:(i + 1) * P], k.xn[:, slot, i * C:(i + 1) * C], k.ident[:, :])
        mm.then_inc(self.turned.sem, 1)

    def scalar_store(self, act, it, e, bank, col):
        k = self.k
        act.wait_ge(self.turned.sem, self.turned.at(it, e))
        k.nc.scalar.copy(k.xT[:, ds(col, 512)], bank[:, 0:512]).then_inc(self.xT_ready.sem, 1)


def load_x(k):
    nc = k.nc
    with ExitStack() as ctx:
        sem = lambda n: k.sem("in_" + n, ctx)
        loaded, made, zeroed = sem("x_loaded"), sem("ident_made"), sem("xT_zeroed")
        turned, taken = sem("x_turned"), sem("x_taken")
        block = ctx.enter_context(nc.Block())

        @block.sync
        def _(sp):
            sp.dma_start(k.x_tok[:, :].rearrange("p (t c) -> p t c", c=C),
                         k.dram["L0_attn_x"].rearrange("b (t p) c -> p (b t) c", p=P)).then_inc(loaded, 16)

        @block.gpsimd
        def _(pool):
            nc.gpsimd.memset(k.ident[:, :], 0.0).then_inc(made, 1)
            nc.gpsimd.memset(k.ones[:, :], 1.0).then_inc(made, 1)
            pool.wait_ge(made, 2)
            nc.gpsimd.affine_select(out=k.ident[:, :], in_=k.ident[:, :], compare_op=ALU.not_equal, fill=1.0,
                                    base=0, pattern=[[-1, P]], channel_multiplier=1).then_inc(made, 1)
            for b in range(B):
                nc.gpsimd.memset(k.xT[:, b * XB:b * XB + PAD], 0.0)
                nc.gpsimd.memset(k.xT[:, b * XB + PAD + L:(b + 1) * XB], 0.0).then_inc(zeroed, 1)
            pool.wait_ge(zeroed, 2)

        @block.tensor
        def _(pe):
            pe.wait_ge(made, 3)
            pe.wait_ge(loaded, 16)
            for g in range(NG):
                if g >= 2:
                    pe.wait_ge(taken, g - 1)
                for i in range(GROUP):
                    mm = pe.transpose(k.ps_turned[g % 2][:, i * P:(i + 1) * P],
                                      k.x_tok[:, (GROUP * g + i) * C:(GROUP * g + i + 1) * C], k.ident[:, :])
                mm.then_inc(turned, 1)

        @block.scalar
        def _(act):
            for g in range(NG):
                act.wait_ge(turned, g + 1)
                nc.scalar.copy(k.xT[:, xcol(g):xcol(g) + 512], k.ps_turned[g % 2][:, :]).then_inc(taken, 1)
            act.wait_ge(taken, NG)


def project_out(k, name, o_tok, chunks, wo, w_dram, bias, bias_dram, normed=True):
    nc = k.nc
    with ExitStack() as ctx:
        sem = lambda n: k.sem(name + n, ctx)
        oT = k.sb(name + "_oT", [P, 2, 512], ctx=ctx)
        w_loaded = sem("_w_loaded")
        o_turned = Signal(sem("_o_turned"), NG * chunks)
        o_taken = Signal(sem("_o_taken"), NG * chunks)
        own = sem("_own_dve")
        norm = Norm(k, ctx, name, NG)
        block = ctx.enter_context(nc.Block())

        @block.sync
        def _(sp):
            if w_dram is not None:
                sp.dma_start(wo, w_dram).then_inc(w_loaded, 16)
                if bias is not None:
                    sp.dma_start(bias, bias_dram).then_inc(w_loaded, 16)

        @block.tensor
        def _(pe):
            norm.start(pe, None, None)
            o_turned.start(pe)
            if w_dram is not None:
                pe.wait_ge(w_loaded, 32 if bias is not None else 16)
            for g in range(NG + 1):
                if g < NG:
                    y = k.ps_out[g % 2]
                    for c in range(chunks):
                        n = g * chunks + c
                        bank = k.ps_turned[n % 2]
                        pe.wait_ge(o_taken.sem, o_taken.at(0, n - 2))
                        for i in range(GROUP):
                            mm = pe.transpose(bank[:, i * P:(i + 1) * P],
                                              o_tok[:, GROUP * g + i, c * P:(c + 1) * P], k.ident[:, :])
                        mm.then_inc(o_turned.sem, 1)
                        if c == 0:
                            pe.wait_ge(norm.y_free.sem, norm.y_free.at(0, g - 2))
                        pe.wait_ge(o_taken.sem, o_taken.at(0, n))
                        for i in range(GROUP):
                            last = c == chunks - 1 and bias is None
                            mm = pe.matmul(y[:, i * C:(i + 1) * C], oT[:, n % 2, i * P:(i + 1) * P],
                                           wo[:, c * C:(c + 1) * C], start=(c == 0 and i == 0),
                                           stop=last and i == GROUP - 1, skip_group_check=True)
                    if bias is not None:
                        for i in range(GROUP):
                            mm = pe.matmul(y[:, i * C:(i + 1) * C], k.ones[0:1, 0:P], bias,
                                           start=False, stop=i == GROUP - 1, skip_group_check=True)
                    mm.then_inc(norm.y_full.sem, 1)
                if g >= 1:
                    norm.tensor(pe, 0, g - 1, (g - 1) % 2, k.ps_scores[0])

        @block.scalar
        def _(act):
            norm.start(None, None, act)
            o_taken.start(act)
            for g in range(NG + 1):
                if g < NG:
                    for c in range(chunks):
                        n = g * chunks + c
                        act.wait_ge(o_turned.sem, o_turned.at(0, n))
                        nc.scalar.copy(oT[:, n % 2, :], k.ps_turned[n % 2][:, :]).then_inc(o_taken.sem, 1)
                if g >= 1:
                    norm.scalar_store(act, 0, g - 1, k.ps_scores[0], xcol(g - 1))
                if g < NG and normed:
                    norm.scalar_root(act, 0, g, g % 2)
            act.wait_ge(norm.xT_ready.sem, norm.xT_ready.at(0, NG - 1))

        @block.vector
        def _(dve):
            norm.start(None, dve, None)
            chain = Count(dve, own)
            for g in range(NG):
                norm.vector(dve, chain, 0, g, g % 2, GROUP * g, k.ps_out[g % 2][:, :], normed=normed)


def add_norm(k, name, y):
    nc = k.nc
    with ExitStack() as ctx:
        own = k.sem(name + "_own_dve", ctx)
        norm = Norm(k, ctx, name, NG)
        block = ctx.enter_context(nc.Block())

        @block.tensor
        def _(pe):
            norm.start(pe, None, None)
            for g in range(NG):
                norm.tensor(pe, 0, g, g % 2, k.ps_scores[0])

        @block.scalar
        def _(act):
            norm.start(None, None, act)
            for g in range(NG + 1):
                if g < NG:
                    norm.scalar_root(act, 0, g, g % 2)
                if g >= 1:
                    norm.scalar_store(act, 0, g - 1, k.ps_scores[0], xcol(g - 1))
            act.wait_ge(norm.xT_ready.sem, norm.xT_ready.at(0, NG - 1))

        @block.vector
        def _(dve):
            norm.start(None, dve, None)
            chain = Count(dve, own)
            norm.vector_pipelined(dve, chain, 0, [((g, g % 2, GROUP * g, y[:, g * 512:(g + 1) * 512]),
                                                   dict(wait_y=False)) for g in range(NG)])


def project_turned(k, name, groups, chunks, oT, w, w_dram, bias, bias_dram, normed=True):
    nc = k.nc
    n_g = len(groups)
    with ExitStack() as ctx:
        sem = lambda n: k.sem(name + n, ctx)
        w_loaded = sem("_w_loaded")
        own = sem("_own_dve")
        norm = Norm(k, ctx, name, n_g)
        block = ctx.enter_context(nc.Block())

        @block.sync
        def _(sp):
            if w_dram is not None:
                sp.dma_start(w, w_dram).then_inc(w_loaded, 16)
                if bias is not None:
                    sp.dma_start(bias, bias_dram).then_inc(w_loaded, 16)

        @block.tensor
        def _(pe):
            norm.start(pe, None, None)
            if w_dram is not None:
                pe.wait_ge(w_loaded, 32 if bias is not None else 16)
            for e in range(n_g + 2):
                if e < n_g:
                    y = k.ps_out[e % 2]
                    pe.wait_ge(norm.y_free.sem, norm.y_free.at(0, e - 2) if e >= 2 else 1)
                    for i in range(GROUP):
                        for c in range(chunks):
                            mm = pe.matmul(y[:, i * C:(i + 1) * C], oT(c, GROUP * groups[e] + i), w[:, c, :],
                                           start=c == 0, stop=c == chunks - 1 and bias is None)
                        if bias is not None:
                            mm = pe.matmul(y[:, i * C:(i + 1) * C], k.ones[0:1, 0:P], bias, start=False, stop=True)
                    mm.then_inc(norm.y_full.sem, 1)
                if e >= 2:
                    norm.tensor(pe, 0, e - 2, e % 2, k.ps_scores[0])

        @block.scalar
        def _(act):
            norm.start(None, None, act)
            for e in range(n_g + 2):
                if e < n_g and normed:
                    norm.scalar_root(act, 0, e, e % 2)
                if e >= 2:
                    norm.scalar_store(act, 0, e - 2, k.ps_scores[0], xcol(groups[e - 2]))
            act.wait_ge(norm.xT_ready.sem, norm.xT_ready.at(0, n_g - 1))

        @block.vector
        def _(dve):
            norm.start(None, dve, None)
            chain = Count(dve, own)
            norm.vector_pipelined(dve, chain, 0, [((e, e % 2, GROUP * groups[e], k.ps_out[e % 2][:, :]),
                                                   dict(normed=normed)) for e in range(n_g)])



L0_HEADS, L0_D, SEG, DIL = 16, 8, 64, 4
L0_HID, L0_STAGES = 512, 9
L0_GROUPS = 10


class Butterflies:

    PASS = 2 * L0_STAGES

    def __init__(self, k, ctx):
        sb = lambda n, s: k.sb("f0_" + n, s, ctx=ctx)
        self.up = sb("up", [P, 2, L0_HID])
        self.upb = sb("up_bias_row", [1, 2, L0_HID])
        self.down = sb("down", [P, 2, L0_HID])

    def work_space(self, k, ctx):
        self.coef = k.sb("f0_coef", [P, L0_STAGES * 1024], ctx=ctx)
        self.tmp = k.sb("f0_tmp", [P, 2, L0_HID], ctx=ctx)

    def load(self, sp, k, loaded, own):
        d = k.dram
        sp.dma_start(self.coef[:, :], d["L0_down_weights"].partition_broadcast(P)).then_inc(loaded[0], 16)
        sp.dma_start(self.down[:, 0, :], d["L0_W_con_T"]).then_inc(loaded[0], 16)
        sp.dma_start(self.up[:, 0, :], d["L0_ffn_W_exp"]).then_inc(loaded[1], 16)
        sp.dma_start(self.upb[:, 0, :], d["L0_ffn_b_exp"]).then_inc(loaded[1], 16)
        sp.wait_ge(own, L0_STAGES * 6)
        sp.dma_start(self.coef[:, :], d["L0_up_weights"].partition_broadcast(P)).then_inc(loaded[1], 16)

    def part(self, eng, own, pass_, n):
        rows, buf = ((P, self.down), (P, self.up), (1, self.upb))[pass_]
        down = pass_ == 0
        n, sums = divmod(n, 2)
        stage = L0_STAGES - 1 - n if down else n
        s = 2 ** stage
        own.wait()
        if sums:
            dst = buf[0:rows, (n + 1) % 2, :].rearrange("p (n o s) -> p n o s", o=2, s=s)
            t = self.tmp[0:rows, :, :].rearrange("p i (o n s) -> p i n o s", o=2, s=s)
            for o in range(2):
                own.done(eng.tensor_tensor(dst[:, :, o, :], t[:, 0, :, o, :], t[:, 1, :, o, :], ALU.add))
            return
        src = buf[0:rows, n % 2, :].rearrange("p (n i s) -> p n i s", i=2, s=s)
        w = self.coef[0:rows, stage * 1024:(stage + 1) * 1024].rearrange("p (n s o i) -> p n o i s", s=s, o=2, i=2)
        for o in range(2):
            for i in range(2):
                block = w[:, :, i, o, :] if down else w[:, :, o, i, :]
                t = self.tmp[0:rows, i, o * 256:(o + 1) * 256].rearrange("p (n s) -> p n s", s=s)
                own.done(eng.tensor_tensor(t, src[:, :, i, :], block, ALU.mult))


def l0(k):
    with ExitStack() as ctx:
        mats = Butterflies(k, ctx)
        l0_attention(k, mats)
        l0_ffn(k, mats)


def l0_attention(k, mats):
    nc, d = k.nc, k.dram
    with ExitStack() as ctx:
        sem = lambda n: k.sem("l0_" + n, ctx)
        sb = lambda n, s: k.sb("l0_" + n, s, ctx=ctx)
        wq, wk, wv, wo = (sb(n, [P, C]) for n in ("wq", "wk", "wv", "wo"))
        bqk = sb("bqk", [P, 2])
        bv, bo = sb("bv", [P, C]), sb("bo", [1, C])
        hmask = sb("hmask", [P, L0_HEADS])
        gweight = sb("gweight", [P, TPB, L0_GROUPS])
        qT = sb("qT", [P, B * L])
        kT = sb("kT", [P, B * XB])
        v_own = sb("v_own", [P, TILES, C])
        v_dil = sb("v_dil", [P, TILES, C])
        qm = sb("q_masked", [P, 2, B * L])
        o_tok = sb("o_tok", [P, TILES, C])
        probs = sb("probs", [P, 4, 1024])
        probsT = sb("probsT", [P, 2, 1024])
        gmax = sb("gmax", [P, 2, 4, L0_GROUPS])
        gsum = sb("gsum", [P, 2, 4, L0_GROUPS])
        ginv = sb("ginv", [P, 2, 4, L0_GROUPS])
        hcol = sb("hcol", [P, 2])

        with ExitStack() as c2:
            loaded, wo_loaded, proj_full, proj_taken = (k.sem("l0p_" + n, c2) for n in (
                "loaded", "wo_loaded", "full", "taken"))
            block = c2.enter_context(nc.Block())
            xb = lambda t: (t // TPB) * XB + (t % TPB) * P
            jobs = ([("q", i) for i in range(4)] + [("k", i) for i in range(6)]
                    + [("v", i) for i in range(4)] + [("vd", i) for i in range(4)])
            QK_JOBS = 10

            @block.sync
            def _(sp):
                for out, src in ((wq, d["L0_attn_Wq"]), (wk, d["L0_attn_Wk"]), (wv, d["L0_attn_Wv"]),
                                 (bqk, d["L0_bqk"]), (bv, d["L0_bv"].partition_broadcast(P)),
                                 (hmask, d["head_mask8"])):
                    sp.dma_start(out[:, :], src).then_inc(loaded, 16)
                sp.dma_start(gweight[:, :, :], d["L0_group_weights"]).then_inc(loaded, 16)
                sp.dma_start(wo[:, :], d["L0_attn_Wo"]).then_inc(wo_loaded, 16)
                sp.dma_start(bo[:, :], d["L0_attn_bo"]).then_inc(wo_loaded, 16)
                sp.wait_ge(wo_loaded, 32)

            @block.tensor
            def _(pe):
                pe.wait_ge(loaded, 16 * 7)
                for n, (kind, i) in enumerate(jobs):
                    bank = k.ps_out[n % 2]
                    if n >= 2:
                        pe.wait_ge(proj_taken, n - 1)
                    if kind == "q":
                        mm = pe.matmul(bank[:, :], wq[:, :], k.xT[:, xcol(i):xcol(i) + 512], start=True, stop=True)
                    elif kind == "k":
                        w = min(512, B * XB - i * 512)
                        mm = pe.matmul(bank[:, 0:w], wk[:, :], k.xT[:, i * 512:i * 512 + w], start=True, stop=True)
                    else:
                        for s in range(GROUP):
                            c0 = xb(GROUP * i + s)
                            x = (k.xT[:, c0 + PAD:c0 + PAD + P] if kind == "v" else
                                 k.xT[:, c0:c0 + (P - 1) * DIL + 1:DIL])
                            mm = pe.matmul(bank[:, s * C:(s + 1) * C], x, wv[:, :], start=True, stop=True)
                    mm.then_inc(proj_full, 1)

            @block.scalar
            def _(act):
                for n, (kind, i) in enumerate(jobs[:QK_JOBS]):
                    bank = k.ps_out[n % 2]
                    act.wait_ge(proj_full, n + 1)
                    if kind == "q":
                        ins = nc.scalar.activation(qT[:, i * 512:(i + 1) * 512], bank[:, :], ACT.Identity,
                                                   bias=bqk[:, 0:1])
                    elif kind == "k":
                        w = min(512, B * XB - i * 512)
                        ins = nc.scalar.activation(kT[:, i * 512:i * 512 + w], bank[:, 0:w], ACT.Identity,
                                                   bias=bqk[:, 1:2])
                    ins.then_inc(proj_taken, 1)
                act.wait_ge(proj_taken, QK_JOBS)

            @block.vector
            def _(dve):
                dve.wait_ge(proj_taken, QK_JOBS)
                for n, (kind, i) in list(enumerate(jobs))[QK_JOBS:]:
                    dve.wait_ge(proj_full, n + 1)
                    v = v_own if kind == "v" else v_dil
                    nc.vector.tensor_tensor(v[:, GROUP * i:GROUP * (i + 1), :],
                                            k.ps_out[n % 2][:, :].rearrange("p (t c) -> p t c", c=C),
                                            bv[:, :].unsqueeze(1).broadcast_to([P, GROUP, C]), ALU.add
                                            ).then_inc(proj_taken, 1)
                dve.wait_ge(proj_taken, len(jobs))

        with ExitStack() as c2:
            sm = lambda n: k.sem("l0a_" + n, c2)
            U, HEADS_A_TURN, RING, LAG = 8, 2, 4, 3
            PER_HEAD = U // HEADS_A_TURN
            TURNS = L0_HEADS // HEADS_A_TURN
            s_full = [Signal(sm(f"scores_full{i}"), U // 2) for i in range(2)]
            s_free = [Signal(sm(f"scores_free{i}"), U // 2) for i in range(2)]
            q_ready = Signal(sm("q_ready"), HEADS_A_TURN * B)
            shifted = Signal(sm("shifted"), U)
            e_raw = Signal(sm("exp_done"), U)
            e_full = Signal(sm("probs_ready"), U)
            inv_ready = Signal(sm("inv_ready"), U)
            t_full = [Signal(sm(f"turned_full{i}"), U) for i in range(2)]
            t_done = [Signal(sm(f"turned_taken{i}"), U) for i in range(2)]
            o_full = Signal(sm("out_full"), HEADS_A_TURN)
            o_free = Signal(sm("out_taken"), HEADS_A_TURN)
            hc = Signal(sm("mask_column"), HEADS_A_TURN)
            maxed = Signal(sm("own_max"), U * 2)
            subbed = Signal(sm("own_shift"), U)
            added = Signal(sm("own_sums"), U * 3)
            mats_loaded, mats_own = [sm(f"mats_loaded{i}") for i in range(2)], sm("mats_own")
            mats.work_space(k, c2)
            pass_at = (0, 25, 25 + mats.PASS)
            block = c2.enter_context(nc.Block())
            o_bank = [k.ps_out[j][:, 0:TILES * L0_D].rearrange("p (t c) -> p t c", c=L0_D) for j in range(2)]

            def turn_plan(own, before):
                out = []
                for n in range(U):
                    if own:
                        out.append(("S", n, 0))
                    for what, u in (("D", n - 1), ("T", n - LAG), ("V", n - LAG - 1)):
                        if own if u >= 0 else before:
                            out.append((what, u % U, int(u < 0)))
                return out

            def turns(eng, body):
                body(0, turn_plan(True, False))
                with eng.Fori(1, TURNS - 1) as t:
                    body(t, turn_plan(True, True))
                body(TURNS - 1, turn_plan(True, True))
                body(TURNS, turn_plan(False, True))

            def groups(t, s):
                v = t[:, s, :] if len(t.shape) == 3 else t[:, :]
                v = v.rearrange("p (t q) -> p t q", t=4)
                return (v[:, :, 0:P].rearrange("p t (g q) -> p t g q", g=2),
                        v[:, :, P:2 * P].rearrange("p t (g q) -> p t g q", g=8))

            def wide(v, s, shape, a, b):
                return v[:, s, :, a:b].unsqueeze(3).broadcast_to(shape)

            @block.sync
            def _(sp):
                mats.load(sp, k, mats_loaded, mats_own)

            @block.gpsimd
            def _(pool):
                for s in (q_ready, e_full, hc):
                    s.start(pool)

                def mask(t, j, wait=True):
                    pool.wait_ge(q_ready.sem, q_ready.at(t, B * j - 1))
                    nc.gpsimd.tensor_copy(hcol[:, j:j + 1], hmask[:, ds(t * HEADS_A_TURN + j, 1)]
                                          ).then_inc(hc.sem, 1)
                    pool.wait_ge(hc.sem, hc.at(t, j))
                    for b in range(B):
                        if wait:
                            pool.wait_ge(s_full[1].sem, s_full[1].at(t, (PER_HEAD * j + 2 * b + 1) // 2 - U // 2))
                        nc.gpsimd.tensor_tensor(qm[:, j, b * L:(b + 1) * L], qT[:, b * L:(b + 1) * L],
                                                hcol[:, j:j + 1].broadcast_to([P, L]), ALU.mult
                                                ).then_inc(q_ready.sem, 1)

                def body(t, plan):
                    for what, u, back in plan:
                        it = t - back
                        if what == "D":
                            pool.wait_ge(e_raw.sem, e_raw.at(it, u))
                            pool.wait_ge(inv_ready.sem, inv_ready.at(it, u))
                            eo, ed = groups(probs, u % RING)
                            nc.gpsimd.tensor_tensor(eo, eo, wide(ginv, u % 2, [P, 4, 2, SEG], 0, 2), ALU.mult)
                            nc.gpsimd.tensor_tensor(ed, ed, wide(ginv, u % 2, [P, 4, 8, 16], 2, 10), ALU.mult
                                                    ).then_inc(e_full.sem, 1)
                            for i, at in enumerate(pass_at):
                                n = it * U + u - at
                                if n == 0 and i < 2:
                                    pool.wait_ge(mats_loaded[i], (32, 48)[i])
                                if 0 <= n < mats.PASS:
                                    mats.part(nc.gpsimd, own, i, n)
                        elif what == "S" and u == 0:
                            mask(t, 1, t > 0)
                        elif what == "S" and u == PER_HEAD and t < TURNS - 1:
                            mask(t + 1, 0)

                own = Count(pool, mats_own)
                mask(0, 0, False)
                body(0, turn_plan(True, False))
                for t in range(1, TURNS):
                    body(t, turn_plan(True, True))
                body(TURNS, turn_plan(False, True))
                own.wait()

            @block.tensor
            def _(pe):
                for s in (*s_full, *t_full, o_full):
                    s.start(pe)

                def body(t, plan):
                    for what, u, back in plan:
                        it, j, uu = t - back, u // PER_HEAD, u % PER_HEAD
                        if what == "S":
                            slot, b = u % 2, uu // 2
                            pe.wait_ge(s_free[slot].sem, s_free[slot].at(it, u // 2 - 1))
                            if uu % 2 == 0:
                                pe.wait_ge(q_ready.sem, q_ready.at(it, B * j + b))
                            for i in range(4):
                                tile = (4 * uu + i) % TPB
                                qs = qm[:, j, b * L + tile * P:b * L + (tile + 1) * P]
                                c0 = b * XB + tile * P
                                pe.matmul(k.ps_scores[slot][:, i * 256:i * 256 + P], qs,
                                          kT[:, c0 + PAD:c0 + PAD + P], start=True, stop=True)
                                mm = pe.matmul(k.ps_scores[slot][:, i * 256 + P:(i + 1) * 256], qs,
                                               kT[:, c0:c0 + (P - 1) * DIL + 1:DIL], start=True, stop=True)
                            mm.then_inc(s_full[slot].sem, 1)
                        elif what == "T":
                            pe.wait_ge(e_full.sem, e_full.at(it, u))
                            turn(pe, k, probs[:, u % RING, :], t_full, t_done, it, u)
                        elif what == "V":
                            for half in range(2):
                                pe.wait_ge(t_done[half].sem, t_done[half].at(it, u))
                            if uu == 0:
                                pe.wait_ge(o_free.sem, o_free.at(it, j - 2))
                            for i in range(4):
                                tile = 4 * uu + i
                                for part, v in enumerate((v_own, v_dil)):
                                    c0 = (2 * i + part) * P
                                    mm = pe.matmul(o_bank[j][:, tile, :], probsT[:, u % 2, c0:c0 + P],
                                                   v[:, tile, ds((it * HEADS_A_TURN + j) * L0_D, L0_D)],
                                                   start=part == 0, stop=part == 1)
                            if uu == PER_HEAD - 1:
                                mm.then_inc(o_full.sem, 1)

                turns(pe, body)

            @block.vector
            def _(dve):
                for s in (*s_free, shifted, inv_ready, maxed, subbed, added):
                    s.start(dve)

                def body(t, plan):
                    for what, u, back in plan:
                        it, s = t - back, u % 2
                        eo, ed = groups(probs, u % RING)
                        if what == "S":
                            scores, sd = groups(k.ps_scores[s], s)
                            dve.wait_ge(s_full[s].sem, s_full[s].at(it, u // 2))
                            nc.vector.tensor_reduce(gmax[:, s, :, 0:2], scores, AX.X, ALU.max
                                                    ).then_inc(maxed.sem, 1)
                            nc.vector.tensor_reduce(gmax[:, s, :, 2:10], sd, AX.X, ALU.max).then_inc(maxed.sem, 1)
                            dve.wait_ge(maxed.sem, maxed.at(it, 2 * u + 1))
                            dve.wait_ge(t_full[1].sem, t_full[1].at(it, u - RING))
                            nc.vector.tensor_tensor(eo, scores, wide(gmax, s, [P, 4, 2, SEG], 0, 2), ALU.subtract
                                                    ).then_inc(subbed.sem, 1)
                            nc.vector.tensor_tensor(ed, sd, wide(gmax, s, [P, 4, 8, 16], 2, 10), ALU.subtract
                                                    ).then_inc(shifted.sem, 1)
                            dve.wait_ge(shifted.sem, shifted.at(it, u))
                            dve.sem_inc(s_free[s].sem, 1)
                        elif what == "D":
                            dve.wait_ge(e_raw.sem, e_raw.at(it, u))
                            dve.wait_ge(e_full.sem, e_full.at(it, u - 2))
                            nc.vector.tensor_reduce(gsum[:, s, :, 0:2], eo, AX.X, ALU.add).then_inc(added.sem, 1)
                            nc.vector.tensor_reduce(gsum[:, s, :, 2:10], ed, AX.X, ALU.add).then_inc(added.sem, 1)
                            dve.wait_ge(added.sem, added.at(it, 3 * u + 1))
                            nc.vector.reciprocal(ginv[:, s, :, :], gsum[:, s, :, :]).then_inc(added.sem, 1)
                            dve.wait_ge(added.sem, added.at(it, 3 * u + 2))
                            j0 = (4 * u) % TPB
                            nc.vector.tensor_tensor(ginv[:, s, :, :], ginv[:, s, :, :],
                                                    gweight[:, j0:j0 + 4, :], ALU.mult).then_inc(inv_ready.sem, 1)

                turns(dve, body)

            @block.scalar
            def _(act):
                for s in (e_raw, *t_done, o_free):
                    s.start(act)

                def body(t, plan):
                    for what, u, back in plan:
                        it, j = t - back, u // PER_HEAD
                        if what == "S":
                            act.wait_ge(shifted.sem, shifted.at(it, u))
                            nc.scalar.activation(probs[:, u % RING, :], probs[:, u % RING, :], ACT.Exp
                                                 ).then_inc(e_raw.sem, 1)
                        elif what == "T":
                            for half in range(2):
                                take_turned(nc.scalar, k, probsT[:, u % 2, :], t_full, t_done, it, u, half)
                        elif what == "V" and u % PER_HEAD == PER_HEAD - 1:
                            act.wait_ge(o_full.sem, o_full.at(it, j))
                            nc.scalar.copy(o_tok[:, :, ds((it * HEADS_A_TURN + j) * L0_D, L0_D)], o_bank[j]
                                           ).then_inc(o_free.sem, 1)

                turns(act, body)

        project_out(k, "l0o", o_tok, 1, wo[:, :], None, bo[:, :], None)


def every(half, u):
    return u


def turn(pe, k, probs, t_full, t_done, it, u, blocks=8, event=every):
    for half in range((blocks + 3) // 4):
        e = event(half, u)
        pe.wait_ge(t_done[half].sem, t_done[half].at(it, e - 1))
        for c in range(4 * half, min(blocks, 4 * half + 4)):
            mm = pe.transpose(k.ps_turned[half][:, (c % 4) * P:(c % 4 + 1) * P], probs[:, c * P:(c + 1) * P],
                              k.ident[:, :])
        mm.then_inc(t_full[half].sem, 1)


def take_turned(eng, k, probsT, t_full, t_done, it, u, half, blocks=8, event=every):
    n = min(4, blocks - 4 * half)
    eng.wait_ge(t_full[half].sem, t_full[half].at(it, event(half, u)))
    out, src = probsT[:, half * 512:half * 512 + n * P], k.ps_turned[half][:, 0:n * P]
    ins = eng.copy(out, src) if eng is k.nc.scalar else eng.tensor_copy(out, src)
    ins.then_inc(t_done[half].sem, 1)



def l0_ffn(k, mats):
    nc, d = k.nc, k.dram
    CH = L0_HID // P
    with ExitStack() as ctx:
        sb = lambda n, s: k.sb("f0_" + n, s, ctx=ctx)
        up, upb, down = mats.up, mats.upb, mats.down
        w_down = sb("w_down", [P, CH * C])
        bias_h = sb("bias_h", [P, CH])
        up_bias = sb("up_bias", [P, CH])
        bias_y = sb("bias_y", [2, C])
        hid = sb("hid", [P, 2, CH, 512])
        with ExitStack() as c2:
            loaded, turned, taken = (k.sem("f0_" + n, c2) for n in ("loaded", "down_turned", "taken"))
            block = c2.enter_context(nc.Block())

            @block.sync
            def _(sp):
                sp.dma_start(up_bias[:, :], d["L0_up_bias"]).then_inc(loaded, 16)
                sp.dma_start(bias_y[:, :], d["L0_y_bias"]).then_inc(loaded, 16)

            @block.tensor
            def _(pe):
                for c in range(CH):
                    mm = pe.transpose(k.ps_turned[0][:, c * P:(c + 1) * P], down[:, 1, c * P:(c + 1) * P],
                                      k.ident[:, :])
                mm.then_inc(turned, 1)
                for c in range(CH):
                    mm = pe.matmul(k.ps_turned[1][:, c:c + 1], upb[:, 1, c * P:(c + 1) * P], k.ones[0:1, 0:1],
                                   start=True, stop=True)
                mm.then_inc(turned, 1)

            @block.vector
            def _(dve):
                dve.wait_ge(turned, 1)
                nc.vector.tensor_copy(w_down[:, :], k.ps_turned[0][:, :]).then_inc(taken, 1)
                dve.wait_ge(loaded, 32)
                dve.wait_ge(turned, 2)
                nc.vector.tensor_tensor(bias_h[:, :], k.ps_turned[1][:, 0:CH], up_bias[:, :], ALU.add
                                        ).then_inc(taken, 1)
                dve.wait_ge(taken, 2)

        feed_forward(k, "f0", hid, CH, [P] * CH, lambda c: up[:, 1, c * P:(c + 1) * P],
                     lambda c: w_down[:, c * C:(c + 1) * C], bias_y[:, :],
                     lambda c: (ACT.Gelu, bias_h[:, c:c + 1]))


def feed_forward(k, name, hid, chunks, rows, w_up, w_down, bias_y, act_of):
    nc = k.nc
    HALVES = NG // B
    with ExitStack() as ctx:
        sem = lambda n: k.sem(name + n, ctx)
        per = HALVES * chunks // 2
        h_full = [Signal(sem(f"_h_full{i}"), per) for i in range(2)]
        h_ready = [Signal(sem(f"_h_ready{i}"), per) for i in range(2)]
        own = Signal(sem("_own_dve"), HALVES * Norm.DVE_STEPS)
        norm = Norm(k, ctx, name, HALVES)
        block = ctx.enter_context(nc.Block())

        @block.tensor
        def _(pe):
            norm.start(pe, None, None)
            for s in h_full:
                s.start(pe)
            with pe.Fori(0, B) as b:
                for g in range(HALVES):
                    for c in range(chunks):
                        n = g * chunks + c
                        pe.wait_ge(h_ready[n % 2].sem, h_ready[n % 2].at(b, n // 2 - 1))
                        pe.matmul(k.ps_scores[n % 2][0:rows[c], 0:512], w_up(c),
                                  k.xT[:, ds(b * XB + PAD + g * 512, 512)], start=True, stop=True
                                  ).then_inc(h_full[n % 2].sem, 1)
                for g in range(HALVES):
                    y = k.ps_out[g]
                    pe.wait_ge(norm.y_free.sem, norm.y_free.at(b, g - 2))
                    for c in range(chunks):
                        n = g * chunks + c
                        pe.wait_ge(h_ready[n % 2].sem, h_ready[n % 2].at(b, n // 2))
                        for i in range(GROUP):
                            pe.matmul(y[:, i * C:(i + 1) * C], hid[0:rows[c], g, c, i * P:(i + 1) * P], w_down(c),
                                      start=(c == 0 and i == 0), stop=False, skip_group_check=True)
                    kb = bias_y.shape[0]
                    for i in range(GROUP):
                        mm = pe.matmul(y[:, i * C:(i + 1) * C], k.ones[0:kb, 0:P], bias_y, start=False,
                                       stop=i == GROUP - 1, skip_group_check=True)
                    mm.then_inc(norm.y_full.sem, 1)
                for g in range(HALVES):
                    norm.tensor(pe, b, g, g, k.ps_turned[0])

        @block.scalar
        def _(act):
            norm.start(None, None, act)
            for s in h_ready:
                s.start(act)
            with act.Fori(0, B) as b:
                for g in range(HALVES):
                    for c in range(chunks):
                        n = g * chunks + c
                        func, bias = act_of(c)
                        act.wait_ge(h_full[n % 2].sem, h_full[n % 2].at(b, n // 2))
                        nc.scalar.activation(hid[0:rows[c], g, c, :], k.ps_scores[n % 2][0:rows[c], 0:512], func,
                                             bias=bias).then_inc(h_ready[n % 2].sem, 1)
                for g in range(HALVES):
                    norm.scalar_root(act, b, g, g)
                for g in range(HALVES):
                    norm.scalar_store(act, b, g, k.ps_turned[0], b * XB + PAD + g * 512)

        @block.vector
        def _(dve):
            norm.start(None, dve, None)
            own.start(dve)
            with dve.Fori(0, B) as b:
                chain = Chain(dve, own, b)
                for g in range(HALVES):
                    norm.vector(dve, chain, b, g, g, b * TPB + g * GROUP, k.ps_out[g][:, :])
                chain.close()



L1_HEADS, L1_D = 16, 64
PAIRS = L1_HEADS // 2
TABLE = 2 * L - P
TWO_PI = 2 * np.pi
PI_A = 6.28125
PI_B = float(np.floor((TWO_PI - PI_A) * 2 ** 19) / 2 ** 19)
PI_C = float(TWO_PI - PI_A - PI_B)
ROUND = 1.5 * 2 ** 23


def l1_attention(k):
    nc, d = k.nc, k.dram
    LEAD, U = 6, 16
    RING, LAG = 4, 3
    with ExitStack() as ctx:
        sb = lambda n, s: k.sb("l1_" + n, s, ctx=ctx)
        y = sb("y", [P, TILES * C])
        with ExitStack() as c2:
            sb = lambda n, s, dt=F32: k.sb("l1_" + n, s, dt, ctx=c2)
            rope = sb("rope", [P, 4, L])
            dist = sb("dist", [P, TABLE])
            logs_ = sb("logs", [P, 2, TABLE])
            nbias = sb("neg_bias", [P, 2, TABLE])
            ap = sb("bias_ap", [P, 2 * L1_HEADS])
            cols = sb("bias_cols", [P, 4])
            w = sb("w", [P, 5 * P])
            wo = sb("wo", [P, PAIRS * C])
            head = sb("head_rows", [P, 2])
            q = sb("q", [P, B, 2, L])
            kr = sb("k", [P, B, L])
            v = sb("v", [P, B, TPB, P])
            rot = sb("rot", [P, 2, 2, 512])
            probs = sb("probs", [P, RING, 1024])
            probsT = sb("probsT", [P, 2, 1024])
            oT = sb("oT", [P, 2, 512])
            nmax = sb("neg_max", [P, U])
            rsum = sb("row_sum", [P, U])
            rinv = sb("row_inv", [P, U])
            with ExitStack() as c3:
                sem = lambda n: k.sem("l1t_" + n, c3)
                loaded, made, own, roots = sem("loaded"), sem("iotas"), sem("own_dve"), sem("acts")
                wo_loaded = sem("wo_loaded")
                ints = k.sb("l1_ints", [P, TABLE], mybir.dt.int32, ctx=c3)
                posi = k.sb("l1_posi", [P, L], mybir.dt.int32, ctx=c3)
                freq = k.sb("l1_freq", [P, 3], ctx=c3)
                ang, turns = (k.sb("l1_" + n, [P, L], ctx=c3) for n in ("ang", "turns"))
                block = c3.enter_context(nc.Block())

                @block.sync
                def _(sp):
                    sp.dma_start(freq[:, :], d["L1_freq"]).then_inc(loaded, 16)
                    sp.dma_start(ap[:, :], d["L1_bias_ap"].partition_broadcast(P)).then_inc(loaded, 16)
                    sp.dma_start(wo[:, :], d["L1_out_w"]).then_inc(wo_loaded, 16)
                    sp.wait_ge(wo_loaded, 16)

                @block.gpsimd
                def _(pool):
                    nc.gpsimd.iota(posi[:, :], [[1, L]], base=0, channel_multiplier=0).then_inc(made, 1)
                    nc.gpsimd.iota(ints[:, :], [[1, TABLE]], base=P - L, channel_multiplier=-1).then_inc(made, 1)
                    nc.gpsimd.memset(head[:, :], 1.0).then_inc(made, 1)
                    pool.wait_ge(made, 3)
                    nc.gpsimd.affine_select(out=head[:, 0:1], in_=head[:, 0:1], compare_op=ALU.is_ge, fill=0.0,
                                            base=L1_D - 1, pattern=[[0, 1]], channel_multiplier=-1)
                    nc.gpsimd.affine_select(out=head[:, 1:2], in_=head[:, 1:2], compare_op=ALU.is_ge, fill=0.0,
                                            base=-L1_D, pattern=[[0, 1]], channel_multiplier=1).then_inc(made, 1)
                    pool.wait_ge(made, 4)

                @block.vector
                def _(dve):
                    c = Count(dve, own)
                    v_ = nc.vector
                    dve.wait_ge(loaded, 32)
                    dve.wait_ge(made, 2)
                    c.done(v_.tensor_scalar(ap[:, :], ap[:, :], 0.01, None, ALU.max))
                    c.done(v_.tensor_copy(dist[:, :], ints[:, :]))
                    c.step(v_.tensor_copy(turns[:, :], posi[:, :]))
                    c.step(v_.tensor_scalar(ang[:, :], turns[:, :], freq[:, 0:1], None, ALU.mult))
                    c.step(v_.tensor_scalar(turns[:, :], ang[:, :], 1 / TWO_PI, ROUND, ALU.mult, ALU.add))
                    c.step(v_.tensor_scalar(turns[:, :], turns[:, :], ROUND, None, ALU.subtract))
                    for part in (PI_A, PI_B, PI_C):
                        c.step(v_.scalar_tensor_tensor(ang[:, :], turns[:, :], -part, ang[:, :], ALU.mult, ALU.add))
                    c.step(v_.tensor_scalar(ang[:, :], ang[:, :], 3.1415925, -3.1415925, ALU.min, ALU.max))
                    dve.wait_ge(roots, 4)
                    c.done(v_.tensor_scalar(rope[:, 3, :], rope[:, 1, :], freq[:, 1:2], None, ALU.mult))
                    c.done(v_.tensor_scalar(rope[:, 2, :], rope[:, 0, :], 1.0, None, ALU.mult))
                    c.step(v_.tensor_scalar(rope[:, 0, :], rope[:, 0, :], -0.125, None, ALU.mult))
                    c.step(v_.tensor_scalar(rope[:, 1, :], rope[:, 1, :], freq[:, 1:2], -0.125, ALU.mult, ALU.mult))

                @block.scalar
                def _(act):
                    act.wait_ge(own, 2)
                    nc.scalar.activation(dist[:, :], dist[:, :], ACT.Abs).then_inc(roots, 1)
                    act.wait_ge(own, 10)
                    nc.scalar.activation(rope[:, 1, :], ang[:, :], ACT.Sin).then_inc(roots, 1)
                    nc.scalar.activation(turns[:, :], ang[:, :], ACT.Abs).then_inc(roots, 1)
                    act.wait_ge(roots, 3)
                    nc.scalar.activation(rope[:, 0, :], turns[:, :], ACT.Sin, bias=freq[:, 2:3], scale=-1.0
                                         ).then_inc(roots, 1)

            with ExitStack() as c3:
                sm = lambda n: k.sem("l1a_" + n, c3)
                SLOTS = LEAD + U
                lead_full = [sm(f"lead_full{i}") for i in range(2)]
                lead_free = [sm(f"lead_free{i}") for i in range(2)]
                s_full = [Signal(sm(f"slot_full{i}"), SLOTS // 2) for i in range(2)]
                s_free = [Signal(sm(f"slot_free{i}"), SLOTS // 2) for i in range(2)]
                w_loaded = sm("w_loaded")
                cols_ready = Signal(sm("cols"), 4)
                logs = Signal(sm("log1p"), 2)
                bias_ready = Signal(sm("bias_ready"), 2)
                rotated = Signal(sm("rotated"), 4)
                prod = Signal(sm("rot_first"), 4)
                summed = Signal(sm("q_summed"), 2)
                qk_ready = Signal(sm("qk_ready"), 4)
                v_ready = Signal(sm("v_ready"), 2)
                e_full = Signal(sm("exp_done"), U)
                inv_ready = Signal(sm("inv_ready"), U)
                p_full = Signal(sm("probs_ready"), U)
                t_full = [Signal(sm(f"turned_full{i}"), U) for i in range(2)]
                t_done = [Signal(sm(f"turned_taken{i}"), U) for i in range(2)]
                o_full = [Signal(sm(f"out_full{i}"), 1) for i in range(2)]
                o_taken = [Signal(sm(f"out_taken{i}"), 1) for i in range(2)]
                y_full = [Signal(sm(f"y_full{i}"), 1) for i in range(2)]
                y_free = [Signal(sm(f"y_added{i}"), 1) for i in range(2)]
                passed = sm("passed")

                lead_at = {2 * x + 1: x for x in range(LEAD)}

                def turn_plan(own, lead, before):
                    out, slot = [], 0
                    for n in range(U):
                        if own:
                            out.append(("S", n, 0, slot))
                            slot += 1
                        if lead and n in lead_at:
                            out.append(("P", lead_at[n], -1, slot))
                            slot += 1
                        u = n - LAG
                        back = 0 if u > 0 else 1
                        if u % 2 == 0 and (own if u > 0 else before):
                            out.append(("V", (u // 2 - 1) % TPB, back, None))
                        back = 0 if u >= 0 else 1
                        if own if u >= 0 else before:
                            out.append(("T", u % U, back, None))
                        if own and n > 11 or before and 3 < n <= 6:
                            bank = 0 if n > 11 else 1
                            out += {12: [("E", 0, 0, None)], 13: [("Y", 0, 0, None)], 14: [("A", 0, 0, None)],
                                    4: [("E", 1, 1, None)], 5: [("Y", 1, 1, None)], 6: [("A", 1, 1, None)]
                                    }.get(n, [])
                    return out

                def turns(eng, body):
                    body(0, 0, turn_plan(True, True, False))
                    body(0, 1, turn_plan(True, True, True))
                    with eng.Fori(1, PAIRS - 1) as hp:
                        body(hp, 0, turn_plan(True, True, True))
                        body(hp, 1, turn_plan(True, True, True))
                    body(PAIRS - 1, 0, turn_plan(True, True, True))
                    body(PAIRS - 1, 1, turn_plan(True, False, True))
                    body(PAIRS, 0, turn_plan(False, False, True))

                def turn_of(hp, b, back=0):
                    return hp * B + (b - back)

                def lead_tensor(pe, b, x, slot):
                    for i in range(2 if x < 4 else 4):
                        if x < 4:
                            c0, x0 = (x // 2) * 2 * P + i * P, b * XB + PAD + (x % 2) * 512
                            mm = pe.matmul(slot[:, i * 512:(i + 1) * 512], w[:, c0:c0 + P], k.xT[:, x0:x0 + 512],
                                           start=True, stop=True)
                        else:
                            x0 = b * XB + PAD + ((x - 4) * 4 + i) * P
                            mm = pe.matmul(slot[:, i * P:(i + 1) * P], k.xT[:, x0:x0 + P], w[:, 4 * P:5 * P],
                                           start=True, stop=True)
                    return mm

                def lead_vector(dve, it, b, x, slot, free):
                    dve.wait_ge(qk_ready.sem, qk_ready.at(it, x - 2))
                    half = slice((x % 2) * 512, (x % 2 + 1) * 512)
                    nc.vector.tensor_tensor(rot[:, x % 2, 0, :], slot[:, 0:512], rope[:, (x // 2) * 2, half],
                                            ALU.mult).then_inc(prod.sem, 1)
                    nc.vector.tensor_tensor(rot[:, x % 2, 1, :], slot[:, 512:1024], rope[:, (x // 2) * 2 + 1, half],
                                            ALU.mult).then_inc(rotated.sem, 1)
                    dve.wait_ge(rotated.sem, rotated.at(it, x))
                    dve.sem_inc(free, 1)

                def lead_scalar(act, it, b, x, slot, free):
                    nc.scalar.copy(v[:, b, (x - 4) * 4:(x - 3) * 4, :],
                                   slot[:, 0:512].rearrange("p (t c) -> p t c", c=P)).then_inc(v_ready.sem, 1)
                    act.wait_ge(v_ready.sem, v_ready.at(it, x - 4))
                    act.sem_inc(free, 1)

                def lead_pool(pool, it, b, x):
                    pool.wait_ge(rotated.sem, rotated.at(it, x))
                    half = slice((x % 2) * 512, (x % 2 + 1) * 512)
                    r = rot[:, x % 2, :, :]
                    if x < 2:
                        nc.gpsimd.tensor_tensor(r[:, 0, :], r[:, 0, :], r[:, 1, :], ALU.add).then_inc(summed.sem, 1)
                        pool.wait_ge(summed.sem, summed.at(it, x))
                        for j in range(2):
                            ins = nc.gpsimd.tensor_tensor(q[:, b, j, half], r[:, 0, :],
                                                          head[:, j:j + 1].broadcast_to([P, 512]), ALU.mult)
                    else:
                        ins = nc.gpsimd.tensor_tensor(kr[:, b, half], r[:, 0, :], r[:, 1, :], ALU.add)
                    ins.then_inc(qk_ready.sem, 1)

                def columns(pool, hp):
                    for i in range(4):
                        nc.gpsimd.tensor_copy(cols[:, i:i + 1], ap[:, ds(hp * 2 + ((i // 2) * L1_HEADS + i % 2), 1)]
                                              ).then_inc(cols_ready.sem, 1)

                def logarithms(act, hp):
                    act.wait_ge(cols_ready.sem, cols_ready.at(hp, 3))
                    for j in range(2):
                        nc.scalar.activation(logs_[:, j, :], dist[:, :], ACT.Ln, bias=1.0, scale=cols[:, j:j + 1]
                                             ).then_inc(logs.sem, 1)

                with nc.Block() as block:
                    @block.sync
                    def _(sp):
                        sp.dma_start(w[:, :], d["L1_qkv"][0, :, :]).then_inc(w_loaded, 16)

                    @block.gpsimd
                    def _(pool):
                        for s in (cols_ready, summed, qk_ready):
                            s.start(pool)
                        nc.gpsimd.memset(y[:, :], 0.0)
                        columns(pool, 0)
                        for x in range(4):
                            lead_pool(pool, 0, 0, x)

                    @block.tensor
                    def _(pe):
                        pe.wait_ge(w_loaded, 16)
                        for x in range(LEAD):
                            if x >= 2:
                                pe.wait_ge(lead_free[x % 2], x // 2)
                            lead_tensor(pe, 0, x, k.ps_scores[x % 2]).then_inc(lead_full[x % 2], 1)

                    @block.vector
                    def _(dve):
                        for s in (rotated, prod):
                            s.start(dve)
                        for x in range(4):
                            dve.wait_ge(lead_full[x % 2], x // 2 + 1)
                            lead_vector(dve, 0, 0, x, k.ps_scores[x % 2], lead_free[x % 2])

                    @block.scalar
                    def _(act):
                        for s in (logs, v_ready):
                            s.start(act)
                        logarithms(act, 0)
                        for x in range(4, LEAD):
                            act.wait_ge(lead_full[x % 2], x // 2 + 1)
                            lead_scalar(act, 0, 0, x, k.ps_scores[x % 2], lead_free[x % 2])

                block = c3.enter_context(nc.Block())

                @block.sync
                def _(sp):
                    with sp.Fori(0, PAIRS - 1) as hp:
                        last = [p for p in turn_plan(True, True, True) if p[0] == "P"][-1][3]
                        f = s_full[last % 2]
                        sp.wait_ge(f.sem, f.at(turn_of(hp, 0), last // 2))
                        sp.dma_start(w[:, :], d["L1_qkv"][ds(hp + 1, 1), :, :].rearrange("o p c -> p (o c)")
                                     ).then_inc(w_loaded, 16)

                @block.gpsimd
                def _(pool):
                    p_full.start(pool)

                    def body(hp, b, plan):
                        lead = any(what == "P" for what, *_ in plan)
                        if b == 1 and lead:
                            pool.wait_ge(bias_ready.sem, bias_ready.at(hp, 1))
                            pool.sem_inc(passed, 1)
                            columns(pool, hp + 1)
                        for what, n, back, slot in plan:
                            it = turn_of(hp, b, back)
                            if what == "P" and n < 4:
                                lead_pool(pool, it, 1 - b, n)
                            elif what == "S":
                                pool.wait_ge(inv_ready.sem, inv_ready.at(it, n))
                                p = probs[:, n % RING, :]
                                nc.gpsimd.tensor_tensor(p, p, rinv[:, n:n + 1].broadcast_to([P, L]), ALU.mult
                                                        ).then_inc(p_full.sem, 1)

                    turns(pool, body)

                @block.tensor
                def _(pe):
                    for s in (*s_full, *t_full, *o_full, *y_full):
                        s.start(pe)

                    def body(hp, b, plan):
                        for what, n, back, slot in plan:
                            it = turn_of(hp, b, back)
                            if slot is not None:
                                f = s_free[slot % 2]
                                at = turn_of(hp, b)
                                pe.wait_ge(f.sem, f.at(at, slot // 2 - 1))
                            if what == "P":
                                if n == 0 and b == 1:
                                    pe.wait_ge(w_loaded, hp * 16 + 32)
                                lead_tensor(pe, 1 - b, n, k.ps_scores[slot % 2]).then_inc(s_full[slot % 2].sem, 1)
                            elif what == "S":
                                j, qt = n % 2, n // 2
                                if n == 0:
                                    pe.wait_ge(qk_ready.sem, qk_ready.at(it, 3))
                                for i in range(2):
                                    mm = pe.matmul(k.ps_scores[slot % 2][:, i * 512:(i + 1) * 512],
                                                   q[:, b, j, qt * P:(qt + 1) * P], kr[:, b, i * 512:(i + 1) * 512],
                                                   start=True, stop=True)
                                mm.then_inc(s_full[slot % 2].sem, 1)
                            elif what == "T":
                                pe.wait_ge(p_full.sem, p_full.at(it, n))
                                turn(pe, k, probs[:, n % RING, :], t_full, t_done, it, n)
                            elif what == "V":
                                qt, bv = n, (b - back) % 2
                                for half in range(2):
                                    pe.wait_ge(t_done[half].sem, t_done[half].at(it, 2 * qt + 1))
                                if qt == 0:
                                    pe.wait_ge(v_ready.sem, v_ready.at(it, 1))
                                bank, c0 = qt // 4, (qt % 4) * P
                                if qt % 4 == 0:
                                    pe.wait_ge(y_free[bank].sem, y_free[bank].at(it, -1))
                                for t in range(TPB):
                                    for j in range(2):
                                        mm = pe.matmul(k.ps_out[bank][j * L1_D:(j + 1) * L1_D, c0:c0 + P],
                                                       v[:, bv, t, j * L1_D:(j + 1) * L1_D],
                                                       probsT[:, j, t * P:(t + 1) * P],
                                                       start=qt % 4 == 0 and t == 0,
                                                       stop=qt % 4 == 3 and t == TPB - 1, skip_group_check=True)
                                if qt % 4 == 3:
                                    mm.then_inc(o_full[bank].sem, 1)
                            elif what == "Y":
                                pe.wait_ge(o_taken[n].sem, o_taken[n].at(it, 0))
                                pair = hp - 1 if back > b else hp
                                for i in range(GROUP):
                                    mm = pe.matmul(k.ps_out[n][:, i * C:(i + 1) * C], oT[:, n, i * P:(i + 1) * P],
                                                   wo[:, ds(pair * C, C)], start=True, stop=True)
                                mm.then_inc(y_full[n].sem, 1)

                    turns(pe, body)

                @block.vector
                def _(dve):
                    for s in (*s_free, t_done[1], o_taken[1], inv_ready, *y_free):
                        s.start(dve)

                    def body(hp, b, plan):
                        def inverse(u):
                            it = turn_of(hp, b)
                            dve.wait_ge(e_full.sem, e_full.at(it, u))
                            nc.vector.reciprocal(rinv[:, u:u + 1], rsum[:, u:u + 1]).then_inc(inv_ready.sem, 1)

                        for what, n, back, slot in plan:
                            it = turn_of(hp, b, back)
                            if slot is not None and (what, n) not in (("P", 4), ("P", 5)):
                                f = s_full[slot % 2]
                                dve.wait_ge(f.sem, f.at(turn_of(hp, b), slot // 2))
                            if what == "P" and n < 4:
                                lead_vector(dve, it, 1 - b, n, k.ps_scores[slot % 2], s_free[slot % 2].sem)
                            elif what == "S":
                                j, qt = n % 2, n // 2
                                dve.wait_ge(t_full[1].sem, t_full[1].at(it, n - RING))
                                if qt == 0 and b == 0:
                                    dve.wait_ge(bias_ready.sem, bias_ready.at(hp, j))
                                dve.sem_inc(passed, 1)
                                c0 = L - P - qt * P
                                nc.vector.tensor_tensor_reduce(
                                    probs[:, n % RING, :], k.ps_scores[slot % 2][:, :], nbias[:, j, c0:c0 + L], 1.0,
                                    HUGE, ALU.add, ALU.min, nmax[:, n:n + 1]).then_inc(s_free[slot % 2].sem, 1)
                                if n >= 1:
                                    inverse(n - 1)
                                if n == U - 1:
                                    inverse(n)
                            elif what == "T":
                                take_turned(nc.vector, k, probsT[:, n % 2, :], t_full, t_done, it, n, 1)
                            elif what == "E" and n == 1:
                                dve.wait_ge(o_full[1].sem, o_full[1].at(it, 0))
                                nc.vector.tensor_copy(oT[:, 1, :], k.ps_out[1][:, :]).then_inc(o_taken[1].sem, 1)
                            elif what == "A":
                                dve.wait_ge(y_full[n].sem, y_full[n].at(it, 0))
                                c0 = ((b - back) % 2) * L + n * 512
                                nc.vector.tensor_tensor(y[:, c0:c0 + 512], y[:, c0:c0 + 512], k.ps_out[n][:, :],
                                                        ALU.add).then_inc(y_free[n].sem, 1)

                    turns(dve, body)

                @block.scalar
                def _(act):
                    for s in (bias_ready, e_full, t_done[0], o_taken[0]):
                        s.start(act)

                    def body(hp, b, plan):
                        own = any(what == "S" for what, *_ in plan)
                        lead = any(what == "P" for what, *_ in plan)
                        if b == 0 and own:
                            act.wait_ge(logs.sem, logs.at(hp, 1))
                            if not isinstance(hp, int) or hp:
                                f = s_free[(SLOTS - 1) % 2]
                                act.wait_ge(f.sem, f.at(turn_of(hp, b), -1))
                            act.sem_inc(passed, 1)
                            for j in range(2):
                                nc.scalar.activation(nbias[:, j, :], logs_[:, j, :], ACT.Identity,
                                                     scale=cols[:, 2 + j:3 + j]).then_inc(bias_ready.sem, 1)
                        for what, n, back, slot in plan:
                            it = turn_of(hp, b, back)
                            if what == "P" and n >= 4:
                                f = s_full[slot % 2]
                                act.wait_ge(f.sem, f.at(turn_of(hp, b), slot // 2))
                                lead_scalar(act, it, 1 - b, n, k.ps_scores[slot % 2], s_free[slot % 2].sem)
                            elif what == "S":
                                f = s_free[slot % 2]
                                act.wait_ge(f.sem, f.at(it, slot // 2))
                                p = probs[:, n % RING, :]
                                nc.scalar.activation(p, p, ACT.Exp, bias=nmax[:, n:n + 1], scale=-1.0,
                                                     accum_out=rsum[:, n:n + 1]).then_inc(e_full.sem, 1)
                                if n == 8 and b == 1 and lead:
                                    act.wait_ge(bias_ready.sem, bias_ready.at(hp, 1))
                                    logarithms(act, hp + 1)
                            elif what == "T":
                                take_turned(nc.scalar, k, probsT[:, n % 2, :], t_full, t_done, it, n, 0)
                            elif what == "E" and n == 0:
                                act.wait_ge(o_full[0].sem, o_full[0].at(it, 0))
                                nc.scalar.copy(oT[:, 0, :], k.ps_out[0][:, :]).then_inc(o_taken[0].sem, 1)

                    turns(act, body)

        add_norm(k, "l1o", y)



F1_DEPTH, F1_HEADS, F1_D, WINDOW = 2, 8, 64, 64
F1_INNER = F1_HEADS * F1_D
F1_HID = 341
HEAD_AT = (0, 2, 1, 3)
F1_ROWS = [P, P, F1_HID - 2 * P]


def l1_ffn(k):
    nc, d = k.nc, k.dram
    x_in = nc.dram_tensor("f1_x_in", (P, TILES * C), F32, kind="Internal").ap()
    with ExitStack() as ctx:
        kept = k.sem("f1_kept", ctx)
        block = ctx.enter_context(nc.Block())

        @block.sync
        def _(sp):
            sp.dma_start(x_in, k.x_tok[:, :]).then_inc(kept, 16)
            sp.wait_ge(kept, 16)

    for layer in range(F1_DEPTH):
        l1_local_attention(k, layer)
        l1_geglu(k, layer, x_in)


def shifted(g, own, dst, xT, col, width):
    own.step(g.tensor_copy(dst[:, 0:width], xT[:, ds(col - 1, width)]))
    return g.tensor_copy(dst[0:64, 0:width], xT[0:64, ds(col, width)])


def l1_local_attention(k, layer):
    nc, d = k.nc, k.dram
    name = f"f1a{layer}"
    PAIRS_, T = F1_HEADS // 2, TPB
    R_LAG, LAG, RING = 2, 3, 4
    with ExitStack() as ctx:
        oT = k.sb(name + "_oT", [P, PAIRS_, B * L], ctx=ctx)
        with ExitStack() as c2:
            sb = lambda n, s: k.sb(name + n, s, ctx=c2)
            w = sb("_w", [P, 3 * F1_INNER])
            scales = sb("_scales", [P, 2, 2, F1_D])
            tab = sb("_tab", [P, 2, T, 2, F1_D])
            mask = sb("_mask", [P, 2, P])
            hs = sb("_h", [P, WINDOW + L])
            buf = sb("_buf", [P, 6, 1024])
            sq, qkn, t1 = buf[:, 0:2, :], buf[:, 2:4, :], buf[:, 4:6, :]
            probs, probsT = buf[:, 0:RING, :], buf[:, 4:6, :]
            ss = sb("_ss", [P, T, 16])
            root = sb("_root", [P, T, 16])
            rn = sb("_rn", [P, 2, 2, 16])
            qT = sb("_qT", [P, 2, PAIRS_, L])
            kT = sb("_kT", [P, PAIRS_, WINDOW + L])
            v = sb("_v", [P, 2, T, F1_INNER])
            nmax = sb("_nmax", [P, 2, F1_HEADS])
            rsum = sb("_rsum", [P, T, F1_HEADS])
            rinv = sb("_rinv", [P, T, F1_HEADS])
            sm = lambda n: k.sem(name + "_" + n, c2)
            w_loaded = sm("w_loaded")
            tab_ready = sm("tab_ready")
            cleared = sm("cleared")
            h_ready = Signal(sm("h_ready"), 2)
            qk_full = Signal(sm("qk_full"), T)
            qk_free = Signal(sm("qk_free"), T)
            v_full = Signal(sm("v_full"), 2 * T)
            v_ready = Signal(sm("v_ready"), 2 * T)
            squared = Signal(sm("squared"), T)
            summed = Signal(sm("summed"), T)
            rooted = Signal(sm("rooted"), T)
            inverse = Signal(sm("inverse"), 2 * T)
            first = Signal(sm("first"), T)
            second = Signal(sm("second"), T)
            roped = Signal(sm("roped"), T)
            r_full = Signal(sm("rope_turned"), 2 * T)
            r_done = Signal(sm("qkT_ready"), 2 * T)
            s_full = Signal(sm("scores_full"), T)
            s_free = Signal(sm("scores_taken"), T)
            max_ready = Signal(sm("max_ready"), T)
            e_full = Signal(sm("exp_done"), T)
            inv_ready = Signal(sm("inv_ready"), T)
            p_full = Signal(sm("probs_ready"), T)
            t_full = [Signal(sm(f"turned_full{i}"), T) for i in range(2)]
            t_done = [Signal(sm(f"turned_taken{i}"), T) for i in range(2)]
            o_full = Signal(sm("out_full"), T)
            o_free = Signal(sm("out_taken"), T)
            passed = sm("passed")
            block = c2.enter_context(nc.Block())
            plan = order(T, 0, T, LAG)

            def heads(t):
                return t.rearrange("p (a h e) -> p a h e", a=2, e=F1_D)

            def swapped(out, src, table):
                hf = F1_D // 2
                for lo, hi in ((0, hf), (hf, 0)):
                    yield (heads(out)[:, :, :, lo:lo + hf], heads(src)[:, :, :, hi:hi + hf],
                           table[:, :, lo:lo + hf].unsqueeze(2).broadcast_to([P, 2, F1_HEADS, hf]))

            @block.sync
            def _(sp):
                for out, src in ((tab[:, :, :, :, :], d["F1_xpos"]), (mask[:, :, :], d["F1_mask"]),
                                 (scales[:, :, :, :], d[f"F1_scales{layer}"].partition_broadcast(P)),
                                 (w[:, :], d["L1_ffn_wqkv"][layer, :, :])):
                    sp.dma_start(out, src).then_inc(w_loaded, 16)

            @block.gpsimd
            def _(pool):
                for s in (first, roped, p_full):
                    s.start(pool)
                nc.gpsimd.memset(kT[:, :, 0:WINDOW], 0.0)
                nc.gpsimd.memset(qT[:, :, :, :], 0.0).then_inc(cleared, 1)
                pool.wait_ge(cleared, 1)
                pool.wait_ge(tab_ready, 4)
                with pool.Fori(0, B) as b:
                    for t in range(T):
                        s = t % 2
                        pool.wait_ge(qk_free.sem, qk_free.at(b, t))
                        if t >= 2:
                            pool.wait_ge(r_full.sem, r_full.at(b, 2 * (t - 2) + 1))
                        for a in range(2):
                            ins = nc.gpsimd.tensor_tensor(
                                heads(t1[:, s, :])[:, a, :, :], heads(qkn[:, s, :])[:, a, :, :],
                                tab[:, 0, t, a, :].unsqueeze(1).broadcast_to([P, F1_HEADS, F1_D]), ALU.mult)
                        ins.then_inc(first.sem, 1)
                        pool.wait_ge(first.sem, first.at(b, t))
                        pool.wait_ge(second.sem, second.at(b, t))
                        nc.gpsimd.tensor_tensor(t1[:, s, :], t1[:, s, :], sq[:, s, :], ALU.add
                                                ).then_inc(roped.sem, 1)
                    for t in range(T):
                        pool.wait_ge(inv_ready.sem, inv_ready.at(b, t))
                        p3 = probs[:, t % RING, :].rearrange("p (h q) -> p h q", q=P)
                        nc.gpsimd.tensor_tensor(p3, p3, rinv[:, t, :].unsqueeze(2).broadcast_to([P, F1_HEADS, P]),
                                                ALU.mult).then_inc(p_full.sem, 1)

            @block.tensor
            def _(pe):
                for s in (qk_full, v_full, r_full, s_full, *t_full, o_full):
                    s.start(pe)
                pe.wait_ge(w_loaded, 64)
                pe.wait_ge(cleared, 1)
                with pe.Fori(0, B) as b:
                    for t in range(T + R_LAG):
                        if t < T:
                            if t % (T // 2) == 0:
                                pe.wait_ge(h_ready.sem, h_ready.at(b, t // (T // 2)))
                            f = qk_free if t >= 2 else s_free
                            pe.wait_ge(f.sem, f.at(b, t - 2))
                            own, before = (hs[:, c0:c0 + P] for c0 in (WINDOW + t * P, t * P))
                            for c in range(2):
                                mm = pe.matmul(k.ps_scores[t % 2][:, c * 512:(c + 1) * 512], own,
                                               w[:, c * 512:(c + 1) * 512], start=True, stop=True)
                            mm.then_inc(qk_full.sem, 1)
                            for i, h in enumerate((before, own)):
                                f, e = (v_ready, 2 * t - 2 + i) if t else (o_free, i - 2)
                                pe.wait_ge(f.sem, f.at(b, e))
                                pe.matmul(k.ps_out[i][:, :], h, w[:, 2 * F1_INNER:3 * F1_INNER],
                                          start=True, stop=True).then_inc(v_full.sem, 1)
                        if t >= R_LAG:
                            r = t - R_LAG
                            pe.wait_ge(roped.sem, roped.at(b, r))
                            for i in range(2):
                                if r:
                                    pe.wait_ge(r_done.sem, r_done.at(b, 2 * r - 2 + i))
                                else:
                                    pe.wait_ge(t_done[i].sem, t_done[i].at(b, -1))
                                for c in range(4):
                                    c0 = (4 * i + c) * P
                                    mm = pe.transpose(k.ps_turned[i][:, c * P:(c + 1) * P], t1[:, r % 2, c0:c0 + P],
                                                      k.ident[:, :])
                                mm.then_inc(r_full.sem, 1)
                    for what, t in plan:
                        if what == "S":
                            f, e = (s_free, t - 2) if t >= 2 else (qk_free, T - 2 + t)
                            pe.wait_ge(f.sem, f.at(b, e))
                            pe.wait_ge(r_done.sem, r_done.at(b, 2 * t + 1))
                            for h in range(F1_HEADS):
                                for win in range(2):
                                    q0 = t * P + win * WINDOW
                                    mm = pe.matmul(
                                        k.ps_scores[t % 2][win * WINDOW:(win + 1) * WINDOW, h * P:(h + 1) * P],
                                        qT[:, h % 2, h // 2, q0:q0 + WINDOW], kT[:, h // 2, q0:q0 + P],
                                        start=True, stop=True)
                            mm.then_inc(s_full.sem, 1)
                        elif what == "T":
                            pe.wait_ge(p_full.sem, p_full.at(b, t))
                            if t == 0:
                                for i in range(2):
                                    pe.wait_ge(r_done.sem, r_done.at(b, 2 * T - 2 + i))
                            turn(pe, k, probs[:, t % RING, :], t_full, t_done, b, t)
                        else:
                            for half in range(2):
                                pe.wait_ge(t_done[half].sem, t_done[half].at(b, t))
                            if t < 2:
                                pe.wait_ge(v_ready.sem, v_ready.at(b, 2 * T - 1))
                            else:
                                pe.wait_ge(o_free.sem, o_free.at(b, t - 2))
                            for pair in range(PAIRS_):
                                for win in range(2):
                                    for j in range(2):
                                        h = 2 * pair + j
                                        c0 = win * WINDOW
                                        mm = pe.matmul(
                                            k.ps_out[t % 2][j * F1_D:(j + 1) * F1_D,
                                                            pair * P + c0:pair * P + c0 + WINDOW],
                                            v[:, win, t, h * F1_D:(h + 1) * F1_D],
                                            probsT[:, t % 2, h * P + c0:h * P + c0 + WINDOW], start=True, stop=True)
                            mm.then_inc(o_full.sem, 1)

            @block.vector
            def _(dve):
                for s in (summed, inverse, qk_free, second, s_free, max_ready, inv_ready, t_done[1], o_free):
                    s.start(dve)
                dve.wait_ge(w_loaded, 64)
                for a in range(2):
                    for qk in range(2):
                        nc.vector.tensor_tensor(tab[:, a, :, qk, :], tab[:, a, :, qk, :],
                                                scales[:, a, qk, :].unsqueeze(1).broadcast_to([P, T, F1_D]),
                                                ALU.mult).then_inc(tab_ready, 1)
                dve.wait_ge(tab_ready, 4)
                with dve.Fori(0, B) as b:
                    own = Chain(dve, inverse, b)
                    for t in range(T):
                        s = t % 2
                        if t < T:
                            dve.wait_ge(squared.sem, squared.at(b, t))
                            nc.vector.tensor_reduce(ss[:, t, :], sq[:, s, :].rearrange(
                                "p (h e) -> p h e", e=F1_D), AX.X, ALU.add).then_inc(summed.sem, 1)
                        if t < T:
                            dve.wait_ge(rooted.sem, rooted.at(b, t))
                            own.step(nc.vector.tensor_scalar(rn[:, s, 0, :], root[:, t, :], 1e-12, None, ALU.max))
                            own.step(nc.vector.reciprocal(rn[:, s, 1, :], rn[:, s, 0, :]))
                            if t >= 2:
                                dve.wait_ge(first.sem, first.at(b, t - 2))
                            nc.vector.tensor_tensor(
                                qkn[:, s, :].rearrange("p (h e) -> p h e", e=F1_D),
                                k.ps_scores[s][:, :].rearrange("p (h e) -> p h e", e=F1_D),
                                rn[:, s, 1, :].unsqueeze(2).broadcast_to([P, 16, F1_D]), ALU.mult
                                ).then_inc(qk_free.sem, 1)
                            dve.wait_ge(qk_free.sem, qk_free.at(b, t))
                            u = t
                            for out, src, table in swapped(sq[:, u % 2, :], qkn[:, u % 2, :], tab[:, 1, u, :, :]):
                                for a in range(2):
                                    ins = nc.vector.tensor_tensor(out[:, a], src[:, a], table[:, a], ALU.mult)
                            ins.then_inc(second.sem, 1)
                    dve.wait_ge(roped.sem, roped.at(b, T - 1))
                    for what, t in plan:
                        if what == "S":
                            dve.wait_ge(s_full.sem, s_full.at(b, t))
                            if t >= RING:
                                dve.wait_ge(t_full[1].sem, t_full[1].at(b, t - RING))
                            p3 = probs[:, t % RING, :].rearrange("p (h q) -> p h q", q=P)
                            nc.vector.tensor_tensor(
                                p3, k.ps_scores[t % 2][:, :].rearrange("p (h q) -> p h q", q=P),
                                mask[:, min(t, 1):min(t, 1) + 1, :].broadcast_to([P, F1_HEADS, P]), ALU.add
                                ).then_inc(s_free.sem, 1)
                            dve.wait_ge(s_free.sem, s_free.at(b, t))
                            nc.vector.tensor_reduce(nmax[:, t % 2, :], p3, AX.X, ALU.max, negate=True
                                                    ).then_inc(max_ready.sem, 1)
                        if what == "S" and t >= 1 or what == "T" and t == T - LAG:
                            u = t - 1 if what == "S" else T - 1
                            dve.wait_ge(e_full.sem, e_full.at(b, u))
                            nc.vector.reciprocal(rinv[:, u, :], rsum[:, u, :]).then_inc(inv_ready.sem, 1)
                        if what == "T":
                            take_turned(nc.vector, k, probsT[:, t % 2, :], t_full, t_done, b, t, 1)
                        elif what == "V":
                            dve.wait_ge(o_full.sem, o_full.at(b, t))
                            nc.vector.tensor_scalar(oT[:, :, ds(b * L + t * P, P)],
                                                    k.ps_out[t % 2][:, :].rearrange("p (c q) -> p c q", q=P), 1.0,
                                                    None, ALU.mult).then_inc(o_free.sem, 1)

            @block.scalar
            def _(act):
                for s in (h_ready, squared, rooted, r_done, v_ready, e_full, t_done[0]):
                    s.start(act)
                with act.Fori(0, B) as b:
                    act.wait_ge(v_full.sem, v_full.at(b, -1))
                    act.sem_inc(passed, 1)
                    edges = (0, WINDOW + L // 2, WINDOW + L)
                    for half in range(2):
                        c0, c1 = edges[half:half + 2]
                        for lo in (0, 64):
                            at = b * XB + (PAD - WINDOW - lo // 64 + c0)
                            ins = nc.scalar.activation(hs[lo:lo + 64, c0:c1], k.xT[lo:lo + 64, ds(at, c1 - c0)],
                                                       ACT.Copy)
                        ins.then_inc(h_ready.sem, 1)
                    for t in range(T + R_LAG):
                        if t < T:
                            act.wait_ge(qk_full.sem, qk_full.at(b, t))
                            if t >= 2:
                                act.wait_ge(roped.sem, roped.at(b, t - 2))
                            nc.scalar.activation(sq[:, t % 2, :], k.ps_scores[t % 2][:, :], ACT.Square
                                                 ).then_inc(squared.sem, 1)
                            for i in range(2):
                                act.wait_ge(v_full.sem, v_full.at(b, 2 * t + i))
                                nc.scalar.copy(v[:, i, t, :], k.ps_out[i][:, :]).then_inc(v_ready.sem, 1)
                                if i == 0:
                                    act.wait_ge(summed.sem, summed.at(b, t))
                                    nc.scalar.activation(root[:, t, :], ss[:, t, :], ACT.Sqrt
                                                         ).then_inc(rooted.sem, 1)
                        if t >= R_LAG:
                            r = t - R_LAG
                            act.wait_ge(r_full.sem, r_full.at(b, 2 * r))
                            for j in range(2):
                                rows = slice(j * F1_D, (j + 1) * F1_D)
                                ins = nc.scalar.copy(qT[rows, j, :, r * P:(r + 1) * P],
                                                     k.ps_turned[0][rows, :].rearrange("p (c q) -> p c q", q=P))
                            ins.then_inc(r_done.sem, 1)
                            act.wait_ge(r_full.sem, r_full.at(b, 2 * r + 1))
                            nc.scalar.copy(kT[:, :, WINDOW + r * P:WINDOW + (r + 1) * P],
                                           k.ps_turned[1][:, :].rearrange("p (c q) -> p c q", q=P)
                                           ).then_inc(r_done.sem, 1)
                    for what, t in plan:
                        if what == "S":
                            act.wait_ge(max_ready.sem, max_ready.at(b, t))
                            for h in range(F1_HEADS):
                                p1 = probs[:, t % RING, h * P:(h + 1) * P]
                                ins = nc.scalar.activation(p1, p1, ACT.Exp, bias=nmax[:, t % 2, h:h + 1],
                                                           accum_out=rsum[:, t, h:h + 1])
                            ins.then_inc(e_full.sem, 1)
                        elif what == "T":
                            take_turned(nc.scalar, k, probsT[:, t % 2, :], t_full, t_done, b, t, 0)

        wo = k.sb(name + "_wo", [P, 4, C], ctx=ctx)
        project_turned(k, name + "o", range(NG), 4, lambda c, t: oT[:, c, t * P:(t + 1) * P], wo[:, :, :],
                       d["F1_wo"][layer, :, :, :], None, None, normed=False)


def l1_geglu(k, layer, x_in):
    nc, d = k.nc, k.dram
    name = f"f1g{layer}"
    last = layer == F1_DEPTH - 1
    CH, HALVES = 3, NG // B
    with ExitStack() as ctx:
        sb = lambda n, s: k.sb(name + n, s, ctx=ctx)
        sem = lambda n: k.sem(name + n, ctx)
        w1 = sb("_w1", [P, 2 * F1_HID])
        w2 = sb("_w2", [P, CH, C])
        cols = sb("_cols", [P, 8])
        b2 = sb("_b2", [1, C])
        hs = sb("_h", [P, 2, 512])
        hn = sb("_hn", [P, 2, 512])
        hT = sb("_hT", [P, 2, 512])
        stats = sb("_stats", [P, 2, GROUP, 6])
        mv = sb("_mv", [P, 2, GROUP, 2])
        rs = sb("_rs", [P, 2, 3, GROUP])
        gate = sb("_gate", [P, 2, 512])
        hid = sb("_hid", [P, 2, CH, 512])
        x0 = sb("_x_in", [P, TILES * C]) if last else None
        w_loaded, x_loaded = sem("_w_loaded"), sem("_x_loaded")
        own_pool = Signal(sem("_own_pool"), HALVES)
        h_ready = Signal(sem("_h_ready"), HALVES)
        ht_full = Signal(sem("_ht_full"), HALVES)
        var = Signal(sem("_var"), HALVES)
        root = Signal(sem("_root"), HALVES)
        hn_ready = Signal(sem("_hn_ready"), HALVES)
        hb_full = Signal(sem("_hb_full"), HALVES)
        hT_ready = Signal(sem("_hT_ready"), HALVES)
        per = HALVES * CH // 2
        u_full = [Signal(sem(f"_u_full{i}"), per) for i in range(2)]
        gate_ready = Signal(sem("_gate_ready"), HALVES * CH)
        hid_ready = [Signal(sem(f"_hid_ready{i}"), per) for i in range(2)]
        passed = sem("_passed")
        own = Signal(sem("_own_dve"), HALVES * ((Norm.DVE_STEPS + 1 if last else 1) + 12))
        norm = Norm(k, ctx, name + "n", HALVES)
        block = ctx.enter_context(nc.Block())

        @block.sync
        def _(sp):
            for out, src in ((w1, d["L1_ffn_w1"][layer, :, :]), (cols, d["F1_cols"][layer, :, :]),
                             (b2, d["L1_ffn_b2"][layer:layer + 1, :])):
                sp.dma_start(out[:, :], src).then_inc(w_loaded, 16)
            sp.dma_start(w2[:, :, :], d["F1_w2"][layer, :, :, :]).then_inc(w_loaded, 16)
            if last:
                sp.dma_start(x0[:, :], x_in).then_inc(x_loaded, 16)

        @block.gpsimd
        def _(pool):
            h_ready.start(pool)
            own_pool.start(pool)
            with pool.Fori(0, B) as b:
                chain = Chain(pool, own_pool, b)
                for g in range(HALVES):
                    pool.wait_ge(ht_full.sem, ht_full.at(b, g - HALVES))
                    shifted(nc.gpsimd, chain, hs[:, g, :], k.xT, b * XB + PAD + g * 512, 512).then_inc(h_ready.sem, 1)

        @block.tensor
        def _(pe):
            norm.start(pe, None, None)
            for s in (ht_full, hb_full, *u_full):
                s.start(pe)
            pe.wait_ge(w_loaded, 64)
            with pe.Fori(0, B) as b:
                for g in range(HALVES):
                    pe.wait_ge(h_ready.sem, h_ready.at(b, g))
                    pe.wait_ge(norm.xT_ready.sem, norm.xT_ready.at(b, -1))
                    for i in range(GROUP):
                        mm = pe.transpose(k.ps_turned[g][:, i * P:(i + 1) * P], hs[:, g, i * P:(i + 1) * P],
                                          k.ident[:, :])
                    mm.then_inc(ht_full.sem, 1)
                for g in range(HALVES):
                    pe.wait_ge(hn_ready.sem, hn_ready.at(b, g))
                    for i in range(GROUP):
                        mm = pe.transpose(k.ps_turned[g][:, i * P:(i + 1) * P], hn[:, g, i * P:(i + 1) * P],
                                          k.ident[:, :])
                    mm.then_inc(hb_full.sem, 1)
                for g in range(HALVES):
                    pe.wait_ge(hT_ready.sem, hT_ready.at(b, g))
                    for c in range(CH):
                        n = g * CH + c
                        pe.wait_ge(hid_ready[n % 2].sem, hid_ready[n % 2].at(b, n // 2 - 1))
                        for part in range(2):
                            c0 = part * F1_HID + c * P
                            mm = pe.matmul(k.ps_scores[n % 2][0:F1_ROWS[c], part * 512:(part + 1) * 512],
                                           w1[:, c0:c0 + F1_ROWS[c]], hT[:, g, :], start=True, stop=True)
                        mm.then_inc(u_full[n % 2].sem, 1)
                for g in range(HALVES):
                    y = k.ps_out[g]
                    pe.wait_ge(norm.y_free.sem, norm.y_free.at(b, g - 2))
                    for c in range(CH):
                        n = g * CH + c
                        pe.wait_ge(hid_ready[n % 2].sem, hid_ready[n % 2].at(b, n // 2))
                        for i in range(GROUP):
                            pe.matmul(y[:, i * C:(i + 1) * C], hid[0:F1_ROWS[c], g, c, i * P:(i + 1) * P],
                                      w2[0:F1_ROWS[c], c, :], start=(c == 0 and i == 0), stop=False,
                                      skip_group_check=True)
                    for i in range(GROUP):
                        mm = pe.matmul(y[:, i * C:(i + 1) * C], k.ones[0:1, 0:P], b2[:, :], start=False,
                                       stop=i == GROUP - 1, skip_group_check=True)
                    mm.then_inc(norm.y_full.sem, 1)
                for g in range(HALVES):
                    norm.tensor(pe, b, g, g, k.ps_turned[0])

        @block.scalar
        def _(act):
            norm.start(None, None, act)
            for s in (root, hT_ready, gate_ready):
                s.start(act)
            with act.Fori(0, B) as b:
                for g in range(HALVES):
                    act.wait_ge(var.sem, var.at(b, g))
                    nc.scalar.activation(rs[:, g, 1, :], rs[:, g, 0, :], ACT.Sqrt).then_inc(root.sem, 1)
                for g in range(HALVES):
                    act.wait_ge(hb_full.sem, hb_full.at(b, g))
                    nc.scalar.activation(hT[:, g, :], k.ps_turned[g][:, :], ACT.Identity, bias=cols[:, 1:2],
                                         scale=cols[:, 0:1]).then_inc(hT_ready.sem, 1)
                for g in range(HALVES):
                    for c in range(CH):
                        n = g * CH + c
                        act.wait_ge(u_full[n % 2].sem, u_full[n % 2].at(b, n // 2))
                        act.wait_ge(hid_ready[n % 2].sem, hid_ready[n % 2].at(b, n // 2 - 1))
                        nc.scalar.activation(gate[0:F1_ROWS[c], n % 2, :],
                                             k.ps_scores[n % 2][0:F1_ROWS[c], 512:1024], ACT.Gelu,
                                             bias=cols[0:F1_ROWS[c], 5 + c:6 + c]).then_inc(gate_ready.sem, 1)
                if last:
                    for g in range(HALVES):
                        norm.scalar_root(act, b, g, g)
                for g in range(HALVES):
                    norm.scalar_store(act, b, g, k.ps_turned[0], b * XB + PAD + g * 512)

        @block.vector
        def _(dve):
            norm.start(None, dve, None)
            for s in (var, hn_ready, *hid_ready, own):
                s.start(dve)
            if last:
                dve.wait_ge(x_loaded, 16)
            with dve.Fori(0, B) as b:
                chain = Chain(dve, own, b)
                for g in range(HALVES):
                    dve.wait_ge(ht_full.sem, ht_full.at(b, g))
                    dve.sem_inc(passed, 1)
                    for i in range(GROUP):
                        chain.done(nc.vector.bn_stats(stats[:, g, i, :], k.ps_turned[g][:, i * P:(i + 1) * P]))
                    chain.wait_apart(passed)
                    for i in range(GROUP):
                        chain.done(nc.vector.bn_aggr(mv[:, g, i, :], stats[:, g, i, :]))
                    chain.wait()
                    nc.vector.tensor_scalar(rs[:, g, 0, :], mv[:, g, :, 1], EPS, None, ALU.add).then_inc(var.sem, 1)
                for g in range(HALVES):
                    dve.wait_ge(root.sem, root.at(b, g))
                    chain.step(nc.vector.reciprocal(rs[:, g, 2, :], rs[:, g, 1, :]))
                    for i in range(GROUP):
                        ins = nc.vector.tensor_scalar(hn[:, g, i * C:(i + 1) * C],
                                                      k.ps_turned[g][:, i * P:(i + 1) * P], mv[:, g, i, 0:1],
                                                      rs[:, g, 2, i:i + 1], ALU.subtract, ALU.mult)
                        if i < GROUP - 1:
                            chain.done(ins)
                    ins.then_inc(hn_ready.sem, 1)
                for g in range(HALVES):
                    for c in range(CH):
                        n = g * CH + c
                        r = F1_ROWS[c]
                        dve.wait_ge(gate_ready.sem, gate_ready.at(b, n))
                        nc.vector.scalar_tensor_tensor(hid[0:r, g, c, :], k.ps_scores[n % 2][0:r, 0:512],
                                                       cols[0:r, 2 + c:3 + c], gate[0:r, n % 2, :], ALU.add,
                                                       ALU.mult).then_inc(hid_ready[n % 2].sem, 1)
                for g in range(HALVES):
                    tile0 = b * TPB + g * GROUP
                    norm.vector(dve, chain, b, g, g, tile0, k.ps_out[g][:, :], normed=last,
                                also=x0[:, ds(tile0 * C, 512)] if last else None)
                chain.close()



def small_head_attention(k, name, inputs, causal, denom, wo_dram, bo_dram):
    nc, d = k.nc, k.dram
    H, D = 16, 8
    SET_PAIRS = 2
    PAIRS_ALL = B * H // 2
    SETS = PAIRS_ALL // SET_PAIRS
    STEPS = 2 * TPB
    LEADS = 6
    steps = [(0, n) for n in range(LEADS)]
    for n in range(TPB - LEADS):
        steps += [(1, n), (0, LEADS + n)]
    steps += [(1, n) for n in range(TPB - LEADS, TPB)]
    step_of = {s: m for m, s in enumerate(steps)}
    v_slot = lambda kb: step_of[1, 0] + 2 + 2 * kb
    MAX_ROW, PARTS = 96, 3
    q_parts = nc.dram_tensor(f"{name}_parts_q", (PARTS, B * P, L), BF16, kind="Internal").ap()
    k_parts = nc.dram_tensor(f"{name}_parts_k", (B * P * PARTS, L), BF16, kind="Internal").ap()
    with ExitStack() as ctx:
        sb = lambda n, s, dt=F32: k.sb(name + n, s, dt, ctx=ctx)
        w = sb("_w", [P, 3 * C])
        wo, bo = sb("_wo", [P, 1, C]), sb("_bo", [1, C])
        extra = sb("_extra", [P, 1])
        tri = sb("_tri", [P, 512])
        tile_rows = sb("_tile_rows", [P, TPB])
        gather = sb("_gather", [P, 4, P + 96])
        v = sb("_v", [P, B * C, TPB])
        acc = sb("_acc", [P, SETS, 512])
        qs = sb("_q_rows", [P, 2, 2, L], BF16)
        ks = sb("_k_rows", [P, 2, 2, L], BF16)
        zeros = sb("_zeros", [P, L], BF16)
        vz = sb("_v_pair", [P, 2, 2, TPB, 32])
        mins = sb("_mins", [P, 2, 2, TPB])
        oT = sb("_oT", [P, B * L])
        with ExitStack() as c2:
            loaded, full, taken, own, split, moved, cleared = (k.sem(name + "p_" + n, c2) for n in (
                "loaded", "full", "taken", "own", "split", "moved", "cleared"))
            raw = k.sb(name + "_raw", [P, 2, 512], ctx=c2)
            rest = k.sb(name + "_rest", [P, 2, 2, 512], ctx=c2)
            parts = k.sb(name + "_parts", [P, 2, PARTS, B * L], BF16, ctx=c2)
            block = c2.enter_context(nc.Block())
            jobs = [(kind, i) for i in range(NG) for kind in range(2)] + [(2, i) for i in range(NG)]

            @block.sync
            def _(sp):
                sp.dma_start(w[:, :], d[inputs]).then_inc(loaded, 16)
                if denom is not None:
                    sp.dma_start(extra[:, :], d[denom]).then_inc(loaded, 16)
                sp.dma_start(tile_rows[:, :], d["tile_rows"]).then_inc(moved, 16)
                sp.dma_start(gather[:, :, :], d["gather"]).then_inc(moved, 16)
                sp.dma_start(wo[:, :, :], d[wo_dram]).then_inc(moved, 16)
                sp.dma_start(bo[:, :], d[bo_dram]).then_inc(moved, 16)
                for b in range(B):
                    tokens = slice(b * L, (b + 1) * L)
                    sp.wait_ge(split, 4 * (2 * (2 * b + 1) + 1))
                    sp.dma_start(q_parts[:, b * P:(b + 1) * P, :].rearrange("s p t -> p s t"), parts[:, 0, :, tokens]
                                 ).then_inc(moved, 16)
                    sp.wait_ge(split, 4 * (2 * (2 * b + 1) + 2))
                    k_batch = k_parts[b * P * PARTS:(b + 1) * P * PARTS, :].rearrange(
                        "(h s d) t -> s h d t", s=PARTS, d=D)
                    for i in range(PARTS):
                        sp.dma_start(k_batch[i], parts[:, 1, i, tokens]).then_inc(moved, 16)
                sp.wait_ge(moved, 16 * (4 + B * (1 + PARTS)))

            @block.gpsimd
            def _(pool):
                if denom is None:
                    nc.gpsimd.memset(extra[:, :], 1e-8).then_inc(own, 1)
                if causal:
                    nc.gpsimd.memset(tri[:, :], 0.0).then_inc(own, 1)
                    pool.wait_ge(own, 1)
                    nc.gpsimd.affine_select(out=tri[:, :], in_=tri[:, :], compare_op=ALU.is_ge, fill=HUGE,
                                            base=3 * P, pattern=[[-1, 512]], channel_multiplier=1).then_inc(own, 1)
                    pool.wait_ge(own, 2)
                nc.gpsimd.memset(mins[:, :, :, :], HUGE)
                nc.gpsimd.memset(qs[:, :, :, :], 0.0)
                nc.gpsimd.memset(zeros[:, :], 0.0)
                for par in range(2):
                    nc.gpsimd.memset(vz[:, par, :, :, :], 0.0)
                nc.gpsimd.memset(ks[:, :, :, :], 0.0).then_inc(cleared, 1)
                pool.wait_ge(cleared, 1)
                for par in range(2):
                    ins = nc.gpsimd.memset(vz[:, par, :, :, 16 * par + D:16 * par + 2 * D], 1.0)
                ins.then_inc(cleared, 1)
                pool.wait_ge(cleared, 2)
                nc.gpsimd.memset(ks[MAX_ROW:P, :, :, :], -1.0).then_inc(cleared, 1)
                pool.wait_ge(cleared, 3)
                pool.wait_ge(own, 1)

            @block.tensor
            def _(pe):
                pe.wait_ge(loaded, 16 if denom is None else 32)
                for n, (kind, i) in enumerate(jobs):
                    bank = k.ps_out[n % 2]
                    if n >= 2:
                        pe.wait_ge(taken, n - 1)
                    if kind < 2:
                        mm = pe.matmul(bank[:, :], w[:, kind * C:(kind + 1) * C], k.xT[:, xcol(i):xcol(i) + 512],
                                       start=True, stop=True)
                    else:
                        for t in range(GROUP):
                            c0 = xcol(i) + t * P
                            mm = pe.matmul(bank[:, t * C:(t + 1) * C], k.xT[:, c0:c0 + P], w[:, 2 * C:3 * C],
                                           start=True, stop=True)
                    mm.then_inc(full, 1)

            @block.scalar
            def _(act):
                for n, (kind, i) in enumerate(jobs):
                    act.wait_ge(full, n + 1)
                    bank = k.ps_out[n % 2][:, :]
                    if kind < 2:
                        if n >= 2:
                            act.wait_ge(split, 4 * (n - 1))
                        nc.scalar.activation(raw[:, n % 2, :], bank, ACT.Copy,
                                             scale=-float(D ** -0.5) if kind == 0 else 1.0).then_inc(taken, 1)
                    else:
                        b, t0 = i // 2, (i % 2) * GROUP
                        nc.scalar.copy(v[:, b * C:(b + 1) * C, t0:t0 + GROUP],
                                       bank.rearrange("p (t c) -> p c t", c=C)).then_inc(taken, 1)
                if denom is not None:
                    act.wait_ge(loaded, 32)
                    nc.scalar.activation(extra[:, :], extra[:, :], ACT.Exp).then_inc(taken, 1)
                act.wait_ge(taken, len(jobs) + (denom is not None))

            @block.vector
            def _(dve):
                own_ = Count(dve, split)
                for n, (kind, i) in enumerate(jobs[:2 * NG]):
                    dve.wait_ge(taken, n + 1)
                    c = slice(i * 512, (i + 1) * 512)
                    x, r = raw[:, n % 2, :], rest[:, n % 2, :, :]
                    own_.step(nc.vector.tensor_copy(parts[:, kind, 0, c], x))
                    own_.step(nc.vector.tensor_tensor(r[:, 0, :], x, parts[:, kind, 0, c], ALU.subtract))
                    own_.step(nc.vector.tensor_copy(parts[:, kind, 1, c], r[:, 0, :]))
                    own_.step(nc.vector.tensor_tensor(parts[:, kind, 2, c], r[:, 0, :], parts[:, kind, 1, c],
                                                      ALU.subtract))

        with ExitStack() as c2:
            sb = lambda n, s, dt=F32: k.sb(name + n, s, dt, ctx=c2)
            pT = sb("_probs_T", [P, STEPS, L])
            junk = sb("_junk", [P, 512])
            low = sb("_lowest", [P, 2, 2, TPB])
            low_b = sb("_low_bf16", [P, 2, 2, TPB], BF16)
            low_p = sb("_low_parts", [P, 2, PARTS * TPB])
            sm = lambda n: k.sem(name + "a_" + n, c2)

            pieces = []
            for qt in range(TPB):
                seen = (qt + 1) * P if causal else L
                pieces += [(qt, c, min(512, seen - c)) for c in range(0, seen, 512)]
            per_head = len(pieces)
            last_piece = {qt: max(i for i, p in enumerate(pieces) if p[0] == qt) for qt in range(TPB)}
            first_query = (lambda kb: kb * P) if causal else (lambda kb: 0)

            rows_ready = [[Signal(sm(f"rows_ready{par}{j}"), 5, 16) for j in range(2)] for par in range(2)]
            s_full = [Signal(sm(f"s_full{i}"), per_head) for i in range(2)]
            min_ready = Signal(sm("min_ready"), 2 * per_head)
            lowest = Signal(sm("lowest"), 2)
            low_ready = Signal(sm("low_ready"), 12)
            turned = Signal(sm("low_turned"), 2)
            max_rows = Signal(sm("max_rows"), 2)
            r_full = [Signal(sm(f"r_full{i}"), TPB) for i in range(2)]
            e_full = Signal(sm("exp_done"), STEPS)
            cut = Signal(sm("cut"), STEPS)
            v_ready = Signal(sm("v_ready"), 1)
            v_done = Signal(sm("v_done"), TPB)
            acc_free = Signal(sm("acc_taken"), 1)
            passed, passed_dve = sm("passed"), sm("passed_dve")
            block = c2.enter_context(nc.Block())
            s_bank, r_slot, acc_bank, low_bank = k.ps_turned, k.ps_scores, k.ps_out[0], k.ps_out[1]

            def turn_plan(scores, values, before):
                out = []
                for n in range(STEPS):
                    first, second = ([("S", n // TPB, (n % TPB, half))] if scores else [] for half in range(2))
                    r = [("R", 1, n)] if values else []
                    maxima = []
                    if scores:
                        maxima += {TPB: [("split", 0, 0)], TPB + 3: [("turn", 0, 0)], TPB + 4: [("rows", 0, 0)]
                                   }.get(n, [])
                    if values:
                        maxima += {0: [("split", 1, 1)], 3: [("turn", 1, 1)], 4: [("rows", 1, 1)]}.get(n, [])
                    v_ = [("V", 1, kb) for kb in range(TPB) if values and v_slot(kb) == n]
                    v_ += [("V", 2, kb) for kb in range(TPB) if before and v_slot(kb) == n + STEPS]
                    out += (first + second + r + maxima + v_) if causal else (first + maxima + v_ + second + r)
                return out

            def turns(eng, body):
                body(0, 0, turn_plan(True, False, False))
                body(0, 1, turn_plan(True, True, False))
                with eng.Fori(1, SETS) as s:
                    body(s, 0, turn_plan(True, True, True))
                    body(s, 1, turn_plan(True, True, True))
                body(SETS, 0, turn_plan(False, True, True))
                body(SETS, 1, turn_plan(False, False, True))

            def pair(s, par, back=0):
                return s * 2 + (par - back)

            @block.sync
            def _(sp):
                for par in range(2):
                    for j in range(2):
                        rows_ready[par][j].start(sp)

                def load(s, par):
                    for j in range(2):
                        if not isinstance(s, int):
                            m = step_of[j, TPB - 1]
                            f = r_full[m % 2]
                            sp.wait_ge(f.sem, f.at(pair(s, par, 2), m // 2))
                        r0 = s * (4 * D) + (2 * par + j) * D
                        done = rows_ready[par][j].sem
                        sp.dma_start(qs[MAX_ROW:P, par, j, :], zeros[MAX_ROW:P, :]).then_inc(done, 16)
                        for i in range(PARTS):
                            block_rows = slice(PARTS * i * D, PARTS * (i + 1) * D)
                            q_rows = q_parts[i, ds(r0, D), :].unsqueeze(0).broadcast_to([PARTS, D, L])
                            sp.dma_start(qs[block_rows, par, j, :], q_rows).then_inc(done, 16)
                        k_rows = k_parts[ds(PARTS * r0, PARTS * D), :]
                        sp.dma_start(ks[0:PARTS * PARTS * D, par, j, :],
                                     k_rows.unsqueeze(0).broadcast_to([PARTS, PARTS * D, L])).then_inc(done, 16)

                load(0, 0)
                load(0, 1)
                with sp.Fori(1, SETS) as s:
                    load(s, 0)
                    load(s, 1)

            @block.gpsimd
            def _(pool):
                for s in (low_ready, cut, v_ready):
                    s.start(pool)
                def body(s, par, plan):
                    if ("R", 1, 0) in plan:
                        c = (par - 1) % 2
                        p = pair(s, par, 1)
                        if not isinstance(s, int) or p >= 2:
                            pool.wait_ge(v_done.sem, v_done.at(pair(s, par, 3), TPB - 1))
                            pool.sem_inc(passed, 1)
                        for j in range(2):
                            at = p * (2 * D) + j * D
                            ins = nc.gpsimd.tensor_copy(
                                vz[:, c, j, :, 16 * c:16 * c + D].rearrange("p t d -> p d t"), v[:, ds(at, D), :])
                        ins.then_inc(v_ready.sem, 1)
                    for what, x, n in plan:
                        if what == "split":
                            p = pair(s, par, n)
                            j = x
                            pool.wait_ge(lowest.sem, lowest.at(p, j))
                            chain = Chain(pool, low_ready, p)
                            chain.n = 6 * j
                            lo, lb, lp = low[:, j, :, :], low_b[:, j, :, :], low_p[:, j, :]
                            g, one = nc.gpsimd, k.ones[:, 0:TPB]
                            chain.step(g.tensor_tensor(lb[:, 0, :], lo[:, 0, :], one, ALU.mult))
                            chain.step(g.tensor_tensor(lp[:, 0:TPB], lb[:, 0, :], one, ALU.mult))
                            chain.step(g.tensor_tensor(lo[:, 1, :], lo[:, 0, :], lp[:, 0:TPB], ALU.subtract))
                            chain.step(g.tensor_tensor(lb[:, 1, :], lo[:, 1, :], one, ALU.mult))
                            chain.step(g.tensor_tensor(lp[:, TPB:2 * TPB], lb[:, 1, :], one, ALU.mult))
                            chain.done(g.tensor_tensor(lp[:, 2 * TPB:], lo[:, 1, :], lp[:, TPB:2 * TPB],
                                                       ALU.subtract))
                        elif what == "R" and causal:
                            kb = steps[n][1]
                            pool.wait_ge(e_full.sem, e_full.at(pair(s, par, 1), n))
                            pool.sem_inc(passed, 1)
                            diag = pT[:, n, kb * P:(kb + 1) * P]
                            nc.gpsimd.affine_select(out=diag, in_=diag, compare_op=ALU.is_ge, fill=0.0, base=0,
                                                    pattern=[[1, P]], channel_multiplier=-1).then_inc(cut.sem, 1)

                turns(pool, body)

            @block.tensor
            def _(pe):
                for s in (*s_full, turned, *r_full, v_done):
                    s.start(pe)

                def body(s, par, plan):
                    for what, x, n in plan:
                        if what == "S":
                            j, (qt, half) = x, n
                            p = pair(s, par)
                            if qt == 0 and half == 0:
                                r = rows_ready[par][j]
                                pe.wait_ge(r.sem, r.at(s, 4))
                            for i, (t, c, width) in enumerate(pieces):
                                if (t, c // 512) != (qt, half):
                                    continue
                                e = j * per_head + i
                                pe.wait_ge(min_ready.sem, min_ready.at(p, e - 2))
                                pe.matmul(s_bank[e % 2][:, 0:width], qs[0:P, par, j, qt * P:(qt + 1) * P],
                                          ks[0:P, par, j, c:c + width], start=True, stop=True
                                          ).then_inc(s_full[e % 2].sem, 1)
                        elif what == "turn":
                            p, j = pair(s, par, n), x
                            pe.wait_ge(low_ready.sem, low_ready.at(p, 6 * j + 5))
                            pe.transpose(low_bank[0:PARTS * TPB, j * P:(j + 1) * P], low_p[:, j, :],
                                         k.ident[:, :]).then_inc(turned.sem, 1)
                        elif what == "R":
                            p, c = pair(s, par, 1), (par - 1) % 2
                            j, kb = steps[n]
                            if kb == 0:
                                pe.wait_ge(max_rows.sem, max_rows.at(p, j))
                            pe.wait_ge(e_full.sem, e_full.at(p, n - 2))
                            for half in range(2):
                                c0 = max(first_query(kb), half * 512)
                                if c0 < (half + 1) * 512:
                                    mm = pe.matmul(r_slot[n % 2][:, c0:(half + 1) * 512],
                                                   ks[:, c, j, kb * P:(kb + 1) * P], qs[:, c, j, c0:(half + 1) * 512],
                                                   start=True, stop=True)
                            mm.then_inc(r_full[n % 2].sem, 1)
                        elif what == "V":
                            p, c, kb = pair(s, par, x), (par - x) % 2, n
                            if kb == 0:
                                pe.wait_ge(v_ready.sem, v_ready.at(p, 0))
                                if c == 0:
                                    set_ = s if par == 1 else s - 1
                                    pe.wait_ge(acc_free.sem, acc_free.at(set_, -1))
                            ready = cut if causal else e_full
                            pe.wait_ge(ready.sem, ready.at(p, step_of[1, kb]))
                            for j in range(2):
                                for half in range(2):
                                    c0 = max(first_query(kb), half * 512)
                                    if c0 < (half + 1) * 512:
                                        g = 2 * j + half
                                        mm = pe.matmul(acc_bank[32 * g:32 * g + 32, c0 - half * 512:512],
                                                       vz[:, c, j, kb, :],
                                                       pT[:, step_of[j, kb], c0:(half + 1) * 512],
                                                       start=c == 0 and kb == 0, stop=c == 1 and kb == TPB - 1,
                                                       skip_group_check=True)
                            mm.then_inc(v_done.sem, 1)

                turns(pe, body)

            @block.vector
            def _(dve):
                for s in (min_ready, lowest):
                    s.start(dve)

                def body(s, par, plan):
                    for what, x, n in plan:
                        if what == "S":
                            j, (qt, half) = x, n
                            p = pair(s, par)
                            for i, (t, c, width) in enumerate(pieces):
                                if (t, c // 512) != (qt, half):
                                    continue
                                e = j * per_head + i
                                f = s_full[e % 2]
                                dve.wait_ge(f.sem, f.at(p, e // 2))
                                bank = s_bank[e % 2][:, 0:width]
                                low_ = mins[:, j, c // 512, qt:qt + 1]
                                if causal and i == last_piece[qt]:
                                    dve.wait_ge(min_ready.sem, min_ready.at(p, e - 1))
                                    dve.sem_inc(passed_dve, 1)
                                    ins = nc.vector.tensor_tensor_reduce(
                                        junk[:, 0:width], bank, tri[:, 512 - width:512], 1.0, HUGE, ALU.add,
                                        ALU.min, low_)
                                else:
                                    ins = nc.vector.tensor_reduce(low_, bank, AX.X, ALU.min)
                                ins.then_inc(min_ready.sem, 1)
                        elif what == "split":
                            p, j = pair(s, par, n), x
                            dve.wait_ge(min_ready.sem, min_ready.at(p, (j + 1) * per_head - 1))
                            nc.vector.tensor_tensor(low[:, j, 0, :], mins[:, j, 0, :], mins[:, j, 1, :], ALU.min
                                                    ).then_inc(lowest.sem, 1)

                turns(dve, body)

            @block.scalar
            def _(act):
                for s in (e_full, acc_free, max_rows):
                    s.start(act)

                def body(s, par, plan):
                    for what, x, n in plan:
                        if what == "R":
                            p, kb = pair(s, par, 1), steps[n][1]
                            f = r_full[n % 2]
                            act.wait_ge(f.sem, f.at(p, n // 2))
                            c0 = first_query(kb)
                            nc.scalar.activation(pT[:, n, c0:L], r_slot[n % 2][:, c0:L], ACT.Exp, scale=-1.0
                                                 ).then_inc(e_full.sem, 1)
                        elif what == "rows":
                            p, c, j = pair(s, par, n), (par - n) % 2, x
                            act.wait_ge(turned.sem, turned.at(p, j))
                            rows = PARTS * TPB
                            for t in range(TPB):
                                ins = nc.scalar.activation(
                                    qs[MAX_ROW:MAX_ROW + rows, c, j, t * P:(t + 1) * P],
                                    low_bank[0:rows, j * P:(j + 1) * P], ACT.Copy, scale=tile_rows[0:rows, t:t + 1])
                            ins.then_inc(max_rows.sem, 1)
                        elif what == "V" and (par - x) % 2 == 1 and n == TPB - 1:
                            act.wait_ge(v_done.sem, v_done.at(pair(s, par, x), n))
                            nc.scalar.copy(acc[:, ds(s - 1, 1), :],
                                           acc_bank[:, :].rearrange("p (o c) -> p o c", o=1)
                                           ).then_inc(acc_free.sem, 1)

                turns(act, body)

        with ExitStack() as c2:
            full, used, ready = (k.sem(name + "g_" + n, c2) for n in ("gathered", "used", "inverse"))
            den = k.sb(name + "_den", [P, 2, 512], ctx=c2)
            block = c2.enter_context(nc.Block())
            PER = SETS // B

            @block.tensor
            def _(pe):
                for n in range(NG):
                    if n >= 2:
                        pe.wait_ge(used, n - 1)
                    for kind in (1, 0):
                        bank = k.ps_scores[n % 2][:, kind * 512:(kind + 1) * 512]
                        for s in range(PER):
                            w0 = 96 - 32 * s
                            mm = pe.matmul(bank, gather[:, 2 * (n % 2) + kind, w0:w0 + P],
                                           acc[:, (n // 2) * PER + s, :], start=s == 0, stop=s == PER - 1)
                        mm.then_inc(full, 1)

            @block.vector
            def _(dve):
                own_ = Count(dve, ready)
                for n in range(NG):
                    slot = k.ps_scores[n % 2]
                    dve.wait_ge(full, 2 * n + 1)
                    own_.step(nc.vector.tensor_scalar(den[:, 0, :], slot[:, 512:1024], extra[:, 0:1], None, ALU.add))
                    own_.step(nc.vector.reciprocal(den[:, 1, :], den[:, 0, :]))
                    dve.wait_ge(full, 2 * n + 2)
                    nc.vector.tensor_tensor(oT[:, n * 512:(n + 1) * 512], slot[:, 0:512], den[:, 1, :], ALU.mult
                                            ).then_inc(used, 1)
                    dve.wait_ge(used, n + 1)

        project_turned(k, name + "o", range(NG), 1, lambda c, t: oT[:, t * P:(t + 1) * P], wo[:, :, :],
                       None, bo[:, :], None)


def l2_attention(k):
    small_head_attention(k, "l2", "L2_qkv", True, "L2_denom_bias", "L2_wo", "L2_attn_bo")


def l3_attention(k):
    small_head_attention(k, "l3", "L3_qkv", False, None, "L3_wo", "L3_attn_bo")



EXPERTS = 8


def softmax_rows(dve, own, probs, scores, tmp, passes, acts, n):
    v = dve
    T, E = probs.shape[1], probs.shape[2]
    own.step(v.tensor_reduce(tmp, scores, AX.X, ALU.max))
    v.tensor_tensor(probs, scores, tmp.unsqueeze(2).broadcast_to([P, T, E]), ALU.subtract).then_inc(passes, 1)
    own.eng.wait_ge(acts, n)
    own.step(v.tensor_reduce(tmp, probs, AX.X, ALU.add))
    own.step(v.reciprocal(tmp, tmp))
    own.step(v.tensor_tensor(probs, probs, tmp.unsqueeze(2).broadcast_to([P, T, E]), ALU.mult))


def top_two(dve, own, gates, probs, rank, tmp, hit, scale):
    v = dve
    T, E = probs.shape[1], probs.shape[2]
    wide = tmp.unsqueeze(2).broadcast_to([P, T, E])
    for n in range(2):
        own.step(v.tensor_reduce(tmp, probs, AX.X, ALU.max))
        own.step(v.tensor_tensor(hit, probs, wide, ALU.is_equal))
        own.step(v.tensor_tensor(hit, hit, rank, ALU.mult))
        own.step(v.tensor_reduce(tmp, hit, AX.X, ALU.max))
        own.step(v.tensor_tensor(hit, rank, wide, ALU.is_equal))
        if n == 0:
            own.step(v.scalar_tensor_tensor(gates, probs, scale, hit, ALU.mult, ALU.mult))
            own.step(v.scalar_tensor_tensor(probs, hit, -4.0, probs, ALU.mult, ALU.add))
        else:
            own.step(v.scalar_tensor_tensor(probs, probs, scale, hit, ALU.mult, ALU.mult))
            own.step(v.tensor_tensor(gates, gates, probs, ALU.add))


def route(k, name, w_dram, b_dram, rank, gates, scale, groups):
    nc, d = k.nc, k.dram
    n_in = EXPERTS + groups
    with ExitStack() as ctx:
        sb = lambda n, s: k.sb(name + n, s, ctx=ctx)
        loaded, logits, own_s, passes, acts = (k.sem(name + n, ctx) for n in (
            "_loaded", "_logits", "_own", "_passes", "_acts"))
        w, bias = sb("_w", [P, n_in]), sb("_b", [1, n_in])
        lg = sb("_lg", [P, TILES, n_in])
        probs = sb("_probs", [P, TILES, EXPERTS])
        hit = sb("_hit", [P, TILES, EXPERTS])
        tmp = sb("_tmp", [P, TILES])
        gp = sb("_gp", [P, TILES, 2])
        sel = sb("_sel", [P, TILES, 2])
        best = sb("_best", [P, TILES])
        block = ctx.enter_context(nc.Block())
        bank = k.ps_out[0][:, 0:TILES * n_in].rearrange("p (t e) -> p t e", e=n_in)

        @block.sync
        def _(sp):
            sp.dma_start(w[:, :], d[w_dram]).then_inc(loaded, 16)
            sp.dma_start(rank[:, :, :], d["rank"]).then_inc(loaded, 16)
            if b_dram:
                sp.dma_start(bias[:, :], d[b_dram]).then_inc(loaded, 16)

        @block.tensor
        def _(pe):
            pe.wait_ge(loaded, 48 if b_dram else 32)
            for t in range(TILES):
                c0 = xcol(t // GROUP) + (t % GROUP) * P
                mm = pe.matmul(bank[:, t, :], k.xT[:, c0:c0 + P], w[:, :], start=True, stop=not b_dram)
                if b_dram:
                    mm = pe.matmul(bank[:, t, :], k.ones[0:1, 0:P], bias[:, :], start=False, stop=True)
            mm.then_inc(logits, 1)

        @block.scalar
        def _(act):
            if groups:
                act.wait_ge(passes, 1)
                nc.scalar.activation(gp[:, :, :], gp[:, :, :], ACT.Exp).then_inc(acts, 1)
            n = 2 if groups else 1
            act.wait_ge(passes, n)
            nc.scalar.activation(probs[:, :, :], probs[:, :, :], ACT.Exp).then_inc(acts, 1)
            act.wait_ge(acts, n)

        @block.vector
        def _(dve):
            own = Count(dve, own_s)
            v = nc.vector
            dve.wait_ge(logits, 1)
            dve.wait_ge(loaded, 48 if b_dram else 32)
            own.step(v.tensor_copy(lg[:, :, :], bank))
            if groups:
                softmax_rows(v, own, gp[:, :, :], lg[:, :, 0:groups], tmp[:, :], passes, acts, 1)
                own.done(v.tensor_tensor(best[:, :], gp[:, :, 0], gp[:, :, 1], ALU.max))
                own.done(v.tensor_tensor(sel[:, :, 0], gp[:, :, 0], gp[:, :, 1], ALU.is_ge))
                own.step(v.tensor_tensor(sel[:, :, 1], gp[:, :, 1], gp[:, :, 0], ALU.is_gt))
                own.step(v.tensor_scalar(sel[:, :, :], sel[:, :, :], HUGE, -HUGE, ALU.mult, ALU.add))
                per = EXPERTS // groups
                for g in range(groups):
                    e = lg[:, :, groups + g * per:groups + (g + 1) * per]
                    own.done(v.tensor_tensor(e, e, sel[:, :, g].unsqueeze(2).broadcast_to([P, TILES, per]), ALU.add))
                own.wait()
            softmax_rows(v, own, probs[:, :, :], lg[:, :, groups:n_in], tmp[:, :], passes, acts, 2 if groups else 1)
            if groups:
                own.step(v.tensor_tensor(probs[:, :, :], probs[:, :, :],
                                         best[:, :].unsqueeze(2).broadcast_to([P, TILES, EXPERTS]), ALU.mult))
            top_two(v, own, gates[:, :, :], probs[:, :, :], rank[:, :, :], tmp[:, :], hit[:, :, :], scale)



F2_HID = 256


def l2_ffn(k):
    nc, d = k.nc, k.dram
    CH, HALVES = F2_HID // P, NG // B
    NP = 2 * CH
    with ExitStack() as ctx:
        sb = lambda n, s: k.sb("f2" + n, s, ctx=ctx)
        rank = sb("_rank", [P, TILES, EXPERTS])
        gates = sb("_gates", [P, TILES, EXPERTS])
        w_up = sb("_w_up", [P, NP, 2, P])
        w_out = sb("_w_out", [P, CH, C])
        w2 = sb("_w2", [P, CH, EXPERTS * C])
        silu = sb("_silu", [P, 2, 512])
        hid = sb("_hid", [P, 2, NP, 512])
        prod = sb("_prod", [P, 2, EXPERTS, C])
        part = sb("_part", [P, 2, C])
        route(k, "f2r", "L2_router_w", "L2_router_b", rank, gates, 1.0, 2)
        sem = lambda n: k.sem("f2" + n, ctx)
        w_loaded = sem("_w_loaded")
        per = HALVES * NP // 2
        u_full = [Signal(sem(f"_u_full{i}"), per) for i in range(2)]
        silu_ready = Signal(sem("_silu_ready"), HALVES * NP)
        hid_ready = [Signal(sem(f"_hid_ready{i}"), per) for i in range(2)]
        r_full = [Signal(sem(f"_r_full{i}"), HALVES * GROUP // 2) for i in range(2)]
        r_free = [Signal(sem(f"_r_free{i}"), HALVES * GROUP // 2) for i in range(2)]
        own = Signal(sem("_own_dve"), HALVES * (Norm.DVE_STEPS + 2 * GROUP))
        norm = Norm(k, ctx, "f2n", HALVES)
        block = ctx.enter_context(nc.Block())

        @block.sync
        def _(sp):
            sp.dma_start(w_up[:, :, :, :], d["L2_w_up"]).then_inc(w_loaded, 16)
            sp.dma_start(w_out[:, :, :], d["L2_w_out"]).then_inc(w_loaded, 16)
            sp.dma_start(w2[:, :, :], d["L2_w2"]).then_inc(w_loaded, 16)

        @block.tensor
        def _(pe):
            norm.start(pe, None, None)
            for s in (*u_full, *r_full):
                s.start(pe)
            pe.wait_ge(w_loaded, 48)
            with pe.Fori(0, B) as b:
                for g in range(HALVES):
                    for c in range(NP):
                        n = g * NP + c
                        pe.wait_ge(hid_ready[n % 2].sem, hid_ready[n % 2].at(b, n // 2 - 1))
                        pe.wait_ge(r_free[n % 2].sem, r_free[n % 2].at(b, -1))
                        for i in range(2):
                            mm = pe.matmul(k.ps_scores[n % 2][:, i * 512:(i + 1) * 512], w_up[:, c, i, :],
                                           k.xT[:, ds(b * XB + PAD + g * 512, 512)], start=True, stop=True)
                        mm.then_inc(u_full[n % 2].sem, 1)
                for g in range(HALVES):
                    y = k.ps_out[g]
                    pe.wait_ge(norm.y_free.sem, norm.y_free.at(b, g - 2))
                    for c in range(CH):
                        n = g * NP + c
                        pe.wait_ge(hid_ready[n % 2].sem, hid_ready[n % 2].at(b, n // 2))
                        for i in range(GROUP):
                            mm = pe.matmul(y[:, i * C:(i + 1) * C], hid[:, g, c, i * P:(i + 1) * P], w_out[:, c, :],
                                           start=(c == 0 and i == 0), stop=c == CH - 1 and i == GROUP - 1,
                                           skip_group_check=True)
                    mm.then_inc(norm.y_full.sem, 1)
                for s in range(2):
                    pe.wait_ge(hid_ready[s].sem, hid_ready[s].at(b, per - 1))
                for g in range(HALVES):
                    for i in range(GROUP):
                        n = g * GROUP + i
                        slot = k.ps_scores[n % 2]
                        pe.wait_ge(r_free[n % 2].sem, r_free[n % 2].at(b, n // 2 - 1))
                        for h in range(2):
                            for c in range(CH):
                                mm = pe.matmul(slot[:, h * 512:(h + 1) * 512], hid[:, g, CH + c, i * P:(i + 1) * P],
                                               w2[:, c, h * 512:(h + 1) * 512], start=c == 0, stop=c == CH - 1)
                        mm.then_inc(r_full[n % 2].sem, 1)
                for g in range(HALVES):
                    norm.tensor(pe, b, g, g, k.ps_turned[0])

        @block.scalar
        def _(act):
            norm.start(None, None, act)
            silu_ready.start(act)
            with act.Fori(0, B) as b:
                for g in range(HALVES):
                    for c in range(NP):
                        n = g * NP + c
                        act.wait_ge(u_full[n % 2].sem, u_full[n % 2].at(b, n // 2))
                        act.wait_ge(hid_ready[n % 2].sem, hid_ready[n % 2].at(b, n // 2 - 1))
                        nc.scalar.activation(silu[:, n % 2, :], k.ps_scores[n % 2][:, 0:512], ACT.Silu
                                             ).then_inc(silu_ready.sem, 1)
                for g in range(HALVES):
                    norm.scalar_root(act, b, g, g)
                for g in range(HALVES):
                    norm.scalar_store(act, b, g, k.ps_turned[0], b * XB + PAD + g * 512)

        @block.vector
        def _(dve):
            norm.start(None, dve, None)
            for s in (*hid_ready, *r_free, own):
                s.start(dve)
            with dve.Fori(0, B) as b:
                chain = Chain(dve, own, b)
                for g in range(HALVES):
                    for c in range(NP):
                        n = g * NP + c
                        dve.wait_ge(silu_ready.sem, silu_ready.at(b, n))
                        nc.vector.tensor_tensor(hid[:, g, c, :], k.ps_scores[n % 2][:, 512:1024], silu[:, n % 2, :],
                                                ALU.mult).then_inc(hid_ready[n % 2].sem, 1)
                for g in range(HALVES):
                    tile0 = b * TPB + g * GROUP

                    def routed(res):
                        for i in range(GROUP):
                            n = g * GROUP + i
                            s = n % 2
                            dve.wait_ge(r_full[s].sem, r_full[s].at(b, n // 2))
                            gate = gates[:, ds(tile0 + i, 1), :].rearrange("p o e -> p (o e)")
                            nc.vector.tensor_tensor(
                                prod[:, s, :, :], k.ps_scores[s][:, :].rearrange("p (e c) -> p e c", c=C),
                                gate.unsqueeze(2).broadcast_to([P, EXPERTS, C]), ALU.mult).then_inc(r_free[s].sem, 1)
                            dve.wait_ge(r_free[s].sem, r_free[s].at(b, n // 2))
                            chain.step(nc.vector.tensor_reduce(
                                part[:, s, :], prod[:, s, :, :].rearrange("p e c -> p c e"), AX.X, ALU.add))
                            r = res[:, i * C:(i + 1) * C]
                            chain.step(nc.vector.tensor_tensor(r, r, part[:, s, :], ALU.add))

                    norm.vector(dve, chain, b, g, g, tile0, k.ps_out[g][:, :], more=routed)
                chain.close()



F3_HID = 512
F3_SCALE = float(1.0 / np.sqrt(1.25))


def l3_ffn(k):
    nc, d = k.nc, k.dram
    CH, HALVES, E = F3_HID // P, NG // B, EXPERTS + 1
    with ExitStack() as ctx:
        sb = lambda n, s: k.sb("f3" + n, s, ctx=ctx)
        rank = sb("_rank", [P, TILES, EXPERTS])
        gates = sb("_gates", [P, TILES, EXPERTS])
        w1 = sb("_w1", [P, E, F3_HID])
        w2 = sb("_w2", [P, E, CH, C])
        b1 = sb("_b1", [P, E * CH])
        b2 = sb("_b2_shared", [1, C])
        b2r = sb("_b2_routed", [P, EXPERTS, C])
        hid = sb("_hid", [P, 2, CH, 512])
        scaled = sb("_scaled", [P, 2, 512])
        route(k, "f3r", "L3_router_w", None, rank, gates, F3_SCALE, 0)
        sem = lambda n: k.sem("f3" + n, ctx)
        w_loaded, b2_loaded = sem("_w_loaded"), sem("_b2_loaded")
        per = HALVES * E * CH // 4
        h_full = [Signal(sem(f"_h_full{i}"), per) for i in range(4)]
        h_ready = [Signal(sem(f"_h_ready{i}"), per) for i in range(4)]
        e_full = [Signal(sem(f"_e_full{i}"), HALVES * E // 2) for i in range(2)]
        e_free = [Signal(sem(f"_e_free{i}"), HALVES * E // 2) for i in range(2)]
        own = Signal(sem("_own_dve"), HALVES * (Norm.DVE_STEPS + 2 * EXPERTS))
        norm = Norm(k, ctx, "f3n", HALVES)
        block = ctx.enter_context(nc.Block())

        def bank(n):
            return k.ps_scores[(n % 4) // 2][:, (n % 2) * 512:(n % 2 + 1) * 512]

        @block.sync
        def _(sp):
            sp.dma_start(w1[:, :, :], d["L3_w1"]).then_inc(w_loaded, 16)
            sp.dma_start(w2[:, :, :, :], d["L3_w2"]).then_inc(w_loaded, 16)
            sp.dma_start(b1[:, :], d["L3_b1"]).then_inc(w_loaded, 16)
            sp.dma_start(b2[:, :], d["L3_b2_shared"]).then_inc(w_loaded, 16)
            sp.dma_start(b2r[:, :, :], d["L3_b2_routed"].partition_broadcast(P)).then_inc(b2_loaded, 16)

        @block.tensor
        def _(pe):
            norm.start(pe, None, None)
            for s in (*h_full, *e_full):
                s.start(pe)
            pe.wait_ge(w_loaded, 64)

            def up(b, m):
                g, e = m // E, m % E
                for c in range(CH):
                    n = m * CH + c
                    pe.wait_ge(h_ready[n % 4].sem, h_ready[n % 4].at(b, n // 4 - 1))
                    if c == 0:
                        pe.wait_ge(e_full[m % 2].sem, e_full[m % 2].at(b, m // 2 - 1))
                    pe.matmul(bank(n), w1[:, e, c * P:(c + 1) * P], k.xT[:, ds(b * XB + PAD + g * 512, 512)],
                              start=True, stop=True).then_inc(h_full[n % 4].sem, 1)

            def down(b, m):
                g, e = m // E, m % E
                y = k.ps_out[m % 2]
                pe.wait_ge(e_free[m % 2].sem, e_free[m % 2].at(b, m // 2 - 1))
                for c in range(CH):
                    n = m * CH + c
                    pe.wait_ge(h_ready[n % 4].sem, h_ready[n % 4].at(b, n // 4))
                    for i in range(GROUP):
                        last = e > 0 and c == CH - 1 and i == GROUP - 1
                        mm = pe.matmul(y[:, i * C:(i + 1) * C], hid[:, m % 2, c, i * P:(i + 1) * P],
                                       w2[:, e, c, :], start=(c == 0 and i == 0), stop=last, skip_group_check=True)
                if e == 0:
                    for i in range(GROUP):
                        mm = pe.matmul(y[:, i * C:(i + 1) * C], k.ones[0:1, 0:P], b2[:, :], start=False,
                                       stop=i == GROUP - 1, skip_group_check=True)
                mm.then_inc(e_full[m % 2].sem, 1)

            with pe.Fori(0, B) as b:
                for m in range(HALVES * E):
                    up(b, m)
                    if m >= 1:
                        down(b, m - 1)
                down(b, HALVES * E - 1)
                for g in range(HALVES):
                    norm.tensor(pe, b, g, g, k.ps_turned[0])

        @block.scalar
        def _(act):
            norm.start(None, None, act)
            for s in h_ready:
                s.start(act)
            with act.Fori(0, B) as b:
                for n in range(HALVES * E * CH):
                    m, c = n // CH, n % CH
                    act.wait_ge(h_full[n % 4].sem, h_full[n % 4].at(b, n // 4))
                    if c == 0:
                        act.wait_ge(e_full[m % 2].sem, e_full[m % 2].at(b, m // 2 - 1))
                    at = (m % E) * CH + c
                    nc.scalar.activation(hid[:, m % 2, c, :], bank(n), ACT.Gelu_apprx_tanh, bias=b1[:, at:at + 1]
                                         ).then_inc(h_ready[n % 4].sem, 1)
                    if n == (E + 1) * CH - 1:
                        norm.scalar_root(act, b, 0, 0)
                norm.scalar_root(act, b, 1, 1)
                for g in range(HALVES):
                    norm.scalar_store(act, b, g, k.ps_turned[0], b * XB + PAD + g * 512)

        @block.vector
        def _(dve):
            norm.start(None, dve, None)
            for s in (*e_free, own):
                s.start(dve)
            dve.wait_ge(b2_loaded, 16)
            with dve.Fori(0, B) as b:
                chain = Chain(dve, own, b)
                for g in range(HALVES):
                    tile0 = b * TPB + g * GROUP

                    def experts(res):
                        for e in range(1, E):
                            m = g * E + e
                            s = m % 2
                            dve.wait_ge(e_full[s].sem, e_full[s].at(b, m // 2))
                            gate = gates[:, ds(tile0, GROUP), e - 1:e].broadcast_to([P, GROUP, C])
                            y = scaled[:, s, :].rearrange("p (t c) -> p t c", c=C)
                            nc.vector.tensor_tensor(
                                y, k.ps_out[s][:, :].rearrange("p (t c) -> p t c", c=C),
                                b2r[:, e - 1:e, :].broadcast_to([P, GROUP, C]), ALU.add).then_inc(e_free[s].sem, 1)
                            dve.wait_ge(e_free[s].sem, e_free[s].at(b, m // 2))
                            chain.step(nc.vector.tensor_tensor(y, y, gate, ALU.mult))
                            chain.step(nc.vector.tensor_tensor(res, res, scaled[:, s, :], ALU.add))

                    m0 = g * E
                    norm.vector(dve, chain, b, g, g, tile0, k.ps_out[m0 % 2][:, :], scale=F3_SCALE, more=experts,
                                y_full=(e_full[m0 % 2], m0 // 2), y_free=(e_free[m0 % 2], m0 // 2))
                chain.close()



def layouts(inputs):
    a = {n: np.asarray(v) for n, v in inputs.items()}
    out = {n: a[n] for n in ("L0_attn_x", "L0_attn_Wq", "L0_attn_Wk", "L0_attn_Wv", "L0_attn_Wo")}
    out["L0_bqk"] = np.stack([a["L0_attn_bq"], a["L0_attn_bk"]], 1)
    out["L0_bv"], out["L0_attn_bo"] = a["L0_attn_bv"], a["L0_attn_bo"][None, :]
    f32 = np.float32
    p = np.arange(P)
    out["head_mask8"] = ((p[:, None] // 8 == np.arange(16)[None, :]) / np.sqrt(8.0)).astype(f32)
    w = np.zeros((P, TPB, L0_GROUPS), f32)
    for j in range(TPB):
        for half in range(2):
            rows = slice(64 * half, 64 * half + 64)
            w[rows, j, half] = 1.0
            for off in (-2, -1, 1, 2):
                if 0 <= 2 * j + half + off < L // SEG:
                    w[rows, j, 2 + half + off + 3] = 0.25
    out["L0_group_weights"] = w
    out["L0_ffn_W_exp"] = a["L0_ffn_W_exp"]
    out["L0_W_con_T"] = a["L0_ffn_W_con"].T
    out["L0_ffn_b_exp"] = a["L0_ffn_b_exp"][None, :]
    out["L0_up_bias"] = a["L0_ffn_up_bias"].reshape(4, P).T
    out["L0_y_bias"] = np.stack([a["L0_ffn_b_con"], a["L0_ffn_down_bias"]])
    out["L0_up_weights"] = a["L0_ffn_up_weights"].reshape(-1)
    out["L0_down_weights"] = a["L0_ffn_down_weights"].reshape(-1)
    w = a["L1_attn_qkv_w"].reshape(3, PAIRS, 2, L1_D, C)
    swap = np.roll(w, L1_D // 2, axis=3)
    w = np.stack([w[0], swap[0], w[1], swap[1], w[2]], 1)
    out["L1_qkv"] = w.transpose(0, 4, 1, 2, 3).reshape(PAIRS, C, 5 * P)
    out["L1_out_w"] = a["L1_attn_out_w"].T.reshape(8, P, C).transpose(1, 0, 2).reshape(P, 8 * C)
    sign = np.where(p % L1_D < L1_D // 2, -1.0, 1.0).astype(f32)
    out["L1_freq"] = np.stack([np.tile(a["L1_attn_rope_freqs"], 4), sign, np.full(P, np.pi / 2, f32)], 1)
    out["L1_bias_ap"] = np.concatenate([a["L1_attn_bias_a"].reshape(-1), a["L1_attn_bias_p"].reshape(-1)])
    half = np.arange(0, F1_D, 2, dtype=f32)
    t = np.arange(L, dtype=f32)
    fr = t[:, None] * (f32(1.0) / f32(10000.0) ** (half / f32(F1_D)))[None, :]
    base = (half + f32(0.4 * F1_D)) / f32(1.4 * F1_D)
    scale = base[None, :] ** ((t - L // 2) / f32(WINDOW // 2))[:, None]
    cos, sin = np.cos(fr.astype(np.float64)).astype(f32), np.sin(fr.astype(np.float64)).astype(f32)
    two = lambda x, y: np.concatenate([x, y], 1)
    cq, sq = two(cos * scale, cos * scale) * f32(8), two(-sin * scale, sin * scale) * f32(8)
    ck, sk = two(cos / scale, cos / scale), two(-sin / scale, sin / scale)
    xpos = np.stack([np.stack([cq, ck]), np.stack([sq, sk])]).astype(f32)
    out["F1_xpos"] = xpos.reshape(2, 2, TPB, P, F1_D).transpose(3, 0, 2, 1, 4)
    for layer in range(F1_DEPTH):
        both = np.stack([a["L1_ffn_q_scale"][layer], a["L1_ffn_k_scale"][layer]])
        out[f"F1_scales{layer}"] = np.stack([both, np.roll(both, F1_D // 2, axis=1)])
    for n in ("L1_ffn_wqkv", "L1_ffn_w1", "L1_ffn_b2"):
        out[n] = a[n]
    out["F1_wo"] = a["L1_ffn_wo"].reshape(F1_DEPTH, 4, P, C).transpose(0, 2, 1, 3)
    cols = np.zeros((F1_DEPTH, P, 8), f32)
    w2 = np.zeros((F1_DEPTH, P, 3, C), f32)
    cols[:, :, 0], cols[:, :, 1] = a["L1_ffn_ln_g"], a["L1_ffn_ln_b"]
    for c, r in enumerate(F1_ROWS):
        cols[:, 0:r, 2 + c] = a["L1_ffn_b1"][:, c * P:c * P + r]
        cols[:, 0:r, 5 + c] = a["L1_ffn_b1"][:, F1_HID + c * P:F1_HID + c * P + r]
        w2[:, 0:r, c, :] = a["L1_ffn_w2"][:, c * P:c * P + r, :]
    out["F1_cols"], out["F1_w2"] = cols, w2
    for n in ("L2", "L3"):
        out[n + "_qkv"] = np.concatenate([a[f"{n}_attn_W{m}"].T for m in "qkv"], 1)
        out[n + "_wo"] = a[n + "_attn_Wo"].T[:, None, :]
        out[n + "_attn_bo"] = a[n + "_attn_bo"][None, :]
    out["L2_denom_bias"] = np.repeat(a["L2_attn_denom_bias"].reshape(-1), 8)[:, None]
    gather = np.zeros((2, 2, 2, 2, 8, 2, 2, P + 96), f32)
    for j, half, pair, kind, e in np.ndindex(2, 2, 2, 2, 8):
        gather[j, half, pair, kind, e, half, kind, 96 + 16 * pair + 8 * j + e] = 1.0
    out["gather"] = gather.reshape(P, 4, P + 96)
    i, j = (p % WINDOW)[:, None], np.arange(P)[None, :]
    seen = (j >= i) & (j <= i + WINDOW)
    seen = np.stack([seen & ((p[:, None] >= WINDOW) | (j >= WINDOW)), seen], 1)
    out["F1_mask"] = np.where(seen, 0.0, -HUGE).astype(f32)
    out["tile_rows"] = (p[:, None] % TPB == np.arange(TPB)[None, :]).astype(f32)
    out["rank"] = np.broadcast_to(np.arange(EXPERTS, 0, -1, dtype=f32), (P, TILES, EXPERTS))
    out["L2_router_w"] = np.concatenate([a["L2_ffn_wg"], a["L2_ffn_we"]], 0).T
    out["L2_router_b"] = np.concatenate([a["L2_ffn_gb"], a["L2_ffn_eb"]])[None, :]
    pairs = lambda w: w.reshape(2, F2_HID // P, P, C).transpose(3, 1, 0, 2)
    out["L2_w_up"] = np.concatenate([pairs(a["L2_ffn_w_in"]), pairs(a["L2_ffn_w1"])], 1)
    out["L2_w_out"] = a["L2_ffn_w_out"].T.reshape(F2_HID // P, P, C).transpose(1, 0, 2)
    out["L2_w2"] = a["L2_ffn_w2"].reshape(EXPERTS, C, F2_HID // P, P).transpose(3, 2, 0, 1).reshape(
        P, F2_HID // P, EXPERTS * C)
    out["L3_router_w"] = a["L3_ffn_w_router"].T
    all_of = lambda s, e: np.concatenate([a["L3_ffn_" + s][None], a["L3_ffn_" + e]], 0)
    out["L3_w1"] = all_of("Ws1", "W1").transpose(2, 0, 1)
    out["L3_w2"] = all_of("Ws2", "W2").reshape(9, C, 4, P).transpose(3, 0, 2, 1)
    out["L3_b1"] = all_of("bs1", "b1").reshape(9 * 4, P).T
    out["L3_b2_shared"], out["L3_b2_routed"] = a["L3_ffn_bs2"][None, :], a["L3_ffn_b2"]
    return {n: np.ascontiguousarray(v) for n, v in out.items()}


STAGES = [l0, l1_attention, l1_ffn, l2_attention, l2_ffn, l3_attention, l3_ffn]


def build(nc, dram, out, stages=99):
    with ExitStack() as ctx:
        k = Kernel(nc, ctx, dram)
        load_x(k)
        for stage in STAGES[:stages]:
            stage(k)
        with ExitStack() as c2:
            stored = k.sem("stored", c2)
            block = c2.enter_context(nc.Block())

            @block.sync
            def _(sp):
                sp.dma_start(out.rearrange("b (t p) c -> p (b t) c", p=P),
                             k.x_tok[:, :].rearrange("p (t c) -> p t c", c=C)).then_inc(stored, 16)
                sp.wait_ge(stored, 16)


def kernel(**inputs):
    import concourse.bacc as bacc
    from concourse.bass_utils import run_bass_kernel_spmd

    nc = bacc.Bacc("TRN2", target_bir_lowering=False, num_devices=1)
    arrays = layouts(inputs)
    dram = {n: nc.dram_tensor("in_" + n, v.shape, mybir.dt.from_np(v.dtype), kind="ExternalInput").ap()
            for n, v in arrays.items()}
    out = nc.dram_tensor("out_x", (B, L, C), F32, kind="ExternalOutput").ap()
    build(nc, dram, out)
    r = run_bass_kernel_spmd(nc, [{"in_" + n: v for n, v in arrays.items()}], core_ids=[0])
    return r.results[0]["out_x"]
```
